# Optimizing a Trainium2 kernel written in Bass

```python
import numpy as np
import jax
import jax.numpy as jnp

def _softmax(x, axis=-1):
    return jax.nn.softmax(x, axis=axis)
def _gelu(x):
    return jax.nn.gelu(x, approximate=True)
def _silu(x):
    return jax.nn.silu(x)
def _sigmoid(x):
    return jax.nn.sigmoid(x)
def _layernorm(x, axis=-1, eps=1e-5):
    m = jnp.mean(x, axis=axis, keepdims=True)
    v = jnp.var(x, axis=axis, keepdims=True)
    return (x - m) / jnp.sqrt(v + eps)
def _scatter_add(tgt, idx, src, axis=0):
    return tgt.at[idx].add(src)
def _segment_sum(src, seg, n):
    return jax.ops.segment_sum(src, seg, n)

kernel_name = 'mk_conv_attn_hybrid_d4_conv_nhwc128_04dadd'

def setup_inputs(seed: int = 0):
    np.random.seed(seed)
    _w = jnp.asarray
    def _rec_inputs():
        import jax
        import jax.numpy as jnp
        _gk = jax.random.key(seed)
        x = -0.0005207 + 1.001 * jax.random.normal(jax.random.fold_in(_gk, 1), (4, 32, 128, 128), jnp.float32)
        return x
    x = _rec_inputs()
    def _L0_conv_setup():
        import jax, jax.numpy as jnp
        import numpy as np
        import math
        D_MODEL = 128
        HEADS = 4
        HD = D_MODEL // HEADS
        D_INNER = 2 * D_MODEL
        D_STATE = 16
        D_CONV = 4
        DT_RANK = math.ceil(D_MODEL / 16)
        BSZ, TLEN, NNODE = (4, 32, 128)
        LN_EPS = 1e-05

        def layernorm(x, g, b):
            m = jnp.mean(x, axis=-1, keepdims=True)
            v = jnp.var(x, axis=-1, keepdims=True)
            return (x - m) * jax.lax.rsqrt(v + LN_EPS) * g + b

        def _gat(h, adj, Wq, Wk, Wv, Wo, bo):
            BT, N, _ = h.shape
            q = (h @ Wq).reshape(BT, N, HEADS, HD)
            k = (h @ Wk).reshape(BT, N, HEADS, HD)
            v = (h @ Wv).reshape(BT, N, HEADS, HD)
            scores = jnp.einsum('bnhd,bmhd->bhnm', q, k) / math.sqrt(HD)
            scores = jnp.where(adj[None, None] == 0, -1000000000.0, scores)
            attn = jax.nn.softmax(scores, axis=-1)
            o = jnp.einsum('bhnm,bmhd->bnhd', attn, v).reshape(BT, N, D_MODEL)
            return h + o @ Wo + bo

        def _mamba(xt, in_proj, conv_w, conv_b, x_proj, dt_w, dt_b, A_log, Dp, out_w, out_b):
            BN, T, _ = xt.shape
            xz = xt @ in_proj
            xc, z = (xz[..., :D_INNER], xz[..., D_INNER:])
            xp = jnp.pad(xc, ((0, 0), (D_CONV - 1, 0), (0, 0)))
            xconv = conv_b
            for kk in range(D_CONV):
                xconv = xconv + conv_w[:, kk] * xp[:, kk:kk + T, :]
            xc = jax.nn.silu(xconv)
            dbc = xc @ x_proj
            dt = jax.nn.softplus(dbc[..., :DT_RANK] @ dt_w + dt_b)
            Bm = dbc[..., DT_RANK:DT_RANK + D_STATE]
            Cm = dbc[..., DT_RANK + D_STATE:]
            A = -jnp.exp(A_log)
            dA = jnp.exp(dt[..., None] * A)
            dBx = (dt * xc)[..., None] * Bm[:, :, None, :]

            def step(hprev, inp):
                dA_t, dBx_t, C_t = inp
                hnew = dA_t * hprev + dBx_t
                y_t = jnp.einsum('bds,bs->bd', hnew, C_t)
                return (hnew, y_t)
            h0 = jnp.zeros((BN, D_INNER, D_STATE), xt.dtype)
            _, ys = jax.lax.scan(step, h0, (jnp.swapaxes(dA, 0, 1), jnp.swapaxes(dBx, 0, 1), jnp.swapaxes(Cm, 0, 1)))
            y = jnp.swapaxes(ys, 0, 1) + Dp * xc
            y = y * jax.nn.silu(z)
            return y @ out_w + out_b
        key = jax.random.key(seed)
        ks = jax.random.split(key, 16)
        f32 = jnp.float32

        def rn(k, shape, sc):
            return jax.random.normal(k, shape, f32) * sc
        x = rn(ks[0], (BSZ, TLEN, NNODE, D_MODEL), 1.0)
        adj = (jax.random.uniform(ks[1], (NNODE, NNODE)) < 0.08).astype(f32)
        adj = jnp.clip(adj + jnp.eye(NNODE, dtype=f32), 0.0, 1.0)
        s_in = 1.0 / math.sqrt(D_MODEL)
        return {'x': x, 'adj': adj, 'Wq': rn(ks[2], (D_MODEL, D_MODEL), s_in), 'Wk': rn(ks[3], (D_MODEL, D_MODEL), s_in), 'Wv': rn(ks[4], (D_MODEL, D_MODEL), s_in), 'Wo': rn(ks[5], (D_MODEL, D_MODEL), s_in), 'bo': jnp.zeros((D_MODEL,), f32), 'ns_g': jnp.ones((D_MODEL,), f32), 'ns_b': jnp.zeros((D_MODEL,), f32), 'nt_g': jnp.ones((D_MODEL,), f32), 'nt_b': jnp.zeros((D_MODEL,), f32), 'in_proj': rn(ks[6], (D_MODEL, 2 * D_INNER), s_in), 'conv_w': rn(ks[7], (D_INNER, D_CONV), 1.0 / math.sqrt(D_CONV)), 'conv_b': jnp.zeros((D_INNER,), f32), 'x_proj': rn(ks[8], (D_INNER, DT_RANK + 2 * D_STATE), 1.0 / math.sqrt(D_INNER)), 'dt_w': rn(ks[9], (DT_RANK, D_INNER), 1.0 / math.sqrt(DT_RANK)), 'dt_b': rn(ks[10], (D_INNER,), 0.1) - 4.0, 'A_log': jnp.log(jnp.broadcast_to(jnp.arange(1, D_STATE + 1, dtype=f32), (D_INNER, D_STATE))), 'Dp': jnp.ones((D_INNER,), f32), 'out_w': rn(ks[11], (D_INNER, D_MODEL), 1.0 / math.sqrt(D_INNER)), 'out_b': jnp.zeros((D_MODEL,), f32)}
    _L0_conv_all = _L0_conv_setup()
    _L0_conv_in = {k: v for k, v in _L0_conv_all.items() if k in ('adj', 'Wq', 'Wk', 'Wv', 'Wo', 'bo', 'ns_g', 'ns_b', 'nt_g', 'nt_b', 'in_proj', 'conv_w', 'conv_b', 'x_proj', 'dt_w', 'dt_b', 'A_log', 'Dp', 'out_w', 'out_b', )}
    del _L0_conv_all

    def _L1_conv_setup():
        import jax, jax.numpy as jnp
        import numpy as np
        N_HEADS = 16
        TEMPERATURE = 1.0
        EPS = 1e-05

        def _gelu(z):
            return jax.nn.gelu(z, approximate=False)

        def instance_norm(x, g, b):
            mu = jnp.mean(x, axis=(-2, -1), keepdims=True)
            var = jnp.var(x, axis=(-2, -1), keepdims=True)
            return (x - mu) * jax.lax.rsqrt(var + EPS) * g[:, None, None] + b[:, None, None]

        def conv1x1(x, w, b):
            return jnp.einsum('bihw,io->bohw', x, w) + b[None, :, None, None]

        def fourier_resample(x, out_shape):
            if tuple(x.shape[-2:]) == tuple(out_shape):
                return x
            Ho, Wo = out_shape
            xft = jnp.fft.rfftn(x, axes=(-2, -1), norm='forward')
            out = jnp.zeros(x.shape[:-2] + (Ho, Wo // 2 + 1), dtype=xft.dtype)
            hk = min(x.shape[-2], Ho) // 2
            wk = min(xft.shape[-1], Wo // 2 + 1)
            out = out.at[..., :hk, :wk].set(xft[..., :hk, :wk])
            out = out.at[..., -hk:, :wk].set(xft[..., -hk:, :wk])
            return jnp.fft.irfftn(out, s=out_shape, axes=(-2, -1), norm='forward')

        def spectral_conv(x, w, out_shape):
            wc = w[..., 0] + 1j * w[..., 1]
            mh = wc.shape[2] // 2
            mw = wc.shape[3]
            Ho, Wo = out_shape
            xft = jnp.fft.rfftn(x, axes=(-2, -1), norm='forward')
            top = jnp.einsum('bihw,iohw->bohw', xft[:, :, :mh, :mw], wc[:, :, :mh])
            bot = jnp.einsum('bihw,iohw->bohw', xft[:, :, -mh:, :mw], wc[:, :, mh:])
            out_ft = jnp.zeros((x.shape[0], wc.shape[1], Ho, Wo // 2 + 1), dtype=xft.dtype)
            out_ft = out_ft.at[:, :, :mh, :mw].set(top)
            out_ft = out_ft.at[:, :, -mh:, :mw].set(bot)
            return jnp.fft.irfftn(out_ft, s=out_shape, axes=(-2, -1), norm='forward')

        def fno_layer(x, spec_w, skip_w, skip_b, out_shape, norm=None, act=None):
            xs = fourier_resample(conv1x1(x, skip_w, skip_b), out_shape)
            xf = spectral_conv(x, spec_w, out_shape)
            if norm is not None:
                xf = instance_norm(xf, *norm)
            y = xf + xs
            return act(y) if act is not None else y

        def codano_forward(x, key_w, key_skip_w, key_skip_b, query_w, query_skip_w, query_skip_b, value_w, value_skip_w, value_skip_b, proj_w, proj_skip_w, proj_skip_b, norm1_g, norm1_b, attn_norm_g, attn_norm_b, norm2_g, norm2_b, mixer_w1, mixer_skip_w1, mixer_skip_b1, mixer_norm_g1, mixer_norm_b1, mixer_w2, mixer_skip_w2, mixer_skip_b2, mixer_norm_g2, mixer_norm_b2, mixer_out_g, mixer_out_b):
            b, t, H, W = x.shape
            tokens = x.reshape(b * t, 1, H, W)
            tokens_norm = instance_norm(tokens, norm1_g, norm1_b)
            Hs, Ws = (H // 2, W // 2)
            k = fno_layer(tokens_norm, key_w, key_skip_w, key_skip_b, (Hs, Ws))
            q = fno_layer(tokens_norm, query_w, query_skip_w, query_skip_b, (Hs, Ws))
            v = fno_layer(tokens_norm, value_w, value_skip_w, value_skip_b, (H, W))

            def heads_flat(z):
                hh, ww = z.shape[-2:]
                return z.reshape(b, t, N_HEADS, hh * ww).transpose(0, 2, 1, 3)
            kf, qf, vf = (heads_flat(k), heads_flat(q), heads_flat(v))
            scale = jnp.sqrt(jnp.asarray(kf.shape[-1], jnp.float32)) * TEMPERATURE
            dprod = jax.nn.softmax(jnp.einsum('bhtd,bhsd->bhts', qf, kf) / scale, axis=-1)
            attn = jnp.einsum('bhts,bhsd->bhtd', dprod, vf)
            attn = attn.transpose(0, 2, 1, 3).reshape(b * t, N_HEADS, H, W)
            attn = fno_layer(attn, proj_w, proj_skip_w, proj_skip_b, (H, W))
            attn = instance_norm(attn + tokens, attn_norm_g, attn_norm_b)
            m = instance_norm(attn, norm2_g, norm2_b)
            m = fno_layer(m, mixer_w1, mixer_skip_w1, mixer_skip_b1, (H, W), norm=(mixer_norm_g1, mixer_norm_b1), act=_gelu)
            m = fno_layer(m, mixer_w2, mixer_skip_w2, mixer_skip_b2, (H, W), norm=(mixer_norm_g2, mixer_norm_b2))
            out = instance_norm(m, mixer_out_g, mixer_out_b) + attn
            return out.reshape(b, t, H, W)
        key = jax.random.key(seed)
        ks = list(jax.random.split(key, 32))
        f32 = jnp.float32

        def W_(k, shape, s=0.02):
            return (s * jax.random.normal(k, shape)).astype(f32)
        B, T, H, Wd = (4, 32, 128, 128)
        mh_s, mw_s = (16, 9)
        mh_f, mw_f = (32, 17)
        return {'x': jax.random.normal(ks[0], (B, T, H, Wd), dtype=f32), 'key_w': W_(ks[1], (1, N_HEADS, mh_s, mw_s, 2)), 'key_skip_w': W_(ks[2], (1, N_HEADS), 0.5), 'key_skip_b': W_(ks[3], (N_HEADS,)), 'query_w': W_(ks[4], (1, N_HEADS, mh_s, mw_s, 2)), 'query_skip_w': W_(ks[5], (1, N_HEADS), 0.5), 'query_skip_b': W_(ks[6], (N_HEADS,)), 'value_w': W_(ks[7], (1, N_HEADS, mh_s, mw_s, 2)), 'value_skip_w': W_(ks[8], (1, N_HEADS), 0.5), 'value_skip_b': W_(ks[9], (N_HEADS,)), 'proj_w': W_(ks[10], (N_HEADS, 1, mh_f, mw_f, 2)), 'proj_skip_w': W_(ks[11], (N_HEADS, 1), 0.25), 'proj_skip_b': W_(ks[12], (1,)), 'norm1_g': jnp.ones((1,), f32), 'norm1_b': jnp.zeros((1,), f32), 'attn_norm_g': jnp.ones((1,), f32), 'attn_norm_b': jnp.zeros((1,), f32), 'norm2_g': jnp.ones((1,), f32), 'norm2_b': jnp.zeros((1,), f32), 'mixer_w1': W_(ks[13], (1, 1, mh_f, mw_f, 2)), 'mixer_skip_w1': W_(ks[14], (1, 1), 0.5), 'mixer_skip_b1': W_(ks[15], (1,)), 'mixer_norm_g1': jnp.ones((1,), f32), 'mixer_norm_b1': jnp.zeros((1,), f32), 'mixer_w2': W_(ks[16], (1, 1, mh_f, mw_f, 2)), 'mixer_skip_w2': W_(ks[17], (1, 1), 0.5), 'mixer_skip_b2': W_(ks[18], (1,)), 'mixer_norm_g2': jnp.ones((1,), f32), 'mixer_norm_b2': jnp.zeros((1,), f32), 'mixer_out_g': jnp.ones((1,), f32), 'mixer_out_b': jnp.zeros((1,), f32)}
    _L1_conv_all = _L1_conv_setup()
    _L1_conv_in = {k: v for k, v in _L1_conv_all.items() if k in ('key_w', 'key_skip_w', 'key_skip_b', 'query_w', 'query_skip_w', 'query_skip_b', 'value_w', 'value_skip_w', 'value_skip_b', 'proj_w', 'proj_skip_w', 'proj_skip_b', 'norm1_g', 'norm1_b', 'attn_norm_g', 'attn_norm_b', 'norm2_g', 'norm2_b', 'mixer_w1', 'mixer_skip_w1', 'mixer_skip_b1', 'mixer_norm_g1', 'mixer_norm_b1', 'mixer_w2', 'mixer_skip_w2', 'mixer_skip_b2', 'mixer_norm_g2', 'mixer_norm_b2', 'mixer_out_g', 'mixer_out_b', )}
    del _L1_conv_all

    def _L2_attn_setup():
        import jax, jax.numpy as jnp
        import numpy as np
        BS, L, D_MODEL, N_HEADS = (8, 16384, 128, 8)
        HEAD_DIM = D_MODEL // N_HEADS
        EPS = 1e-05
        key = jax.random.key(seed)
        ks = jax.random.split(key, 9)
        scale = 1.0 / np.sqrt(D_MODEL)
        return {'Q': jax.random.normal(ks[0], (BS, L, D_MODEL), dtype=jnp.float32), 'Wq': jax.random.normal(ks[1], (D_MODEL, D_MODEL), dtype=jnp.float32) * scale, 'bq': jax.random.normal(ks[2], (D_MODEL,), dtype=jnp.float32) * 0.01, 'Wk': jax.random.normal(ks[3], (D_MODEL, D_MODEL), dtype=jnp.float32) * scale, 'bk': jax.random.normal(ks[4], (D_MODEL,), dtype=jnp.float32) * 0.01, 'Wv': jax.random.normal(ks[5], (D_MODEL, D_MODEL), dtype=jnp.float32) * scale, 'bv': jax.random.normal(ks[6], (D_MODEL,), dtype=jnp.float32) * 0.01, 'Wo': jax.random.normal(ks[7], (D_MODEL, D_MODEL), dtype=jnp.float32) * scale, 'bo': jax.random.normal(ks[8], (D_MODEL,), dtype=jnp.float32) * 0.01}
    _L2_attn_all = _L2_attn_setup()
    _L2_attn_in = {k: v for k, v in _L2_attn_all.items() if k in ('Wq', 'bq', 'Wk', 'bk', 'Wv', 'bv', 'Wo', 'bo', )}
    del _L2_attn_all

    def _L2_ffn_setup():
        import jax, jax.numpy as jnp
        import numpy as np
        B, S, D, E, H, O, K = (512, 2048, 128, 64, 512, 128, 8)
        key = jax.random.key(seed)
        k0, k1, k2, k3 = jax.random.split(key, 4)
        x = jax.random.normal(k0, (B, S, D), dtype=jnp.float32)
        gate_w = jax.random.normal(k1, (E, D), dtype=jnp.float32) * (1.0 / np.sqrt(D))
        gate_b = jnp.zeros((E,), dtype=jnp.float32)
        weight1 = jax.random.uniform(k2, (E, D + 1, H), dtype=jnp.float32, minval=-1.0, maxval=1.0) * (1.0 / np.sqrt(D + 1))
        weight2 = jax.random.uniform(k3, (E, H + 1, O), dtype=jnp.float32, minval=-1.0, maxval=1.0) * (1.0 / np.sqrt(H + 1))
        return {'x': x, 'gate_w': gate_w, 'gate_b': gate_b, 'weight1': weight1, 'weight2': weight2}
    _L2_ffn_all = _L2_ffn_setup()
    _L2_ffn_in = {k: v for k, v in _L2_ffn_all.items() if k in ('gate_w', 'gate_b', 'weight1', 'weight2', )}
    del _L2_ffn_all

    def _L3_attn_setup():
        import jax, jax.numpy as jnp
        import numpy as np
        HEADS = 4
        DIM_HEAD = 32
        EPS = 1e-05
        key = jax.random.key(seed)
        k1, k2, k3 = jax.random.split(key, 3)
        H, W, C = (512, 512, 128)
        dim = HEADS * DIM_HEAD
        x = jax.random.normal(k1, (H, W, C), dtype=jnp.float32)
        w_in = jax.random.normal(k2, (3 * dim, C), dtype=jnp.float32) / np.sqrt(C)
        w_out = jax.random.normal(k3, (C, dim), dtype=jnp.float32) / np.sqrt(dim)
        b_out = jnp.zeros((C,), dtype=jnp.float32)
        ln_w = jnp.ones((C,), dtype=jnp.float32)
        return {'x': x, 'w_in': w_in, 'w_out': w_out, 'b_out': b_out, 'ln_w': ln_w}
    _L3_attn_all = _L3_attn_setup()
    _L3_attn_in = {k: v for k, v in _L3_attn_all.items() if k in ('w_in', 'w_out', 'b_out', 'ln_w', )}
    del _L3_attn_all

    def _L3_ffn_setup():
        import jax, jax.numpy as jnp
        import numpy as np
        BN_EPS = 1e-05
        key = jax.random.key(seed)
        k1, k2, k3 = jax.random.split(key, 3)
        B, T, I, H = (64, 2048, 128, 128)
        x = jax.random.normal(k1, (B, T, I), dtype=jnp.float32)
        W = jax.random.normal(k2, (H, I), dtype=jnp.float32) * (1.0 / np.sqrt(I))
        V = jnp.linalg.qr(jax.random.normal(k3, (H, H), dtype=jnp.float32))[0]
        gamma = jnp.ones((H,), dtype=jnp.float32)
        beta = jnp.zeros((H,), dtype=jnp.float32)
        return {'x': x, 'W': W, 'V': V, 'gamma': gamma, 'beta': beta}
    _L3_ffn_all = _L3_ffn_setup()
    _L3_ffn_in = {k: v for k, v in _L3_ffn_all.items() if k in ('W', 'V', 'gamma', 'beta', )}
    del _L3_ffn_all

    return {
        "x": x,
        "L0_conv_adj": _L0_conv_in["adj"],
        "L0_conv_Wq": _L0_conv_in["Wq"],
        "L0_conv_Wk": _L0_conv_in["Wk"],
        "L0_conv_Wv": _L0_conv_in["Wv"],
        "L0_conv_Wo": _L0_conv_in["Wo"],
        "L0_conv_bo": _L0_conv_in["bo"],
        "L0_conv_ns_g": _L0_conv_in["ns_g"],
        "L0_conv_ns_b": _L0_conv_in["ns_b"],
        "L0_conv_nt_g": _L0_conv_in["nt_g"],
        "L0_conv_nt_b": _L0_conv_in["nt_b"],
        "L0_conv_in_proj": _L0_conv_in["in_proj"],
        "L0_conv_conv_w": _L0_conv_in["conv_w"],
        "L0_conv_conv_b": _L0_conv_in["conv_b"],
        "L0_conv_x_proj": _L0_conv_in["x_proj"],
        "L0_conv_dt_w": _L0_conv_in["dt_w"],
        "L0_conv_dt_b": _L0_conv_in["dt_b"],
        "L0_conv_A_log": _L0_conv_in["A_log"],
        "L0_conv_Dp": _L0_conv_in["Dp"],
        "L0_conv_out_w": _L0_conv_in["out_w"],
        "L0_conv_out_b": _L0_conv_in["out_b"],
        "L1_conv_key_w": _L1_conv_in["key_w"],
        "L1_conv_key_skip_w": _L1_conv_in["key_skip_w"],
        "L1_conv_key_skip_b": _L1_conv_in["key_skip_b"],
        "L1_conv_query_w": _L1_conv_in["query_w"],
        "L1_conv_query_skip_w": _L1_conv_in["query_skip_w"],
        "L1_conv_query_skip_b": _L1_conv_in["query_skip_b"],
        "L1_conv_value_w": _L1_conv_in["value_w"],
        "L1_conv_value_skip_w": _L1_conv_in["value_skip_w"],
        "L1_conv_value_skip_b": _L1_conv_in["value_skip_b"],
        "L1_conv_proj_w": _L1_conv_in["proj_w"],
        "L1_conv_proj_skip_w": _L1_conv_in["proj_skip_w"],
        "L1_conv_proj_skip_b": _L1_conv_in["proj_skip_b"],
        "L1_conv_norm1_g": _L1_conv_in["norm1_g"],
        "L1_conv_norm1_b": _L1_conv_in["norm1_b"],
        "L1_conv_attn_norm_g": _L1_conv_in["attn_norm_g"],
        "L1_conv_attn_norm_b": _L1_conv_in["attn_norm_b"],
        "L1_conv_norm2_g": _L1_conv_in["norm2_g"],
        "L1_conv_norm2_b": _L1_conv_in["norm2_b"],
        "L1_conv_mixer_w1": _L1_conv_in["mixer_w1"],
        "L1_conv_mixer_skip_w1": _L1_conv_in["mixer_skip_w1"],
        "L1_conv_mixer_skip_b1": _L1_conv_in["mixer_skip_b1"],
        "L1_conv_mixer_norm_g1": _L1_conv_in["mixer_norm_g1"],
        "L1_conv_mixer_norm_b1": _L1_conv_in["mixer_norm_b1"],
        "L1_conv_mixer_w2": _L1_conv_in["mixer_w2"],
        "L1_conv_mixer_skip_w2": _L1_conv_in["mixer_skip_w2"],
        "L1_conv_mixer_skip_b2": _L1_conv_in["mixer_skip_b2"],
        "L1_conv_mixer_norm_g2": _L1_conv_in["mixer_norm_g2"],
        "L1_conv_mixer_norm_b2": _L1_conv_in["mixer_norm_b2"],
        "L1_conv_mixer_out_g": _L1_conv_in["mixer_out_g"],
        "L1_conv_mixer_out_b": _L1_conv_in["mixer_out_b"],
        "L2_attn_Wq": _L2_attn_in["Wq"],
        "L2_attn_bq": _L2_attn_in["bq"],
        "L2_attn_Wk": _L2_attn_in["Wk"],
        "L2_attn_bk": _L2_attn_in["bk"],
        "L2_attn_Wv": _L2_attn_in["Wv"],
        "L2_attn_bv": _L2_attn_in["bv"],
        "L2_attn_Wo": _L2_attn_in["Wo"],
        "L2_attn_bo": _L2_attn_in["bo"],
        "L2_ffn_gate_w": _L2_ffn_in["gate_w"],
        "L2_ffn_gate_b": _L2_ffn_in["gate_b"],
        "L2_ffn_weight1": _L2_ffn_in["weight1"],
        "L2_ffn_weight2": _L2_ffn_in["weight2"],
        "L3_attn_w_in": _L3_attn_in["w_in"],
        "L3_attn_w_out": _L3_attn_in["w_out"],
        "L3_attn_b_out": _L3_attn_in["b_out"],
        "L3_attn_ln_w": _L3_attn_in["ln_w"],
        "L3_ffn_W": _L3_ffn_in["W"],
        "L3_ffn_V": _L3_ffn_in["V"],
        "L3_ffn_gamma": _L3_ffn_in["gamma"],
        "L3_ffn_beta": _L3_ffn_in["beta"],
    }

def reference(x, L0_conv_adj, L0_conv_Wq, L0_conv_Wk, L0_conv_Wv, L0_conv_Wo, L0_conv_bo, L0_conv_ns_g, L0_conv_ns_b, L0_conv_nt_g, L0_conv_nt_b, L0_conv_in_proj, L0_conv_conv_w, L0_conv_conv_b, L0_conv_x_proj, L0_conv_dt_w, L0_conv_dt_b, L0_conv_A_log, L0_conv_Dp, L0_conv_out_w, L0_conv_out_b, L1_conv_key_w, L1_conv_key_skip_w, L1_conv_key_skip_b, L1_conv_query_w, L1_conv_query_skip_w, L1_conv_query_skip_b, L1_conv_value_w, L1_conv_value_skip_w, L1_conv_value_skip_b, L1_conv_proj_w, L1_conv_proj_skip_w, L1_conv_proj_skip_b, L1_conv_norm1_g, L1_conv_norm1_b, L1_conv_attn_norm_g, L1_conv_attn_norm_b, L1_conv_norm2_g, L1_conv_norm2_b, L1_conv_mixer_w1, L1_conv_mixer_skip_w1, L1_conv_mixer_skip_b1, L1_conv_mixer_norm_g1, L1_conv_mixer_norm_b1, L1_conv_mixer_w2, L1_conv_mixer_skip_w2, L1_conv_mixer_skip_b2, L1_conv_mixer_norm_g2, L1_conv_mixer_norm_b2, L1_conv_mixer_out_g, L1_conv_mixer_out_b, L2_attn_Wq, L2_attn_bq, L2_attn_Wk, L2_attn_bk, L2_attn_Wv, L2_attn_bv, L2_attn_Wo, L2_attn_bo, L2_ffn_gate_w, L2_ffn_gate_b, L2_ffn_weight1, L2_ffn_weight2, L3_attn_w_in, L3_attn_w_out, L3_attn_b_out, L3_attn_ln_w, L3_ffn_W, L3_ffn_V, L3_ffn_gamma, L3_ffn_beta):
    import jax
    import jax.numpy as jnp
    def _L0_conv_ref(x, adj, Wq, Wk, Wv, Wo, bo, ns_g, ns_b, nt_g, nt_b, in_proj, conv_w, conv_b, x_proj, dt_w, dt_b, A_log, Dp, out_w, out_b):
        import jax, jax.numpy as jnp
        import numpy as np
        import math
        D_MODEL = 128
        HEADS = 4
        HD = D_MODEL // HEADS
        D_INNER = 2 * D_MODEL
        D_STATE = 16
        D_CONV = 4
        DT_RANK = math.ceil(D_MODEL / 16)
        BSZ, TLEN, NNODE = (4, 32, 128)
        LN_EPS = 1e-05

        def layernorm(x, g, b):
            m = jnp.mean(x, axis=-1, keepdims=True)
            v = jnp.var(x, axis=-1, keepdims=True)
            return (x - m) * jax.lax.rsqrt(v + LN_EPS) * g + b

        def _gat(h, adj, Wq, Wk, Wv, Wo, bo):
            BT, N, _ = h.shape
            q = (h @ Wq).reshape(BT, N, HEADS, HD)
            k = (h @ Wk).reshape(BT, N, HEADS, HD)
            v = (h @ Wv).reshape(BT, N, HEADS, HD)
            scores = jnp.einsum('bnhd,bmhd->bhnm', q, k) / math.sqrt(HD)
            scores = jnp.where(adj[None, None] == 0, -1000000000.0, scores)
            attn = jax.nn.softmax(scores, axis=-1)
            o = jnp.einsum('bhnm,bmhd->bnhd', attn, v).reshape(BT, N, D_MODEL)
            return h + o @ Wo + bo

        def _mamba(xt, in_proj, conv_w, conv_b, x_proj, dt_w, dt_b, A_log, Dp, out_w, out_b):
            BN, T, _ = xt.shape
            xz = xt @ in_proj
            xc, z = (xz[..., :D_INNER], xz[..., D_INNER:])
            xp = jnp.pad(xc, ((0, 0), (D_CONV - 1, 0), (0, 0)))
            xconv = conv_b
            for kk in range(D_CONV):
                xconv = xconv + conv_w[:, kk] * xp[:, kk:kk + T, :]
            xc = jax.nn.silu(xconv)
            dbc = xc @ x_proj
            dt = jax.nn.softplus(dbc[..., :DT_RANK] @ dt_w + dt_b)
            Bm = dbc[..., DT_RANK:DT_RANK + D_STATE]
            Cm = dbc[..., DT_RANK + D_STATE:]
            A = -jnp.exp(A_log)
            dA = jnp.exp(dt[..., None] * A)
            dBx = (dt * xc)[..., None] * Bm[:, :, None, :]

            def step(hprev, inp):
                dA_t, dBx_t, C_t = inp
                hnew = dA_t * hprev + dBx_t
                y_t = jnp.einsum('bds,bs->bd', hnew, C_t)
                return (hnew, y_t)
            h0 = jnp.zeros((BN, D_INNER, D_STATE), xt.dtype)
            _, ys = jax.lax.scan(step, h0, (jnp.swapaxes(dA, 0, 1), jnp.swapaxes(dBx, 0, 1), jnp.swapaxes(Cm, 0, 1)))
            y = jnp.swapaxes(ys, 0, 1) + Dp * xc
            y = y * jax.nn.silu(z)
            return y @ out_w + out_b
        B, T, N, Fd = x.shape
        h = x.reshape(B * T, N, Fd)
        h = layernorm(h + _gat(h, adj, Wq, Wk, Wv, Wo, bo), ns_g, ns_b)
        xt = h.reshape(B, T, N, Fd).transpose(0, 2, 1, 3).reshape(B * N, T, Fd)
        xt = layernorm(xt + _mamba(xt, in_proj, conv_w, conv_b, x_proj, dt_w, dt_b, A_log, Dp, out_w, out_b), nt_g, nt_b)
        return xt.reshape(B, N, T, Fd).transpose(0, 2, 1, 3)

    def _L1_conv_ref(x, key_w, key_skip_w, key_skip_b, query_w, query_skip_w, query_skip_b, value_w, value_skip_w, value_skip_b, proj_w, proj_skip_w, proj_skip_b, norm1_g, norm1_b, attn_norm_g, attn_norm_b, norm2_g, norm2_b, mixer_w1, mixer_skip_w1, mixer_skip_b1, mixer_norm_g1, mixer_norm_b1, mixer_w2, mixer_skip_w2, mixer_skip_b2, mixer_norm_g2, mixer_norm_b2, mixer_out_g, mixer_out_b):
        import jax, jax.numpy as jnp
        import numpy as np
        N_HEADS = 16
        TEMPERATURE = 1.0
        EPS = 1e-05

        def _gelu(z):
            return jax.nn.gelu(z, approximate=False)

        def instance_norm(x, g, b):
            mu = jnp.mean(x, axis=(-2, -1), keepdims=True)
            var = jnp.var(x, axis=(-2, -1), keepdims=True)
            return (x - mu) * jax.lax.rsqrt(var + EPS) * g[:, None, None] + b[:, None, None]

        def conv1x1(x, w, b):
            return jnp.einsum('bihw,io->bohw', x, w) + b[None, :, None, None]

        def fourier_resample(x, out_shape):
            if tuple(x.shape[-2:]) == tuple(out_shape):
                return x
            Ho, Wo = out_shape
            xft = jnp.fft.rfftn(x, axes=(-2, -1), norm='forward')
            out = jnp.zeros(x.shape[:-2] + (Ho, Wo // 2 + 1), dtype=xft.dtype)
            hk = min(x.shape[-2], Ho) // 2
            wk = min(xft.shape[-1], Wo // 2 + 1)
            out = out.at[..., :hk, :wk].set(xft[..., :hk, :wk])
            out = out.at[..., -hk:, :wk].set(xft[..., -hk:, :wk])
            return jnp.fft.irfftn(out, s=out_shape, axes=(-2, -1), norm='forward')

        def spectral_conv(x, w, out_shape):
            wc = w[..., 0] + 1j * w[..., 1]
            mh = wc.shape[2] // 2
            mw = wc.shape[3]
            Ho, Wo = out_shape
            xft = jnp.fft.rfftn(x, axes=(-2, -1), norm='forward')
            top = jnp.einsum('bihw,iohw->bohw', xft[:, :, :mh, :mw], wc[:, :, :mh])
            bot = jnp.einsum('bihw,iohw->bohw', xft[:, :, -mh:, :mw], wc[:, :, mh:])
            out_ft = jnp.zeros((x.shape[0], wc.shape[1], Ho, Wo // 2 + 1), dtype=xft.dtype)
            out_ft = out_ft.at[:, :, :mh, :mw].set(top)
            out_ft = out_ft.at[:, :, -mh:, :mw].set(bot)
            return jnp.fft.irfftn(out_ft, s=out_shape, axes=(-2, -1), norm='forward')

        def fno_layer(x, spec_w, skip_w, skip_b, out_shape, norm=None, act=None):
            xs = fourier_resample(conv1x1(x, skip_w, skip_b), out_shape)
            xf = spectral_conv(x, spec_w, out_shape)
            if norm is not None:
                xf = instance_norm(xf, *norm)
            y = xf + xs
            return act(y) if act is not None else y

        def codano_forward(x, key_w, key_skip_w, key_skip_b, query_w, query_skip_w, query_skip_b, value_w, value_skip_w, value_skip_b, proj_w, proj_skip_w, proj_skip_b, norm1_g, norm1_b, attn_norm_g, attn_norm_b, norm2_g, norm2_b, mixer_w1, mixer_skip_w1, mixer_skip_b1, mixer_norm_g1, mixer_norm_b1, mixer_w2, mixer_skip_w2, mixer_skip_b2, mixer_norm_g2, mixer_norm_b2, mixer_out_g, mixer_out_b):
            b, t, H, W = x.shape
            tokens = x.reshape(b * t, 1, H, W)
            tokens_norm = instance_norm(tokens, norm1_g, norm1_b)
            Hs, Ws = (H // 2, W // 2)
            k = fno_layer(tokens_norm, key_w, key_skip_w, key_skip_b, (Hs, Ws))
            q = fno_layer(tokens_norm, query_w, query_skip_w, query_skip_b, (Hs, Ws))
            v = fno_layer(tokens_norm, value_w, value_skip_w, value_skip_b, (H, W))

            def heads_flat(z):
                hh, ww = z.shape[-2:]
                return z.reshape(b, t, N_HEADS, hh * ww).transpose(0, 2, 1, 3)
            kf, qf, vf = (heads_flat(k), heads_flat(q), heads_flat(v))
            scale = jnp.sqrt(jnp.asarray(kf.shape[-1], jnp.float32)) * TEMPERATURE
            dprod = jax.nn.softmax(jnp.einsum('bhtd,bhsd->bhts', qf, kf) / scale, axis=-1)
            attn = jnp.einsum('bhts,bhsd->bhtd', dprod, vf)
            attn = attn.transpose(0, 2, 1, 3).reshape(b * t, N_HEADS, H, W)
            attn = fno_layer(attn, proj_w, proj_skip_w, proj_skip_b, (H, W))
            attn = instance_norm(attn + tokens, attn_norm_g, attn_norm_b)
            m = instance_norm(attn, norm2_g, norm2_b)
            m = fno_layer(m, mixer_w1, mixer_skip_w1, mixer_skip_b1, (H, W), norm=(mixer_norm_g1, mixer_norm_b1), act=_gelu)
            m = fno_layer(m, mixer_w2, mixer_skip_w2, mixer_skip_b2, (H, W), norm=(mixer_norm_g2, mixer_norm_b2))
            out = instance_norm(m, mixer_out_g, mixer_out_b) + attn
            return out.reshape(b, t, H, W)
        return codano_forward(x, key_w, key_skip_w, key_skip_b, query_w, query_skip_w, query_skip_b, value_w, value_skip_w, value_skip_b, proj_w, proj_skip_w, proj_skip_b, norm1_g, norm1_b, attn_norm_g, attn_norm_b, norm2_g, norm2_b, mixer_w1, mixer_skip_w1, mixer_skip_b1, mixer_norm_g1, mixer_norm_b1, mixer_w2, mixer_skip_w2, mixer_skip_b2, mixer_norm_g2, mixer_norm_b2, mixer_out_g, mixer_out_b)

    def _L2_attn_ref(Q, Wq, bq, Wk, bk, Wv, bv, Wo, bo):
        import jax, jax.numpy as jnp
        import numpy as np
        BS, L, D_MODEL, N_HEADS = (8, 16384, 128, 8)
        HEAD_DIM = D_MODEL // N_HEADS
        EPS = 1e-05
        bs, seq, _ = Q.shape
        q = (Q @ Wq + bq).reshape(bs, seq, N_HEADS, HEAD_DIM)
        k = (Q @ Wk + bk).reshape(bs, seq, N_HEADS, HEAD_DIM)
        v = (Q @ Wv + bv).reshape(bs, seq, N_HEADS, HEAD_DIM)
        phi_q = jax.nn.elu(q) + 1.0
        phi_k = jax.nn.elu(k) + 1.0
        KV = jnp.einsum('blhd,blhm->bhdm', phi_k, v)
        K_sum = phi_k.sum(axis=1)
        Z = 1.0 / (jnp.einsum('blhd,bhd->blh', phi_q, K_sum) + EPS)
        V_new = jnp.einsum('blhd,bhdm->blhm', phi_q, KV) * Z[..., None]
        out = V_new.reshape(bs, seq, N_HEADS * HEAD_DIM) @ Wo + bo
        return out

    def _L2_ffn_ref(x, gate_w, gate_b, weight1, weight2):
        import jax, jax.numpy as jnp
        import numpy as np
        B, S, D, E, H, O, K = (512, 2048, 128, 64, 512, 128, 8)
        Bn, Sn, Dn = x.shape
        logits = jnp.einsum('bsd,ed->bse', x, gate_w) + gate_b
        probs = jax.nn.softmax(logits, axis=1)
        vals, idx = jax.lax.top_k(probs.transpose(0, 2, 1), K)
        topv = vals.transpose(0, 2, 1)
        topi = idx.transpose(0, 2, 1)
        flat_idx = topi.reshape(Bn, K * E)
        gathered = jnp.take_along_axis(x, flat_idx[:, :, None], axis=1)
        gathered = gathered.reshape(Bn, K, E, Dn)
        pooled = jnp.einsum('bked,bke->bed', gathered, topv)
        ones = jnp.ones((E, Bn, 1), dtype=x.dtype)
        h = jnp.concatenate([pooled.transpose(1, 0, 2), ones], axis=-1)
        h = jax.nn.gelu(jnp.einsum('ebd,edh->ebh', h, weight1), approximate=False)
        h = jnp.concatenate([h, ones], axis=-1)
        out = jnp.einsum('ebh,eho->ebo', h, weight2)
        out = out.transpose(1, 0, 2)
        weighted = jnp.einsum('beo,bke->bkeo', out, topv).reshape(Bn, K * E, O)
        outputs = jnp.zeros((Bn, Sn, O), dtype=x.dtype)
        outputs = outputs.at[jnp.arange(Bn)[:, None], flat_idx].add(weighted)
        return outputs

    def _L3_attn_ref(x, w_in, w_out, b_out, ln_w):
        import jax, jax.numpy as jnp
        import numpy as np
        HEADS = 4
        DIM_HEAD = 32
        EPS = 1e-05
        H, W, C = x.shape
        N = H * W
        qkv = jnp.einsum('hwc,oc->hwo', x, w_in).reshape(N, 3, HEADS, DIM_HEAD)
        q, k, v = (qkv[:, 0], qkv[:, 1], qkv[:, 2])
        q = jax.nn.softmax(q, axis=-1) / np.sqrt(DIM_HEAD)
        k = jax.nn.softmax(k, axis=0)
        v = v / N
        context = jnp.einsum('nhd,nhe->hde', k, v)
        out = jnp.einsum('hde,nhd->nhe', context, q)
        out = out.reshape(H, W, HEADS * DIM_HEAD)
        out = jnp.einsum('hwd,cd->hwc', out, w_out) + b_out
        mean = out.mean(axis=-1, keepdims=True)
        var = out.var(axis=-1, keepdims=True)
        out = (out - mean) / jnp.sqrt(var + EPS) * ln_w
        return out

    def _L3_ffn_ref(x, W, V, gamma, beta):
        import jax, jax.numpy as jnp
        import numpy as np
        BN_EPS = 1e-05
        B, T, H = (x.shape[0], x.shape[1], W.shape[0])
        Wx = jnp.einsum('bti,hi->bth', x, W)
        flat = Wx.reshape(B * T, H)
        mean = jnp.mean(flat, axis=0)
        var = jnp.var(flat, axis=0)
        Wx = ((flat - mean) * jax.lax.rsqrt(var + BN_EPS) * gamma + beta).reshape(B, T, H)
        Vt = V.T

        def step(yt, wx_t):
            yt = jax.nn.sigmoid(wx_t + yt @ Vt)
            return (yt, yt)
        y0 = jnp.zeros((B, H), dtype=Wx.dtype)
        _, ys = jax.lax.scan(step, y0, jnp.swapaxes(Wx, 0, 1))
        return jnp.swapaxes(ys, 0, 1)

    def _gn(v, G=32, eps=1e-5):
        B_, H_, W_, C_ = v.shape
        g = v.reshape(B_, H_, W_, G, C_ // G)
        m = jnp.mean(g, axis=(1, 2, 4), keepdims=True)
        s = jnp.var(g, axis=(1, 2, 4), keepdims=True)
        return ((g - m) / jnp.sqrt(s + eps)).reshape(v.shape)

    def _ln_c(v, eps=1e-6):
        m = jnp.mean(v, axis=-1, keepdims=True)
        s = jnp.var(v, axis=-1, keepdims=True)
        return (v - m) / jnp.sqrt(s + eps)

    def _ln_t(v, eps=1e-5):
        m = jnp.mean(v, axis=-1, keepdims=True)
        s = jnp.var(v, axis=-1, keepdims=True)
        return (v - m) / jnp.sqrt(s + eps)

    def _to_tokens(v):
        B_, H_, W_, C_ = v.shape
        return v.reshape(B_, H_ * W_, C_)
    def _from_tokens(t, like):
        return t.reshape(like.shape)

    x = x + _L0_conv_ref(_gn(x), L0_conv_adj, L0_conv_Wq, L0_conv_Wk, L0_conv_Wv, L0_conv_Wo, L0_conv_bo, L0_conv_ns_g, L0_conv_ns_b, L0_conv_nt_g, L0_conv_nt_b, L0_conv_in_proj, L0_conv_conv_w, L0_conv_conv_b, L0_conv_x_proj, L0_conv_dt_w, L0_conv_dt_b, L0_conv_A_log, L0_conv_Dp, L0_conv_out_w, L0_conv_out_b)
    x = x + _L1_conv_ref(_gn(x), L1_conv_key_w, L1_conv_key_skip_w, L1_conv_key_skip_b, L1_conv_query_w, L1_conv_query_skip_w, L1_conv_query_skip_b, L1_conv_value_w, L1_conv_value_skip_w, L1_conv_value_skip_b, L1_conv_proj_w, L1_conv_proj_skip_w, L1_conv_proj_skip_b, L1_conv_norm1_g, L1_conv_norm1_b, L1_conv_attn_norm_g, L1_conv_attn_norm_b, L1_conv_norm2_g, L1_conv_norm2_b, L1_conv_mixer_w1, L1_conv_mixer_skip_w1, L1_conv_mixer_skip_b1, L1_conv_mixer_norm_g1, L1_conv_mixer_norm_b1, L1_conv_mixer_w2, L1_conv_mixer_skip_w2, L1_conv_mixer_skip_b2, L1_conv_mixer_norm_g2, L1_conv_mixer_norm_b2, L1_conv_mixer_out_g, L1_conv_mixer_out_b)
    t = _to_tokens(x)
    t = t + _L2_attn_ref(_ln_t(t), L2_attn_Wq, L2_attn_bq, L2_attn_Wk, L2_attn_bk, L2_attn_Wv, L2_attn_bv, L2_attn_Wo, L2_attn_bo)
    t = t + _L2_ffn_ref(_ln_t(t), L2_ffn_gate_w, L2_ffn_gate_b, L2_ffn_weight1, L2_ffn_weight2)
    t = t + _L3_attn_ref(_ln_t(t), L3_attn_w_in, L3_attn_w_out, L3_attn_b_out, L3_attn_ln_w)
    t = t + _L3_ffn_ref(_ln_t(t), L3_ffn_W, L3_ffn_V, L3_ffn_gamma, L3_ffn_beta)
    x = _from_tokens(t, x)
    return x


_drawn_inputs = setup_inputs


def setup_inputs(seed=0):
    import zlib

    import numpy as np

    out = dict(_drawn_inputs(seed))
    spreads = {'L0_conv_bo': (0.0, 0.338),
     'L0_conv_ns_g': (1.0, 0.2),
     'L0_conv_ns_b': (0.0, 0.1),
     'L0_conv_nt_g': (1.0, 0.2),
     'L0_conv_nt_b': (0.0, 0.1),
     'L0_conv_conv_b': (0.0, 0.444),
     'L0_conv_Dp': (1.0, 0.2),
     'L0_conv_out_b': (0.0, 0.1),
     'L2_ffn_gate_b': (0.0, 2.0),
     'L3_attn_b_out': (0.0, 0.1),
     'L3_attn_ln_w': (1.0, 0.2),
     'L3_ffn_gamma': (1.0, 0.6),
     'L3_ffn_beta': (0.0, 0.8)}
    factors = {'L0_conv_x_proj': 2.724,
     'L0_conv_dt_w': 4.804,
     'L0_conv_dt_b': 8.0,
     'L0_conv_A_log': 6.616,
     'L1_conv_key_w': 64.0,
     'L1_conv_key_skip_w': 8.0,
     'L1_conv_key_skip_b': 200.0,
     'L1_conv_query_w': 58.228,
     'L1_conv_query_skip_b': 200.0,
     'L1_conv_value_w': 8.0,
     'L1_conv_value_skip_b': 200.0,
     'L1_conv_proj_w': 7.163,
     'L2_attn_Wq': 8.0,
     'L2_attn_bq': 200.0,
     'L2_attn_Wk': 8.0,
     'L2_attn_bk': 200.0,
     'L2_attn_Wv': 2.973,
     'L2_attn_bv': 8.0,
     'L2_attn_Wo': 3.174,
     'L2_attn_bo': 8.0,
     'L2_ffn_gate_w': 8.0,
     'L2_ffn_weight1': 8.0,
     'L2_ffn_weight2': 8.0,
     'L3_attn_w_in': 64.0,
     'L3_attn_w_out': 64.0}
    for name, (base, spread) in spreads.items():
        noise = np.random.default_rng([zlib.crc32(name.encode()), seed]).standard_normal(out[name].shape)
        drawn = base * np.exp(spread * noise) if base else spread * noise
        out[name] = jnp.asarray(drawn.astype(out[name].dtype))
    for name, factor in factors.items():
        out[name] = (out[name] * factor).astype(out[name].dtype)
    return out
```

```python
import math
from contextlib import ExitStack, contextmanager

import concourse.bass as bass
import numpy as np
from concourse import mybir

f32 = mybir.dt.float32
bf16 = mybir.dt.bfloat16
u8 = mybir.dt.uint8
ALU = mybir.AluOpType
ACT = mybir.ActivationFunctionType
AX = mybir.AxisListType

P = 128
B, T, W, C = 4, 32, 128, 128
BT = B * T


class Chain:

    def __init__(self, eng, sem):
        self.eng, self.sem, self.base, self.k = eng, sem, 0, 0

    def __call__(self, ins):
        ins.then_inc(self.sem, 1)
        self.k += 1
        self.eng.wait_ge(self.sem, self.base + self.k)

    def mark(self, ins):
        ins.then_inc(self.sem, 1)
        self.k += 1

    def join(self):
        self.eng.wait_ge(self.sem, self.base + self.k)

    @contextmanager
    def loop(self, turns, per):
        base, k = self.base, self.k
        with self.eng.Fori(0, turns) as i:
            self.base, self.k = base + k + i * per, 0
            yield i
            assert self.k == per, (self.k, per)
        self.base, self.k = base, k + turns * per


class Scope:

    def __init__(self, nc, ctx, tag):
        self.nc, self.ctx, self.tag, self.sems = nc, ctx, tag, []
        ctx.callback(self.clear)

    def sb(self, name, shape, dt=f32):
        return self.ctx.enter_context(self.nc.sbuf_tensor(f"{self.tag}_{name}", shape, dt))

    def ps(self, name, shape=(P, 512), dt=f32):
        return self.ctx.enter_context(self.nc.psum_tensor(f"{self.tag}_{name}", list(shape), dt))

    def sem(self, name):
        self.sems.append(self.nc.alloc_semaphore(f"{self.tag}_{name}"))
        return self.sems[-1]

    def clear(self):
        if self.sems:
            with self.nc.Block() as block:
                @block.sync
                def _(sp):
                    for q in self.sems:
                        sp.sem_clear(q)
            for q in self.sems:
                self.nc.release_semaphore(q)


def fill_identity(pool, chain, ident):
    chain(pool.memset(ident[:, :], 0.0))
    chain(pool.affine_select(out=ident[:, :], in_=ident[:, :], compare_op=ALU.not_equal, fill=1.0,
                             base=0, pattern=[[-1, ident.shape[1]]], channel_multiplier=1))


def group_norm(nc, src, hg, tag, G=32, eps=1e-5):
    J = C // G
    N = T * W * J
    with ExitStack() as ctx:
        s = Scope(nc, ctx, tag)
        xb = s.sb("xb", [P, 2, T * C])
        sq = s.sb("sq", [P, T * C])
        ones = s.sb("ones", [P, P])
        sums = s.sb("sums", [P, 2, G])
        var = s.sb("var", [P, G])
        rstd = s.sb("rstd", [P, G])
        half = s.sb("half", [P, G])
        ps = [s.ps(f"ps{j}") for j in range(2)]
        loaded, squared, summed, var_done, rstd_done, normed, ready = (
            s.sem(n) for n in ("loaded", "squared", "summed", "var_done", "rstd_done", "normed", "ready"))
        dch = s.sem("dch")
        block = ctx.enter_context(nc.Block())

        @block.sync
        def _(sp):
            for b in range(B):
                if b >= 2:
                    sp.wait_ge(normed, b - 1)
                sp.dma_start(xb[:, b % 2, :].rearrange("w (t c) -> w t c", t=T),
                             src[b].rearrange("t w c -> w t c")).then_inc(loaded, 16)
                sp.wait_ge(loaded, 16 * b + 16)

        @block.scalar
        def _(act):
            for b in range(B):
                act.wait_ge(loaded, 16 * b + 16)
                if b >= 1:
                    act.wait_ge(summed, b)
                act.activation(sq[:, :], xb[:, b % 2, :], ACT.Square).then_inc(squared, 1)

        @block.tensor
        def _(pe):
            pe.wait_ge(ready, 1)
            for b in range(B):
                pe.wait_ge(loaded, 16 * b + 16)
                if b >= 1:
                    pe.wait_ge(var_done, b)
                for j in range(8):
                    pe.matmul(ps[0][:, :], ones[:, :], xb[:, b % 2, 512 * j:512 * j + 512],
                              start=(j == 0), stop=(j == 7))
                pe.wait_ge(squared, b + 1)
                for j in range(8):
                    last = pe.matmul(ps[1][:, :], ones[:, :], sq[:, 512 * j:512 * j + 512],
                                     start=(j == 0), stop=(j == 7))
                last.then_inc(summed, 1)

        @block.gpsimd
        def _(pool):
            pool.memset(ones[:, :], 1.0 / N).then_inc(ready, 1)
            pool.memset(half[:, :], -0.5).then_inc(rstd_done, 1)
            pool.wait_ge(rstd_done, 1)
            for b in range(B):
                pool.wait_ge(var_done, b + 1)
                pool.tensor_tensor(rstd[:, :], var[:, :], half[:, :], ALU.pow).then_inc(rstd_done, 1)

        @block.vector
        def _(dve):
            step = Chain(dve, dch)
            for b in range(B):
                dve.wait_ge(summed, b + 1)
                for j in range(2):
                    step.mark(dve.tensor_reduce(
                        sums[:, j, :], ps[j][:, :].rearrange("p (q g j) -> p g q j", q=4, g=G), AX.XY, ALU.add))
                step.join()
                step(dve.tensor_tensor(var[:, :], sums[:, 0, :], sums[:, 0, :], ALU.mult))
                step(dve.scalar_tensor_tensor(out=var[:, :], in0=sums[:, 1, :], scalar=eps, in1=var[:, :],
                                              op0=ALU.add, op1=ALU.subtract))
                dve.sem_inc(var_done, 1)
                dve.wait_ge(rstd_done, b + 2)
                xv = xb[:, b % 2, :].rearrange("p (t g j) -> p t g j", t=T, g=G)
                hv = hg[:, b * T:(b + 1) * T, :].rearrange("p t (g j) -> p t g j", g=G)
                mean = sums[:, 0, :].unsqueeze(1).unsqueeze(3).broadcast_to([P, T, G, J])
                scale = rstd[:, :].unsqueeze(1).unsqueeze(3).broadcast_to([P, T, G, J])
                step(dve.tensor_tensor(hv, xv, mean, ALU.subtract))
                dve.tensor_tensor(hv, hv, scale, ALU.mult).then_inc(normed, 1)
                dve.wait_ge(normed, b + 1)


def graph_attention(nc, hg, adj, Wq, Wk, Wv, Wo, bo, gain, shift, h0, tag="gat", eps=1e-5):
    R, H = 4, 4
    D = C // H
    TURNS = BT // R
    BIG = 1e9 * math.sqrt(D)
    with ExitStack() as ctx:
        s = Scope(nc, ctx, tag)
        wq, wk, wv, wo = (s.sb(n, [P, C]) for n in ("wq", "wk", "wv", "wo"))
        ident = s.sb("ident", [P, P])
        ones1 = s.sb("ones1", [1, P])
        bo_row = s.sb("bo_row", [1, C])
        adj_sb = s.sb("adj", [P, P])
        keep = s.sb("keep", [P, P])
        lift = s.sb("lift", [P, P])
        gain_b = s.sb("gain", [P, C])
        shift_b = s.sb("shift", [P, C])
        hl = s.sb("hl", [P, R, C])
        hT = s.sb("hT", [P, R * W])
        qT = s.sb("qT", [P, R * W])
        kT = s.sb("kT", [P, R * W])
        vt = s.sb("vt", [P, R, C])
        sc = s.sb("sc", [P, 2, H, W])
        mx = s.sb("mx", [P, 2, H])
        ex = s.sb("ex", [P, 2, H, W])
        den = s.sb("den", [P, 2, H])
        pT = s.sb("pT", [P, 2, H, W])
        oT = s.sb("oT", [P, R * W])
        z = s.sb("z", [P, R, C])
        out = s.sb("out", [P, R, C])
        st = s.sb("st", [P, R, 6])
        mv = s.sb("mv", [P, R, 2])
        ve = s.sb("ve", [P, R])
        rstd = s.sb("rstd", [P, R])
        half = s.sb("half", [P, R])
        ps_h, ps_q, ps_k, ps_v = (s.ps(n) for n in ("ps_h", "ps_q", "ps_k", "ps_v"))
        ps_s = [s.ps(f"ps_s{j}") for j in range(2)]
        ps_p = [s.ps(f"ps_p{j}") for j in range(2)]
        ps_o, ps_z = ps_h, ps_v

        (loaded, made, staged, turned, hT_ready, projected, q_ready, k_ready, v_ready, scored, masked,
         exped, normed, flipped, pT_ready, mixed, oT_ready, outed, z_ready, ve_ready, rstd_ready,
         out_ready, stored, dch, pch) = (
            s.sem(n) for n in (
                "loaded", "made", "staged", "turned", "hT_ready", "projected", "q_ready", "k_ready",
                "v_ready", "scored", "masked", "exped", "normed", "flipped", "pT_ready", "mixed",
                "oT_ready", "outed", "z_ready", "ve_ready", "rstd_ready", "out_ready", "stored", "dch", "pch"))
        tick = s.sem("tick")
        LOADS = 8
        block = ctx.enter_context(nc.Block())

        @block.sync
        def _(sp):
            for dst, src in ((wq, Wq), (wk, Wk), (wv, Wv), (wo, Wo), (adj_sb, adj)):
                sp.dma_start(dst[:, :], src).then_inc(loaded, 16)
            sp.dma_start(bo_row[:, :], bo.unsqueeze(0)).then_inc(loaded, 16)
            sp.dma_start(gain_b[:, :], gain.unsqueeze(0).broadcast_to([P, C])).then_inc(loaded, 16)
            sp.dma_start(shift_b[:, :], shift.unsqueeze(0).broadcast_to([P, C])).then_inc(loaded, 16)
            rows = h0.rearrange("(i r) w c -> i w r c", r=R)
            with sp.Fori(0, TURNS) as i:
                sp.wait_ge(out_ready, i + 1)
                sp.dma_start(rows[i], out[:, :, :]).then_inc(stored, 16)
            sp.wait_ge(stored, 16 * TURNS)

        @block.gpsimd
        def _(pool):
            step = Chain(pool, pch)
            fill_identity(pool, step, ident)
            step(pool.memset(half[:, :], -0.5))
            step(pool.memset(ones1[:, :], 1.0))
            pool.sem_inc(made, 1)
            with pool.Fori(0, TURNS) as i:
                pool.wait_ge(turned, i)
                pool.tensor_copy(hl[:, :, :], hg[:, bass.ds(i * R, R), :]).then_inc(staged, 1)
                pool.wait_ge(ve_ready, i + 1)
                pool.tensor_tensor(rstd[:, :], ve[:, :], half[:, :], ALU.pow).then_inc(rstd_ready, 1)

        @block.tensor
        def _(pe):
            pe.wait_ge(loaded, 16 * LOADS)
            pe.wait_ge(made, 1)
            with pe.Fori(0, TURNS) as i:
                pe.wait_ge(staged, i + 1)
                pe.wait_ge(oT_ready, i)
                for r in range(R):
                    last = pe.transpose(ps_h[:, r * W:(r + 1) * W], hl[:, r, :], ident[:, :])
                last.then_inc(turned, 1)
                pe.wait_ge(hT_ready, i + 1)
                pe.matmul(ps_q[:, :], wq[:, :], hT[:, :], start=True, stop=True)
                pe.matmul(ps_k[:, :], wk[:, :], hT[:, :], start=True, stop=True)
                pe.wait_ge(z_ready, i)
                for r in range(R):
                    last = pe.matmul(ps_v[:, r * C:(r + 1) * C], hT[:, r * W:(r + 1) * W], wv[:, :],
                                     start=True, stop=True)
                last.then_inc(projected, 1)

                def scores(h):
                    d = slice(h * D, (h + 1) * D)
                    for r in range(R):
                        last = pe.matmul(ps_s[h % 2][:, r * W:(r + 1) * W], qT[d, r * W:(r + 1) * W],
                                         kT[d, r * W:(r + 1) * W], start=True, stop=True,
                                         tile_position=(h * D, 0))
                    last.then_inc(scored, 1)

                pe.wait_ge(q_ready, i + 1)
                pe.wait_ge(k_ready, i + 1)
                scores(0)
                scores(1)
                for h in range(H):
                    pe.wait_ge(normed, i * H + h + 1)
                    for r in range(R):
                        last = pe.transpose(ps_p[h % 2][:, r * W:(r + 1) * W], ex[:, h % 2, r, :], ident[:, :])
                    last.then_inc(flipped, 1)
                    if h + 2 < H:
                        scores(h + 2)
                    pe.wait_ge(pT_ready, i * H + h + 1)
                    if h == 0:
                        pe.wait_ge(v_ready, i + 1)
                    d = slice(h * D, (h + 1) * D)
                    for r in range(R):
                        last = pe.matmul(ps_o[d, r * W:(r + 1) * W], vt[:, r, d], pT[:, h % 2, r, :],
                                         start=True, stop=True, tile_position=(0, h * D))
                last.then_inc(mixed, 1)
                pe.wait_ge(oT_ready, i + 1)
                for r in range(R):
                    pe.matmul(ps_z[:, r * C:(r + 1) * C], oT[:, r * W:(r + 1) * W], wo[:, :],
                              start=True, stop=False)
                    last = pe.matmul(ps_z[:, r * C:(r + 1) * C], ones1[:, :], bo_row[:, :],
                                     start=False, stop=True)
                last.then_inc(outed, 1)

        @block.scalar
        def _(act):
            with act.Fori(0, TURNS) as i:
                act.wait_ge(turned, i + 1)
                act.wait_ge(projected, i)
                act.copy(hT[:, :], ps_h[:, :]).then_inc(hT_ready, 1)
                act.wait_ge(projected, i + 1)
                act.copy(qT[:, :], ps_q[:, :]).then_inc(q_ready, 1)
                act.copy(vt[:, :, :], ps_v[:, :].rearrange("p (r c) -> p r c", r=R)).then_inc(v_ready, 1)
                for r in range(R):
                    act.wait_ge(masked, i * R + r + 1)
                    act.wait_ge(flipped, i * R + r - 1) if r >= 2 else act.wait_ge(mixed, i)
                    act.activation(ex[:, r % 2, :, :], sc[:, r % 2, :, :], ACT.Exp,
                                   scale=1.0 / math.sqrt(D)).then_inc(exped, 1)
                    act.wait_ge(flipped, i * R + r + 1)
                    act.copy(pT[:, r % 2, :, :], ps_p[r % 2][:, :].rearrange("p (h w) -> p h w", h=H)
                             ).then_inc(pT_ready, 1)
                act.wait_ge(mixed, i + 1)
                act.copy(oT[:, :], ps_o[:, :]).then_inc(oT_ready, 1)

        @block.vector
        def _(dve):
            step = Chain(dve, dch)
            dve.wait_ge(loaded, 16 * LOADS)
            dve.wait_ge(made, 1)
            step(dve.tensor_scalar(keep[:, :], adj_sb[:, :], 0.0, None, ALU.not_equal))
            step(dve.tensor_scalar(lift[:, :], keep[:, :], 1.0, BIG, ALU.subtract, ALU.mult))
            keep_b = keep[:, :].unsqueeze(1).broadcast_to([P, H, W])
            lift_b = lift[:, :].unsqueeze(1).broadcast_to([P, H, W])

            def mask(i, r):
                q = r % 2
                dve.wait_ge(scored, i * R + r + 1)
                step(dve.tensor_tensor(sc[:, q, :, :], ps_s[q][:, :].rearrange("p (h w) -> p h w", h=H),
                                       keep_b, ALU.mult))
                step(dve.tensor_tensor(sc[:, q, :, :], sc[:, q, :, :], lift_b, ALU.add))
                step(dve.tensor_reduce(mx[:, q, :], sc[:, q, :, :], AX.X, ALU.max))
                step(dve.tensor_tensor(sc[:, q, :, :], sc[:, q, :, :],
                                       mx[:, q, :].unsqueeze(2).broadcast_to([P, H, W]), ALU.subtract))
                dve.sem_inc(masked, 1)

            def norm(i, r):
                q = r % 2
                dve.wait_ge(exped, i * R + r + 1)
                step(dve.tensor_reduce(den[:, q, :], ex[:, q, :, :], AX.X, ALU.add))
                step(dve.reciprocal(den[:, q, :], den[:, q, :]))
                step(dve.tensor_tensor(ex[:, q, :, :], ex[:, q, :, :],
                                       den[:, q, :].unsqueeze(2).broadcast_to([P, H, W]), ALU.mult))
                dve.sem_inc(normed, 1)

            with step.loop(TURNS, 7 * R + 1 + 2 * R + 1 + R + 2) as i:
                dve.wait_ge(projected, i + 1)
                dve.tensor_copy(kT[:, :], ps_k[:, :]).then_inc(k_ready, 1)
                mask(i, 0)
                for r in range(R):
                    if r + 1 < R:
                        mask(i, r + 1)
                    norm(i, r)
                dve.wait_ge(outed, i + 1)
                step(dve.scalar_tensor_tensor(
                    out=z[:, :, :], in0=hg[:, bass.ds(i * R, R), :], scalar=2.0,
                    in1=ps_z[:, :].rearrange("p (r c) -> p r c", r=R), op0=ALU.mult, op1=ALU.add))
                dve.sem_inc(z_ready, 1)
                for r in range(R):
                    step.mark(dve.bn_stats(st[:, r, :], z[:, r, :]))
                step.join()
                dve.sem_inc(tick, 1)
                for r in range(R):
                    step.mark(dve.bn_aggr(mv[:, r, :], st[:, r, :]))
                step.join()
                step(dve.tensor_scalar(ve[:, :], mv[:, :, 1], eps, None, ALU.add))
                dve.sem_inc(ve_ready, 1)
                dve.wait_ge(rstd_ready, i + 1)
                dve.wait_ge(stored, i * 16)
                for r in range(R):
                    step.mark(dve.tensor_scalar(out[:, r, :], z[:, r, :], mv[:, r, 0:1], rstd[:, r:r + 1],
                                                ALU.subtract, ALU.mult))
                step.join()
                step(dve.tensor_tensor(out[:, :, :], out[:, :, :],
                                       gain_b[:, :].unsqueeze(1).broadcast_to([P, R, C]), ALU.mult))
                step(dve.tensor_tensor(out[:, :, :], out[:, :, :],
                                       shift_b[:, :].unsqueeze(1).broadcast_to([P, R, C]), ALU.add))
                dve.sem_inc(out_ready, 1)


def mamba(nc, h0, x, in_proj, conv_w, conv_b, x_proj, dt_w, dt_b, A_log, Dp, out_w, out_b, gain, shift,
          x1, tag="mam", eps=1e-5):
    Q = 16
    G, J = 4, 4
    NQ = W // Q
    N = Q * T
    K = conv_w.shape[1]
    S = A_log.shape[1]
    DI = A_log.shape[0]
    HV = DI // P
    RK = dt_w.shape[0]
    PADT = T + K - 1
    TURNS = B * NQ
    with ExitStack() as ctx:
        s = Scope(nc, ctx, tag)
        w_in = s.sb("w_in", [P, 2 * DI])
        w_conv = s.sb("w_conv", [P, K, DI])
        cw_b = s.sb("cw_b", [P, DI, K])
        cb = s.sb("cb", [P, HV])
        xp = s.sb("xp", [P, HV, RK + 2 * S])
        xp3 = s.sb("xp3", [P, HV, 3, 2 * S])
        dtw = s.sb("dtw", [RK, DI])
        dtb = s.sb("dtb", [P, HV])
        A = s.sb("A", [P, HV, S])
        dp = s.sb("dp", [P, HV])
        ow = s.sb("ow", [P, HV, C])
        ob = s.sb("ob", [1, C])
        gain_b = s.sb("gain", [P, C])
        shift_b = s.sb("shift", [P, C])
        ident = s.sb("ident", [P, P])
        ones1 = s.sb("ones1", [1, P])
        half_c = s.sb("half", [P, G])
        sel = s.sb("sel", [96, 2 * S, P], bf16)

        ht = s.sb("ht", [P, G, C])
        xt = s.sb("xt", [P, G, C])
        hT = s.sb("hT", [P, Q, PADT])
        xs = s.sb("xs", [P, HV, N])
        sz = s.sb("sz", [P, HV, N])
        dtr = s.sb("dtr", [RK, N])
        bcf = s.sb("bcf", [96, N])
        bc3 = s.sb("bc3", [96, N], bf16)
        mid = s.sb("mid", [96, N], bf16)
        e = s.sb("e", [P, HV, N])
        ln = s.sb("ln", [P, HV, N])
        po = s.sb("po", [P, HV, N])
        small = s.sb("small", [P, HV, N], u8)
        dt = s.sb("dt", [P, HV, N])
        dtx = s.sb("dtx", [P, HV, N])
        dA = [s.sb(f"dA{j}", [P, Q, T]) for j in range(4)]
        dBx = [s.sb(f"dBx{j}", [P, N]) for j in range(2)]
        hs = [s.sb(f"hs{j}", [P, N]) for j in range(2)]
        hc = [s.sb(f"hc{j}", [P, N]) for j in range(4)]
        y = s.sb("y", [P, HV, N])
        z = s.sb("z", [P, G, C])
        out = s.sb("out", [P, G, C])
        st = s.sb("st", [P, G, 6])
        mv = s.sb("mv", [P, G, 2])
        ve = s.sb("ve", [P, G])
        rstd = s.sb("rstd", [P, G])
        ps_b = [s.ps(f"ps_b{j}") for j in range(2)]
        ps_c = [s.ps(f"ps_c{j}") for j in range(2)]
        ps_y = [s.ps(f"ps_y{j}") for j in range(2)]
        ps_0, ps_1 = s.ps("ps_0"), s.ps("ps_1")

        (loaded, made, prepared, xin, turned, hT_ready, convd, silud, bc_made, bc_copied, dtr_ready,
         bc_ready, dt_made, exps, dt_ready, spread, dA_ready, product, scanned, y_done, y_ready, outed,
         z_ready, ve_ready, rstd_ready, out_ready, stored, dch, pch, ach, tick) = (
            s.sem(n) for n in (
                "loaded", "made", "prepared", "xin", "turned", "hT_ready", "convd", "silud", "bc_made",
                "bc_copied", "dtr_ready", "bc_ready", "dt_made", "exps", "dt_ready", "spread", "dA_ready",
                "product", "scanned", "y_done", "y_ready", "outed", "z_ready", "ve_ready", "rstd_ready",
                "out_ready", "stored", "dch", "pch", "ach", "tick"))
        block = ctx.enter_context(nc.Block())
        LOADS = 13
        soft_step = s.sem("soft_step")

        def tokens(v, b, k, j):
            return v[b].rearrange("t (k g j) c -> k j t g c", k=NQ, g=G)[k, j]

        h0v = h0.rearrange("(b t) w c -> b t w c", b=B)

        @block.sync
        def _(sp):
            sp.dma_start(w_in[:, :], in_proj).then_inc(loaded, 16)
            sp.dma_start(cw_b[:, :, :], conv_w.rearrange("d k -> (d k)").unsqueeze(0)
                         .broadcast_to([P, DI * K]).rearrange("p (d k) -> p d k", k=K)).then_inc(loaded, 16)
            sp.dma_start(xp[:, :, :], x_proj.rearrange("(h d) r -> d h r", h=HV)).then_inc(loaded, 16)
            sp.dma_start(dtw[:, :], dt_w).then_inc(loaded, 16)
            sp.dma_start(A[:, :, :], A_log.rearrange("(h d) s -> d h s", h=HV)).then_inc(loaded, 16)
            sp.dma_start(ow[:, :, :], out_w.rearrange("(h d) c -> d h c", h=HV)).then_inc(loaded, 16)
            for dst, src in ((cb, conv_b), (dtb, dt_b), (dp, Dp)):
                for h in range(HV):
                    sp.dma_start(dst[:, h:h + 1], src[h * P:(h + 1) * P].unsqueeze(1)).then_inc(loaded, 16)
            sp.dma_start(ob[:, :], out_b.unsqueeze(0)).then_inc(loaded, 16)
            for dst, src in ((gain_b, gain), (shift_b, shift)):
                sp.dma_start(dst[:, :], src.unsqueeze(0).broadcast_to([P, C])).then_inc(made, 16)
            with sp.Fori(0, B) as b:
                with sp.Fori(0, NQ) as k:
                    i = b * NQ + k
                    sp.wait_ge(out_ready, i)
                    for j in range(J):
                        sp.dma_start(ht[j * T:(j + 1) * T, :, :], tokens(h0v, b, k, j)).then_inc(xin, 16)
                        sp.dma_start(xt[j * T:(j + 1) * T, :, :], tokens(x, b, k, j)).then_inc(xin, 16)
                    sp.wait_ge(out_ready, i + 1)
                    for j in range(J):
                        sp.dma_start(tokens(x1, b, k, j), out[j * T:(j + 1) * T, :, :]).then_inc(stored, 16)
            sp.wait_ge(stored, 16 * J * TURNS)

        XIN = 16 * 2 * J

        @block.gpsimd
        def _(pool):
            step = Chain(pool, pch)
            fill_identity(pool, step, ident)
            step(pool.memset(half_c[:, :], -0.5))
            step(pool.memset(ones1[:, :], 1.0))
            step(pool.memset(hT[:, :, :], 0.0))
            for a in dA:
                step(pool.memset(a[:, :, :], 0.0))
            step(pool.memset(sel[:, :, :], 0.0))
            for j in range(3):
                step(pool.affine_select(out=sel[:, :, :], in_=sel[:, :, :], compare_op=ALU.not_equal, fill=1.0,
                                        base=-32 * j, pattern=[[-1, 2 * S], [0, P]], channel_multiplier=1))
            pool.wait_ge(loaded, 16 * LOADS)
            for k in range(K):
                step(pool.tensor_tensor(w_conv[:, k, :], w_in[:, 0:DI], cw_b[:, :, k], ALU.mult))
            for j in range(3):
                step(pool.tensor_copy(xp3[:, :, j, :], xp[:, :, RK:RK + 2 * S]))
            pool.sem_inc(prepared, 1)
            with pool.Fori(0, TURNS) as i:
                pool.wait_ge(ve_ready, i + 1)
                pool.tensor_tensor(rstd[:, :], ve[:, :], half_c[:, :], ALU.pow).then_inc(rstd_ready, 1)

        @block.tensor
        def _(pe):
            pe.wait_ge(loaded, 16 * LOADS)
            pe.wait_ge(prepared, 1)
            with pe.Fori(0, TURNS) as i:
                pe.wait_ge(xin, XIN * (i + 1))
                for g in range(G):
                    last = pe.transpose(ps_0[:, g * P:(g + 1) * P], ht[:, g, :], ident[:, :])
                last.then_inc(turned, 1)
                pe.wait_ge(hT_ready, i + 1)
                for h in range(HV):
                    for k in range(K):
                        pe.matmul(ps_b[h][:, :].rearrange("p (q t) -> p q t", q=Q),
                                  w_conv[:, k, h * P:(h + 1) * P], hT[:, :, k:k + T],
                                  start=(k == 0), stop=(k == K - 1))
                    last = pe.matmul(ps_c[h][:, :].rearrange("p (q t) -> p q t", q=Q),
                                     w_in[:, DI + h * P:DI + (h + 1) * P], hT[:, :, K - 1:K - 1 + T],
                                     start=True, stop=True)
                last.then_inc(convd, 1)
                pe.wait_ge(silud, i + 1)
                for h in range(HV):
                    pe.matmul(ps_1[0:RK, :], xp[:, h, 0:RK], xs[:, h, :], start=(h == 0), stop=(h == HV - 1))
                for h in range(HV):
                    last = pe.matmul(ps_0[0:96, :], xp3[:, h, :, :].rearrange("p a s -> p (a s)"), xs[:, h, :],
                                     start=(h == 0), stop=(h == HV - 1))
                last.then_inc(bc_made, 1)
                pe.wait_ge(dtr_ready, i + 1)
                for h in range(HV):
                    last = pe.matmul(ps_b[h][:, :], dtw[:, h * P:(h + 1) * P], dtr[:, :], start=True, stop=True)
                last.then_inc(dt_made, 1)
                pe.wait_ge(bc_ready, i + 1)
                pe.wait_ge(exps, i + 1)

                def spread_state(n):
                    pe.matmul(ps_b[n % 2][:, :], sel[:, n, :], bc3[:, :], start=True, stop=True)
                    pe.matmul(ps_c[n % 2][:, :], sel[:, S + n, :], bc3[:, :], start=True, stop=True
                              ).then_inc(spread, 1)

                spread_state(0)
                spread_state(1)
                for n in range(S):
                    for h in range(HV):
                        pe.wait_ge(scanned, (i * S + n) * HV + h + 1)
                        last = pe.matmul(ps_y[h][:, :], ident[:, :], hc[(n * HV + h) % 4][:, :],
                                         start=(n == 0), stop=(n == S - 1))
                        last.then_inc(y_done, 1)
                    if n + 2 < S:
                        spread_state(n + 2)
                pe.wait_ge(y_ready, i + 1)
                for g in range(G):
                    cols = slice(g * P, (g + 1) * P)
                    for h in range(HV):
                        pe.matmul(ps_1[:, cols], y[:, h, cols], ow[:, h, :], start=(h == 0), stop=False)
                    last = pe.matmul(ps_1[:, cols], ones1[:, :], ob[:, :], start=False, stop=True)
                last.then_inc(outed, 1)

        @block.scalar
        def _(act):
            step = Chain(act, ach)
            act.wait_ge(loaded, 16 * LOADS)
            step(act.activation(A[:, :, :], A[:, :, :], ACT.Exp))
            step(act.mul(A[:, :, :], A[:, :, :], -1.0))
            act.wait_ge(prepared, 1)
            with act.Fori(0, TURNS) as i:
                act.wait_ge(turned, i + 1)
                act.copy(hT[:, :, K - 1:], ps_0[:, :].rearrange("p (q t) -> p q t", q=Q)).then_inc(hT_ready, 1)
                act.wait_ge(convd, i + 1)
                for h in range(HV):
                    act.activation(xs[:, h, :], ps_b[h][:, :], ACT.Silu, bias=cb[:, h:h + 1])
                    last = act.activation(sz[:, h, :], ps_c[h][:, :], ACT.Silu)
                last.then_inc(silud, 1)
                act.wait_ge(bc_made, i + 1)
                act.copy(dtr[:, :], ps_1[0:RK, :]).then_inc(dtr_ready, 1)
                act.copy(bc3[:, :], ps_0[0:96, :]).then_inc(bc_copied, 1)
                act.wait_ge(dt_made, i + 1)
                for h in range(HV):
                    act.activation(e[:, h, :], ps_b[h][:, :], ACT.Abs, bias=dtb[:, h:h + 1])
                    last = act.activation(dt[:, h, :], ps_b[h][:, :], ACT.Relu, bias=dtb[:, h:h + 1])
                last.then_inc(soft_step, 1)
                act.wait_ge(soft_step, 2 * i + 1)
                act.activation(e[:, :, :], e[:, :, :], ACT.Exp, scale=-1.0).then_inc(soft_step, 1)
                act.wait_ge(soft_step, 2 * i + 2)
                act.activation(ln[:, :, :], e[:, :, :], ACT.Ln, bias=1.0).then_inc(exps, 1)
                act.wait_ge(dt_ready, i + 1)
                for n in range(S):
                    for h in range(HV):
                        m = n * HV + h
                        if m >= 4:
                            act.wait_ge(scanned, (i * S) * HV + m - 3)
                        act.activation(dA[m % 4][:, :, 1:],
                                       dt[:, h, :].rearrange("p (q t) -> p q t", q=Q)[:, :, 1:],
                                       ACT.Exp, scale=A[:, h, n:n + 1]).then_inc(dA_ready, 1)


        @block.vector
        def _(dve):
            step = Chain(dve, dch)
            dve.wait_ge(loaded, 16 * LOADS)
            dve.wait_ge(made, 32)
            dve.wait_ge(prepared, 1)
            with step.loop(TURNS, 4 + 7 + 3 * S * HV + 2 * HV + 1 + 2 * G + 1 + G + 3) as i:
                dve.wait_ge(bc_copied, i + 1)
                step(dve.tensor_tensor(bcf[:, :], ps_0[0:96, :], bc3[:, :], ALU.subtract))
                step(dve.tensor_copy(mid[:, :], bcf[:, :]))
                step.mark(dve.tensor_copy(bc3[32:64, :], mid[32:64, :]))
                step(dve.tensor_tensor(bc3[64:96, :], bcf[64:96, :], mid[64:96, :], ALU.subtract))
                dve.sem_inc(bc_ready, 1)
                dve.wait_ge(exps, i + 1)
                step(dve.tensor_scalar(po[:, :, :], e[:, :, :], -0.25, 1.0 / 3, ALU.mult, ALU.add))
                step(dve.tensor_tensor(po[:, :, :], po[:, :, :], e[:, :, :], ALU.mult))
                step(dve.scalar_tensor_tensor(out=po[:, :, :], in0=po[:, :, :], scalar=-0.5, in1=e[:, :, :],
                                              op0=ALU.add, op1=ALU.mult))
                step(dve.scalar_tensor_tensor(out=po[:, :, :], in0=po[:, :, :], scalar=1.0, in1=e[:, :, :],
                                              op0=ALU.add, op1=ALU.mult))
                step(dve.tensor_scalar(small[:, :, :], e[:, :, :], 0.06, None, ALU.is_lt))
                dve.sem_inc(tick, 1)
                step(dve.copy_predicated(ln[:, :, :], small[:, :, :], po[:, :, :]))
                step(dve.tensor_tensor(dt[:, :, :], dt[:, :, :], ln[:, :, :], ALU.add))
                dve.tensor_tensor(dtx[:, :, :], dt[:, :, :], xs[:, :, :], ALU.mult).then_inc(dt_ready, 1)
                dve.wait_ge(dt_ready, i + 1)
                for n in range(S):
                    dve.wait_ge(spread, i * S + n + 1)
                    for h in range(HV):
                        m = n * HV + h
                        step(dve.tensor_tensor(dBx[m % 2][:, :], dtx[:, h, :], ps_b[n % 2][:, :], ALU.mult))
                        dve.wait_ge(dA_ready, i * S * HV + m + 1)
                        step(dve.tensor_tensor_scan(hs[m % 2][:, :], dA[m % 4][:, :, :].rearrange("p q t -> p (q t)"),
                                                    dBx[m % 2][:, :], 0.0, ALU.mult, ALU.add))
                        if m >= 4:
                            dve.wait_ge(y_done, i * S * HV + m - 3)
                        step(dve.tensor_tensor(hc[m % 4][:, :], hs[m % 2][:, :], ps_c[n % 2][:, :], ALU.mult))
                        dve.sem_inc(scanned, 1)
                dve.wait_ge(y_done, (i + 1) * S * HV)
                for h in range(HV):
                    step(dve.scalar_tensor_tensor(out=y[:, h, :], in0=xs[:, h, :], scalar=dp[:, h:h + 1],
                                                  in1=ps_y[h][:, :], op0=ALU.mult, op1=ALU.add))
                    step(dve.tensor_tensor(y[:, h, :], y[:, h, :], sz[:, h, :], ALU.mult))
                dve.sem_inc(y_ready, 1)
                dve.wait_ge(outed, i + 1)
                step(dve.tensor_tensor(z[:, :, :], ht[:, :, :], ps_1[:, :].rearrange("p (g c) -> p g c", g=G), ALU.add))
                for g in range(G):
                    step.mark(dve.bn_stats(st[:, g, :], z[:, g, :]))
                step.join()
                dve.sem_inc(tick, 1)
                for g in range(G):
                    step.mark(dve.bn_aggr(mv[:, g, :], st[:, g, :]))
                step.join()
                step(dve.tensor_scalar(ve[:, :], mv[:, :, 1], eps, None, ALU.add))
                dve.sem_inc(ve_ready, 1)
                dve.wait_ge(rstd_ready, i + 1)
                dve.wait_ge(stored, i * 16 * J)
                for g in range(G):
                    step.mark(dve.tensor_scalar(out[:, g, :], z[:, g, :], mv[:, g, 0:1], rstd[:, g:g + 1],
                                                ALU.subtract, ALU.mult))
                step.join()
                step(dve.tensor_tensor(out[:, :, :], out[:, :, :],
                                       gain_b[:, :].unsqueeze(1).broadcast_to([P, G, C]), ALU.mult))
                step(dve.tensor_tensor(out[:, :, :], out[:, :, :],
                                       shift_b[:, :].unsqueeze(1).broadcast_to([P, G, C]), ALU.add))
                step(dve.tensor_tensor(out[:, :, :], out[:, :, :], xt[:, :, :], ALU.add))
                dve.sem_inc(out_ready, 1)


NKY, NKX = 32, 17
LKY, LKX = 16, 9
SR = 64
ROWS = [k if k < NKY // 2 else k - NKY for k in range(NKY)]
IMG = W * C


def fourier_tables():
    n = np.arange(W, dtype=np.float64)
    al = 2 * np.pi / W
    r2 = SR // 2
    k = np.arange(r2 + 1)
    cos, sin = np.cos(al * np.outer(n, k)), np.sin(al * np.outer(n, k))
    scale = np.where((k == 0) | (k == r2), 1.0, np.sqrt(2.0))
    t = {}
    t["rows_all"] = np.concatenate([cos, sin[:, 1:]], 1) / W
    t["gram_cols"] = np.concatenate([cos * scale, sin * scale], 1) / W
    cx, sx = cos[:, :NKX], sin[:, :NKX]
    t["tok_cols"] = np.concatenate([cx, -sx, -sx, -cx, sx, cx], 1) / W
    kr = np.array(ROWS)
    cr, sr = np.cos(al * np.outer(n, kr)), np.sin(al * np.outer(n, kr))
    t["rows_fwd"] = np.concatenate([cr, -sr], 1) / W
    z = np.zeros((W, 32 - NKX))
    t["cols_fwd"] = np.concatenate([cx, z, -sx, z, sx, z, cx, z], 1) / W
    m = np.where(np.arange(NKX) == 0, 1.0, 2.0)[:, None]
    mc, ms, zz = m * cx.T, m * sx.T, np.zeros((32 - NKX, W))
    g1 = np.concatenate([np.concatenate([mc, zz, -ms, zz]), np.concatenate([ms, zz, mc, zz])], 1)
    g2 = np.concatenate([np.concatenate([-ms, zz, -mc, zz]), np.concatenate([mc, zz, -ms, zz])], 1)
    t["cols_inv"] = np.concatenate([g1, g2], 1)
    t["rows_inv"] = np.concatenate([cr.T, -sr.T], 1)
    return {a: np.ascontiguousarray(b.astype(np.float32)) for a, b in t.items()}


def inline_tables(nc):
    return {a: nc.inline_tensor(b, name=f"table_{a}").ap()
            for a, b in fourier_tables().items()}


def token_images(nc, hg, g1, b1, tok, tnd, tag="l1n", eps=1e-5):
    with ExitStack() as ctx:
        s = Scope(nc, ctx, tag)
        sq = s.sb("sq", [P, 8, C])
        sums = s.sb("sums", [P, 2, BT])
        ones = s.sb("ones", [P, P])
        gb = s.sb("gb", [P, 2])
        var, rstd, half, scale, bias = (s.sb(n, [P, BT]) for n in ("var", "rstd", "half", "scale", "bias"))
        ps = s.ps("ps")
        loaded, made, saved, squared, reduced, summed, var_ready, rstd_ready, ready, dch = (
            s.sem(n) for n in ("loaded", "made", "saved", "squared", "reduced", "summed", "var_ready",
                               "rstd_ready", "ready", "dch"))
        block = ctx.enter_context(nc.Block())

        @block.sync
        def _(sp):
            for j, src in enumerate((g1, b1)):
                sp.dma_start(gb[:, j:j + 1], src.unsqueeze(0).broadcast_to([P, 1])).then_inc(loaded, 16)
            sp.dma_start(tok.rearrange("n r c -> r n c"), hg[:, :, :]).then_inc(saved, 16)
            sp.wait_ge(ready, BT // 8)
            sp.dma_start(tnd.rearrange("n r c -> r n c"), hg[:, :, :]).then_inc(saved, 16)
            sp.wait_ge(saved, 32)

        @block.gpsimd
        def _(pool):
            pool.memset(ones[:, :], 1.0 / IMG).then_inc(made, 1)
            pool.memset(half[:, :], -0.5).then_inc(made, 1)
            pool.wait_ge(made, 2)
            pool.wait_ge(var_ready, 1)
            pool.tensor_tensor(rstd[:, :], var[:, :], half[:, :], ALU.pow).then_inc(rstd_ready, 1)

        @block.scalar
        def _(act):
            with act.Fori(0, BT // 8) as i:
                act.wait_ge(reduced, i)
                act.activation(sq[:, :, :], hg[:, bass.ds(i * 8, 8), :], ACT.Square).then_inc(squared, 1)

        @block.tensor
        def _(pe):
            pe.wait_ge(made, 2)
            pe.wait_ge(reduced, BT // 8)
            pe.matmul(ps[:, 0:2 * BT], ones[:, :], sums[:, :, :].rearrange("p a n -> p (a n)"),
                      start=True, stop=True).then_inc(summed, 1)

        @block.vector
        def _(dve):
            step = Chain(dve, dch)
            with step.loop(BT // 8, 2) as i:
                step.mark(dve.tensor_reduce(sums[:, 0, bass.ds(i * 8, 8)], hg[:, bass.ds(i * 8, 8), :], AX.X, ALU.add))
                dve.wait_ge(squared, i + 1)
                step(dve.tensor_reduce(sums[:, 1, bass.ds(i * 8, 8)], sq[:, :, :], AX.X, ALU.add))
                dve.sem_inc(reduced, 1)
            dve.wait_ge(summed, 1)
            dve.wait_ge(loaded, 32)
            step(dve.tensor_copy(sums[:, :, :], ps[:, 0:2 * BT].rearrange("p (a n) -> p a n", a=2)))
            step(dve.tensor_tensor(var[:, :], sums[:, 0, :], sums[:, 0, :], ALU.mult))
            step(dve.scalar_tensor_tensor(out=var[:, :], in0=sums[:, 1, :], scalar=eps, in1=var[:, :],
                                          op0=ALU.add, op1=ALU.subtract))
            dve.sem_inc(var_ready, 1)
            dve.wait_ge(rstd_ready, 1)
            step(dve.tensor_scalar(scale[:, :], rstd[:, :], gb[:, 0:1], None, ALU.mult))
            step(dve.tensor_tensor(bias[:, :], sums[:, 0, :], scale[:, :], ALU.mult))
            step(dve.tensor_scalar(bias[:, :], bias[:, :], -1.0, gb[:, 1:2], ALU.mult, ALU.add))
            dve.wait_ge(saved, 16)
            with step.loop(BT // 8, 2) as i:
                v = hg[:, bass.ds(i * 8, 8), :]
                step(dve.tensor_tensor(v, v, scale[:, bass.ds(i * 8, 8)].unsqueeze(2).broadcast_to([P, 8, C]), ALU.mult))
                step(dve.tensor_tensor(v, v, bias[:, bass.ds(i * 8, 8)].unsqueeze(2).broadcast_to([P, 8, C]), ALU.add))
                dve.sem_inc(ready, 1)


def token_spectra(nc, tn, tabs, xh, gram_d, tag="l1f"):
    R = 4
    KA = SR + 1
    h = SR // 2
    with ExitStack() as ctx:
        s = Scope(nc, ctx, tag)
        rows = s.sb("rows", [P, KA])
        cols = s.sb("cols", [P, 2 * (h + 1)])
        tcols = s.sb("tcols", [P, 3, 2 * NKX])
        o1 = s.sb("o1", [P, KA, BT])
        img = [s.sb(f"img{j}", [P, R, C]) for j in range(2)]
        loaded, staged, done, copied = (s.sem(n) for n in ("loaded", "staged", "done", "copied"))
        with ExitStack() as c2:
            s2 = Scope(nc, c2, tag + "a")
            ps = [s2.ps(f"ps{j}") for j in range(2)]
            block = c2.enter_context(nc.Block())

            @block.sync
            def _(sp):
                for dst, src in ((rows[:, :], tabs["rows_all"]), (cols[:, :], tabs["gram_cols"]),
                                 (tcols[:, :, :].rearrange("p a k -> p (a k)"), tabs["tok_cols"])):
                    sp.dma_start(dst, src).then_inc(loaded, 16)

            @block.gpsimd
            def _(pool):
                with pool.Fori(0, BT // R // 2) as i:
                    for j in range(2):
                        pool.wait_ge(done, 2 * i + j - 1) if j else pool.wait_ge(done, 2 * i)
                        pool.tensor_copy(img[j][:, :, :], tn[:, bass.ds(i * 2 * R + j * R, R), :]).then_inc(staged, 1)

            @block.tensor
            def _(pe):
                pe.wait_ge(loaded, 48)
                with pe.Fori(0, BT // R // 2) as i:
                    for j in range(2):
                        pe.wait_ge(staged, 2 * i + j + 1)
                        pe.wait_ge(copied, 2 * i)
                        for r in range(R):
                            last = pe.matmul(ps[j][:, r * KA:(r + 1) * KA], img[j][:, r, :], rows[:, :],
                                             start=True, stop=True)
                        last.then_inc(done, 1)

            @block.scalar
            def _(act):
                with act.Fori(0, BT // R // 2) as i:
                    for j in range(2):
                        act.wait_ge(done, 2 * i + j + 1)
                        act.copy(o1[:, :, bass.ds(i * 2 * R + j * R, R)],
                                 ps[j][:, 0:R * KA].rearrange("p (r k) -> p k r", r=R)).then_inc(copied, 1)

        with ExitStack() as c2:
            s2 = Scope(nc, c2, tag + "b")
            NB = 4
            ps = [s2.ps(f"ps{j}") for j in range(NB)]
            made, read = s2.sem("made"), s2.sem("read")
            PER = 8
            block = c2.enter_context(nc.Block())

            @block.tensor
            def _(pe):
                for n, ky in enumerate(ROWS):
                    at = (n % PER) * 2 * NKX
                    dst = ps[n // PER][:, at:at + 2 * NKX]
                    last = pe.matmul(dst, o1[:, abs(ky), :], tcols[:, 0, :], start=True, stop=(ky == 0))
                    if ky:
                        last = pe.matmul(dst, o1[:, h + abs(ky), :], tcols[:, 1 if ky > 0 else 2, :],
                                         start=False, stop=True)
                    if n % PER == PER - 1:
                        last.then_inc(made, 1)

            @block.scalar
            def _(act):
                for n in range(NB):
                    act.wait_ge(made, n + 1)
                    act.copy(xh[:, n * PER:(n + 1) * PER, :, :],
                             ps[n][:, 0:PER * 2 * NKX].rearrange("p (k a x) -> p k a x", k=PER, a=2)).then_inc(read, 1)

        with ExitStack() as c2:
            s2 = Scope(nc, c2, tag + "c")
            H1 = h + 1
            z = [s2.sb(f"z{j}", [H1, KA, BT]) for j in range(2)]
            p12 = s2.sb("p12", [H1, 2, BT])
            inner = s2.sb("inner", [H1, 1])
            gs = s2.sb("gs", [P, BT])
            ps = [s2.ps(f"ps{j}") for j in range(4)]
            ps_g = s2.ps("ps_g")
            made, read, zready, gdone, gcopied, stored, dch, pch = (
                s2.sem(n) for n in ("made", "read", "zready", "gdone", "gcopied", "stored", "dch", "pch"))
            block = c2.enter_context(nc.Block())
            PER = 4
            parts = [(k, min(PER, KA - k)) for k in range(0, KA, PER)]
            units = [(k, n, a) for k, n in parts for a in range(2)]

            @block.tensor
            def _(pe):
                for u, (k, n, a) in enumerate(units):
                    if u >= 4:
                        pe.wait_ge(read, u - 3)
                    pe.matmul(ps[u % 4][0:H1, 0:n * BT], cols[:, a * H1:(a + 1) * H1],
                              o1[:, k:k + n, :].rearrange("p k n -> p (k n)"),
                              start=True, stop=True).then_inc(made, 1)
                pe.wait_ge(zready, 1)
                first = True
                for k in range(KA):
                    if k == h or k == 2 * h:
                        continue
                    pe.matmul(ps_g[:, 0:BT], z[0][:, k, :], z[0][:, k, :], start=first, stop=False)
                    pe.matmul(ps_g[:, 0:BT], z[1][0:h, k, :], z[1][0:h, k, :], start=False, stop=False)
                    first = False
                pe.matmul(ps_g[:, 0:BT], p12[:, 0, :], p12[:, 0, :], start=False, stop=False)
                pe.matmul(ps_g[:, 0:BT], p12[0:h, 1, :], p12[0:h, 1, :], start=False, stop=True).then_inc(gdone, 1)

            @block.gpsimd
            def _(pool):
                step = Chain(pool, pch)
                step(pool.memset(inner[:, :], 1.0))
                step(pool.affine_select(out=inner[:, :], in_=inner[:, :], compare_op=ALU.not_equal, fill=0.0,
                                        base=0, pattern=[[0, 1]], channel_multiplier=1))

            @block.scalar
            def _(act):
                for u, (k, n, a) in enumerate(units):
                    act.wait_ge(made, u + 1)
                    act.mul(z[a][:, k:k + n, :], ps[u % 4][0:H1, 0:n * BT].rearrange("p (k n) -> p k n", k=n),
                            math.sqrt(2.0)).then_inc(read, 1)
                act.wait_ge(gdone, 1)
                act.copy(gs[:, :], ps_g[:, 0:BT]).then_inc(gcopied, 1)

            @block.vector
            def _(dve):
                step = Chain(dve, dch)
                dve.wait_ge(read, len(units))
                for a in range(2):
                    for k in (0, h, 2 * h):
                        step(dve.tensor_scalar(z[a][:, k, :], z[a][:, k, :], math.sqrt(0.5), None, ALU.mult))
                step(dve.tensor_tensor(p12[:, 0, :], z[0][:, h, :], z[1][:, 2 * h, :], ALU.add))
                step(dve.tensor_tensor(p12[:, 1, :], z[0][:, 2 * h, :], z[1][:, h, :], ALU.subtract))
                dve.wait_ge(pch, 2)
                step(dve.tensor_scalar(p12[:, 1, :], p12[:, 1, :], inner[:, 0:1], None, ALU.mult))
                dve.sem_inc(zready, 1)

            @block.sync
            def _(sp):
                sp.wait_ge(gcopied, 1)
                sp.dma_start(gram_d, gs[:, :]).then_inc(stored, 16)
                sp.wait_ge(stored, 16)


NH = 16


def token_attention(nc, xh, gram_d, tabs, wts, prob_d, pt, mt, tag="l1s"):
    L = LKX - 1
    MA = LKY * L
    MB = LKY // 2 + 1
    low = [n for n in range(NKY) if -LKY // 2 <= ROWS[n] < LKY // 2]
    unit = float(SR * SR) / math.sqrt(SR * SR)
    with ExitStack() as ctx:
        s = Scope(nc, ctx, tag)
        ident = s.sb("ident", [P, P])
        skips = s.sb("skips", [P, 6, NH])
        qa, ka = (s.sb(n, [MA, NH, 2]) for n in ("qa", "ka"))
        qb, kb, qr, kr = (s.sb(n, [MB, NH, 2]) for n in ("qb", "kb", "qr", "kr"))
        da = s.sb("da", [MA, 3, NH])
        db = s.sb("db", [MB, 3, NH])
        two = s.sb("two", [MB, 1])
        sgn = s.sb("sgn", [MB, 1])
        tmp = s.sb("tmp", [P, 4, NH])
        row = s.sb("row", [1, 2, NH])
        xlow = s.sb("xlow", [P, 2, LKY, L])
        xlob = s.sb("xlob", [P, 2, MB])
        xa = s.sb("xa", [MA, 2, BT])
        xb = s.sb("xb", [MB, 2, BT])
        grow = s.sb("grow", [1, B, T, T])
        xrow = s.sb("xrow", [1, BT, T])
        pa = s.sb("pa", [MA, 4, T, T])
        pb = s.sb("pb", [MB, 4, T, T])
        sc = s.sb("sc", [NH, B * T, T])
        mx = s.sb("mx", [NH, B * T])
        pl = s.sb("pl", [P, NH, BT])
        coef = s.sb("coef", [P, NH])
        mtt = s.sb("mtt", [P, NH, BT])
        ps_t = s.ps("ps_t")
        ps = [s.ps(f"ps{j}") for j in range(2)]
        ps_p = [s.ps(f"ps_p{j}") for j in range(4)]
        (loaded, zeroed, made, turned, x_ready, d_ready, prods, scored, sc_ready, e_ready, p_ready, p_out,
         p_in, flipped, pt_ready, dch, pch, low_ready) = (
            s.sem(n) for n in ("loaded", "zeroed", "made", "turned", "x_ready", "d_ready", "prods", "scored",
                               "sc_ready", "e_ready", "p_ready", "p_out", "p_in", "flipped", "pt_ready", "dch",
                               "pch", "low_ready"))
        LOADS = 6 + 2 * (LKY + 2) + 2 * (LKY // 2) + 1
        block = ctx.enter_context(nc.Block())

        @block.sync
        def _(sp):
            n = 0
            names = ("query_skip_w", "key_skip_w", "value_skip_w", "proj_skip_w", "query_skip_b", "key_skip_b")
            for j, name in enumerate(names):
                src = wts[name]
                flat = src.rearrange("a b -> (a b)") if len(src.shape) == 2 else src
                sp.dma_start(skips[:, j, :], flat.unsqueeze(0).broadcast_to([P, NH])).then_inc(loaded, 16)
                n += 1
            sp.wait_ge(zeroed, 1)
            for w, ta, tb, tr in (("query_w", qa, qb, qr), ("key_w", ka, kb, kr)):
                src = wts[w][0].rearrange("h y x a -> y x h a")
                for y in range(LKY):
                    sp.dma_start(ta[y * L:(y + 1) * L, :, :], src[y, 1:LKX]).then_inc(loaded, 16)
                    n += 1
                sp.dma_start(tb[0:LKY // 2, :, :], src[0:LKY // 2, 0]).then_inc(loaded, 16)
                sp.dma_start(tr[0:1, :, :], src[0:1, 0]).then_inc(loaded, 16)
                n += 2
                for y in range(1, MB):
                    sp.dma_start(tr[y:y + 1, :, :], src[LKY - y:LKY - y + 1, 0]).then_inc(loaded, 16)
                    n += 1
            for b in range(B):
                sp.dma_start(grow[:, b, :, :], gram_d[b * T:(b + 1) * T, b * T:(b + 1) * T].unsqueeze(0)
                             ).then_inc(made, 16)
            assert n == LOADS - 1, n
            sp.wait_ge(p_ready, 1)
            sp.dma_start(prob_d.rearrange("h b t s -> h (b t) s"), sc[:, :, :]).then_inc(p_out, 16)
            sp.wait_ge(p_out, 16)
            for b in range(B):
                sp.dma_start(pl[b * T:(b + 1) * T, :, b * T:(b + 1) * T],
                             prob_d[:, b].rearrange("h t s -> t h s")).then_inc(p_in, 16)
            sp.wait_ge(p_in, 16 * B)

        @block.gpsimd
        def _(pool):
            step = Chain(pool, pch)
            for t in (qb, kb, qr, kr):
                step(pool.memset(t[:, :, :], 0.0))
            pool.sem_inc(zeroed, 1)
            fill_identity(pool, step, ident)
            step(pool.memset(pl[:, :, :], 0.0))
            step(pool.memset(two[:, :], 2.0 * unit))
            step(pool.affine_select(out=two[:, :], in_=two[:, :], compare_op=ALU.not_equal, fill=unit,
                                    base=0, pattern=[[0, 1]], channel_multiplier=1))

        @block.tensor
        def _(pe):
            pe.wait_ge(pch, 6)
            pe.wait_ge(low_ready, 1)
            for a in range(2):
                pe.transpose(ps_t[0:MA, a * BT:(a + 1) * BT], xlow[:, a, :, :].rearrange("p y x -> p (y x)"), ident[:, :])
                pe.transpose(ps_t[0:MB, (2 + a) * BT:(3 + a) * BT], xlob[:, a, :], ident[:, :]).then_inc(turned, 1)
            pe.wait_ge(d_ready, 1)
            pe.wait_ge(made, 16 * B)
            NS = T // 2
            for b in range(B):
                pe.wait_ge(prods, b + 1)
                if b:
                    pe.wait_ge(sc_ready, 2 * b)
                for g in range(2):
                    rows = slice(g * NS, (g + 1) * NS)
                    dst = ps[g][0:NH, :]
                    for n, (d, j) in enumerate(((0, 0), (0, 1), (2, 2), (1, 3))):
                        pe.matmul(dst, da[:, d, :], pa[:, j, rows, :].rearrange("p t s -> p (t s)"),
                                  start=(n == 0), stop=False)
                        pe.matmul(dst, db[:, d, :], pb[:, j, rows, :].rearrange("p t s -> p (t s)"),
                                  start=False, stop=False)
                    pe.matmul(dst, row[:, 0, :], grow[:, b, rows, :].rearrange("p t s -> p (t s)"),
                              start=False, stop=False)
                    pe.matmul(dst, row[:, 1, :], xrow[:, b * T + g * NS:b * T + (g + 1) * NS, :].rearrange("p t s -> p (t s)"),
                              start=False, stop=True).then_inc(scored, 1)
            pe.wait_ge(p_in, 16 * B)
            for h in range(NH):
                last = pe.transpose(ps_p[h // 4][:, (h % 4) * BT:(h % 4 + 1) * BT], pl[:, h, :], ident[:, :])
            last.then_inc(flipped, 1)

        @block.scalar
        def _(act):
            for k in range(2 * B):
                b, g = divmod(k, 2)
                act.wait_ge(scored, k + 1)
                act.copy(sc[:, b * T + g * (T // 2):b * T + (g + 1) * (T // 2), :],
                         ps[g][0:NH, :].rearrange("p (t s) -> p t s", s=T)).then_inc(sc_ready, 1)
            act.wait_ge(e_ready, 1)
            act.activation(sc[:, :, :], sc[:, :, :], ACT.Exp).then_inc(e_ready, 1)
            act.wait_ge(flipped, 1)
            for j in range(4):
                act.copy(pt[:, 4 * j:4 * j + 4, :], ps_p[j][:, :].rearrange("p (h t) -> p h t", h=4)).then_inc(pt_ready, 1)

        @block.vector
        def _(dve):
            step = Chain(dve, dch)
            n0 = LKY // 2
            for a in range(2):
                for j, n in ((0, 0), (1, NKY - n0)):
                    step.mark(dve.tensor_copy(xlow[:, a, j * n0:(j + 1) * n0, :], xh[:, n:n + n0, a, 1:LKX]))
                step.mark(dve.tensor_copy(xlob[:, a, :], xh[:, 0:MB, a, 0]))
            step.join()
            dve.sem_inc(low_ready, 1)
            dve.wait_ge(loaded, 16 * (LOADS - 1))
            dve.wait_ge(pch, 9)
            TT, STT = dve.tensor_tensor, dve.scalar_tensor_tensor
            for t, r in ((qb, qr), (kb, kr)):
                step(TT(t[:, :, 0], t[:, :, 0], r[:, :, 0], ALU.add))
                step(TT(t[:, :, 1], t[:, :, 1], r[:, :, 1], ALU.subtract))
                step(dve.tensor_scalar(t[:, :, :], t[:, :, :], 0.5, None, ALU.mult))
            for q, k, d, m in ((qa, ka, da, MA), (qb, kb, db, MB)):
                wq, wk = skips[0:m, 0, :], skips[0:m, 1, :]
                a, c = tmp[0:m, 0, :], tmp[0:m, 1, :]
                step(TT(a, wq, q[:, :, 0], ALU.add))
                step(TT(d[:, 0, :], a, k[:, :, 0], ALU.mult))
                step(TT(c, q[:, :, 1], k[:, :, 1], ALU.mult))
                step(TT(d[:, 0, :], d[:, 0, :], c, ALU.add))
                step(TT(c, wk, q[:, :, 0], ALU.mult))
                step(TT(d[:, 0, :], d[:, 0, :], c, ALU.add))
                step(TT(a, a, k[:, :, 1], ALU.mult))
                step(TT(c, wk, k[:, :, 0], ALU.add))
                step(TT(c, c, q[:, :, 1], ALU.mult))
                step(TT(d[:, 1, :], c, a, ALU.subtract))
                scale = 2.0 * unit if d is da else two[:, 0:1]
                step(dve.tensor_scalar(d[:, 0:2, :], d[:, 0:2, :], scale, None, ALU.mult))
                step(dve.tensor_scalar(d[:, 2, :], d[:, 1, :], -1.0, None, ALU.mult))
            step(TT(row[:, 0, :], skips[0:1, 0, :], skips[0:1, 1, :], ALU.mult))
            step(TT(row[:, 1, :], skips[0:1, 1, :], kb[0:1, :, 0], ALU.add))
            step(TT(row[:, 1, :], row[:, 1, :], skips[0:1, 4, :], ALU.mult))
            step(dve.tensor_scalar(row[:, :, :], row[:, :, :], unit, None, ALU.mult))
            dve.wait_ge(turned, 2)
            step(dve.tensor_copy(xa[:, :, :], ps_t[0:MA, 0:2 * BT].rearrange("p (a n) -> p a n", a=2)))
            step(dve.tensor_copy(xb[:, :, :], ps_t[0:MB, 2 * BT:4 * BT].rearrange("p (a n) -> p a n", a=2)))
            for b in range(B):
                step(dve.tensor_copy(xrow[:, b * T:(b + 1) * T, :],
                                     xb[0:1, 0, b * T:(b + 1) * T].unsqueeze(1).broadcast_to([1, T, T])))
            dve.sem_inc(d_ready, 1)
            for b in range(B):
                if b:
                    dve.wait_ge(scored, 2 * b)
                for x, p, m in ((xa, pa, MA), (xb, pb, MB)):
                    xt = [x[:, a, b * T:(b + 1) * T].unsqueeze(2).broadcast_to([m, T, T]) for a in range(2)]
                    xs = [x[:, a, b * T:(b + 1) * T].unsqueeze(1).broadcast_to([m, T, T]) for a in range(2)]
                    for j, (u, v) in enumerate(((0, 0), (1, 1), (1, 0), (0, 1))):
                        step.mark(TT(p[:, j, :, :], xt[u], xs[v], ALU.mult))
                step.join()
                dve.sem_inc(prods, 1)
            dve.wait_ge(sc_ready, 2 * B)
            step(dve.tensor_reduce(mx[:, :], sc[:, :, :], AX.X, ALU.max))
            step(TT(sc[:, :, :], sc[:, :, :], mx[:, :].unsqueeze(2).broadcast_to([NH, B * T, T]), ALU.subtract))
            dve.sem_inc(e_ready, 1)
            dve.wait_ge(e_ready, 2)
            step(dve.tensor_reduce(mx[:, :], sc[:, :, :], AX.X, ALU.add))
            step(dve.reciprocal(mx[:, :], mx[:, :]))
            step(TT(sc[:, :, :], sc[:, :, :], mx[:, :].unsqueeze(2).broadcast_to([NH, B * T, T]), ALU.mult))
            dve.sem_inc(p_ready, 1)
            step(TT(coef[:, :], skips[:, 2, :], skips[:, 3, :], ALU.mult))
            dve.wait_ge(pt_ready, 4)
            step(TT(mtt[:, :, :], pt[:, :, :], coef[:, :].unsqueeze(2).broadcast_to([P, NH, BT]), ALU.mult))
            step(dve.tensor_reduce(mt[:, :], mtt[:, :, :].rearrange("p h t -> p t h"), AX.X, ALU.add))


def attended_spectrum(nc, xh, pt, wts, wd, spec, const, tag="l1y"):
    K2 = 2 * NKX
    HF = LKY // 2
    with ExitStack() as ctx:
        s = Scope(nc, ctx, tag)
        ident = s.sb("ident", [P, P])
        sv = s.sb("sv", [NKY, NH, LKX, 2])
        rv = s.sb("rv", [NKY, NH, 2])
        pw = s.sb("pw", [NKY, NH, NKX, 2])
        sk = s.sb("sk", [P, 3, NH])
        pb0 = s.sb("pb0", [P, 1])
        p00 = s.sb("p00", [P, NH])
        a, c, d = (s.sb(n, [NKY, NH, NKX]) for n in ("a", "c", "d"))
        w = s.sb("w", [NKY, NH, 2, NKX])
        ccon = s.sb("ccon", [P, 2, NH])
        wh = [s.sb(f"wh{j}", [P, NKY, 2, NKX]) for j in range(2)]
        xw = [s.sb(f"xw{j}", [P, NKY, 2, NKX]) for j in range(2)]
        t1, t2 = (s.sb(n, [P, NKY, 2, NKX]) for n in ("t1", "t2"))
        yp = s.sb("yp", [P, NKY, 2, 32])
        ps = [s.ps(f"ps{j}") for j in range(3)]
        ps_t = [s.ps(f"ps_t{j}") for j in range(4)]
        (zeroed, loaded, w_ready, w_out, w_in, xw_ready, mixed, yp_ready, turned, copied, dch, pch, made) = (
            s.sem(n) for n in ("zeroed", "loaded", "w_ready", "w_out", "w_in", "xw_ready", "mixed",
                               "yp_ready", "turned", "copied", "dch", "pch", "made"))
        block = ctx.enter_context(nc.Block())
        NL = 1 + 2 + (1 + LKY) + 3 + 2

        @block.sync
        def _(sp):
            n = 0
            sp.wait_ge(zeroed, 1)
            src = wts["value_w"][0].rearrange("h y x a -> y h x a")
            vrow = lambda k: k % LKY
            sp.dma_start(pw[:, :, :, :], wts["proj_w"][:, 0].rearrange("h y x a -> y h x a")).then_inc(loaded, 16)
            sp.dma_start(sv[0:HF, :, :, :], src[0:HF]).then_inc(loaded, 16)
            sp.dma_start(sv[NKY - HF:NKY, :, :, :], src[HF:LKY]).then_inc(loaded, 16)
            n += 3
            for k in range(-HF + 1, HF + 1):
                at = k % NKY
                sp.dma_start(rv[at:at + 1, :, :], src[vrow(-k):vrow(-k) + 1, :, 0, :]).then_inc(loaded, 16)
                n += 1
            for j, name in enumerate(("value_skip_w", "proj_skip_w", "value_skip_b")):
                v = wts[name]
                flat = v.rearrange("a b -> (a b)") if len(v.shape) == 2 else v
                sp.dma_start(sk[:, j, :], flat.unsqueeze(0).broadcast_to([P, NH])).then_inc(loaded, 16)
                n += 1
            sp.dma_start(p00[:, :], wts["proj_w"][:, 0, 0, 0, 0].unsqueeze(0).broadcast_to([P, NH]),
                         allow_slow_non_contiguous=True).then_inc(loaded, 16)
            sp.dma_start(pb0[:, :], wts["proj_skip_b"].unsqueeze(0).broadcast_to([P, 1])).then_inc(loaded, 16)
            n += 2
            assert n == NL - 1, n
            sp.wait_ge(w_ready, 1)
            sp.dma_start(wd.rearrange("h y a x -> y h a x"), w[:, :, :, :]).then_inc(w_out, 16)
            sp.wait_ge(w_out, 16)
            for h in range(NH):
                if h >= 2:
                    sp.wait_ge(xw_ready, h - 1)
                sp.dma_start(wh[h % 2][:, :, :, :], wd[h].unsqueeze(0).broadcast_to([P, NKY, 2, NKX])).then_inc(w_in, 16)
                sp.wait_ge(w_in, 16 * h + 16)

        @block.gpsimd
        def _(pool):
            step = Chain(pool, pch)
            step(pool.memset(sv[:, :, :, :], 0.0))
            step(pool.memset(rv[:, :, :], 0.0))
            pool.sem_inc(zeroed, 1)
            fill_identity(pool, step, ident)
            step(pool.memset(yp[:, :, :, :], 0.0))
            pool.sem_inc(made, 1)

        @block.vector
        def _(dve):
            step = Chain(dve, dch)
            TT = dve.tensor_tensor
            dve.wait_ge(loaded, 16 * (NL - 1))
            dve.wait_ge(made, 1)
            step(TT(sv[:, :, 0, 0], sv[:, :, 0, 0], rv[:, :, 0], ALU.add))
            step(TT(sv[:, :, 0, 1], sv[:, :, 0, 1], rv[:, :, 1], ALU.subtract))
            step(dve.tensor_scalar(sv[:, :, 0, :], sv[:, :, 0, :], 0.5, None, ALU.mult))
            vs = sk[0:NKY, 0, :].unsqueeze(2)
            ps_ = sk[0:NKY, 1, :].unsqueeze(2)
            full, lowx = [NKY, NH, NKX], [NKY, NH, LKX]
            pr, pi = pw[:, :, :, 0], pw[:, :, :, 1]
            step(TT(w[:, :, 0, :], pr, vs.broadcast_to(full), ALU.mult))
            step(TT(w[:, :, 1, :], pi, vs.broadcast_to(full), ALU.mult))
            A_, C_, D_ = a[:, :, 0:LKX], c[:, :, 0:LKX], d[:, :, 0:LKX]
            vr, vi = sv[:, :, :, 0], sv[:, :, :, 1]
            prl, pil = pw[:, :, 0:LKX, 0], pw[:, :, 0:LKX, 1]
            step(TT(A_, prl, ps_.broadcast_to(lowx), ALU.add))
            for part, (u, v, op) in enumerate(((vr, vi, ALU.subtract), (vi, vr, ALU.add))):
                step(TT(C_, A_, u, ALU.mult))
                step(TT(D_, pil, v, ALU.mult))
                step(TT(C_, C_, D_, op))
                step(TT(w[:, :, part, 0:LKX], w[:, :, part, 0:LKX], C_, ALU.add))
            dve.sem_inc(w_ready, 1)
            step(TT(ccon[:, 0, :], p00[:, :], sk[:, 1, :], ALU.add))
            step(TT(ccon[:, 1, :], ccon[:, 0, :], sk[:, 2, :], ALU.mult))
            step(dve.tensor_reduce(const[:, 0:1], ccon[:, 1, :], AX.X, ALU.add))
            step(TT(const[:, 0:1], const[:, 0:1], pb0[:, :], ALU.add))
            for h in range(NH):
                W_ = wh[h % 2]
                dve.wait_ge(w_in, 16 * h + 16)
                if h >= 2:
                    dve.wait_ge(mixed, h - 1)
                both = [P, NKY, 2, NKX]
                step.mark(TT(t1[:, :, :, :], xh[:, :, :, :], W_[:, :, 0:1, :].broadcast_to(both), ALU.mult))
                step(TT(t2[:, :, :, :], xh[:, :, :, :], W_[:, :, 1:2, :].broadcast_to(both), ALU.mult))
                step.mark(TT(xw[h % 2][:, :, 0, :], t1[:, :, 0, :], t2[:, :, 1, :], ALU.subtract))
                step(TT(xw[h % 2][:, :, 1, :], t1[:, :, 1, :], t2[:, :, 0, :], ALU.add))
                dve.sem_inc(xw_ready, 1)
            dve.wait_ge(mixed, NH)
            n = 15
            for j in range(3):
                k0, k1 = n * j, min(n * j + n, NKY)
                step.mark(dve.tensor_copy(yp[:, k0:k1, :, 0:NKX],
                                          ps[j][:, 0:(k1 - k0) * K2].rearrange("p (k a x) -> p k a x", a=2, x=NKX)))
            step.join()
            dve.sem_inc(yp_ready, 1)
            for j in range(NKY // 4):
                dve.wait_ge(turned, j + 1)
                step(dve.tensor_copy(spec[:, :, 4 * j:4 * j + 4],
                                     ps_t[j % 4][0:2 * 32, :].rearrange("p (k t) -> p t k", k=4)))
                dve.sem_inc(copied, 1)

        @block.tensor
        def _(pe):
            pe.wait_ge(made, 1)
            n = 15
            for h in range(NH):
                pe.wait_ge(xw_ready, h + 1)
                for j in range(3):
                    k0, k1 = n * j, min(n * j + n, NKY)
                    last = pe.matmul(ps[j][:, 0:(k1 - k0) * K2], pt[:, h, :],
                                     xw[h % 2][:, k0:k1, :, :].rearrange("p k a x -> p (k a x)"),
                                     start=(h == 0), stop=(h == NH - 1))
                last.then_inc(mixed, 1)
            pe.wait_ge(yp_ready, 1)
            for j in range(NKY // 4):
                if j >= 4:
                    pe.wait_ge(copied, j - 3)
                for k in range(4):
                    last = pe.transpose(ps_t[j % 4][0:64, k * BT:(k + 1) * BT],
                                        yp[:, 4 * j + k, :, :].rearrange("p a x -> p (a x)"), ident[:, :])
                last.then_inc(turned, 1)


def mixed_images(nc, tnd, mt, u, tag="l1m"):
    N = 512
    CH = 4
    with ExitStack() as ctx:
        s = Scope(nc, ctx, tag)
        src = [s.sb(f"src{j}", [P, CH * N]) for j in range(2)]
        dst = [s.sb(f"dst{j}", [P, CH * N]) for j in range(2)]
        ps = [s.ps(f"ps{j}") for j in range(2 * CH)]
        mixed, stored, copied = (s.sem(n) for n in ("mixed", "stored", "copied"))
        loaded = [s.sem(f"loaded{j}") for j in range(2)]
        flat_in = tnd.rearrange("n r c -> n (r c)").rearrange("n (i j k) -> i j n k", j=2, k=CH * N)
        flat_out = u.rearrange("n r c -> n (r c)").rearrange("n (i j k) -> i j n k", j=2, k=CH * N)
        TURNS = IMG // (CH * N)
        block = ctx.enter_context(nc.Block())

        @block.sync
        def _(sp):
            with sp.Fori(0, TURNS // 2) as i:
                for j in range(2):
                    sp.wait_ge(mixed, 2 * i)
                    sp.dma_start(src[j][:, :], flat_in[i, j]).then_inc(loaded[j], 16)

        @block.tensor
        def _(pe):
            with pe.Fori(0, TURNS // 2) as i:
                for j in range(2):
                    pe.wait_ge(loaded[j], 16 * i + 16)
                    pe.wait_ge(copied, 2 * i)
                    for k in range(CH):
                        last = pe.matmul(ps[j * CH + k][:, :], mt[:, :], src[j][:, k * N:(k + 1) * N],
                                         start=True, stop=True)
                    last.then_inc(mixed, 1)

        @block.vector
        def _(dve):
            with dve.Fori(0, TURNS // 2) as i:
                for j in range(2):
                    dve.wait_ge(mixed, 2 * i + j + 1)
                    dve.wait_ge(stored, 32 * i)
                    for k in range(CH):
                        last = dve.tensor_copy(dst[j][:, k * N:(k + 1) * N], ps[j * CH + k][:, :])
                    last.then_inc(copied, 1)

        @block.scalar
        def _(act):
            with act.Fori(0, TURNS // 2) as i:
                for j in range(2):
                    act.wait_ge(copied, 2 * i + j + 1)
                    act.dma_start(flat_out[i, j], dst[j][:, :]).then_inc(stored, 16)
            act.wait_ge(stored, 16 * TURNS)


def token_mixer(nc, spec, const, u, tok, x1, wts, tabs, x2, tag="l1t", eps=1e-5):
    R = 4
    TURNS = BT // R
    NF = R * NKY
    with ExitStack() as ctx:
        s = Scope(nc, ctx, tag)
        rows_fwd = s.sb("rows_fwd", [P, 2 * NKY])
        cols_fwd = s.sb("cols_fwd", [P, 2, 64])
        cols_inv = s.sb("cols_inv", [64, 2, 2 * C])
        rows_inv = s.sb("rows_inv", [NKY, 2, P])
        names = ["attn_norm_g", "attn_norm_b", "norm2_g", "norm2_b", "mixer_norm_g1", "mixer_norm_b1",
                 "mixer_norm_g2", "mixer_norm_b2", "mixer_out_g", "mixer_out_b", "mixer_skip_w1",
                 "mixer_skip_b1", "mixer_skip_w2", "mixer_skip_b2"]
        par = s.sb("par", [P, len(names)])
        col = {n: par[:, j:j + 1] for j, n in enumerate(names)}
        mw = [s.sb(f"mw{j}", [64, NKY, 2]) for j in range(2)]
        ones = s.sb("ones", [P, P])
        half = s.sb("half", [P, R])
        sg = s.sb("sg", [64, R, NKY])
        ut = s.sb("ut", [P, R, C])
        tk = s.sb("tk", [P, R, C])
        xx = s.sb("xx", [P, R, C])
        iv = s.sb("iv", [NKY, 2, R, C])
        a = s.sb("a", [P, R, C])
        xf = s.sb("xf", [P, R, C])
        attn = s.sb("attn", [P, R, C])
        m = s.sb("m", [P, R, C])
        m1 = s.sb("m1", [P, R, C])
        f = s.sb("f", [P, R, C])
        sk = s.sb("sk", [P, R, C])
        sq = s.sb("sq", [P, R, C])
        out = s.sb("out", [P, R, C])
        o = s.sb("o", [P, 2, R, NKY])
        t1, t2 = s.sb("t1", [64, R, NKY]), s.sb("t2", [64, R, NKY])
        sums = s.sb("sums", [P, 2 * R])
        mean, var, rstd, scale, bias, v2 = (s.sb(n, [P, R]) for n in ("mean", "var", "rstd", "scale", "bias", "v2"))
        ps_f, ps_g, ps_a, ps_s = (s.ps(n) for n in ("ps_f", "ps_g", "ps_a", "ps_s"))
        ps_i = [s.ps(f"ps_i{j}") for j in range(2)]
        sem = s.sem
        loaded, made, zeroed, xin, staged, stored, out_ready = (sem(n) for n in (
            "loaded", "made", "zeroed", "xin", "staged", "stored", "out_ready"))
        inv1 = [sem(f"inv1_{j}") for j in range(3)]
        ivr = [sem(f"iv_ready{j}") for j in range(3)]
        inv2 = [sem(f"inv2_{j}") for j in range(3)]
        img = [sem(f"img_ready{j}") for j in range(2)]
        fwd1 = [sem(f"fwd1_{j}") for j in range(2)]
        o_ready = [sem(f"o_ready{j}") for j in range(2)]
        fwd2 = [sem(f"fwd2_{j}") for j in range(2)]
        t_ready = [sem(f"t_ready{j}") for j in range(2)]
        have = [sem(f"have{j}") for j in range(4)]
        squared = [sem(f"squared{j}") for j in range(4)]
        summed = [sem(f"summed{j}") for j in range(4)]
        totals = [sem(f"totals{j}") for j in range(4)]
        varr = [sem(f"var_ready{j}") for j in range(5)]
        rstdr = [sem(f"rstd_ready{j}") for j in range(5)]
        pre, tick, dch = sem("pre"), sem("tick"), sem("dch")
        xf_ready = [sem(f"xf_ready{j}") for j in range(3)]
        block = ctx.enter_context(nc.Block())
        NL = 4 + len(names) + 4

        def view(t, n0=0):
            return t.rearrange("(i r) w c -> i w r c", r=R)

        x1v = x1.rearrange("b t w c -> (b t) w c")
        x2v = x2.rearrange("b t w c -> (b t) w c")

        @block.sync
        def _(sp):
            sp.wait_ge(zeroed, 1)
            for dst, src in ((rows_fwd[:, :], "rows_fwd"), (cols_fwd[:, :, :].rearrange("p a k -> p (a k)"), "cols_fwd"),
                             (cols_inv[:, :, :].rearrange("p a k -> p (a k)"), "cols_inv"),
                             (rows_inv[:, :, :].rearrange("p a k -> p (a k)"), "rows_inv")):
                sp.dma_start(dst, tabs[src]).then_inc(loaded, 16)
            for n in names:
                v = wts[n]
                flat = v.rearrange("a b -> (a b)") if len(v.shape) == 2 else v
                sp.dma_start(col[n], flat.unsqueeze(0).broadcast_to([P, 1])).then_inc(loaded, 16)
            for j in range(2):
                src = wts[f"mixer_w{j + 1}"][0, 0].rearrange("y x a -> x y a")
                for q in range(2):
                    sp.dma_start(mw[j][32 * q:32 * q + NKX, :, :], src).then_inc(loaded, 16)
            uv, tv, xv, ov = view(u), view(tok), view(x1v), view(x2v)
            with sp.Fori(0, TURNS) as i:
                sp.wait_ge(out_ready, i)
                sp.dma_start(ut[:, :, :], uv[i]).then_inc(xin, 16)
                sp.dma_start(tk[:, :, :], tv[i]).then_inc(xin, 16)
                sp.dma_start(xx[:, :, :], xv[i]).then_inc(xin, 16)
                sp.wait_ge(out_ready, i + 1)
                sp.dma_start(ov[i], out[:, :, :]).then_inc(stored, 16)
            sp.wait_ge(stored, 16 * TURNS)

        @block.gpsimd
        def _(pool):
            for j in range(2):
                pool.memset(mw[j][:, :, :], 0.0).then_inc(made, 1)
            pool.wait_ge(made, 2)
            pool.sem_inc(zeroed, 1)
            pool.memset(ones[:, :], 1.0 / IMG).then_inc(made, 1)
            pool.memset(half[:, :], -0.5).then_inc(made, 1)
            pool.wait_ge(made, 4)
            with pool.Fori(0, TURNS) as i:
                pool.wait_ge(inv1[0], i)
                pool.tensor_copy(sg[:, :, :], spec[:, bass.ds(i * R, R), :]).then_inc(staged, 1)
                for j in range(5):
                    pool.wait_ge(varr[j], i + 1)
                    pool.tensor_tensor(rstd[:, :], var[:, :], half[:, :], ALU.pow).then_inc(rstdr[j], 1)

        @block.tensor
        def _(pe):
            pe.wait_ge(loaded, 16 * NL)
            pe.wait_ge(made, 4)

            def inverse(n, i, srcs):
                pe.sem_inc(tick, 1)
                for r in range(R):
                    dst = ps_i[r // 2][0:NKY, (r % 2) * 2 * C:(r % 2 + 1) * 2 * C]
                    for k, src in enumerate(srcs):
                        last = pe.matmul(dst, src[:, r, :], cols_inv[:, k, :], start=(k == 0), stop=(k == len(srcs) - 1))
                last.then_inc(inv1[n], 1)
                pe.wait_ge(ivr[n], i + 1)
                for k in range(2):
                    last = pe.matmul(ps_a[:, :], rows_inv[:, k, :], iv[:, k, :, :].rearrange("p r c -> p (r c)"),
                                     start=(k == 0), stop=(k == 1))
                last.then_inc(inv2[n], 1)

            def forward(n, i, src):
                pe.wait_ge(img[n], i + 1)
                for r in range(R):
                    last = pe.matmul(ps_f[:, r * 64:(r + 1) * 64], src[:, r, :], rows_fwd[:, :], start=True, stop=True)
                last.then_inc(fwd1[n], 1)
                pe.wait_ge(o_ready[n], i + 1)
                for k in range(2):
                    last = pe.matmul(ps_g[0:64, 0:NF], cols_fwd[:, k, :], o[:, k, :, :].rearrange("p r k -> p (r k)"),
                                     start=(k == 0), stop=(k == 1))
                last.then_inc(fwd2[n], 1)
                pe.wait_ge(t_ready[n], i + 1)

            def total(n, i):
                pe.wait_ge(summed[n], i + 1)
                pe.matmul(ps_s[:, 0:2 * R], ones[:, :], sums[:, :], start=True, stop=True).then_inc(totals[n], 1)

            with pe.Fori(0, TURNS) as i:
                pe.wait_ge(staged, i + 1)
                inverse(0, i, [sg])
                total(0, i)
                forward(0, i, m)
                inverse(1, i, [t1, t2])
                total(1, i)
                forward(1, i, m1)
                inverse(2, i, [t1, t2])
                total(2, i)
                total(3, i)

        @block.scalar
        def _(act):
            def copy_iv(n, i):
                act.wait_ge(inv1[n], i + 1)
                for q in range(2):
                    last = act.copy(iv[:, :, 2 * q:2 * q + 2, :],
                                    ps_i[q][0:NKY, :].rearrange("p (r a c) -> p a r c", r=2, a=2))
                last.then_inc(ivr[n], 1)

            def square(n, i, src):
                act.wait_ge(have[n], i + 1)
                act.activation(sq[:, :, :], src, ACT.Square).then_inc(squared[n], 1)

            def copy_o(n, i):
                act.wait_ge(fwd1[n], i + 1)
                act.copy(o[:, :, :, :], ps_f[:, 0:R * 64].rearrange("p (r a k) -> p a r k", r=R, a=2)).then_inc(o_ready[n], 1)

            pa = ps_a[:, :].rearrange("p (r c) -> p r c", r=R)

            def image(n, i):
                act.wait_ge(inv2[n], i + 1)
                act.copy(xf[:, :, :], pa).then_inc(xf_ready[n], 1)
                act.wait_ge(xf_ready[n], i + 1)
                act.activation(sq[:, :, :], xf[:, :, :], ACT.Square).then_inc(squared[n], 1)

            with act.Fori(0, TURNS) as i:
                copy_iv(0, i)
                square(0, i, a[:, :, :])
                copy_o(0, i)
                copy_iv(1, i)
                image(1, i)
                act.wait_ge(pre, i + 1)
                act.activation(m1[:, :, :], f[:, :, :], ACT.Gelu).then_inc(img[1], 1)
                copy_o(1, i)
                copy_iv(2, i)
                image(2, i)
                square(3, i, f[:, :, :])

        @block.vector
        def _(dve):
            step = Chain(dve, dch)
            TT, TS, STT = dve.tensor_tensor, dve.tensor_scalar, dve.scalar_tensor_tensor
            dve.wait_ge(loaded, 16 * NL)
            pa = ps_a[:, :].rearrange("p (r c) -> p r c", r=R)

            def affine(n, i, g, b):
                dve.wait_ge(rstdr[n], i + 1)
                step(TS(scale[:, :], rstd[:, :], col[g], None, ALU.mult))
                step(TT(bias[:, :], mean[:, :], scale[:, :], ALU.mult))
                step(TS(bias[:, :], bias[:, :], -1.0, col[b], ALU.mult, ALU.add))

            def stats(n, i, src):
                dve.sem_inc(have[n], 1)
                step.mark(dve.tensor_reduce(sums[:, 0:R], src, AX.X, ALU.add))
                dve.wait_ge(squared[n], i + 1)
                step(dve.tensor_reduce(sums[:, R:2 * R], sq[:, :, :], AX.X, ALU.add))
                dve.sem_inc(summed[n], 1)
                dve.wait_ge(totals[n], i + 1)
                step(dve.tensor_copy(mean[:, :], ps_s[:, 0:R]))
                step(TT(var[:, :], mean[:, :], mean[:, :], ALU.mult))
                step(STT(out=var[:, :], in0=ps_s[:, R:2 * R], scalar=eps, in1=var[:, :], op0=ALU.add, op1=ALU.subtract))

            STATS, AFF = 5, 3

            def apply(dst, src):
                for r in range(R):
                    step.mark(TS(dst[:, r, :], src[:, r, :], scale[:, r:r + 1], bias[:, r:r + 1], ALU.mult, ALU.add))
                step.join()

            def spectral(n, i):
                dve.wait_ge(fwd2[n], i + 1)
                g = ps_g[0:64, 0:NF].rearrange("p (r k) -> p r k", r=R)
                for k, t in ((0, t1), (1, t2)):
                    step.mark(TT(t[:, :, :], g, mw[n][:, :, k].unsqueeze(1).broadcast_to([64, R, NKY]), ALU.mult))
                step.join()
                dve.sem_inc(t_ready[n], 1)

            per = (2 + STATS + AFF + R) + (4 + AFF + R) + 2 + (STATS + AFF + R + 2) + 2 + (STATS + AFF + R + 2) + (STATS + AFF + R + 2)
            with step.loop(TURNS, per) as i:
                dve.wait_ge(xin, 48 * (i + 1))
                dve.wait_ge(inv2[0], i + 1)
                step(STT(out=a[:, :, :], in0=pa, scalar=const[:, 0:1], in1=ut[:, :, :], op0=ALU.add, op1=ALU.add))
                step(TT(a[:, :, :], a[:, :, :], tk[:, :, :], ALU.add))
                stats(0, i, a[:, :, :])
                dve.sem_inc(varr[0], 1)
                affine(0, i, "attn_norm_g", "attn_norm_b")
                apply(attn, a)
                step(STT(out=v2[:, :], in0=var[:, :], scalar=-eps, in1=scale[:, :], op0=ALU.add, op1=ALU.mult))
                step(TT(v2[:, :], v2[:, :], scale[:, :], ALU.mult))
                step(TS(var[:, :], v2[:, :], eps, None, ALU.add))
                step(TS(mean[:, :], half[:, :], 0.0, col["attn_norm_b"], ALU.mult, ALU.add))
                dve.sem_inc(varr[1], 1)
                affine(1, i, "norm2_g", "norm2_b")
                apply(m, attn)
                dve.sem_inc(img[0], 1)
                spectral(0, i)
                dve.wait_ge(xf_ready[1], i + 1)
                stats(1, i, xf[:, :, :])
                dve.sem_inc(varr[2], 1)
                affine(2, i, "mixer_norm_g1", "mixer_norm_b1")
                apply(f, xf)
                step(STT(out=f[:, :, :], in0=m[:, :, :], scalar=col["mixer_skip_w1"], in1=f[:, :, :], op0=ALU.mult, op1=ALU.add))
                step(TS(f[:, :, :], f[:, :, :], col["mixer_skip_b1"], None, ALU.add))
                dve.sem_inc(pre, 1)
                spectral(1, i)
                dve.wait_ge(xf_ready[2], i + 1)
                stats(2, i, xf[:, :, :])
                dve.sem_inc(varr[3], 1)
                affine(3, i, "mixer_norm_g2", "mixer_norm_b2")
                apply(f, xf)
                step(STT(out=f[:, :, :], in0=m1[:, :, :], scalar=col["mixer_skip_w2"], in1=f[:, :, :], op0=ALU.mult, op1=ALU.add))
                step(TS(f[:, :, :], f[:, :, :], col["mixer_skip_b2"], None, ALU.add))
                stats(3, i, f[:, :, :])
                dve.sem_inc(varr[4], 1)
                affine(4, i, "mixer_out_g", "mixer_out_b")
                dve.wait_ge(stored, 16 * i)
                apply(out, f)
                step(TT(out[:, :, :], out[:, :, :], attn[:, :, :], ALU.add))
                step(TT(out[:, :, :], out[:, :, :], xx[:, :, :], ALU.add))
                dve.sem_inc(out_ready, 1)


def batch_tokens(x, b):
    return x[b].rearrange("t w c -> w t c")


def linear_attention(nc, x2, Wq, bq, Wk, bk, Wv, bv, Wo, bo, x3, tag="lin", eps=1e-5):
    H = 8
    D = C // H
    R = 4
    KT = T // R
    with ExitStack() as ctx:
        s = Scope(nc, ctx, tag)
        wq, wk, wv, wo = (s.sb(n, [P, C]) for n in ("wq", "wk", "wv", "wo"))
        bqc = s.sb("bqc", [P, 1])
        bk_row, bo_row, ones1 = (s.sb(n, [1, C]) for n in ("bk_row", "bo_row", "ones1"))
        bv_b = s.sb("bv_b", [P, C])
        ident, ones = s.sb("ident", [P, P]), s.sb("ones", [P, P])
        heads = s.sb("heads", [P, H, D])
        xb = s.sb("xb", [P, T, C])
        u = s.sb("u", [P, T, C])
        uT = s.sb("uT", [P, T * W])
        us = s.sb("us", [P, R, C])
        uTs = s.sb("uTs", [P, R * W])
        st = s.sb("st", [P, T, 6])
        mv = s.sb("mv", [P, T, 2])
        ve, rstd, half = (s.sb(n, [P, T]) for n in ("ve", "rstd", "half"))
        mn, ex, phi = (s.sb(n, [P, R * C]) for n in ("mn", "ex", "phi"))
        acc = s.sb("acc", [P, 2, C])
        kv, kvt, g, kb = (s.sb(n, [P, C]) for n in ("kv", "kvt", "g", "kb"))
        rd = s.sb("rd", [P, R * W])
        phz = s.sb("phz", [P, R * W])
        out = s.sb("out", [P, R, C])
        ps_t, ps_k, ps_m, ps_n, ps_x, ps_q, ps_d, ps_o = (
            s.ps(n) for n in ("ps_t", "ps_k", "ps_m", "ps_n", "ps_x", "ps_q", "ps_d", "ps_o"))
        (loaded, made, xin, ve_ready, rstd_ready, u_ready, staged, turned, uT_ready, kept, k_done, mn_ready,
         ex_ready, phi_ready, acc_done, acc_read, kv_done, kv_ready, kvt_done, kvt_ready, g_done, g_ready,
         q_done, qmn, qex, qphi, den_done, phz_ready, o_done, out_ready, stored, dch, pch, tick) = (
            s.sem(n) for n in (
                "loaded", "made", "xin", "ve_ready", "rstd_ready", "u_ready", "staged", "turned", "uT_ready",
                "kept", "k_done", "mn_ready", "ex_ready", "phi_ready", "acc_done", "acc_read", "kv_done",
                "kv_ready", "kvt_done", "kvt_ready", "g_done", "g_ready", "q_done", "qmn", "qex", "qphi",
                "den_done", "phz_ready", "o_done", "out_ready", "stored", "dch", "pch", "tick"))
        block = ctx.enter_context(nc.Block())
        NL = 8

        @block.sync
        def _(sp):
            for dst, src in ((wq, Wq), (wk, Wk), (wv, Wv), (wo, Wo)):
                sp.dma_start(dst[:, :], src).then_inc(loaded, 16)
            sp.dma_start(bqc[:, :], bq.unsqueeze(1)).then_inc(loaded, 16)
            sp.dma_start(bk_row[:, :], bk.unsqueeze(0)).then_inc(loaded, 16)
            sp.dma_start(bo_row[:, :], bo.unsqueeze(0)).then_inc(loaded, 16)
            sp.dma_start(bv_b[:, :], bv.unsqueeze(0).broadcast_to([P, C])).then_inc(loaded, 16)
            rows = x3.rearrange("b (k r) w c -> b k w r c", r=R)
            with sp.Fori(0, B) as b:
                sp.wait_ge(out_ready, b * KT)
                for k in range(KT):
                    sp.dma_start(xb[:, k * R:(k + 1) * R, :], x2[b][k * R:(k + 1) * R].rearrange("t w c -> w t c")
                                 ).then_inc(xin, 16)
                with sp.Fori(0, KT) as k:
                    sp.wait_ge(out_ready, b * KT + k + 1)
                    sp.dma_start(rows[b, k], out[:, :, :]).then_inc(stored, 16)
            sp.wait_ge(stored, 16 * B * KT)

        @block.gpsimd
        def _(pool):
            step = Chain(pool, pch)
            fill_identity(pool, step, ident)
            step(pool.memset(ones[:, :], 1.0))
            step(pool.memset(ones1[:, :], 1.0))
            step(pool.memset(half[:, :], -0.5))
            step(pool.memset(heads[:, :, :], 1.0))
            step(pool.affine_select(out=heads[:, :, :], in_=heads[:, :, :], compare_op=ALU.is_ge, fill=0.0,
                                    base=0, pattern=[[-D, H], [0, D]], channel_multiplier=1))
            step(pool.affine_select(out=heads[:, :, :], in_=heads[:, :, :], compare_op=ALU.is_ge, fill=0.0,
                                    base=D - 1, pattern=[[D, H], [0, D]], channel_multiplier=-1))
            pool.sem_inc(made, 1)
            with pool.Fori(0, B) as b:
                pool.wait_ge(ve_ready, b + 1)
                pool.tensor_tensor(rstd[:, :], ve[:, :], half[:, :], ALU.pow).then_inc(rstd_ready, 1)
                pool.wait_ge(u_ready, b + 1)
                pool.sem_inc(tick, 1)
                with pool.Fori(0, KT) as k:
                    pool.wait_ge(acc_done, b * KT + k)
                    pool.tensor_copy(us[:, :, :], u[:, bass.ds(k * R, R), :]).then_inc(staged, 1)
                    pool.wait_ge(uT_ready, b * KT + k + 1)
                    pool.tensor_copy(uT[:, bass.ds(k * R * W, R * W)], uTs[:, :]).then_inc(kept, 1)

        @block.tensor
        def _(pe):
            pe.wait_ge(loaded, 16 * NL)
            pe.wait_ge(made, 1)
            with pe.Fori(0, B) as b:
                with pe.Fori(0, KT) as k:
                    n = b * KT + k
                    pe.wait_ge(staged, n + 1)
                    for r in range(R):
                        last = pe.transpose(ps_t[:, r * W:(r + 1) * W], us[:, r, :], ident[:, :])
                    last.then_inc(turned, 1)
                    pe.wait_ge(uT_ready, n + 1)
                    for r in range(R):
                        cols = slice(r * C, (r + 1) * C)
                        pe.matmul(ps_k[:, cols], uTs[:, r * W:(r + 1) * W], wk[:, :], start=True, stop=False)
                        last = pe.matmul(ps_k[:, cols], ones1[:, :], bk_row[:, :], start=False, stop=True)
                    last.then_inc(k_done, 1)
                    pe.wait_ge(phi_ready, n + 1)
                    pe.wait_ge(acc_read, n)
                    for r in range(R):
                        pe.matmul(ps_m[:, 0:C], us[:, r, :], phi[:, r * C:(r + 1) * C], start=(r == 0), stop=(r == R - 1))
                    for r in range(R):
                        last = pe.matmul(ps_n[:, 0:C], phi[:, r * C:(r + 1) * C], ones[:, :], start=(r == 0), stop=(r == R - 1))
                    last.then_inc(acc_done, 1)
                pe.wait_ge(acc_read, (b + 1) * KT)
                pe.matmul(ps_x[:, 0:C], acc[:, 0, :], wv[:, :], start=True, stop=True).then_inc(kv_done, 1)
                pe.wait_ge(kv_ready, b + 1)
                pe.transpose(ps_x[:, C:2 * C], kv[:, :], ident[:, :]).then_inc(kvt_done, 1)
                pe.wait_ge(kvt_ready, b + 1)
                pe.matmul(ps_x[:, 2 * C:3 * C], kvt[:, :], wo[:, :], start=True, stop=True).then_inc(g_done, 1)
                pe.wait_ge(g_ready, b + 1)
                pe.wait_ge(kept, (b + 1) * KT)
                pe.sem_inc(tick, 1)
                with pe.Fori(0, KT) as k:
                    n = b * KT + k
                    pe.matmul(ps_q[:, :], wq[:, :], uT[:, bass.ds(k * R * W, R * W)], start=True, stop=True).then_inc(q_done, 1)
                    pe.wait_ge(qphi, n + 1)
                    pe.matmul(ps_d[:, :], kb[:, :], phi[:, :], start=True, stop=True).then_inc(den_done, 1)
                    pe.wait_ge(phz_ready, n + 1)
                    for r in range(R):
                        cols = slice(r * C, (r + 1) * C)
                        pe.matmul(ps_o[:, cols], phz[:, r * W:(r + 1) * W], g[:, :], start=True, stop=False)
                        last = pe.matmul(ps_o[:, cols], ones1[:, :], bo_row[:, :], start=False, stop=True)
                    last.then_inc(o_done, 1)

        @block.scalar
        def _(act):
            with act.Fori(0, B) as b:
                with act.Fori(0, KT) as k:
                    n = b * KT + k
                    act.wait_ge(turned, n + 1)
                    act.wait_ge(kept, n)
                    act.copy(uTs[:, :], ps_t[:, :]).then_inc(uT_ready, 1)
                    act.wait_ge(mn_ready, n + 1)
                    act.activation(ex[:, :], mn[:, :], ACT.Exp).then_inc(ex_ready, 1)
                with act.Fori(0, KT) as k:
                    n = b * KT + k
                    act.wait_ge(qmn, n + 1)
                    act.activation(ex[:, :], mn[:, :], ACT.Exp).then_inc(qex, 1)

        @block.vector
        def _(dve):
            step = Chain(dve, dch)
            TT, TS, STT = dve.tensor_tensor, dve.tensor_scalar, dve.scalar_tensor_tensor
            dve.wait_ge(loaded, 16 * NL)
            dve.wait_ge(made, 1)
            hm = heads[:, :, :].rearrange("p h d -> p (h d)")
            BASE = 2 * T + 4
            P1, FIN, P2 = 3, 5, 6
            per = BASE + P1 * KT + FIN + P2 * KT
            with dve.Fori(0, B) as b:
                start = b * per
                step.base, step.k = start, 0
                dve.wait_ge(xin, 16 * KT * (b + 1))
                for t in range(T):
                    step.mark(dve.bn_stats(st[:, t, :], xb[:, t, :]))
                step.join()
                dve.sem_inc(tick, 1)
                for t in range(T):
                    step.mark(dve.bn_aggr(mv[:, t, :], st[:, t, :]))
                step.join()
                step(TS(ve[:, :], mv[:, :, 1], eps, None, ALU.add))
                dve.sem_inc(ve_ready, 1)
                dve.wait_ge(rstd_ready, b + 1)
                step(TT(u[:, :, :], xb[:, :, :], mv[:, :, 0:1].broadcast_to([P, T, C]), ALU.subtract))
                step(TT(u[:, :, :], u[:, :, :], rstd[:, :].unsqueeze(2).broadcast_to([P, T, C]), ALU.mult))
                dve.sem_inc(u_ready, 1)
                step(dve.memset(acc[:, :, :], 0.0))
                assert step.k == BASE
                dve.sem_inc(tick, 1)
                with dve.Fori(0, KT) as k:
                    n = b * KT + k
                    step.base, step.k = start + BASE + k * P1, 0
                    dve.wait_ge(k_done, n + 1)
                    dve.tensor_scalar(mn[:, :], ps_k[:, :], 0.0, None, ALU.min).then_inc(mn_ready, 1)
                    dve.wait_ge(ex_ready, n + 1)
                    step(STT(out=phi[:, :], in0=ps_k[:, :], scalar=0.0, in1=ex[:, :], op0=ALU.max, op1=ALU.add))
                    dve.sem_inc(phi_ready, 1)
                    dve.wait_ge(acc_done, n + 1)
                    step(TT(acc[:, 0, :], acc[:, 0, :], ps_m[:, 0:C], ALU.add))
                    step(TT(acc[:, 1, :], acc[:, 1, :], ps_n[:, 0:C], ALU.add))
                    dve.sem_inc(acc_read, 1)
                    assert step.k == P1
                step.base, step.k = start + BASE + P1 * KT, 0
                dve.wait_ge(kv_done, b + 1)
                step(TT(kv[:, :], acc[:, 1, :], bv_b[:, :], ALU.mult))
                step(TT(kv[:, :], kv[:, :], ps_x[:, 0:C], ALU.add))
                step(TT(kv[:, :], kv[:, :], hm, ALU.mult))
                dve.sem_inc(kv_ready, 1)
                step(TT(kb[:, :], acc[:, 1, :], hm, ALU.mult))
                dve.wait_ge(kvt_done, b + 1)
                dve.tensor_copy(kvt[:, :], ps_x[:, C:2 * C]).then_inc(kvt_ready, 1)
                dve.wait_ge(g_done, b + 1)
                step(dve.tensor_copy(g[:, :], ps_x[:, 2 * C:3 * C]))
                dve.sem_inc(g_ready, 1)
                assert step.k == FIN
                dve.sem_inc(tick, 1)
                with dve.Fori(0, KT) as k:
                    n = b * KT + k
                    step.base, step.k = start + BASE + P1 * KT + FIN + k * P2, 0
                    dve.wait_ge(q_done, n + 1)
                    dve.tensor_scalar(mn[:, :], ps_q[:, :], bqc[:, 0:1], 0.0, ALU.add, ALU.min).then_inc(qmn, 1)
                    step(TS(phi[:, :], ps_q[:, :], bqc[:, 0:1], 0.0, ALU.add, ALU.max))
                    dve.wait_ge(qex, n + 1)
                    step(TT(phi[:, :], phi[:, :], ex[:, :], ALU.add))
                    dve.sem_inc(qphi, 1)
                    dve.wait_ge(den_done, n + 1)
                    step(TS(rd[:, :], ps_d[:, :], eps, None, ALU.add))
                    step(dve.reciprocal(rd[:, :], rd[:, :]))
                    step(TT(phz[:, :], phi[:, :], rd[:, :], ALU.mult))
                    dve.sem_inc(phz_ready, 1)
                    dve.wait_ge(o_done, n + 1)
                    dve.wait_ge(stored, 16 * n)
                    step(TT(out[:, :, :], ps_o[:, :].rearrange("p (r c) -> p r c", r=R), xb[:, bass.ds(k * R, R), :], ALU.add))
                    dve.sem_inc(out_ready, 1)
                    assert step.k == P2


def routed_experts(nc, x3, gate_w, gate_b, w1, w2, x4, tag="moe", eps=1e-5):
    E = gate_w.shape[0]
    HID = w1.shape[2]
    HC = HID // P
    R = 4
    KT = T // R
    L = T * W
    NEG = -3.0e38
    with ExitStack() as ctx:
        s = Scope(nc, ctx, tag)
        ident = s.sb("ident", [P, P])
        gT = s.sb("gT", [P, E])
        wt = s.sb("wt", [P, 2, L])
        poolT = s.sb("poolT", [P, E, B])
        eo = s.sb("eo", [P, 2, C])
        u_d = nc.dram_tensor(f"{tag}_u", (BT, W, C), f32, kind="Internal").ap()
        with ExitStack() as c2:
            s2 = Scope(nc, c2, tag + "a")
            gw = s2.sb("gw", [E, C])
            gb = s2.sb("gb", [P, 1])
            xb = s2.sb("xb", [P, T, C])
            u = s2.sb("u", [P, T, C])
            us = s2.sb("us", [P, R, C])
            uTs = s2.sb("uTs", [P, R * W])
            st = s2.sb("st", [P, T, 6])
            mv = s2.sb("mv", [P, T, 2])
            ve, rstd, half = (s2.sb(n, [P, T]) for n in ("ve", "rstd", "half"))
            ps_t, ps_l, ps_g = s2.ps("ps_t"), s2.ps("ps_l"), s2.ps("ps_g")
            (loaded, made, g_done, g_ready, xin, ve_ready, rstd_ready, u_ready, staged, turned, uT_ready,
             l_done, l_ready, saved, dch, pch, tick) = (
                s2.sem(n) for n in ("loaded", "made", "g_done", "g_ready", "xin", "ve_ready", "rstd_ready",
                                    "u_ready", "staged", "turned", "uT_ready", "l_done", "l_ready", "saved",
                                    "dch", "pch", "tick"))
            block = c2.enter_context(nc.Block())

            @block.sync
            def _(sp):
                sp.dma_start(gw[:, :], gate_w).then_inc(loaded, 16)
                for j in range(2):
                    sp.dma_start(gb[j * E:(j + 1) * E, :], gate_b.unsqueeze(1)).then_inc(loaded, 16)
                for b in range(B):
                    if b:
                        sp.wait_ge(u_ready, b)
                    sp.dma_start(xb[:, :, :], batch_tokens(x3, b)).then_inc(xin, 16)
                    sp.wait_ge(u_ready, b + 1)
                    sp.dma_start(u_d[b * T:(b + 1) * T].rearrange("t w c -> w t c"), u[:, :, :]).then_inc(saved, 16)
                sp.wait_ge(saved, 16 * B)

            @block.gpsimd
            def _(pool):
                step = Chain(pool, pch)
                fill_identity(pool, step, ident)
                step(pool.memset(half[:, :], -0.5))
                pool.sem_inc(made, 1)
                for b in range(B):
                    pool.wait_ge(ve_ready, b + 1)
                    pool.tensor_tensor(rstd[:, :], ve[:, :], half[:, :], ALU.pow).then_inc(rstd_ready, 1)
                    pool.wait_ge(u_ready, b + 1)
                    with pool.Fori(0, KT) as k:
                        pool.wait_ge(turned, k + b * KT)
                        pool.tensor_copy(us[:, :, :], u[:, bass.ds(k * R, R), :]).then_inc(staged, 1)

            @block.tensor
            def _(pe):
                pe.wait_ge(loaded, 48)
                pe.wait_ge(made, 1)
                pe.transpose(ps_g[:, 0:E], gw[:, :], ident[0:E, 0:E]).then_inc(g_done, 1)
                pe.wait_ge(g_ready, 1)
                for b in range(B):
                    rows = slice((b % 2) * E, (b % 2 + 1) * E)
                    with pe.Fori(0, KT) as k:
                        n = k + b * KT
                        pe.wait_ge(staged, n + 1)
                        pe.wait_ge(uT_ready, n)
                        for r in range(R):
                            last = pe.transpose(ps_t[:, r * W:(r + 1) * W], us[:, r, :], ident[:, :])
                        last.then_inc(turned, 1)
                        pe.wait_ge(uT_ready, n + 1)
                        pe.wait_ge(l_ready, n)
                        pe.matmul(ps_l[rows, :], gT[:, :], uTs[:, :], start=True, stop=True,
                                  tile_position=(0, (b % 2) * E)).then_inc(l_done, 1)

            @block.scalar
            def _(act):
                act.wait_ge(g_done, 1)
                act.copy(gT[:, :], ps_g[:, 0:E]).then_inc(g_ready, 1)
                for b in range(B):
                    rows = slice((b % 2) * E, (b % 2 + 1) * E)
                    with act.Fori(0, KT) as k:
                        n = k + b * KT
                        act.wait_ge(turned, n + 1)
                        act.wait_ge(l_done, n)
                        act.copy(uTs[:, :], ps_t[:, :]).then_inc(uT_ready, 1)
                        act.wait_ge(l_done, n + 1)
                        act.activation(wt[rows, b // 2, bass.ds(k * R * W, R * W)], ps_l[rows, :], ACT.Identity,
                                       bias=gb[rows, 0:1]).then_inc(l_ready, 1)

            @block.vector
            def _(dve):
                step = Chain(dve, dch)
                TT = dve.tensor_tensor
                for b in range(B):
                    dve.wait_ge(xin, 16 * (b + 1))
                    for t in range(T):
                        step.mark(dve.bn_stats(st[:, t, :], xb[:, t, :]))
                    step.join()
                    for t in range(T):
                        step.mark(dve.bn_aggr(mv[:, t, :], st[:, t, :]))
                    step.join()
                    step(dve.tensor_scalar(ve[:, :], mv[:, :, 1], eps, None, ALU.add))
                    dve.sem_inc(ve_ready, 1)
                    dve.wait_ge(rstd_ready, b + 1)
                    if b:
                        dve.wait_ge(staged, b * KT)
                        dve.wait_ge(saved, 16 * b)
                    step(TT(u[:, :, :], xb[:, :, :], mv[:, :, 0:1].broadcast_to([P, T, C]), ALU.subtract))
                    step(TT(u[:, :, :], u[:, :, :], rstd[:, :].unsqueeze(2).broadcast_to([P, T, C]), ALU.mult))
                    dve.sem_inc(u_ready, 1)

        with ExitStack() as c2:
            s2 = Scope(nc, c2, tag + "b")
            top = s2.sb("top", [P, 2, 8])
            nmx = s2.sb("nmx", [P, 2])
            den = s2.sb("den", [P, 2])
            rest = s2.sb("rest", [P, 2, L])
            pr = s2.sb("pr", [P, 2, L])
            neg_ready, ex_ready, dch = s2.sem("neg_ready"), s2.sem("ex_ready"), s2.sem("dch")
            block = c2.enter_context(nc.Block())

            @block.scalar
            def _(act):
                for j in range(2):
                    act.wait_ge(neg_ready, j + 1)
                    act.activation(pr[:, j, :], wt[:, j, :], ACT.Exp, bias=nmx[:, j:j + 1],
                                   accum_out=den[:, j:j + 1]).then_inc(ex_ready, 1)

            @block.vector
            def _(dve):
                step = Chain(dve, dch)
                for j in range(2):
                    step(dve.max(top[:, j, :], wt[:, j, :]))
                    step(dve.tensor_scalar(nmx[:, j:j + 1], top[:, j, 0:1], -1.0, None, ALU.mult))
                    dve.sem_inc(neg_ready, 1)
                    step(dve.match_replace(rest[:, j, :], top[:, j, :], wt[:, j, :], NEG))
                for j in range(2):
                    dve.wait_ge(ex_ready, j + 1)
                    step(dve.tensor_tensor(rest[:, j, :], rest[:, j, :], wt[:, j, :], ALU.not_equal))
                    step(dve.reciprocal(den[:, j:j + 1], den[:, j:j + 1]))
                    step(dve.scalar_tensor_tensor(out=wt[:, j, :], in0=pr[:, j, :], scalar=den[:, j:j + 1],
                                                  in1=rest[:, j, :], op0=ALU.mult, op1=ALU.mult))

        with ExitStack() as c2:
            s2 = Scope(nc, c2, tag + "c")
            ur = [s2.sb(f"ur{j}", [P, R, C]) for j in range(2)]
            ws = s2.sb("ws", [P, R * W])
            wT = [s2.sb(f"wT{j}", [P, R, E]) for j in range(2)]
            acc = s2.sb("acc", [P, B, E])
            ps_w = s2.ps("ps_w")
            ps_p = [s2.ps(f"ps_p{j}") for j in range(2)]
            uin = [s2.sem(f"uin{j}") for j in range(2)]
            staged, turned, wT_ready, pooled, added, dch = (s2.sem(n) for n in (
                "staged", "turned", "wT_ready", "pooled", "added", "dch"))
            block = c2.enter_context(nc.Block())
            uv = u_d.rearrange("(b i j r) w c -> b i j w r c", b=B, j=2, r=R)

            @block.sync
            def _(sp):
                for b in range(B):
                    with sp.Fori(0, KT // 2) as i:
                        for j in range(2):
                            sp.wait_ge(pooled, i * 2 + b * KT + j - 1) if j else sp.wait_ge(pooled, i * 2 + b * KT)
                            sp.dma_start(ur[j][:, :, :], uv[b][i, j]).then_inc(uin[j], 16)

            @block.gpsimd
            def _(pool):
                for b in range(B):
                    rows = slice((b % 2) * E, (b % 2 + 1) * E)
                    with pool.Fori(0, KT) as k:
                        pool.wait_ge(turned, k + b * KT)
                        pool.tensor_copy(ws[:, :], wt[:, b // 2, bass.ds(k * R * W, R * W)]).then_inc(staged, 1)

            @block.tensor
            def _(pe):
                for b in range(B):
                    with pe.Fori(0, KT // 2) as i:
                        for j in range(2):
                            n = i * 2 + b * KT + j
                            pe.wait_ge(staged, n + 1)
                            pe.wait_ge(wT_ready, n)
                            for r in range(R):
                                last = pe.transpose(ps_w[:, r * P:(r + 1) * P], ws[:, r * W:(r + 1) * W], ident[:, :])
                            last.then_inc(turned, 1)
                            pe.wait_ge(wT_ready, n + 1)
                            pe.wait_ge(uin[j], i * 16 + b * 16 * (KT // 2) + 16)
                            pe.wait_ge(added, i * 2 + b * KT)
                            for r in range(R):
                                last = pe.matmul(ps_p[j][:, 0:E], ur[j][:, r, :], wT[j][:, r, :],
                                                 start=(r == 0), stop=(r == R - 1))
                            last.then_inc(pooled, 1)

            @block.scalar
            def _(act):
                for b in range(B):
                    cols = slice((b % 2) * E, (b % 2 + 1) * E)
                    with act.Fori(0, KT // 2) as i:
                        for j in range(2):
                            n = i * 2 + b * KT + j
                            act.wait_ge(turned, n + 1)
                            act.wait_ge(pooled, i * 2 + b * KT)
                            act.copy(wT[j][:, :, :], ps_w[:, :].rearrange("p (r e) -> p r e", r=R)[:, :, cols]
                                     ).then_inc(wT_ready, 1)

            @block.vector
            def _(dve):
                step = Chain(dve, dch)
                step(dve.memset(acc[:, :, :], 0.0))
                for b in range(B):
                    with step.loop(KT // 2, 2) as i:
                        for j in range(2):
                            dve.wait_ge(pooled, i * 2 + b * KT + j + 1)
                            step(dve.tensor_tensor(acc[:, b, :], acc[:, b, :], ps_p[j][:, 0:E], ALU.add))
                            dve.sem_inc(added, 1)
                step(dve.tensor_copy(poolT[:, :, :], acc[:, :, :].rearrange("p b e -> p e b")))

        with ExitStack() as c2:
            s2 = Scope(nc, c2, tag + "d")
            NB = 4
            wa = [s2.sb(f"wa{j}", [P, HID]) for j in range(NB)]
            ab = [s2.sb(f"ab{j}", [1, HID]) for j in range(NB)]
            wb = [s2.sb(f"wb{j}", [P, HC, C]) for j in range(NB)]
            bb = [s2.sb(f"bb{j}", [1, C]) for j in range(NB)]
            ones1 = s2.sb("ones1", [1, B])
            h = [s2.sb(f"h{j}", [P, HC * B]) for j in range(2)]
            eoT = s2.sb("eoT", [P, B, E])
            ps_h = [s2.ps(f"ps_h{j}") for j in range(2)]
            ps_e = s2.ps("ps_e")
            ps_f = s2.ps("ps_f")
            win = [s2.sem(f"win{j}") for j in range(NB)]
            made, hid, h_ready, outd, eo_t, flipped, eo_ready = (s2.sem(n) for n in (
                "made", "hid", "h_ready", "outd", "eo_t", "flipped", "eo_ready"))
            tick = s2.sem("tick")
            block = c2.enter_context(nc.Block())
            w1v = w1.rearrange("(i j) d h -> i j d h", j=NB)
            w2v = w2.rearrange("(i j) h o -> i j h o", j=NB)

            @block.sync
            def _(sp):
                with sp.Fori(0, E // NB) as i:
                    for j in range(NB):
                        sp.wait_ge(outd, i * NB)
                        sp.dma_start(wa[j][:, :], w1v[i, j][0:P]).then_inc(win[j], 16)
                        sp.dma_start(ab[j][:, :], w1v[i, j][P:P + 1]).then_inc(win[j], 16)
                        sp.dma_start(wb[j][:, :, :], w2v[i, j][0:HID].rearrange("(k p) o -> p k o", p=P)).then_inc(win[j], 16)
                        sp.dma_start(bb[j][:, :], w2v[i, j][HID:HID + 1]).then_inc(win[j], 16)

            @block.gpsimd
            def _(pool):
                pool.memset(ones1[:, :], 1.0).then_inc(made, 1)

            @block.tensor
            def _(pe):
                pe.wait_ge(made, 1)
                with pe.Fori(0, E // NB) as i:
                    for j in range(NB):
                        e = i * NB + j
                        pe.wait_ge(win[j], i * 64 + 64)
                        pe.wait_ge(h_ready, i * NB + j - 1) if j >= 2 else pe.wait_ge(h_ready, i * NB)
                        pe.sem_inc(tick, 1)
                        for k in range(HC):
                            cols = slice(k * P, (k + 1) * P)
                            dst = ps_h[j % 2][:, k * B:(k + 1) * B]
                            pe.matmul(dst, wa[j][:, cols], poolT[:, bass.ds(i * NB + j, 1), :].rearrange("p a b -> p (a b)"),
                                      start=True, stop=False)
                            last = pe.matmul(dst, ab[j][:, cols], ones1[:, :], start=False, stop=True)
                        last.then_inc(hid, 1)
                        pe.wait_ge(h_ready, i * NB + j + 1)
                        pe.sem_inc(tick, 1)
                        dst = ps_e[:, bass.ds((i * NB + j) * B, B)]
                        for k in range(HC):
                            pe.matmul(dst, wb[j][:, k, :], h[j % 2][:, k * B:(k + 1) * B], start=(k == 0), stop=False)
                        pe.matmul(dst, bb[j][:, :], ones1[:, :], start=False, stop=True).then_inc(outd, 1)
                pe.wait_ge(eo_t, 1)
                for j in range(2):
                    pe.transpose(ps_f[:, j * C:(j + 1) * C], eoT[:, 2 * j:2 * j + 2, :].rearrange("p b e -> p (b e)"),
                                 ident[:, :]).then_inc(flipped, 1)

            @block.scalar
            def _(act):
                with act.Fori(0, E // NB) as i:
                    for j in range(NB):
                        act.wait_ge(hid, i * NB + j + 1)
                        act.wait_ge(outd, i * NB + j - 1) if j >= 2 else act.wait_ge(outd, i * NB)
                        act.activation(h[j % 2][:, :], ps_h[j % 2][:, 0:HC * B], ACT.Gelu).then_inc(h_ready, 1)
                act.wait_ge(outd, E)
                act.copy(eoT[:, :, :], ps_e[:, 0:E * B].rearrange("p (e b) -> p b e", b=B)).then_inc(eo_t, 1)
                act.wait_ge(flipped, 2)
                act.copy(eo[:, :, :], ps_f[:, 0:2 * C].rearrange("p (j c) -> p j c", j=2)).then_inc(eo_ready, 1)

        with ExitStack() as c2:
            s2 = Scope(nc, c2, tag + "e")
            xr = [s2.sb(f"xr{j}", [P, R, C]) for j in range(2)]
            out = [s2.sb(f"out{j}", [P, R, C]) for j in range(2)]
            ws = [s2.sb(f"ws{j}", [P, R * W]) for j in range(2)]
            ps = [s2.ps(f"ps{j}") for j in range(2)]
            xin = [s2.sem(f"xin{j}") for j in range(2)]
            staged, given, added, stored = (s2.sem(n) for n in ("staged", "given", "added", "stored"))
            block = c2.enter_context(nc.Block())
            xv = x3.rearrange("b (i j r) w c -> b i j w r c", j=2, r=R)
            ov = x4.rearrange("b (i j r) w c -> b i j w r c", j=2, r=R)

            @block.sync
            def _(sp):
                for b in range(B):
                    with sp.Fori(0, KT // 2) as i:
                        for j in range(2):
                            sp.wait_ge(added, i * 2 + b * KT)
                            sp.dma_start(xr[j][:, :, :], xv[b][i, j]).then_inc(xin[j], 16)

            @block.gpsimd
            def _(pool):
                for b in range(B):
                    rows = slice((b % 2) * E, (b % 2 + 1) * E)
                    with pool.Fori(0, KT // 2) as i:
                        for j in range(2):
                            pool.wait_ge(given, i * 2 + b * KT)
                            pool.tensor_copy(ws[j][rows, :], wt[rows, b // 2, bass.ds(i * 2 * R * W + j * R * W, R * W)]
                                             ).then_inc(staged, 1)

            @block.tensor
            def _(pe):
                for b in range(B):
                    rows = slice((b % 2) * E, (b % 2 + 1) * E)
                    with pe.Fori(0, KT // 2) as i:
                        for j in range(2):
                            n = i * 2 + b * KT + j
                            pe.wait_ge(staged, n + 1)
                            pe.wait_ge(added, i * 2 + b * KT)
                            for r in range(R):
                                last = pe.matmul(ps[j][:, r * C:(r + 1) * C], ws[j][rows, r * W:(r + 1) * W],
                                                 eo[rows, b // 2, :], start=True, stop=True,
                                                 tile_position=((b % 2) * E, 0))
                            last.then_inc(given, 1)

            @block.vector
            def _(dve):
                for b in range(B):
                    with dve.Fori(0, KT // 2) as i:
                        for j in range(2):
                            n = i * 2 + b * KT + j
                            dve.wait_ge(given, n + 1)
                            dve.wait_ge(xin[j], i * 16 + b * 16 * (KT // 2) + 16)
                            dve.wait_ge(stored, (i * 2 + b * KT) * 16)
                            dve.tensor_tensor(out[j][:, :, :], xr[j][:, :, :],
                                              ps[j][:, :].rearrange("p (r c) -> p r c", r=R), ALU.add).then_inc(added, 1)

            @block.scalar
            def _(act):
                for b in range(B):
                    with act.Fori(0, KT // 2) as i:
                        for j in range(2):
                            act.wait_ge(added, i * 2 + b * KT + j + 1)
                            act.dma_start(ov[b][i, j], out[j][:, :, :]).then_inc(stored, 16)
                act.wait_ge(stored, 16 * B * KT)


def normalised_tokens(nc, x, u, tag, eps=1e-5):
    with ExitStack() as ctx:
        s = Scope(nc, ctx, tag)
        xb = [s.sb(f"xb{j}", [P, T // 2, C]) for j in range(2)]
        TH = T // 2
        st = s.sb("st", [P, TH, 6])
        mv = s.sb("mv", [P, TH, 2])
        ve, rstd, half = (s.sb(n, [P, TH]) for n in ("ve", "rstd", "half"))
        xin = [s.sem(f"xin{j}") for j in range(2)]
        made, ve_ready, rstd_ready, u_ready, dch = (s.sem(n) for n in ("made", "ve_ready", "rstd_ready", "u_ready", "dch"))
        block = ctx.enter_context(nc.Block())
        N = 2 * B
        xv = x.rearrange("b (j t) w c -> (b j) w t c", j=2)

        @block.sync
        def _(sp):
            for n in range(N):
                if n >= 2:
                    sp.wait_ge(u_ready, n - 1)
                sp.dma_start(xb[n % 2][:, :, :], xv[n]).then_inc(xin[n % 2], 16)

        @block.gpsimd
        def _(pool):
            pool.memset(half[:, :], -0.5).then_inc(made, 1)
            pool.wait_ge(made, 1)
            for n in range(N):
                pool.wait_ge(ve_ready, n + 1)
                pool.tensor_tensor(rstd[:, :], ve[:, :], half[:, :], ALU.pow).then_inc(rstd_ready, 1)

        @block.vector
        def _(dve):
            step = Chain(dve, dch)
            for n in range(N):
                dve.wait_ge(xin[n % 2], 16 * (n // 2 + 1))
                src = xb[n % 2]
                dst = u[:, n * TH:(n + 1) * TH, :]
                for t in range(TH):
                    step.mark(dve.bn_stats(st[:, t, :], src[:, t, :]))
                step.join()
                for t in range(TH):
                    step.mark(dve.bn_aggr(mv[:, t, :], st[:, t, :]))
                step.join()
                step(dve.tensor_scalar(ve[:, :], mv[:, :, 1], eps, None, ALU.add))
                dve.sem_inc(ve_ready, 1)
                step(dve.tensor_tensor(dst, src[:, :, :], mv[:, :, 0:1].broadcast_to([P, TH, C]), ALU.subtract))
                dve.wait_ge(rstd_ready, n + 1)
                step(dve.tensor_tensor(dst, dst, rstd[:, :].unsqueeze(2).broadcast_to([P, TH, C]), ALU.mult))
                dve.sem_inc(u_ready, 1)


def softmax_attention(nc, x4, w_in, w_out, b_out, ln_w, x5, tag="sma", eps=1e-5):
    H = 4
    D = C // H
    R = 4
    NT = BT // R
    TOK = BT * W
    with ExitStack() as ctx:
        s = Scope(nc, ctx, tag)
        u = s.sb("u", [P, BT, C])
        wT = s.sb("wT", [P, 4, C])
        ident, ones = s.sb("ident", [P, P]), s.sb("ones", [P, P])
        ones1 = s.sb("ones1", [1, P])
        negmax = s.sb("negmax", [1, C])
        heads = s.sb("heads", [P, H, D])
        g = s.sb("g", [P, C])
        normalised_tokens(nc, x4, u, tag + "n")
        with ExitStack() as c2:
            s2 = Scope(nc, c2, tag + "a")
            wl = s2.sb("wl", [P, 4, C])
            us = s2.sb("us", [P, R, C])
            uTs = [s2.sb(f"uTs{j}", [P, R * W]) for j in range(2)]
            mx = s2.sb("mx", [P, NT])
            m1 = s2.sb("m1", [P, 1])
            ps_w, ps_t, ps_m = s2.ps("ps_w"), s2.ps("ps_t"), s2.ps("ps_m")
            ps_k = [s2.ps(f"ps_k{j}") for j in range(2)]
            (loaded, made, w_done, w_ready, staged, turned, uT_ready, k_done, k_read, m_ready, m_done, dch, pch,
             tick) = (s2.sem(n) for n in ("loaded", "made", "w_done", "w_ready", "staged", "turned", "uT_ready",
                                          "k_done", "k_read", "m_ready", "m_done", "dch", "pch", "tick"))
            block = c2.enter_context(nc.Block())

            @block.sync
            def _(sp):
                sp.dma_start(wl[:, 0:3, :], w_in.rearrange("(j o) c -> o j c", j=3)).then_inc(loaded, 16)
                sp.dma_start(wl[:, 3, :], w_out).then_inc(loaded, 16)

            @block.gpsimd
            def _(pool):
                step = Chain(pool, pch)
                fill_identity(pool, step, ident)
                step(pool.memset(ones[:, :], 1.0))
                step(pool.memset(ones1[:, :], 1.0))
                step(pool.memset(heads[:, :, :], 1.0))
                step(pool.affine_select(out=heads[:, :, :], in_=heads[:, :, :], compare_op=ALU.is_ge, fill=0.0,
                                        base=0, pattern=[[-D, H], [0, D]], channel_multiplier=1))
                step(pool.affine_select(out=heads[:, :, :], in_=heads[:, :, :], compare_op=ALU.is_ge, fill=0.0,
                                        base=D - 1, pattern=[[D, H], [0, D]], channel_multiplier=-1))
                pool.sem_inc(made, 1)
                with pool.Fori(0, NT) as i:
                    pool.wait_ge(turned, i)
                    pool.tensor_copy(us[:, :, :], u[:, bass.ds(i * R, R), :]).then_inc(staged, 1)

            @block.tensor
            def _(pe):
                pe.wait_ge(loaded, 32)
                pe.wait_ge(made, 1)
                for j in range(4):
                    last = pe.transpose(ps_w[:, j * C:(j + 1) * C], wl[:, j, :], ident[:, :])
                last.then_inc(w_done, 1)
                pe.wait_ge(w_ready, 1)
                with pe.Fori(0, NT // 2) as i:
                    for j in range(2):
                        n = 2 * i + j
                        pe.wait_ge(staged, 2 * i + j + 1)
                        pe.wait_ge(uT_ready, 2 * i + j)
                        for r in range(R):
                            last = pe.transpose(ps_t[:, r * W:(r + 1) * W], us[:, r, :], ident[:, :])
                        last.then_inc(turned, 1)
                        pe.wait_ge(uT_ready, 2 * i + j + 1)
                        pe.wait_ge(k_read, 2 * i)
                        pe.matmul(ps_k[j][:, :], wT[:, 1, :], uTs[j][:, :], start=True, stop=True).then_inc(k_done, 1)
                pe.wait_ge(m_ready, 1)
                pe.transpose(ps_m[0:1, 0:P], m1[:, :], ident[:, :]).then_inc(m_done, 1)

            @block.scalar
            def _(act):
                act.wait_ge(w_done, 1)
                act.copy(wT[:, :, :], ps_w[:, :].rearrange("p (j c) -> p j c", j=4)).then_inc(w_ready, 1)
                with act.Fori(0, NT // 2) as i:
                    for j in range(2):
                        act.wait_ge(turned, 2 * i + j + 1)
                        act.wait_ge(k_done, 2 * i)
                        act.copy(uTs[j][:, :], ps_t[:, :]).then_inc(uT_ready, 1)
                act.wait_ge(m_done, 1)
                act.copy(negmax[:, :], ps_m[0:1, 0:P]).then_inc(tick, 1)

            @block.vector
            def _(dve):
                step = Chain(dve, dch)
                with dve.Fori(0, NT // 2) as i:
                    for j in range(2):
                        dve.wait_ge(k_done, 2 * i + j + 1)
                        dve.tensor_reduce(mx[:, bass.ds(i * 2 + j, 1)], ps_k[j][:, :], AX.X, ALU.max).then_inc(k_read, 1)
                dve.wait_ge(k_read, NT)
                step(dve.tensor_reduce(m1[:, :], mx[:, :], AX.X, ALU.max, negate=True))
                dve.sem_inc(m_ready, 1)

        with ExitStack() as c2:
            s2 = Scope(nc, c2, tag + "b")
            us = s2.sb("us", [P, R, C])
            uTs = s2.sb("uTs", [P, R * W])
            ek = s2.sb("ek", [P, R * C])
            acc = s2.sb("acc", [P, 2, C])
            ctxm, ctxt = s2.sb("ctxm", [P, C]), s2.sb("ctxt", [P, C])
            rsum = s2.sb("rsum", [P, 1])
            ps_t, ps_k, ps_m, ps_n, ps_x = (s2.ps(n) for n in ("ps_t", "ps_k", "ps_m", "ps_n", "ps_x"))
            (staged, turned, uT_ready, k_done, ek_ready, acc_done, acc_read, c_done, c_ready, ct_done, ct_ready,
             g_done, dch) = (s2.sem(n) for n in (
                 "staged", "turned", "uT_ready", "k_done", "ek_ready", "acc_done", "acc_read", "c_done",
                 "c_ready", "ct_done", "ct_ready", "g_done", "dch"))
            block = c2.enter_context(nc.Block())

            @block.gpsimd
            def _(pool):
                with pool.Fori(0, NT) as i:
                    pool.wait_ge(acc_done, i)
                    pool.tensor_copy(us[:, :, :], u[:, bass.ds(i * R, R), :]).then_inc(staged, 1)

            @block.tensor
            def _(pe):
                with pe.Fori(0, NT) as i:
                    pe.wait_ge(staged, i + 1)
                    for r in range(R):
                        last = pe.transpose(ps_t[:, r * W:(r + 1) * W], us[:, r, :], ident[:, :])
                    last.then_inc(turned, 1)
                    pe.wait_ge(uT_ready, i + 1)
                    for r in range(R):
                        cols = slice(r * C, (r + 1) * C)
                        pe.matmul(ps_k[:, cols], uTs[:, r * W:(r + 1) * W], wT[:, 1, :], start=True, stop=False)
                        last = pe.matmul(ps_k[:, cols], ones1[:, :], negmax[:, :], start=False, stop=True)
                    last.then_inc(k_done, 1)
                    pe.wait_ge(ek_ready, i + 1)
                    pe.wait_ge(acc_read, i)
                    for r in range(R):
                        pe.matmul(ps_m[:, 0:C], us[:, r, :], ek[:, r * C:(r + 1) * C], start=(r == 0), stop=(r == R - 1))
                    for r in range(R):
                        last = pe.matmul(ps_n[:, 0:C], ek[:, r * C:(r + 1) * C], ones[:, :], start=(r == 0), stop=(r == R - 1))
                    last.then_inc(acc_done, 1)
                pe.wait_ge(acc_read, NT)
                pe.matmul(ps_x[:, 0:C], acc[:, 0, :], wT[:, 2, :], start=True, stop=True).then_inc(c_done, 1)
                pe.wait_ge(c_ready, 1)
                pe.transpose(ps_x[:, C:2 * C], ctxm[:, :], ident[:, :]).then_inc(ct_done, 1)
                pe.wait_ge(ct_ready, 1)
                pe.matmul(ps_x[:, 2 * C:3 * C], ctxt[:, :], wT[:, 3, :], start=True, stop=True).then_inc(g_done, 1)

            @block.scalar
            def _(act):
                with act.Fori(0, NT) as i:
                    act.wait_ge(turned, i + 1)
                    act.wait_ge(k_done, i)
                    act.copy(uTs[:, :], ps_t[:, :]).then_inc(uT_ready, 1)
                    act.wait_ge(k_done, i + 1)
                    act.wait_ge(acc_done, i)
                    act.activation(ek[:, :], ps_k[:, :], ACT.Exp).then_inc(ek_ready, 1)

            @block.vector
            def _(dve):
                step = Chain(dve, dch)
                TT = dve.tensor_tensor
                step(dve.memset(acc[:, :, :], 0.0))
                with step.loop(NT, 2) as i:
                    dve.wait_ge(acc_done, i + 1)
                    step(TT(acc[:, 0, :], acc[:, 0, :], ps_m[:, 0:C], ALU.add))
                    step(TT(acc[:, 1, :], acc[:, 1, :], ps_n[:, 0:C], ALU.add))
                    dve.sem_inc(acc_read, 1)
                step(dve.tensor_scalar(rsum[:, :], acc[:, 1, 0:1], float(TOK) * math.sqrt(D), None, ALU.mult))
                step(dve.reciprocal(rsum[:, :], rsum[:, :]))
                dve.wait_ge(c_done, 1)
                step(dve.scalar_tensor_tensor(out=ctxm[:, :], in0=ps_x[:, 0:C], scalar=rsum[:, 0:1],
                                              in1=heads[:, :, :].rearrange("p h d -> p (h d)"), op0=ALU.mult, op1=ALU.mult))
                dve.sem_inc(c_ready, 1)
                dve.wait_ge(ct_done, 1)
                dve.tensor_copy(ctxt[:, :], ps_x[:, C:2 * C]).then_inc(ct_ready, 1)
                dve.wait_ge(g_done, 1)
                step(dve.tensor_copy(g[:, :], ps_x[:, 2 * C:3 * C]))

        with ExitStack() as c2:
            s2 = Scope(nc, c2, tag + "c")
            bo_row = s2.sb("bo_row", [1, C])
            lnw = s2.sb("lnw", [P, C])
            us = s2.sb("us", [P, R, C])
            uTs = s2.sb("uTs", [P, R * W])
            xr = s2.sb("xr", [P, R, C])
            q = s2.sb("q", [P, R * H, D])
            mx, den = s2.sb("mx", [P, R * H]), s2.sb("den", [P, R * H])
            qT = s2.sb("qT", [P, R * W])
            z = s2.sb("z", [P, R, C])
            out = s2.sb("out", [P, R, C])
            st, mv = s2.sb("st", [P, R, 6]), s2.sb("mv", [P, R, 2])
            ve, rstd, half = (s2.sb(n, [P, R]) for n in ("ve", "rstd", "half"))
            ps_t, ps_q, ps_y, ps_o = (s2.ps(n) for n in ("ps_t", "ps_q", "ps_y", "ps_o"))
            (loaded, made, xin, staged, turned, uT_ready, q_done, shifted, ex_ready, q_ready, flipped, qT_ready,
             o_done, ve_ready, rstd_ready, out_ready, stored, dch, tick) = (s2.sem(n) for n in (
                 "loaded", "made", "xin", "staged", "turned", "uT_ready", "q_done", "shifted", "ex_ready",
                 "q_ready", "flipped", "qT_ready", "o_done", "ve_ready", "rstd_ready", "out_ready", "stored",
                 "dch", "tick"))
            block = c2.enter_context(nc.Block())
            xv = x4.rearrange("b t w c -> (b t) w c").rearrange("(i r) w c -> i w r c", r=R)
            ov = x5.rearrange("b t w c -> (b t) w c").rearrange("(i r) w c -> i w r c", r=R)

            @block.sync
            def _(sp):
                sp.dma_start(bo_row[:, :], b_out.unsqueeze(0)).then_inc(loaded, 16)
                sp.dma_start(lnw[:, :], ln_w.unsqueeze(0).broadcast_to([P, C])).then_inc(loaded, 16)
                with sp.Fori(0, NT) as i:
                    sp.wait_ge(out_ready, i)
                    sp.dma_start(xr[:, :, :], xv[i]).then_inc(xin, 16)
                    sp.wait_ge(out_ready, i + 1)
                    sp.dma_start(ov[i], out[:, :, :]).then_inc(stored, 16)
                sp.wait_ge(stored, 16 * NT)

            @block.gpsimd
            def _(pool):
                pool.memset(half[:, :], -0.5).then_inc(made, 1)
                pool.wait_ge(made, 1)
                with pool.Fori(0, NT) as i:
                    pool.wait_ge(turned, i)
                    pool.tensor_copy(us[:, :, :], u[:, bass.ds(i * R, R), :]).then_inc(staged, 1)
                    pool.wait_ge(ve_ready, i + 1)
                    pool.tensor_tensor(rstd[:, :], ve[:, :], half[:, :], ALU.pow).then_inc(rstd_ready, 1)

            @block.tensor
            def _(pe):
                pe.wait_ge(loaded, 32)
                with pe.Fori(0, NT) as i:
                    pe.wait_ge(staged, i + 1)
                    for r in range(R):
                        last = pe.transpose(ps_t[:, r * W:(r + 1) * W], us[:, r, :], ident[:, :])
                    last.then_inc(turned, 1)
                    pe.wait_ge(uT_ready, i + 1)
                    pe.wait_ge(shifted, i)
                    for r in range(R):
                        last = pe.matmul(ps_q[:, r * C:(r + 1) * C], uTs[:, r * W:(r + 1) * W], wT[:, 0, :],
                                         start=True, stop=True)
                    last.then_inc(q_done, 1)
                    pe.wait_ge(q_ready, i + 1)
                    for r in range(R):
                        last = pe.transpose(ps_y[:, r * W:(r + 1) * W],
                                            q[:, r * H:(r + 1) * H, :].rearrange("p h d -> p (h d)"), ident[:, :])
                    last.then_inc(flipped, 1)
                    pe.wait_ge(qT_ready, i + 1)
                    for r in range(R):
                        cols = slice(r * C, (r + 1) * C)
                        pe.matmul(ps_o[:, cols], qT[:, r * W:(r + 1) * W], g[:, :], start=True, stop=False)
                        last = pe.matmul(ps_o[:, cols], ones1[:, :], bo_row[:, :], start=False, stop=True)
                    last.then_inc(o_done, 1)

            @block.scalar
            def _(act):
                with act.Fori(0, NT) as i:
                    act.wait_ge(turned, i + 1)
                    act.wait_ge(q_done, i)
                    act.copy(uTs[:, :], ps_t[:, :]).then_inc(uT_ready, 1)
                    act.wait_ge(shifted, i + 1)
                    act.activation(q[:, :, :], q[:, :, :], ACT.Exp).then_inc(ex_ready, 1)
                    act.wait_ge(flipped, i + 1)
                    act.copy(qT[:, :], ps_y[:, :]).then_inc(qT_ready, 1)

            @block.vector
            def _(dve):
                step = Chain(dve, dch)
                TT = dve.tensor_tensor
                dve.wait_ge(loaded, 32)
                with step.loop(NT, 2 + 3 + 1 + 2 * R + 1 + R + 2) as i:
                    dve.wait_ge(q_done, i + 1)
                    qv = ps_q[:, :].rearrange("p (h d) -> p h d", d=D)
                    step(dve.tensor_reduce(mx[:, :], qv, AX.X, ALU.max))
                    step(TT(q[:, :, :], qv, mx[:, :].unsqueeze(2).broadcast_to([P, R * H, D]), ALU.subtract))
                    dve.sem_inc(shifted, 1)
                    dve.wait_ge(ex_ready, i + 1)
                    step(dve.tensor_reduce(den[:, :], q[:, :, :], AX.X, ALU.add))
                    step(dve.reciprocal(den[:, :], den[:, :]))
                    step(TT(q[:, :, :], q[:, :, :], den[:, :].unsqueeze(2).broadcast_to([P, R * H, D]), ALU.mult))
                    dve.sem_inc(q_ready, 1)
                    dve.wait_ge(o_done, i + 1)
                    step(dve.tensor_copy(z[:, :, :], ps_o[:, :].rearrange("p (r c) -> p r c", r=R)))
                    for r in range(R):
                        step.mark(dve.bn_stats(st[:, r, :], z[:, r, :]))
                    step.join()
                    dve.sem_inc(tick, 1)
                    for r in range(R):
                        step.mark(dve.bn_aggr(mv[:, r, :], st[:, r, :]))
                    step.join()
                    step(dve.tensor_scalar(ve[:, :], mv[:, :, 1], eps, None, ALU.add))
                    dve.sem_inc(ve_ready, 1)
                    dve.wait_ge(rstd_ready, i + 1)
                    dve.wait_ge(stored, 16 * i)
                    for r in range(R):
                        step.mark(dve.tensor_scalar(out[:, r, :], z[:, r, :], mv[:, r, 0:1], rstd[:, r:r + 1],
                                                    ALU.subtract, ALU.mult))
                    step.join()
                    step(TT(out[:, :, :], out[:, :, :], lnw[:, :].unsqueeze(1).broadcast_to([P, R, C]), ALU.mult))
                    dve.wait_ge(xin, 16 * (i + 1))
                    step(TT(out[:, :, :], out[:, :, :], xr[:, :, :], ALU.add))
                    dve.sem_inc(out_ready, 1)


def recurrent_network(nc, x5, Wm, Vm, gamma, beta, y_out, tag="rnn", eps=1e-5):
    L = T * W
    S = 64
    CH = L // S
    N = B * CH
    G = 2
    NG = N // G
    WARM = 32
    TOL = 2.0 ** -19
    R = 4
    HALVES = W // S
    NT = BT // R
    with ExitStack() as ctx:
        s = Scope(nc, ctx, tag)
        uT = s.sb("uT", [P, S, N])
        ident = s.sb("ident", [P, P])
        wT = s.sb("wT", [P, C])
        wn = s.sb("wn", [P, C])
        wnT, vT = s.sb("wnT", [P, C]), s.sb("vT", [P, C])
        shift = s.sb("shift", [P, 1])
        with ExitStack() as cu:
            u = Scope(nc, cu, tag + "u").sb("u", [P, BT, C])
            normalised_tokens(nc, x5, u, tag + "n")
            s2 = Scope(nc, cu, tag + "a")
            wl = s2.sb("wl", [P, 2, C])
            gb = s2.sb("gb", [P, 2])
            us = [s2.sb(f"us{j}", [P, R, C]) for j in range(2)]
            uTs = [s2.sb(f"uTs{j}", [P, R * W]) for j in range(2)]
            st = s2.sb("st", [P, NT, 6])
            mv = s2.sb("mv", [P, 2])
            ve, rstd, half, a = (s2.sb(n, [P, 1]) for n in ("ve", "rstd", "half", "a"))
            ps_w = s2.ps("ps_w")
            ps_t = [s2.ps(f"ps_t{j}") for j in range(2)]
            ps_x = [s2.ps(f"ps_x{j}") for j in range(2)]
            (loaded, made, w_done, w_ready, staged, turned, uT_ready, placed, x_done, x_read, ve_ready,
             rstd_ready, wn_ready, wn_done, dch, pch, tick) = (s2.sem(n) for n in (
                 "loaded", "made", "w_done", "w_ready", "staged", "turned", "uT_ready", "placed", "x_done",
                 "x_read", "ve_ready", "rstd_ready", "wn_ready", "wn_done", "dch", "pch", "tick"))
            block = cu.enter_context(nc.Block())

            @block.sync
            def _(sp):
                sp.dma_start(wl[:, 0, :], Wm).then_inc(loaded, 16)
                sp.dma_start(wl[:, 1, :], Vm).then_inc(loaded, 16)
                sp.dma_start(gb[:, 0:1], gamma.unsqueeze(1)).then_inc(loaded, 16)
                sp.dma_start(gb[:, 1:2], beta.unsqueeze(1)).then_inc(loaded, 16)

            @block.gpsimd
            def _(pool):
                step = Chain(pool, pch)
                fill_identity(pool, step, ident)
                step(pool.memset(half[:, :], -0.5))
                pool.sem_inc(made, 1)
                with pool.Fori(0, NT // 2) as i:
                    for j in range(2):
                        pool.wait_ge(turned, 2 * i)
                        pool.tensor_copy(us[j][:, :, :], u[:, bass.ds(i * 2 * R + j * R, R), :]).then_inc(staged, 1)
                pool.wait_ge(ve_ready, 1)
                pool.tensor_tensor(rstd[:, :], ve[:, :], half[:, :], ALU.pow).then_inc(rstd_ready, 1)

            @block.tensor
            def _(pe):
                pe.wait_ge(loaded, 64)
                pe.wait_ge(made, 1)
                for j in range(2):
                    last = pe.transpose(ps_w[:, j * C:(j + 1) * C], wl[:, j, :], ident[:, :])
                last.then_inc(w_done, 1)
                pe.wait_ge(w_ready, 1)
                with pe.Fori(0, NT // 2) as i:
                    for j in range(2):
                        pe.wait_ge(staged, 2 * i + j + 1)
                        pe.wait_ge(placed, 2 * i)
                        for r in range(R):
                            last = pe.transpose(ps_t[j][:, r * W:(r + 1) * W], us[j][:, r, :], ident[:, :])
                        last.then_inc(turned, 1)
                        pe.wait_ge(uT_ready, 2 * i + j + 1)
                        pe.wait_ge(x_read, 2 * i)
                        pe.matmul(ps_x[j][:, :], wT[:, :], uTs[j][:, :], start=True, stop=True).then_inc(x_done, 1)
                pe.wait_ge(wn_ready, 1)
                pe.transpose(ps_w[:, 2 * C:3 * C], wn[:, :], ident[:, :]).then_inc(wn_done, 1)

            @block.scalar
            def _(act):
                act.wait_ge(w_done, 1)
                act.copy(wT[:, :], ps_w[:, 0:C]).then_inc(tick, 1)
                act.copy(vT[:, :], ps_w[:, C:2 * C]).then_inc(w_ready, 1)
                with act.Fori(0, NT // 2) as i:
                    for j in range(2):
                        act.wait_ge(turned, 2 * i + j + 1)
                        act.wait_ge(x_done, 2 * i)
                        act.copy(uTs[j][:, :], ps_t[j][:, :]).then_inc(uT_ready, 1)
                        col = bass.ds(i * 2 * R * HALVES + j * R * HALVES, R * HALVES)
                        act.copy(uT[:, :, col], ps_t[j][:, :].rearrange("p (q s) -> p s q", s=S)).then_inc(placed, 1)
                act.wait_ge(wn_done, 1)
                act.copy(wnT[:, :], ps_w[:, 2 * C:3 * C]).then_inc(tick, 1)

            @block.vector
            def _(dve):
                step = Chain(dve, dch)
                with dve.Fori(0, NT // 2) as i:
                    for j in range(2):
                        dve.wait_ge(x_done, 2 * i + j + 1)
                        dve.bn_stats(st[:, bass.ds(i * 2 + j, 1), :].rearrange("p a b -> p (a b)"), ps_x[j][:, :]).then_inc(x_read, 1)
                dve.wait_ge(x_read, NT)
                step(dve.bn_aggr(mv[:, :], st[:, :, :].rearrange("p n k -> p (n k)")))
                step(dve.tensor_scalar(ve[:, :], mv[:, 1:2], eps, None, ALU.add))
                dve.sem_inc(ve_ready, 1)
                dve.wait_ge(rstd_ready, 1)
                step(dve.tensor_tensor(a[:, :], rstd[:, :], gb[:, 0:1], ALU.mult))
                step(dve.tensor_scalar(wn[:, :], wl[:, 0, :], a[:, 0:1], None, ALU.mult))
                dve.sem_inc(wn_ready, 1)
                step(dve.tensor_tensor(shift[:, :], mv[:, 0:1], a[:, :], ALU.mult))
                step(dve.tensor_tensor(shift[:, :], gb[:, 1:2], shift[:, :], ALU.subtract))

        y = s.sb("y", [P, S + 1, N])
        ys = s.sb("ys", [P, 2, N])
        ends = s.sb("ends", [P, B, CH])
        diff = s.sb("diff", [P, N])
        worst = s.sb("worst", [P, 1])
        row = s.sb("row", [1, P])
        flag = s.sb("flag", [1, 1])
        flag_i = s.sb("flag_i", [1, 1], mybir.dt.int32)

        def pe_steps(pe, ps, states, first, steps, z_ready, y_ready):
            with pe.Fori(0, steps // 2) as i:
                for p in range(2):
                    for g in range(G):
                        cols = slice(g * NG, (g + 1) * NG)
                        inp = uT[:, bass.ds(i * 2 + (first + p), 1), cols].rearrange("p a n -> p (a n)")
                        prev = states(i, p)[0][:, :, cols].rearrange("p a n -> p (a n)")
                        dst = ps[p * G + g][:, 0:NG]
                        pe.matmul(dst, wnT[:, :], inp, start=True, stop=False)
                        pe.wait_ge(y_ready[g], i * 2 + p)
                        pe.matmul(dst, vT[:, :], prev, start=False, stop=True).then_inc(z_ready[g], 1)

        def act_steps(act, ps, states, steps, z_ready, y_ready):
            with act.Fori(0, steps // 2) as i:
                for p in range(2):
                    for g in range(G):
                        cols = slice(g * NG, (g + 1) * NG)
                        nxt = states(i, p)[1][:, :, cols].rearrange("p a n -> p (a n)")
                        act.wait_ge(z_ready[g], i * 2 + p + 1)
                        act.activation(nxt, ps[p * G + g][:, 0:NG], ACT.Sigmoid, bias=shift[:, 0:1]).then_inc(y_ready[g], 1)

        def in_y(i, p):
            return y[:, bass.ds(i * 2 + p, 1), :], y[:, bass.ds(i * 2 + p + 1, 1), :]

        def in_ys(i, p):
            return ys[:, p:p + 1, :], ys[:, 1 - p:2 - p, :]

        def block_of(name, states, first, steps, before, after):
            with ExitStack() as c2:
                s2 = Scope(nc, c2, f"{tag}{name}")
                ps = [s2.ps(f"ps{j}") for j in range(2 * G)]
                z_ready = [s2.sem(f"z_ready{g}") for g in range(G)]
                y_ready = [s2.sem(f"y_ready{g}") for g in range(G)]
                begun, dch = s2.sem("begun"), s2.sem("dch")
                block = c2.enter_context(nc.Block())

                @block.tensor
                def _(pe):
                    pe.wait_ge(begun, 1)
                    pe_steps(pe, ps, states, first, steps, z_ready, y_ready)

                @block.scalar
                def _(act):
                    act_steps(act, ps, states, steps, z_ready, y_ready)

                @block.vector
                def _(dve):
                    step = Chain(dve, dch)
                    before(dve, step)
                    dve.sem_inc(begun, 1)
                    for g in range(G):
                        dve.wait_ge(y_ready[g], steps)
                    after(dve, step)

        def starts_from(src):
            def do(dve, step):
                first = y[:, 0, :].rearrange("p (b k) -> p b k", b=B)
                step.mark(dve.memset(first[:, :, 0:1], 0.0))
                step.mark(dve.tensor_copy(first[:, :, 1:CH], src[:, :, 0:CH - 1]))
                step.join()
            return do

        def measure(dve, step):
            first = y[:, 0, :].rearrange("p (b k) -> p b k", b=B)
            d = diff[:, :].rearrange("p (b k) -> p b k", b=B)
            step(dve.tensor_copy(ends[:, :, :], y[:, S, :].rearrange("p (b k) -> p b k", b=B)))
            step(dve.memset(diff[:, :], 0.0))
            step(dve.tensor_tensor(d[:, :, 1:CH], ends[:, :, 0:CH - 1], first[:, :, 1:CH], ALU.subtract))
            step(dve.tensor_reduce(worst[:, :], diff[:, :], AX.X, ALU.max, apply_absolute_value=True))

        nothing = lambda dve, step: None
        block_of("w", in_ys, S - WARM, WARM, lambda dve, step: step(dve.memset(ys[:, 0, :], 0.0)), nothing)
        block_of("m", in_y, 0, S, starts_from(ys[:, 0, :].rearrange("p (b k) -> p b k", b=B)), measure)

        with ExitStack() as c2:
            s2 = Scope(nc, c2, tag + "f")
            ps = s2.ps("ps")
            turned, copied, dch = s2.sem("turned"), s2.sem("copied"), s2.sem("dch")
            block = c2.enter_context(nc.Block())

            @block.tensor
            def _(pe):
                pe.transpose(ps[0:1, 0:P], worst[:, :], ident[:, :]).then_inc(turned, 1)

            @block.vector
            def _(dve):
                step = Chain(dve, dch)
                dve.wait_ge(turned, 1)
                step(dve.tensor_reduce(flag[:, :], ps[0:1, 0:P], AX.X, ALU.max))
                step(dve.tensor_scalar(flag_i[:, :], flag[:, :], TOL, None, ALU.is_gt))

        again = nc.values_load(flag_i[0:1, 0:1], min_val=0, max_val=1)
        with nc.If(again > 0):
            with nc.Fori(0, CH - 1):
                block_of("r", in_y, 0, S, starts_from(ends), measure)

        with ExitStack() as c2:
            s2 = Scope(nc, c2, tag + "o")
            xr = [s2.sb(f"xr{j}", [P, R, C]) for j in range(2)]
            out = [s2.sb(f"out{j}", [P, R, C]) for j in range(2)]
            yst = [s2.sb(f"yst{j}", [P, R * W]) for j in range(2)]
            ps = [s2.ps(f"ps{j}") for j in range(2)]
            xin = [s2.sem(f"xin{j}") for j in range(2)]
            staged, turned, added, stored = (s2.sem(n) for n in ("staged", "turned", "added", "stored"))
            block = c2.enter_context(nc.Block())
            xv = x5.rearrange("b t w c -> (b t) w c").rearrange("(i j r) w c -> i j w r c", j=2, r=R)
            ov = y_out.rearrange("b t w c -> (b t) w c").rearrange("(i j r) w c -> i j w r c", j=2, r=R)

            @block.sync
            def _(sp):
                with sp.Fori(0, NT // 2) as i:
                    for j in range(2):
                        sp.wait_ge(added, 2 * i)
                        sp.dma_start(xr[j][:, :, :], xv[i, j]).then_inc(xin[j], 16)

            @block.gpsimd
            def _(pool):
                with pool.Fori(0, NT // 2) as i:
                    for j in range(2):
                        pool.wait_ge(turned, 2 * i)
                        col = bass.ds(i * 2 * R * HALVES + j * R * HALVES, R * HALVES)
                        pool.tensor_copy(yst[j][:, :].rearrange("p (q s) -> p s q", s=S), y[:, 1:S + 1, col]
                                         ).then_inc(staged, 1)

            @block.tensor
            def _(pe):
                with pe.Fori(0, NT // 2) as i:
                    for j in range(2):
                        pe.wait_ge(staged, 2 * i + j + 1)
                        pe.wait_ge(added, 2 * i)
                        for r in range(R):
                            last = pe.transpose(ps[j][:, r * C:(r + 1) * C], yst[j][:, r * W:(r + 1) * W], ident[:, :])
                        last.then_inc(turned, 1)

            @block.vector
            def _(dve):
                with dve.Fori(0, NT // 2) as i:
                    for j in range(2):
                        dve.wait_ge(turned, 2 * i + j + 1)
                        dve.wait_ge(xin[j], 16 * i + 16)
                        dve.wait_ge(stored, 32 * i)
                        dve.tensor_tensor(out[j][:, :, :], xr[j][:, :, :],
                                          ps[j][:, :].rearrange("p (r c) -> p r c", r=R), ALU.add).then_inc(added, 1)

            @block.scalar
            def _(act):
                with act.Fori(0, NT // 2) as i:
                    for j in range(2):
                        act.wait_ge(added, 2 * i + j + 1)
                        act.dma_start(ov[i, j], out[j][:, :, :]).then_inc(stored, 16)
                act.wait_ge(stored, 16 * NT)


def hybrid_stack(nc, d, out):
    shape = (B, T, W, C)

    def dram(name, shape):
        return nc.dram_tensor(name, shape, f32, kind="Internal").ap()

    def layer(prefix, *names):
        return [d[f"{prefix}_{n}"] for n in names]

    tabs = inline_tables(nc)
    x1, x2, x3, x4, x5 = (dram(f"x{n}", shape) for n in range(1, 6))

    h0 = dram("h0", (BT, W, C))
    with nc.sbuf_tensor("hg0", [P, BT, C], f32) as hg:
        group_norm(nc, d["x"], hg, "gn0")
        graph_attention(nc, hg, *layer("L0_conv", "adj", "Wq", "Wk", "Wv", "Wo", "bo", "ns_g", "ns_b"), h0)
    mamba(nc, h0, d["x"], *layer("L0_conv", "in_proj", "conv_w", "conv_b", "x_proj", "dt_w", "dt_b", "A_log", "Dp",
                                 "out_w", "out_b", "nt_g", "nt_b"), x1)

    wts = {n[len("L1_conv_"):]: v for n, v in d.items() if n.startswith("L1_conv_")}
    tok, tnd, mix = (dram(n, (BT, W, C)) for n in ("tokens", "tokens_normalised", "mix"))
    gram = dram("gram", (BT, BT))
    prob = dram("prob", (NH, B, T, T))
    wd = dram("mode_weights", (NH, NKY, 2, NKX))
    with ExitStack() as ctx:
        def sb(name, shape):
            return ctx.enter_context(nc.sbuf_tensor(name, shape, f32))

        spec = sb("spec", [2 * 32, BT, NKY])
        const = sb("const", [P, 1])
        xh = sb("xh", [P, NKY, 2, NKX])
        with nc.sbuf_tensor("hg1", [P, BT, C], f32) as hg:
            group_norm(nc, x1, hg, "gn1")
            token_images(nc, hg, wts["norm1_g"], wts["norm1_b"], tok, tnd)
            token_spectra(nc, hg, tabs, xh, gram)
        pt = sb("pt", [P, NH, BT])
        mt = sb("mt", [P, BT])
        token_attention(nc, xh, gram, tabs, wts, prob, pt, mt)
        attended_spectrum(nc, xh, pt, wts, wd, spec, const)
        mixed_images(nc, tnd, mt, mix)
        token_mixer(nc, spec, const, mix, tok, x1, wts, tabs, x2)

    linear_attention(nc, x2, *layer("L2_attn", "Wq", "bq", "Wk", "bk", "Wv", "bv", "Wo", "bo"), x3)
    routed_experts(nc, x3, *layer("L2_ffn", "gate_w", "gate_b", "weight1", "weight2"), x4)

    softmax_attention(nc, x4, *layer("L3_attn", "w_in", "w_out", "b_out", "ln_w"), x5)
    recurrent_network(nc, x5, *layer("L3_ffn", "W", "V", "gamma", "beta"), out)


def kernel(**inputs):
    import concourse.bacc as bacc
    from concourse.bass_utils import run_bass_kernel_spmd

    nc = bacc.Bacc("TRN2", target_bir_lowering=False, num_devices=1)
    arrays, d = {}, {}
    for name, a in inputs.items():
        a = np.ascontiguousarray(a)
        arrays[f"in_{name}"] = a
        d[name] = nc.dram_tensor(f"in_{name}", a.shape, mybir.dt.from_np(a.dtype), kind="ExternalInput").ap()
    out = nc.dram_tensor("out_0", (B, T, W, C), f32, kind="ExternalOutput").ap()
    hybrid_stack(nc, d, out)
    r = run_bass_kernel_spmd(nc, [arrays], core_ids=[0])
    return r.results[0]["out_0"]
```

```python
import math
from contextlib import ExitStack, contextmanager

import concourse.bass as bass
import numpy as np
from concourse import mybir

f32 = mybir.dt.float32
bf16 = mybir.dt.bfloat16
u8 = mybir.dt.uint8
ALU = mybir.AluOpType
ACT = mybir.ActivationFunctionType
AX = mybir.AxisListType

P = 128
B, T, W, C = 4, 32, 128, 128
BT = B * T


class Chain:

    def __init__(self, eng, sem):
        self.eng, self.sem, self.base, self.k = eng, sem, 0, 0

    def __call__(self, ins):
        ins.then_inc(self.sem, 1)
        self.k += 1
        self.eng.wait_ge(self.sem, self.base + self.k)

    def mark(self, ins):
        ins.then_inc(self.sem, 1)
        self.k += 1
        return self.k

    def wait(self, k):
        self.eng.wait_ge(self.sem, self.base + k)

    def join(self):
        self.eng.wait_ge(self.sem, self.base + self.k)

    @contextmanager
    def loop(self, turns, per):
        base, k = self.base, self.k
        with self.eng.Fori(0, turns) as i:
            self.base, self.k = base + k + i * per, 0
            yield i
            assert self.k == per, (self.k, per)
        self.base, self.k = base, k + turns * per


class Scope:

    def __init__(self, nc, ctx, tag):
        self.nc, self.ctx, self.tag, self.sems = nc, ctx, tag, []
        ctx.callback(self.clear)

    def sb(self, name, shape, dt=f32):
        return self.ctx.enter_context(self.nc.sbuf_tensor(f"{self.tag}_{name}", shape, dt))

    def ps(self, name, shape=(P, 512), dt=f32):
        return self.ctx.enter_context(self.nc.psum_tensor(f"{self.tag}_{name}", list(shape), dt))

    def sem(self, name):
        self.sems.append(self.nc.alloc_semaphore(f"{self.tag}_{name}"))
        return self.sems[-1]

    def clear(self):
        if self.sems:
            with self.nc.Block() as block:
                @block.sync
                def _(sp):
                    for q in self.sems:
                        sp.sem_clear(q)
            for q in self.sems:
                self.nc.release_semaphore(q)


def fill_identity(pool, chain, ident):
    chain(pool.memset(ident[:, :], 0.0))
    chain(pool.affine_select(out=ident[:, :], in_=ident[:, :], compare_op=ALU.not_equal, fill=1.0,
                             base=0, pattern=[[-1, ident.shape[1]]], channel_multiplier=1))


def group_norm(nc, src, hg, tag, G=32, eps=1e-5):
    J = C // G
    N = T * W * J
    with ExitStack() as ctx:
        s = Scope(nc, ctx, tag)
        xb = s.sb("xb", [P, 2, T * C])
        sq = s.sb("sq", [P, T * C])
        ones = s.sb("ones", [P, P])
        sums = s.sb("sums", [P, 2, G])
        var = s.sb("var", [P, G])
        rstd = s.sb("rstd", [P, G])
        half = s.sb("half", [P, G])
        ps = [s.ps(f"ps{j}") for j in range(2)]
        loaded, squared, summed, var_done, rstd_done, normed, ready = (
            s.sem(n) for n in ("loaded", "squared", "summed", "var_done", "rstd_done", "normed", "ready"))
        dch = s.sem("dch")
        block = ctx.enter_context(nc.Block())

        @block.sync
        def _(sp):
            for b in range(B):
                if b >= 2:
                    sp.wait_ge(normed, b - 1)
                sp.dma_start(xb[:, b % 2, :].rearrange("w (t c) -> w t c", t=T),
                             src[b].rearrange("t w c -> w t c")).then_inc(loaded, 16)
                sp.wait_ge(loaded, 16 * b + 16)

        @block.scalar
        def _(act):
            for b in range(B):
                act.wait_ge(loaded, 16 * b + 16)
                if b >= 1:
                    act.wait_ge(summed, b)
                act.activation(sq[:, :], xb[:, b % 2, :], ACT.Square).then_inc(squared, 1)

        @block.tensor
        def _(pe):
            pe.wait_ge(ready, 1)
            for b in range(B):
                pe.wait_ge(loaded, 16 * b + 16)
                if b >= 1:
                    pe.wait_ge(var_done, b)
                for j in range(8):
                    pe.matmul(ps[0][:, :], ones[:, :], xb[:, b % 2, 512 * j:512 * j + 512],
                              start=(j == 0), stop=(j == 7))
                pe.wait_ge(squared, b + 1)
                for j in range(8):
                    last = pe.matmul(ps[1][:, :], ones[:, :], sq[:, 512 * j:512 * j + 512],
                                     start=(j == 0), stop=(j == 7))
                last.then_inc(summed, 1)

        @block.gpsimd
        def _(pool):
            pool.memset(ones[:, :], 1.0 / N).then_inc(ready, 1)
            pool.memset(half[:, :], -0.5).then_inc(rstd_done, 1)
            pool.wait_ge(rstd_done, 1)
            for b in range(B):
                pool.wait_ge(var_done, b + 1)
                pool.tensor_tensor(rstd[:, :], var[:, :], half[:, :], ALU.pow).then_inc(rstd_done, 1)

        @block.vector
        def _(dve):
            step = Chain(dve, dch)
            for b in range(B):
                dve.wait_ge(summed, b + 1)
                for j in range(2):
                    step.mark(dve.tensor_reduce(
                        sums[:, j, :], ps[j][:, :].rearrange("p (q g j) -> p g q j", q=4, g=G), AX.XY, ALU.add))
                step.join()
                step(dve.tensor_tensor(var[:, :], sums[:, 0, :], sums[:, 0, :], ALU.mult))
                step(dve.scalar_tensor_tensor(out=var[:, :], in0=sums[:, 1, :], scalar=eps, in1=var[:, :],
                                              op0=ALU.add, op1=ALU.subtract))
                dve.sem_inc(var_done, 1)
                dve.wait_ge(rstd_done, b + 2)
                xv = xb[:, b % 2, :].rearrange("p (t g j) -> p t g j", t=T, g=G)
                hv = hg[:, b * T:(b + 1) * T, :].rearrange("p t (g j) -> p t g j", g=G)
                mean = sums[:, 0, :].unsqueeze(1).unsqueeze(3).broadcast_to([P, T, G, J])
                scale = rstd[:, :].unsqueeze(1).unsqueeze(3).broadcast_to([P, T, G, J])
                step(dve.tensor_tensor(hv, xv, mean, ALU.subtract))
                dve.tensor_tensor(hv, hv, scale, ALU.mult).then_inc(normed, 1)
                dve.wait_ge(normed, b + 1)


def graph_attention(nc, hg, adj, Wq, Wk, Wv, Wo, bo, gain, shift, h0, tag="gat", eps=1e-5):
    R, H = 4, 4
    D = C // H
    TURNS = BT // R
    BIG = 1e9 * math.sqrt(D)
    with ExitStack() as ctx:
        s = Scope(nc, ctx, tag)
        wq, wk, wv, wo = (s.sb(n, [P, C]) for n in ("wq", "wk", "wv", "wo"))
        ident = s.sb("ident", [P, P])
        ones1 = s.sb("ones1", [1, P])
        bo_row = s.sb("bo_row", [1, C])
        adj_sb = s.sb("adj", [P, P])
        keep = s.sb("keep", [P, P])
        lift = s.sb("lift", [P, P])
        gain_b = s.sb("gain", [P, C])
        shift_b = s.sb("shift", [P, C])
        hl = s.sb("hl", [P, R, C])
        hT = s.sb("hT", [P, R * W])
        qT = s.sb("qT", [P, R * W])
        kT = s.sb("kT", [P, R * W])
        vt = s.sb("vt", [P, R, C])
        sc = s.sb("sc", [P, 2, H, W])
        mx = s.sb("mx", [P, 2, H])
        ex = s.sb("ex", [P, 2, H, W])
        den = s.sb("den", [P, 2, H])
        pT = s.sb("pT", [P, 2, H, W])
        oT = s.sb("oT", [P, R * W])
        z = s.sb("z", [P, R, C])
        out = s.sb("out", [P, R, C])
        st = s.sb("st", [P, R, 6])
        mv = s.sb("mv", [P, R, 2])
        ve = s.sb("ve", [P, R])
        rstd = s.sb("rstd", [P, R])
        half = s.sb("half", [P, R])
        ps_h, ps_q, ps_k, ps_v = (s.ps(n) for n in ("ps_h", "ps_q", "ps_k", "ps_v"))
        ps_s = [s.ps(f"ps_s{j}") for j in range(2)]
        ps_p = [s.ps(f"ps_p{j}") for j in range(2)]
        ps_o, ps_z = ps_h, ps_v

        (loaded, made, staged, turned, hT_ready, projected, q_ready, k_ready, v_ready, scored, masked,
         exped, normed, flipped, pT_ready, mixed, oT_ready, outed, z_ready, ve_ready, rstd_ready,
         out_ready, stored, dch, pch) = (
            s.sem(n) for n in (
                "loaded", "made", "staged", "turned", "hT_ready", "projected", "q_ready", "k_ready",
                "v_ready", "scored", "masked", "exped", "normed", "flipped", "pT_ready", "mixed",
                "oT_ready", "outed", "z_ready", "ve_ready", "rstd_ready", "out_ready", "stored", "dch", "pch"))
        tick = s.sem("tick")
        LOADS = 8
        block = ctx.enter_context(nc.Block())

        @block.sync
        def _(sp):
            for dst, src in ((wq, Wq), (wk, Wk), (wv, Wv), (wo, Wo), (adj_sb, adj)):
                sp.dma_start(dst[:, :], src).then_inc(loaded, 16)
            sp.dma_start(bo_row[:, :], bo.unsqueeze(0)).then_inc(loaded, 16)
            sp.dma_start(gain_b[:, :], gain.unsqueeze(0).broadcast_to([P, C])).then_inc(loaded, 16)
            sp.dma_start(shift_b[:, :], shift.unsqueeze(0).broadcast_to([P, C])).then_inc(loaded, 16)
            rows = h0.rearrange("(i r) w c -> i w r c", r=R)
            with sp.Fori(0, TURNS) as i:
                sp.wait_ge(out_ready, i + 1)
                sp.dma_start(rows[i], out[:, :, :]).then_inc(stored, 16)
            sp.wait_ge(stored, 16 * TURNS)

        @block.gpsimd
        def _(pool):
            step = Chain(pool, pch)
            fill_identity(pool, step, ident)
            step(pool.memset(half[:, :], -0.5))
            step(pool.memset(ones1[:, :], 1.0))
            pool.sem_inc(made, 1)
            with pool.Fori(0, TURNS) as i:
                pool.wait_ge(turned, i)
                pool.tensor_copy(hl[:, :, :], hg[:, bass.ds(i * R, R), :]).then_inc(staged, 1)
                pool.wait_ge(ve_ready, i + 1)
                pool.tensor_tensor(rstd[:, :], ve[:, :], half[:, :], ALU.pow).then_inc(rstd_ready, 1)

        @block.tensor
        def _(pe):
            pe.wait_ge(loaded, 16 * LOADS)
            pe.wait_ge(made, 1)
            with pe.Fori(0, TURNS) as i:
                pe.wait_ge(staged, i + 1)
                pe.wait_ge(oT_ready, i)
                for r in range(R):
                    last = pe.transpose(ps_h[:, r * W:(r + 1) * W], hl[:, r, :], ident[:, :])
                last.then_inc(turned, 1)
                pe.wait_ge(hT_ready, i + 1)
                pe.matmul(ps_q[:, :], wq[:, :], hT[:, :], start=True, stop=True)
                pe.matmul(ps_k[:, :], wk[:, :], hT[:, :], start=True, stop=True)
                pe.wait_ge(z_ready, i)
                for r in range(R):
                    last = pe.matmul(ps_v[:, r * C:(r + 1) * C], hT[:, r * W:(r + 1) * W], wv[:, :],
                                     start=True, stop=True)
                last.then_inc(projected, 1)

                def scores(h):
                    d = slice(h * D, (h + 1) * D)
                    for r in range(R):
                        last = pe.matmul(ps_s[h % 2][:, r * W:(r + 1) * W], qT[d, r * W:(r + 1) * W],
                                         kT[d, r * W:(r + 1) * W], start=True, stop=True,
                                         tile_position=(h * D, 0))
                    last.then_inc(scored, 1)

                pe.wait_ge(q_ready, i + 1)
                pe.wait_ge(k_ready, i + 1)
                scores(0)
                scores(1)
                for h in range(H):
                    pe.wait_ge(normed, i * H + h + 1)
                    for r in range(R):
                        last = pe.transpose(ps_p[h % 2][:, r * W:(r + 1) * W], ex[:, h % 2, r, :], ident[:, :])
                    last.then_inc(flipped, 1)
                    if h + 2 < H:
                        scores(h + 2)
                    pe.wait_ge(pT_ready, i * H + h + 1)
                    if h == 0:
                        pe.wait_ge(v_ready, i + 1)
                    d = slice(h * D, (h + 1) * D)
                    for r in range(R):
                        last = pe.matmul(ps_o[d, r * W:(r + 1) * W], vt[:, r, d], pT[:, h % 2, r, :],
                                         start=True, stop=True, tile_position=(0, h * D))
                last.then_inc(mixed, 1)
                pe.wait_ge(oT_ready, i + 1)
                for r in range(R):
                    pe.matmul(ps_z[:, r * C:(r + 1) * C], oT[:, r * W:(r + 1) * W], wo[:, :],
                              start=True, stop=False)
                    last = pe.matmul(ps_z[:, r * C:(r + 1) * C], ones1[:, :], bo_row[:, :],
                                     start=False, stop=True)
                last.then_inc(outed, 1)

        @block.scalar
        def _(act):
            with act.Fori(0, TURNS) as i:
                act.wait_ge(turned, i + 1)
                act.wait_ge(projected, i)
                act.copy(hT[:, :], ps_h[:, :]).then_inc(hT_ready, 1)
                act.wait_ge(projected, i + 1)
                act.copy(qT[:, :], ps_q[:, :]).then_inc(q_ready, 1)
                act.copy(vt[:, :, :], ps_v[:, :].rearrange("p (r c) -> p r c", r=R)).then_inc(v_ready, 1)
                for r in range(R):
                    act.wait_ge(masked, i * R + r + 1)
                    act.wait_ge(flipped, i * R + r - 1) if r >= 2 else act.wait_ge(mixed, i)
                    act.activation(ex[:, r % 2, :, :], sc[:, r % 2, :, :], ACT.Exp,
                                   scale=1.0 / math.sqrt(D)).then_inc(exped, 1)
                    act.wait_ge(flipped, i * R + r + 1)
                    act.copy(pT[:, r % 2, :, :], ps_p[r % 2][:, :].rearrange("p (h w) -> p h w", h=H)
                             ).then_inc(pT_ready, 1)
                act.wait_ge(mixed, i + 1)
                act.copy(oT[:, :], ps_o[:, :]).then_inc(oT_ready, 1)

        @block.vector
        def _(dve):
            step = Chain(dve, dch)
            dve.wait_ge(loaded, 16 * LOADS)
            dve.wait_ge(made, 1)
            step(dve.tensor_scalar(keep[:, :], adj_sb[:, :], 0.0, None, ALU.not_equal))
            step(dve.tensor_scalar(lift[:, :], keep[:, :], 1.0, BIG, ALU.subtract, ALU.mult))
            keep_b = keep[:, :].unsqueeze(1).broadcast_to([P, H, W])
            lift_b = lift[:, :].unsqueeze(1).broadcast_to([P, H, W])

            def mask(i, r):
                q = r % 2
                dve.wait_ge(scored, i * R + r + 1)
                step(dve.tensor_tensor(sc[:, q, :, :], ps_s[q][:, :].rearrange("p (h w) -> p h w", h=H),
                                       keep_b, ALU.mult))
                step(dve.tensor_tensor(sc[:, q, :, :], sc[:, q, :, :], lift_b, ALU.add))
                step(dve.tensor_reduce(mx[:, q, :], sc[:, q, :, :], AX.X, ALU.max))
                step(dve.tensor_tensor(sc[:, q, :, :], sc[:, q, :, :],
                                       mx[:, q, :].unsqueeze(2).broadcast_to([P, H, W]), ALU.subtract))
                dve.sem_inc(masked, 1)

            def norm(i, r):
                q = r % 2
                dve.wait_ge(exped, i * R + r + 1)
                step(dve.tensor_reduce(den[:, q, :], ex[:, q, :, :], AX.X, ALU.add))
                step(dve.reciprocal(den[:, q, :], den[:, q, :]))
                step(dve.tensor_tensor(ex[:, q, :, :], ex[:, q, :, :],
                                       den[:, q, :].unsqueeze(2).broadcast_to([P, H, W]), ALU.mult))
                dve.sem_inc(normed, 1)

            with step.loop(TURNS, 7 * R + 1 + 2 * R + 1 + R + 2) as i:
                dve.wait_ge(projected, i + 1)
                dve.tensor_copy(kT[:, :], ps_k[:, :]).then_inc(k_ready, 1)
                mask(i, 0)
                for r in range(R):
                    if r + 1 < R:
                        mask(i, r + 1)
                    norm(i, r)
                dve.wait_ge(outed, i + 1)
                step(dve.scalar_tensor_tensor(
                    out=z[:, :, :], in0=hg[:, bass.ds(i * R, R), :], scalar=2.0,
                    in1=ps_z[:, :].rearrange("p (r c) -> p r c", r=R), op0=ALU.mult, op1=ALU.add))
                dve.sem_inc(z_ready, 1)
                for r in range(R):
                    step.mark(dve.bn_stats(st[:, r, :], z[:, r, :]))
                step.join()
                dve.sem_inc(tick, 1)
                for r in range(R):
                    step.mark(dve.bn_aggr(mv[:, r, :], st[:, r, :]))
                step.join()
                step(dve.tensor_scalar(ve[:, :], mv[:, :, 1], eps, None, ALU.add))
                dve.sem_inc(ve_ready, 1)
                dve.wait_ge(rstd_ready, i + 1)
                dve.wait_ge(stored, i * 16)
                for r in range(R):
                    step.mark(dve.tensor_scalar(out[:, r, :], z[:, r, :], mv[:, r, 0:1], rstd[:, r:r + 1],
                                                ALU.subtract, ALU.mult))
                step.join()
                step(dve.tensor_tensor(out[:, :, :], out[:, :, :],
                                       gain_b[:, :].unsqueeze(1).broadcast_to([P, R, C]), ALU.mult))
                step(dve.tensor_tensor(out[:, :, :], out[:, :, :],
                                       shift_b[:, :].unsqueeze(1).broadcast_to([P, R, C]), ALU.add))
                dve.sem_inc(out_ready, 1)


def mamba(nc, h0, x, in_proj, conv_w, conv_b, x_proj, dt_w, dt_b, A_log, Dp, out_w, out_b, gain, shift,
          x1, tag="mam", eps=1e-5):
    Q = 16
    G, J = 4, 4
    NQ = W // Q
    N = Q * T
    K = conv_w.shape[1]
    S = A_log.shape[1]
    DI = A_log.shape[0]
    HV = DI // P
    RK = dt_w.shape[0]
    PADT = T + K - 1
    TURNS = B * NQ
    with ExitStack() as ctx:
        s = Scope(nc, ctx, tag)
        w_in = s.sb("w_in", [P, 2 * DI])
        w_conv = s.sb("w_conv", [P, K, DI])
        cw_b = s.sb("cw_b", [P, DI, K])
        cb = s.sb("cb", [P, HV])
        xp = s.sb("xp", [P, HV, RK + 2 * S])
        xp3 = s.sb("xp3", [P, HV, 3, 2 * S])
        dtw = s.sb("dtw", [RK, DI])
        dtb = s.sb("dtb", [P, HV])
        A = s.sb("A", [P, HV, S])
        dp = s.sb("dp", [P, HV])
        ow = s.sb("ow", [P, HV, C])
        ob = s.sb("ob", [1, C])
        gain_b = s.sb("gain", [P, C])
        shift_b = s.sb("shift", [P, C])
        ident = s.sb("ident", [P, P])
        ones1 = s.sb("ones1", [1, P])
        half_c = s.sb("half", [P, G])
        sel = s.sb("sel", [96, 2 * S, P], bf16)

        ht = [s.sb(f"ht{j}", [P, G, C]) for j in range(2)]
        hr = [s.sb(f"hr{j}", [P, G, C]) for j in range(2)]
        xt = [s.sb(f"xt{j}", [P, G, C]) for j in range(2)]
        hT = s.sb("hT", [P, Q, PADT])
        xs = [s.sb(f"xs{j}", [P, HV, N]) for j in range(2)]
        sz = [s.sb(f"sz{j}", [P, HV, N]) for j in range(2)]
        dt = [s.sb(f"dt{j}", [P, HV, N]) for j in range(2)]
        dtx = [s.sb(f"dtx{j}", [P, HV, N]) for j in range(2)]
        bc3 = [s.sb(f"bc3_{j}", [96, N], bf16) for j in range(2)]
        dtr = s.sb("dtr", [RK, N])
        bcf = s.sb("bcf", [96, N])
        mid = s.sb("mid", [96, N], bf16)
        e = s.sb("e", [P, HV, N])
        ln = s.sb("ln", [P, HV, N])
        po, lin, e2 = (s.sb(n, [P, HV, N]) for n in ("po", "lin", "e2"))
        small = s.sb("small", [P, HV, N], u8)
        third = s.sb("third", [P, 1])
        dA = [s.sb(f"dA{j}", [P, HV, Q, T]) for j in range(4)]
        dBx = [s.sb(f"dBx{j}", [P, HV, N]) for j in range(2)]
        hs = [s.sb(f"hs{j}", [P, HV, N]) for j in range(2)]
        hc = [s.sb(f"hc{j}", [P, HV, N]) for j in range(4)]
        y = s.sb("y", [P, HV, N])
        z = s.sb("z", [P, G, C])
        out = s.sb("out", [P, G, C])
        st = s.sb("st", [P, G, 6])
        mv = s.sb("mv", [P, G, 2])
        ve = s.sb("ve", [P, G])
        rstd = s.sb("rstd", [P, G])
        ps_b = [s.ps(f"ps_b{j}") for j in range(2)]
        ps_c = [s.ps(f"ps_c{j}") for j in range(2)]
        ps_y = [s.ps(f"ps_y{j}") for j in range(2)]
        ps_0, ps_1 = s.ps("ps_0"), s.ps("ps_1")

        (loaded, made, prepared, turned, hT_ready, conv_done, gate_done, xs_ready, sz_ready, bc_made,
         bc_copied, bc_ready, dt_made, soft_step, e_ready, po_ready, dt_ready, spread, dA_ready, hc_ready,
         y_done, y_taken, y_ready, outed, z_ready, ve_ready, rstd_ready, scaled, out_ready, stored, dch, pch,
         ach, dtick, ptick, ln_ready, stick) = (
            s.sem(n) for n in (
                "loaded", "made", "prepared", "turned", "hT_ready", "conv_done", "gate_done", "xs_ready",
                "sz_ready", "bc_made", "bc_copied", "bc_ready", "dt_made", "soft_step", "e_ready", "po_ready",
                "dt_ready", "spread", "dA_ready", "hc_ready", "y_done", "y_taken", "y_ready", "outed",
                "z_ready", "ve_ready", "rstd_ready", "scaled", "out_ready", "stored", "dch", "pch", "ach",
                "dtick", "ptick", "ln_ready", "stick"))
        hin = [s.sem(f"hin{j}") for j in range(2)]
        rin = [s.sem(f"rin{j}") for j in range(2)]
        block = ctx.enter_context(nc.Block())
        LOADS = 13
        LOAD = 16 * J

        def tokens(v, b, k, j):
            return v[b].rearrange("t (k g j) c -> k j t g c", k=NQ, g=G)[k, j]

        h0v = h0.rearrange("(b t) w c -> b t w c", b=B)


        @block.sync
        def _(sp):
            sp.dma_start(w_in[:, :], in_proj).then_inc(loaded, 16)
            sp.dma_start(cw_b[:, :, :], conv_w.rearrange("d k -> (d k)").unsqueeze(0)
                         .broadcast_to([P, DI * K]).rearrange("p (d k) -> p d k", k=K)).then_inc(loaded, 16)
            sp.dma_start(xp[:, :, :], x_proj.rearrange("(h d) r -> d h r", h=HV)).then_inc(loaded, 16)
            sp.dma_start(dtw[:, :], dt_w).then_inc(loaded, 16)
            sp.dma_start(A[:, :, :], A_log.rearrange("(h d) s -> d h s", h=HV)).then_inc(loaded, 16)
            sp.dma_start(ow[:, :, :], out_w.rearrange("(h d) c -> d h c", h=HV)).then_inc(loaded, 16)
            for dst, src in ((cb, conv_b), (dtb, dt_b), (dp, Dp)):
                for h in range(HV):
                    sp.dma_start(dst[:, h:h + 1], src[h * P:(h + 1) * P].unsqueeze(1)).then_inc(loaded, 16)
            sp.dma_start(ob[:, :], out_b.unsqueeze(0)).then_inc(loaded, 16)
            for dst, src in ((gain_b, gain), (shift_b, shift)):
                sp.dma_start(dst[:, :], src.unsqueeze(0).broadcast_to([P, C])).then_inc(made, 16)
            for b in range(2):
                for j in range(J):
                    sp.dma_start(ht[b][j * T:(j + 1) * T, :, :], tokens(h0v, b, 0, j)).then_inc(hin[b], 16)

            def turn(k, b, first=False, last=False):
                i, p = k * B + b, b % 2
                k2, b2 = (k, b + 2) if b + 2 < B else (k + 1, b + 2 - B)
                k1, b1 = (k, b - 1) if b else (k - 1, B - 1)
                if not (last and b + 2 >= B):
                    sp.wait_ge(turned, i + 1)
                    sp.sem_inc(stick, 1)
                    for j in range(J):
                        sp.dma_start(ht[p][j * T:(j + 1) * T, :, :], tokens(h0v, b2, k2, j)).then_inc(hin[p], 16)
                if not (first and b < 2):
                    sp.wait_ge(out_ready, i - 1)
                    sp.sem_inc(stick, 1)
                for j in range(J):
                    sp.dma_start(hr[p][j * T:(j + 1) * T, :, :], tokens(h0v, b, k, j)).then_inc(rin[p], 16)
                    sp.dma_start(xt[p][j * T:(j + 1) * T, :, :], tokens(x, b, k, j)).then_inc(rin[p], 16)
                if not (first and b == 0):
                    sp.wait_ge(out_ready, i)
                    sp.sem_inc(stick, 1)
                    for j in range(J):
                        sp.dma_start(tokens(x1, b1, k1, j), out[j * T:(j + 1) * T, :, :]).then_inc(stored, 16)

            for b in range(B):
                turn(0, b, first=True)
            with sp.Fori(0, NQ - 2) as k:
                for b in range(B):
                    turn(k + 1, b)
            for b in range(B):
                turn(NQ - 1, b, last=True)
            sp.wait_ge(out_ready, TURNS)
            for j in range(J):
                sp.dma_start(tokens(x1, B - 1, NQ - 1, j), out[j * T:(j + 1) * T, :, :]).then_inc(stored, 16)
            sp.wait_ge(stored, LOAD * TURNS)

        @block.gpsimd
        def _(pool):
            step = Chain(pool, pch)
            fill_identity(pool, step, ident)
            step(pool.memset(half_c[:, :], -0.5))
            step(pool.memset(third[:, :], 1.0 / 3))
            step(pool.memset(ones1[:, :], 1.0))
            step(pool.memset(hT[:, :, :], 0.0))
            for a in dA:
                step(pool.memset(a[:, :, :, :], 0.0))
            step(pool.memset(sel[:, :, :], 0.0))
            for j in range(3):
                step(pool.affine_select(out=sel[:, :, :], in_=sel[:, :, :], compare_op=ALU.not_equal, fill=1.0,
                                        base=-32 * j, pattern=[[-1, 2 * S], [0, P]], channel_multiplier=1))
            pool.wait_ge(loaded, 16 * LOADS)
            for k in range(K):
                step(pool.tensor_tensor(w_conv[:, k, :], w_in[:, 0:DI], cw_b[:, :, k], ALU.mult))
            for j in range(3):
                step(pool.tensor_copy(xp3[:, :, j, :], xp[:, :, RK:RK + 2 * S]))
            pool.sem_inc(prepared, 1)
            pool.wait_ge(made, 32)
            pool.sem_inc(ptick, 1)

            def finish(i, p):
                pool.wait_ge(ve_ready, i + 1)
                pool.tensor_tensor(rstd[:, :], ve[:, :], half_c[:, :], ALU.pow).then_inc(rstd_ready, 1)
                pool.wait_ge(scaled, i + 1)
                wide = [P, G, C]
                step(pool.tensor_tensor(out[:, :, :], out[:, :, :], gain_b[:, :].unsqueeze(1).broadcast_to(wide), ALU.mult))
                step(pool.tensor_tensor(out[:, :, :], out[:, :, :], shift_b[:, :].unsqueeze(1).broadcast_to(wide), ALU.add))
                pool.tensor_tensor(out[:, :, :], out[:, :, :], xt[p][:, :, :], ALU.add).then_inc(out_ready, 1)

            def prepare(i):
                pool.wait_ge(e_ready, i + 1)
                step(pool.tensor_tensor(po[:, :, :], po[:, :, :], e2[:, :, :], ALU.mult))
                step(pool.tensor_tensor(po[:, :, :], po[:, :, :], lin[:, :, :], ALU.add))
                pool.tensor_tensor(po[:, :, :], po[:, :, :], e[:, :, :], ALU.mult).then_inc(po_ready, 1)

            prepare(0)
            prepare(1)
            with step.loop(TURNS // 2 - 1, 2 * 4) as j:
                for p in range(2):
                    finish(2 * j + p, p)
                    prepare(2 * j + p + 2)
            finish(TURNS - 2, 0)
            finish(TURNS - 1, 1)

        @block.tensor
        def _(pe):
            pe.wait_ge(loaded, 16 * LOADS)
            pe.wait_ge(prepared, 1)

            def nodes(ps):
                return ps[:, :].rearrange("p (q t) -> p q t", q=Q)

            def turn_tokens(i, j, p):
                pe.wait_ge(hin[p], LOAD * (j + 1))
                for g in range(G):
                    last = pe.transpose(ps_0[:, g * P:(g + 1) * P], ht[p][:, g, :], ident[:, :])
                last.then_inc(turned, 1)

            def convolve(h, taps, ps):
                for k in taps:
                    last = pe.matmul(nodes(ps), w_conv[:, k, h * P:(h + 1) * P], hT[:, :, k:k + T],
                                     start=(k == 0), stop=(k == K - 1))
                if K - 1 in taps:
                    last.then_inc(conv_done, 1)

            def gate(h):
                pe.matmul(nodes(ps_0), w_in[:, DI + h * P:DI + (h + 1) * P], hT[:, :, K - 1:K - 1 + T],
                          start=True, stop=True).then_inc(gate_done, 1)

            def project():
                for h in range(HV):
                    pe.matmul(ps_1[0:RK, :], xp[:, h, 0:RK], xs_now[:, h, :], start=(h == 0), stop=(h == HV - 1))
                for h in range(HV):
                    last = pe.matmul(ps_0[0:96, :], xp3[:, h, :, :].rearrange("p a s -> p (a s)"), xs_now[:, h, :],
                                     start=(h == 0), stop=(h == HV - 1))
                last.then_inc(bc_made, 1)

            def time_steps():
                pe.matmul(ps_1[:, :], dtw[:, 0:P], dtr[:, :], start=True, stop=True)
                pe.matmul(ps_0[:, :], dtw[:, P:2 * P], dtr[:, :], start=True, stop=True).then_inc(dt_made, 1)

            def spread_state(n, p):
                pe.matmul(ps_b[n % 2][:, :], sel[:, n, :], bc3[p][:, :], start=True, stop=True)
                pe.matmul(ps_c[n % 2][:, :], sel[:, S + n, :], bc3[p][:, :], start=True, stop=True
                          ).then_inc(spread, 1)

            def project_out():
                for g in range(G):
                    cols = slice(g * P, (g + 1) * P)
                    for h in range(HV):
                        pe.matmul(ps_1[:, cols], y[:, h, cols], ow[:, h, :], start=(h == 0), stop=False)
                    last = pe.matmul(ps_1[:, cols], ones1[:, :], ob[:, :], start=False, stop=True)
                last.then_inc(outed, 1)

            xs_now = xs[0]
            turn_tokens(0, 0, 0)
            pe.wait_ge(hT_ready, 1)
            for h, ps in ((0, ps_0), (1, ps_1)):
                convolve(h, range(K), ps)
                pe.wait_ge(xs_ready, h + 1)
                gate(h)
            pe.wait_ge(sz_ready, 2)
            project()
            pe.wait_ge(bc_copied, 1)
            time_steps()
            pe.wait_ge(bc_ready, 1)
            spread_state(0, 0)
            spread_state(1, 0)

            def turn(j, p, first=False, last=False):
                nonlocal xs_now
                i = 2 * j + p
                jn, q = (j, 1) if p == 0 else (j + 1, 0)
                xs_now = xs[q]
                for n in range(S):
                    pe.wait_ge(hc_ready, i * S + n + 1)
                    if n + 2 < S:
                        spread_state(n + 2, p)
                    elif not last:
                        if n + 2 == S:
                            pe.wait_ge(bc_ready, i + 2)
                        spread_state(n + 2 - S, q)
                    if n == 0 and not first:
                        pe.wait_ge(y_taken, i)
                    for h in range(HV):
                        done = pe.matmul(ps_y[h][:, :], ident[:, :], hc[n % 4][:, h, :],
                                         start=(n == 0), stop=(n == S - 1))
                    done.then_inc(y_done, 1)
                    if n == 3 and not first:
                        pe.wait_ge(y_ready, i)
                        project_out()
                    if last:
                        continue
                    if n == 0:
                        pe.wait_ge(e_ready, i + 1)
                        turn_tokens(i + 1, jn, q)
                    elif n == 1:
                        pe.wait_ge(hT_ready, i + 2)
                        convolve(0, (0, 1), ps_0)
                    elif n == 2:
                        convolve(0, (2, 3), ps_0)
                    elif n == 4:
                        pe.wait_ge(xs_ready, 2 * i + 3)
                        gate(0)
                    elif n == 5:
                        if not first:
                            pe.wait_ge(z_ready, i)
                        convolve(1, (0, 1), ps_1)
                    elif n == 6:
                        convolve(1, (2, 3), ps_1)
                        pe.wait_ge(sz_ready, 2 * i + 3)
                        gate(1)
                    elif n == 7:
                        pe.wait_ge(xs_ready, 2 * i + 4)
                        pe.wait_ge(sz_ready, 2 * i + 4)
                        project()
                    elif n == 8:
                        pe.wait_ge(bc_copied, i + 2)
                        time_steps()

            turn(0, 0, first=True)
            turn(0, 1)
            with pe.Fori(0, TURNS // 2 - 2) as j:
                turn(j + 1, 0)
                turn(j + 1, 1)
            turn(TURNS // 2 - 1, 0)
            turn(TURNS // 2 - 1, 1, last=True)
            pe.wait_ge(y_ready, TURNS)
            project_out()

        @block.scalar
        def _(act):
            step = Chain(act, ach)
            act.wait_ge(loaded, 16 * LOADS)
            step(act.activation(A[:, :, :], A[:, :, :], ACT.Exp))
            step(act.mul(A[:, :, :], A[:, :, :], -1.0))
            act.wait_ge(prepared, 1)

            def tokens_in(i):
                act.wait_ge(turned, i + 1)
                act.copy(hT[:, :, K - 1:], ps_0[:, :].rearrange("p (q t) -> p q t", q=Q)).then_inc(hT_ready, 1)

            def silu_x(i, h, q, ps):
                act.wait_ge(conv_done, 2 * i + h + 1)
                act.activation(xs[q][:, h, :], ps[:, :], ACT.Silu, bias=cb[:, h:h + 1]).then_inc(xs_ready, 1)

            def silu_z(i, h, q):
                act.wait_ge(gate_done, 2 * i + h + 1)
                act.activation(sz[q][:, h, :], ps_0[:, :], ACT.Silu).then_inc(sz_ready, 1)

            def projections_in(i, q):
                act.wait_ge(bc_made, i + 1)
                act.copy(bcf[:, :], ps_0[0:96, :])
                act.copy(bc3[q][:, :], ps_0[0:96, :])
                act.copy(dtr[:, :], ps_1[0:RK, :]).then_inc(bc_copied, 1)

            def softplus(i, q):
                act.wait_ge(dt_made, i + 1)
                for h, ps in ((0, ps_1), (1, ps_0)):
                    act.activation(e[:, h, :], ps[:, :], ACT.Abs, bias=dtb[:, h:h + 1])
                    last = act.activation(dt[q][:, h, :], ps[:, :], ACT.Relu, bias=dtb[:, h:h + 1])
                last.then_inc(soft_step, 1)
                act.wait_ge(soft_step, 2 * i + 1)
                act.activation(e[:, :, :], e[:, :, :], ACT.Exp, scale=-1.0).then_inc(soft_step, 1)
                act.wait_ge(soft_step, 2 * i + 2)
                act.activation(e2[:, :, :], e[:, :, :], ACT.Square)
                act.activation(lin[:, :, :], e[:, :, :], ACT.Identity, bias=1.0, scale=-0.5)
                act.activation(po[:, :, :], e[:, :, :], ACT.Identity, bias=third[:, :], scale=-0.25
                               ).then_inc(e_ready, 1)
                act.activation(ln[:, :, :], e[:, :, :], ACT.Ln, bias=1.0).then_inc(ln_ready, 1)

            tokens_in(0)
            silu_x(0, 0, 0, ps_0)
            silu_z(0, 0, 0)
            silu_x(0, 1, 0, ps_1)
            silu_z(0, 1, 0)
            projections_in(0, 0)
            softplus(0, 0)

            def turn(j, p, first=False, last=False):
                i = 2 * j + p
                q = 1 - p
                act.wait_ge(dt_ready, i + 1)
                for n in range(S):
                    if not (first and n < 4):
                        act.wait_ge(hc_ready, i * S + n - 3)
                    for h in range(HV):
                        done = act.activation(dA[n % 4][:, h, :, 1:],
                                              dt[p][:, h, :].rearrange("p (q t) -> p q t", q=Q)[:, :, 1:],
                                              ACT.Exp, scale=A[:, h, n:n + 1])
                    done.then_inc(dA_ready, 1)
                    if last:
                        continue
                    if n == 3:
                        tokens_in(i + 1)
                    elif n == 5:
                        if not first:
                            act.wait_ge(y_ready, i)
                        silu_x(i + 1, 0, q, ps_0)
                    elif n == 7:
                        silu_z(i + 1, 0, q)
                    elif n == 8:
                        silu_x(i + 1, 1, q, ps_1)
                        silu_z(i + 1, 1, q)
                    elif n == 10:
                        projections_in(i + 1, q)
                    elif n == 11:
                        softplus(i + 1, q)

            turn(0, 0, first=True)
            turn(0, 1)
            with act.Fori(0, TURNS // 2 - 2) as j:
                turn(j + 1, 0)
                turn(j + 1, 1)
            turn(TURNS // 2 - 1, 0)
            turn(TURNS // 2 - 1, 1, last=True)

        @block.vector
        def _(dve):
            step = Chain(dve, dch)
            both = [P, HV, N]
            dve.wait_ge(loaded, 16 * LOADS)
            dve.wait_ge(prepared, 1)

            def parts(i, q):
                dve.wait_ge(bc_copied, i + 1)
                step(dve.tensor_tensor(bcf[:, :], bcf[:, :], bc3[q][:, :], ALU.subtract))
                step(dve.tensor_copy(mid[:, :], bcf[:, :]))
                step.mark(dve.tensor_copy(bc3[q][32:64, :], mid[32:64, :]))
                step(dve.tensor_tensor(bc3[q][64:96, :], bcf[64:96, :], mid[64:96, :], ALU.subtract))
                dve.sem_inc(bc_ready, 1)

            def time_step(i, q, part):
                if part == 0:
                    dve.wait_ge(e_ready, i + 1)
                    step.mark(dve.tensor_scalar(small[:, :, :], e[:, :, :], 0.06, None, ALU.is_lt))
                elif part == 1:
                    step.join()
                    dve.wait_ge(po_ready, i + 1)
                    dve.wait_ge(ln_ready, i + 1)
                    dve.sem_inc(dtick, 1)
                    step.mark(dve.copy_predicated(ln[:, :, :], small[:, :, :], po[:, :, :]))
                elif part == 2:
                    step(dve.tensor_tensor(dt[q][:, :, :], dt[q][:, :, :], ln[:, :, :], ALU.add))
                    dve.sem_inc(dt_ready, 1)
                else:
                    step.mark(dve.tensor_tensor(dtx[q][:, :, :], dt[q][:, :, :], xs[q][:, :, :], ALU.mult))

            parts(0, 0)
            for part in range(4):
                time_step(0, 0, part)
                step.join()

            def take_y(i, q):
                dve.wait_ge(y_done, (i + 1) * S)
                for h in range(HV):
                    step.mark(dve.scalar_tensor_tensor(out=y[:, h, :], in0=xs[q][:, h, :], scalar=dp[:, h:h + 1],
                                                       in1=ps_y[h][:, :], op0=ALU.mult, op1=ALU.add))
                step.join()
                dve.sem_inc(y_taken, 1)

            def gate_y(q):
                step(dve.tensor_tensor(y[:, :, :], y[:, :, :], sz[q][:, :, :], ALU.mult))
                dve.sem_inc(y_ready, 1)

            def residual(i, j, q):
                dve.wait_ge(outed, i + 1)
                dve.wait_ge(rin[q], 2 * LOAD * (j + 1))
                step(dve.tensor_tensor(z[:, :, :], hr[q][:, :, :], ps_1[:, :].rearrange("p (g c) -> p g c", g=G), ALU.add))
                dve.sem_inc(z_ready, 1)

            def statistics():
                for g in range(G):
                    step.mark(dve.bn_stats(st[:, g, :], z[:, g, :]))

            def moments():
                dve.sem_inc(dtick, 1)
                for g in range(G):
                    step.mark(dve.bn_aggr(mv[:, g, :], st[:, g, :]))
                step.join()
                step(dve.tensor_scalar(ve[:, :], mv[:, :, 1], eps, None, ALU.add))
                dve.sem_inc(ve_ready, 1)

            def scale(i, fresh=False):
                dve.wait_ge(rstd_ready, i + 1)
                if not fresh:
                    dve.wait_ge(stored, i * LOAD)
                for g in range(G):
                    step.mark(dve.tensor_scalar(out[:, g, :], z[:, g, :], mv[:, g, 0:1], rstd[:, g:g + 1],
                                                ALU.subtract, ALU.mult))
                step.join()
                dve.sem_inc(scaled, 1)

            PREPARE, FINISH = 4 + 4, 2 + 1 + 1 + G + G + 1 + G

            def turn(j, p, first=False, last=False):
                i, q = 2 * j + p, 1 - p
                jq = j if p else j - 1
                dve.wait_ge(spread, i * S + 1)
                ready = step.mark(dve.tensor_tensor(
                    dBx[0][:, :, :], dtx[p][:, :, :], ps_b[0][:, :].unsqueeze(1).broadcast_to(both), ALU.mult))
                if not first:
                    take_y(i - 1, q)
                for n in range(S):
                    dve.wait_ge(dA_ready, i * S + n + 1)
                    step.wait(ready)
                    scanned = step.mark(dve.tensor_tensor_scan(
                        hs[n % 2][:, :, :].rearrange("p h n -> p (h n)"),
                        dA[n % 4][:, :, :, :].rearrange("p h q t -> p (h q t)"),
                        dBx[n % 2][:, :, :].rearrange("p h n -> p (h n)"), 0.0, ALU.mult, ALU.add))
                    if n + 1 < S:
                        dve.wait_ge(spread, i * S + n + 2)
                        ready = step.mark(dve.tensor_tensor(
                            dBx[(n + 1) % 2][:, :, :], dtx[p][:, :, :],
                            ps_b[(n + 1) % 2][:, :].unsqueeze(1).broadcast_to(both), ALU.mult))
                    if not last:
                        if n == 10:
                            parts(i + 1, q)
                        elif n == 11:
                            time_step(i + 1, q, 0)
                        elif n == 13:
                            time_step(i + 1, q, 1)
                        elif n == 14:
                            time_step(i + 1, q, 2)
                        elif n == 15:
                            time_step(i + 1, q, 3)
                    if not first:
                        if n == 1:
                            gate_y(q)
                        elif n == 4:
                            residual(i - 1, jq, q)
                        elif n == 5:
                            statistics()
                        elif n == 6:
                            step.join()
                            moments()
                        elif n == 8:
                            scale(i - 1, fresh=isinstance(i, int) and i == 1)
                    step.wait(scanned)
                    if not (first and n < 4):
                        dve.wait_ge(y_done, i * S + n - 3)
                    dve.tensor_tensor(hc[n % 4][:, :, :], hs[n % 2][:, :, :],
                                      ps_c[n % 2][:, :].unsqueeze(1).broadcast_to(both), ALU.mult
                                      ).then_inc(hc_ready, 1)
                step.join()

            turn(0, 0, first=True)
            turn(0, 1)
            with step.loop(TURNS // 2 - 2, 2 * (2 * S + PREPARE + FINISH)) as j:
                turn(j + 1, 0)
                turn(j + 1, 1)
            turn(TURNS // 2 - 1, 0)
            turn(TURNS // 2 - 1, 1, last=True)
            take_y(TURNS - 1, 1)
            gate_y(1)
            residual(TURNS - 1, TURNS // 2 - 1, 1)
            statistics()
            step.join()
            moments()
            scale(TURNS - 1)


NKY, NKX = 32, 17
LKY, LKX = 16, 9
SR = 64
ROWS = [k if k < NKY // 2 else k - NKY for k in range(NKY)]
IMG = W * C


def fourier_tables():
    n = np.arange(W, dtype=np.float64)
    al = 2 * np.pi / W
    r2 = SR // 2
    k = np.arange(r2 + 1)
    cos, sin = np.cos(al * np.outer(n, k)), np.sin(al * np.outer(n, k))
    scale = np.where((k == 0) | (k == r2), 1.0, np.sqrt(2.0))
    t = {}
    t["rows_all"] = np.concatenate([cos, sin[:, 1:]], 1) / W
    t["gram_cols"] = np.concatenate([cos * scale, sin * scale], 1) / W
    cx, sx = cos[:, :NKX], sin[:, :NKX]
    t["tok_cols"] = np.concatenate([cx, -sx, -sx, -cx, sx, cx], 1) / W
    kr = np.array(ROWS)
    cr, sr = np.cos(al * np.outer(n, kr)), np.sin(al * np.outer(n, kr))
    t["rows_fwd"] = np.concatenate([cr, -sr], 1) / W
    z = np.zeros((W, 32 - NKX))
    t["cols_fwd"] = np.concatenate([cx, z, -sx, z, sx, z, cx, z], 1) / W
    m = np.where(np.arange(NKX) == 0, 1.0, 2.0)[:, None]
    mc, ms, zz = m * cx.T, m * sx.T, np.zeros((32 - NKX, W))
    g1 = np.concatenate([np.concatenate([mc, zz, -ms, zz]), np.concatenate([ms, zz, mc, zz])], 1)
    g2 = np.concatenate([np.concatenate([-ms, zz, -mc, zz]), np.concatenate([mc, zz, -ms, zz])], 1)
    t["cols_inv"] = np.concatenate([g1, g2], 1)
    t["rows_inv"] = np.concatenate([cr.T, -sr.T], 1)
    return {a: np.ascontiguousarray(b.astype(np.float32)) for a, b in t.items()}


def inline_tables(nc):
    return {a: nc.inline_tensor(b, name=f"table_{a}").ap()
            for a, b in fourier_tables().items()}


def token_images(nc, hg, g1, b1, tok, tnd, tag="l1n", eps=1e-5):
    with ExitStack() as ctx:
        s = Scope(nc, ctx, tag)
        sq = s.sb("sq", [P, 8, C])
        sums = s.sb("sums", [P, 2, BT])
        ones = s.sb("ones", [P, P])
        gb = s.sb("gb", [P, 2])
        var, rstd, half, scale, bias = (s.sb(n, [P, BT]) for n in ("var", "rstd", "half", "scale", "bias"))
        ps = s.ps("ps")
        loaded, made, saved, squared, reduced, summed, var_ready, rstd_ready, ready, dch = (
            s.sem(n) for n in ("loaded", "made", "saved", "squared", "reduced", "summed", "var_ready",
                               "rstd_ready", "ready", "dch"))
        block = ctx.enter_context(nc.Block())

        @block.sync
        def _(sp):
            for j, src in enumerate((g1, b1)):
                sp.dma_start(gb[:, j:j + 1], src.unsqueeze(0).broadcast_to([P, 1])).then_inc(loaded, 16)
            sp.dma_start(tok.rearrange("n r c -> r n c"), hg[:, :, :]).then_inc(saved, 16)
            sp.wait_ge(ready, BT // 8)
            sp.dma_start(tnd.rearrange("n r c -> r n c"), hg[:, :, :]).then_inc(saved, 16)
            sp.wait_ge(saved, 32)

        @block.gpsimd
        def _(pool):
            pool.memset(ones[:, :], 1.0 / IMG).then_inc(made, 1)
            pool.memset(half[:, :], -0.5).then_inc(made, 1)
            pool.wait_ge(made, 2)
            pool.wait_ge(var_ready, 1)
            pool.tensor_tensor(rstd[:, :], var[:, :], half[:, :], ALU.pow).then_inc(rstd_ready, 1)

        @block.scalar
        def _(act):
            with act.Fori(0, BT // 8) as i:
                act.wait_ge(reduced, i)
                act.activation(sq[:, :, :], hg[:, bass.ds(i * 8, 8), :], ACT.Square).then_inc(squared, 1)

        @block.tensor
        def _(pe):
            pe.wait_ge(made, 2)
            pe.wait_ge(reduced, BT // 8)
            pe.matmul(ps[:, 0:2 * BT], ones[:, :], sums[:, :, :].rearrange("p a n -> p (a n)"),
                      start=True, stop=True).then_inc(summed, 1)

        @block.vector
        def _(dve):
            step = Chain(dve, dch)
            with step.loop(BT // 8, 2) as i:
                step.mark(dve.tensor_reduce(sums[:, 0, bass.ds(i * 8, 8)], hg[:, bass.ds(i * 8, 8), :], AX.X, ALU.add))
                dve.wait_ge(squared, i + 1)
                step(dve.tensor_reduce(sums[:, 1, bass.ds(i * 8, 8)], sq[:, :, :], AX.X, ALU.add))
                dve.sem_inc(reduced, 1)
            dve.wait_ge(summed, 1)
            dve.wait_ge(loaded, 32)
            step(dve.tensor_copy(sums[:, :, :], ps[:, 0:2 * BT].rearrange("p (a n) -> p a n", a=2)))
            step(dve.tensor_tensor(var[:, :], sums[:, 0, :], sums[:, 0, :], ALU.mult))
            step(dve.scalar_tensor_tensor(out=var[:, :], in0=sums[:, 1, :], scalar=eps, in1=var[:, :],
                                          op0=ALU.add, op1=ALU.subtract))
            dve.sem_inc(var_ready, 1)
            dve.wait_ge(rstd_ready, 1)
            step(dve.tensor_scalar(scale[:, :], rstd[:, :], gb[:, 0:1], None, ALU.mult))
            step(dve.tensor_tensor(bias[:, :], sums[:, 0, :], scale[:, :], ALU.mult))
            step(dve.tensor_scalar(bias[:, :], bias[:, :], -1.0, gb[:, 1:2], ALU.mult, ALU.add))
            dve.wait_ge(saved, 16)
            with step.loop(BT // 8, 2) as i:
                v = hg[:, bass.ds(i * 8, 8), :]
                step(dve.tensor_tensor(v, v, scale[:, bass.ds(i * 8, 8)].unsqueeze(2).broadcast_to([P, 8, C]), ALU.mult))
                step(dve.tensor_tensor(v, v, bias[:, bass.ds(i * 8, 8)].unsqueeze(2).broadcast_to([P, 8, C]), ALU.add))
                dve.sem_inc(ready, 1)


def token_spectra(nc, tn, tabs, xh, gram_d, tag="l1f"):
    R = 4
    KA = SR + 1
    h = SR // 2
    with ExitStack() as ctx:
        s = Scope(nc, ctx, tag)
        rows = s.sb("rows", [P, KA])
        cols = s.sb("cols", [P, 2 * (h + 1)])
        tcols = s.sb("tcols", [P, 3, 2 * NKX])
        o1 = s.sb("o1", [P, KA, BT])
        img = [s.sb(f"img{j}", [P, R, C]) for j in range(2)]
        loaded, staged, done, copied = (s.sem(n) for n in ("loaded", "staged", "done", "copied"))
        with ExitStack() as c2:
            s2 = Scope(nc, c2, tag + "a")
            ps = [s2.ps(f"ps{j}") for j in range(2)]
            block = c2.enter_context(nc.Block())

            @block.sync
            def _(sp):
                for dst, src in ((rows[:, :], tabs["rows_all"]), (cols[:, :], tabs["gram_cols"]),
                                 (tcols[:, :, :].rearrange("p a k -> p (a k)"), tabs["tok_cols"])):
                    sp.dma_start(dst, src).then_inc(loaded, 16)

            @block.gpsimd
            def _(pool):
                with pool.Fori(0, BT // R // 2) as i:
                    for j in range(2):
                        pool.wait_ge(done, 2 * i + j - 1) if j else pool.wait_ge(done, 2 * i)
                        pool.tensor_copy(img[j][:, :, :], tn[:, bass.ds(i * 2 * R + j * R, R), :]).then_inc(staged, 1)

            @block.tensor
            def _(pe):
                pe.wait_ge(loaded, 48)
                with pe.Fori(0, BT // R // 2) as i:
                    for j in range(2):
                        pe.wait_ge(staged, 2 * i + j + 1)
                        pe.wait_ge(copied, 2 * i)
                        for r in range(R):
                            last = pe.matmul(ps[j][:, r * KA:(r + 1) * KA], img[j][:, r, :], rows[:, :],
                                             start=True, stop=True)
                        last.then_inc(done, 1)

            @block.scalar
            def _(act):
                with act.Fori(0, BT // R // 2) as i:
                    for j in range(2):
                        act.wait_ge(done, 2 * i + j + 1)
                        act.copy(o1[:, :, bass.ds(i * 2 * R + j * R, R)],
                                 ps[j][:, 0:R * KA].rearrange("p (r k) -> p k r", r=R)).then_inc(copied, 1)

        with ExitStack() as c2:
            s2 = Scope(nc, c2, tag + "b")
            NB = 4
            ps = [s2.ps(f"ps{j}") for j in range(NB)]
            made, read = s2.sem("made"), s2.sem("read")
            PER = 8
            block = c2.enter_context(nc.Block())

            @block.tensor
            def _(pe):
                for n, ky in enumerate(ROWS):
                    at = (n % PER) * 2 * NKX
                    dst = ps[n // PER][:, at:at + 2 * NKX]
                    last = pe.matmul(dst, o1[:, abs(ky), :], tcols[:, 0, :], start=True, stop=(ky == 0))
                    if ky:
                        last = pe.matmul(dst, o1[:, h + abs(ky), :], tcols[:, 1 if ky > 0 else 2, :],
                                         start=False, stop=True)
                    if n % PER == PER - 1:
                        last.then_inc(made, 1)

            @block.scalar
            def _(act):
                for n in range(NB):
                    act.wait_ge(made, n + 1)
                    act.copy(xh[:, n * PER:(n + 1) * PER, :, :],
                             ps[n][:, 0:PER * 2 * NKX].rearrange("p (k a x) -> p k a x", k=PER, a=2)).then_inc(read, 1)

        with ExitStack() as c2:
            s2 = Scope(nc, c2, tag + "c")
            H1 = h + 1
            z = [s2.sb(f"z{j}", [H1, KA, BT]) for j in range(2)]
            p12 = s2.sb("p12", [H1, 2, BT])
            inner = s2.sb("inner", [H1, 1])
            gs = s2.sb("gs", [P, BT])
            ps = [s2.ps(f"ps{j}") for j in range(4)]
            ps_g = s2.ps("ps_g")
            made, read, zready, gdone, gcopied, stored, dch, pch = (
                s2.sem(n) for n in ("made", "read", "zready", "gdone", "gcopied", "stored", "dch", "pch"))
            block = c2.enter_context(nc.Block())
            PER = 4
            parts = [(k, min(PER, KA - k)) for k in range(0, KA, PER)]
            units = [(k, n, a) for k, n in parts for a in range(2)]

            @block.tensor
            def _(pe):
                for u, (k, n, a) in enumerate(units):
                    if u >= 4:
                        pe.wait_ge(read, u - 3)
                    pe.matmul(ps[u % 4][0:H1, 0:n * BT], cols[:, a * H1:(a + 1) * H1],
                              o1[:, k:k + n, :].rearrange("p k n -> p (k n)"),
                              start=True, stop=True).then_inc(made, 1)
                pe.wait_ge(zready, 1)
                first = True
                for k in range(KA):
                    if k == h or k == 2 * h:
                        continue
                    pe.matmul(ps_g[:, 0:BT], z[0][:, k, :], z[0][:, k, :], start=first, stop=False)
                    pe.matmul(ps_g[:, 0:BT], z[1][0:h, k, :], z[1][0:h, k, :], start=False, stop=False)
                    first = False
                pe.matmul(ps_g[:, 0:BT], p12[:, 0, :], p12[:, 0, :], start=False, stop=False)
                pe.matmul(ps_g[:, 0:BT], p12[0:h, 1, :], p12[0:h, 1, :], start=False, stop=True).then_inc(gdone, 1)

            @block.gpsimd
            def _(pool):
                step = Chain(pool, pch)
                step(pool.memset(inner[:, :], 1.0))
                step(pool.affine_select(out=inner[:, :], in_=inner[:, :], compare_op=ALU.not_equal, fill=0.0,
                                        base=0, pattern=[[0, 1]], channel_multiplier=1))

            @block.scalar
            def _(act):
                for u, (k, n, a) in enumerate(units):
                    act.wait_ge(made, u + 1)
                    act.mul(z[a][:, k:k + n, :], ps[u % 4][0:H1, 0:n * BT].rearrange("p (k n) -> p k n", k=n),
                            math.sqrt(2.0)).then_inc(read, 1)
                act.wait_ge(gdone, 1)
                act.copy(gs[:, :], ps_g[:, 0:BT]).then_inc(gcopied, 1)

            @block.vector
            def _(dve):
                step = Chain(dve, dch)
                dve.wait_ge(read, len(units))
                for a in range(2):
                    for k in (0, h, 2 * h):
                        step(dve.tensor_scalar(z[a][:, k, :], z[a][:, k, :], math.sqrt(0.5), None, ALU.mult))
                step(dve.tensor_tensor(p12[:, 0, :], z[0][:, h, :], z[1][:, 2 * h, :], ALU.add))
                step(dve.tensor_tensor(p12[:, 1, :], z[0][:, 2 * h, :], z[1][:, h, :], ALU.subtract))
                dve.wait_ge(pch, 2)
                step(dve.tensor_scalar(p12[:, 1, :], p12[:, 1, :], inner[:, 0:1], None, ALU.mult))
                dve.sem_inc(zready, 1)

            @block.sync
            def _(sp):
                sp.wait_ge(gcopied, 1)
                sp.dma_start(gram_d, gs[:, :]).then_inc(stored, 16)
                sp.wait_ge(stored, 16)


NH = 16


def token_attention(nc, xh, gram_d, tabs, wts, prob_d, pt, mt, tag="l1s"):
    L = LKX - 1
    MA = LKY * L
    MB = LKY // 2 + 1
    low = [n for n in range(NKY) if -LKY // 2 <= ROWS[n] < LKY // 2]
    unit = float(SR * SR) / math.sqrt(SR * SR)
    with ExitStack() as ctx:
        s = Scope(nc, ctx, tag)
        ident = s.sb("ident", [P, P])
        skips = s.sb("skips", [P, 6, NH])
        qa, ka = (s.sb(n, [MA, NH, 2]) for n in ("qa", "ka"))
        qb, kb, qr, kr = (s.sb(n, [MB, NH, 2]) for n in ("qb", "kb", "qr", "kr"))
        da = s.sb("da", [MA, 3, NH])
        db = s.sb("db", [MB, 3, NH])
        two = s.sb("two", [MB, 1])
        sgn = s.sb("sgn", [MB, 1])
        tmp = s.sb("tmp", [P, 4, NH])
        row = s.sb("row", [1, 2, NH])
        xlow = s.sb("xlow", [P, 2, LKY, L])
        xlob = s.sb("xlob", [P, 2, MB])
        xa = s.sb("xa", [MA, 2, BT])
        xb = s.sb("xb", [MB, 2, BT])
        grow = s.sb("grow", [1, B, T, T])
        xrow = s.sb("xrow", [1, BT, T])
        pa = s.sb("pa", [MA, 4, T, T])
        pb = s.sb("pb", [MB, 4, T, T])
        sc = s.sb("sc", [NH, B * T, T])
        mx = s.sb("mx", [NH, B * T])
        pl = s.sb("pl", [P, NH, BT])
        coef = s.sb("coef", [P, NH])
        mtt = s.sb("mtt", [P, NH, BT])
        ps_t = s.ps("ps_t")
        ps = [s.ps(f"ps{j}") for j in range(2)]
        ps_p = [s.ps(f"ps_p{j}") for j in range(4)]
        (loaded, zeroed, made, turned, x_ready, d_ready, prods, scored, sc_ready, e_ready, p_ready, p_out,
         p_in, flipped, pt_ready, dch, pch, low_ready) = (
            s.sem(n) for n in ("loaded", "zeroed", "made", "turned", "x_ready", "d_ready", "prods", "scored",
                               "sc_ready", "e_ready", "p_ready", "p_out", "p_in", "flipped", "pt_ready", "dch",
                               "pch", "low_ready"))
        LOADS = 6 + 2 * (LKY + 2) + 2 * (LKY // 2) + 1
        block = ctx.enter_context(nc.Block())

        @block.sync
        def _(sp):
            n = 0
            names = ("query_skip_w", "key_skip_w", "value_skip_w", "proj_skip_w", "query_skip_b", "key_skip_b")
            for j, name in enumerate(names):
                src = wts[name]
                flat = src.rearrange("a b -> (a b)") if len(src.shape) == 2 else src
                sp.dma_start(skips[:, j, :], flat.unsqueeze(0).broadcast_to([P, NH])).then_inc(loaded, 16)
                n += 1
            sp.wait_ge(zeroed, 1)
            for w, ta, tb, tr in (("query_w", qa, qb, qr), ("key_w", ka, kb, kr)):
                src = wts[w][0].rearrange("h y x a -> y x h a")
                for y in range(LKY):
                    sp.dma_start(ta[y * L:(y + 1) * L, :, :], src[y, 1:LKX]).then_inc(loaded, 16)
                    n += 1
                sp.dma_start(tb[0:LKY // 2, :, :], src[0:LKY // 2, 0]).then_inc(loaded, 16)
                sp.dma_start(tr[0:1, :, :], src[0:1, 0]).then_inc(loaded, 16)
                n += 2
                for y in range(1, MB):
                    sp.dma_start(tr[y:y + 1, :, :], src[LKY - y:LKY - y + 1, 0]).then_inc(loaded, 16)
                    n += 1
            for b in range(B):
                sp.dma_start(grow[:, b, :, :], gram_d[b * T:(b + 1) * T, b * T:(b + 1) * T].unsqueeze(0)
                             ).then_inc(made, 16)
            assert n == LOADS - 1, n
            sp.wait_ge(p_ready, 1)
            sp.dma_start(prob_d.rearrange("h b t s -> h (b t) s"), sc[:, :, :]).then_inc(p_out, 16)
            sp.wait_ge(p_out, 16)
            for b in range(B):
                sp.dma_start(pl[b * T:(b + 1) * T, :, b * T:(b + 1) * T],
                             prob_d[:, b].rearrange("h t s -> t h s")).then_inc(p_in, 16)
            sp.wait_ge(p_in, 16 * B)

        @block.gpsimd
        def _(pool):
            step = Chain(pool, pch)
            for t in (qb, kb, qr, kr):
                step(pool.memset(t[:, :, :], 0.0))
            pool.sem_inc(zeroed, 1)
            fill_identity(pool, step, ident)
            step(pool.memset(pl[:, :, :], 0.0))
            step(pool.memset(two[:, :], 2.0 * unit))
            step(pool.affine_select(out=two[:, :], in_=two[:, :], compare_op=ALU.not_equal, fill=unit,
                                    base=0, pattern=[[0, 1]], channel_multiplier=1))

        @block.tensor
        def _(pe):
            pe.wait_ge(pch, 6)
            pe.wait_ge(low_ready, 1)
            for a in range(2):
                pe.transpose(ps_t[0:MA, a * BT:(a + 1) * BT], xlow[:, a, :, :].rearrange("p y x -> p (y x)"), ident[:, :])
                pe.transpose(ps_t[0:MB, (2 + a) * BT:(3 + a) * BT], xlob[:, a, :], ident[:, :]).then_inc(turned, 1)
            pe.wait_ge(d_ready, 1)
            pe.wait_ge(made, 16 * B)
            NS = T // 2
            for b in range(B):
                pe.wait_ge(prods, b + 1)
                if b:
                    pe.wait_ge(sc_ready, 2 * b)
                for g in range(2):
                    rows = slice(g * NS, (g + 1) * NS)
                    dst = ps[g][0:NH, :]
                    for n, (d, j) in enumerate(((0, 0), (0, 1), (2, 2), (1, 3))):
                        pe.matmul(dst, da[:, d, :], pa[:, j, rows, :].rearrange("p t s -> p (t s)"),
                                  start=(n == 0), stop=False)
                        pe.matmul(dst, db[:, d, :], pb[:, j, rows, :].rearrange("p t s -> p (t s)"),
                                  start=False, stop=False)
                    pe.matmul(dst, row[:, 0, :], grow[:, b, rows, :].rearrange("p t s -> p (t s)"),
                              start=False, stop=False)
                    pe.matmul(dst, row[:, 1, :], xrow[:, b * T + g * NS:b * T + (g + 1) * NS, :].rearrange("p t s -> p (t s)"),
                              start=False, stop=True).then_inc(scored, 1)
            pe.wait_ge(p_in, 16 * B)
            for h in range(NH):
                last = pe.transpose(ps_p[h // 4][:, (h % 4) * BT:(h % 4 + 1) * BT], pl[:, h, :], ident[:, :])
            last.then_inc(flipped, 1)

        @block.scalar
        def _(act):
            for k in range(2 * B):
                b, g = divmod(k, 2)
                act.wait_ge(scored, k + 1)
                act.copy(sc[:, b * T + g * (T // 2):b * T + (g + 1) * (T // 2), :],
                         ps[g][0:NH, :].rearrange("p (t s) -> p t s", s=T)).then_inc(sc_ready, 1)
            act.wait_ge(e_ready, 1)
            act.activation(sc[:, :, :], sc[:, :, :], ACT.Exp).then_inc(e_ready, 1)
            act.wait_ge(flipped, 1)
            for j in range(4):
                act.copy(pt[:, 4 * j:4 * j + 4, :], ps_p[j][:, :].rearrange("p (h t) -> p h t", h=4)).then_inc(pt_ready, 1)

        @block.vector
        def _(dve):
            step = Chain(dve, dch)
            n0 = LKY // 2
            for a in range(2):
                for j, n in ((0, 0), (1, NKY - n0)):
                    step.mark(dve.tensor_copy(xlow[:, a, j * n0:(j + 1) * n0, :], xh[:, n:n + n0, a, 1:LKX]))
                step.mark(dve.tensor_copy(xlob[:, a, :], xh[:, 0:MB, a, 0]))
            step.join()
            dve.sem_inc(low_ready, 1)
            dve.wait_ge(loaded, 16 * (LOADS - 1))
            dve.wait_ge(pch, 9)
            TT, STT = dve.tensor_tensor, dve.scalar_tensor_tensor
            for t, r in ((qb, qr), (kb, kr)):
                step(TT(t[:, :, 0], t[:, :, 0], r[:, :, 0], ALU.add))
                step(TT(t[:, :, 1], t[:, :, 1], r[:, :, 1], ALU.subtract))
                step(dve.tensor_scalar(t[:, :, :], t[:, :, :], 0.5, None, ALU.mult))
            for q, k, d, m in ((qa, ka, da, MA), (qb, kb, db, MB)):
                wq, wk = skips[0:m, 0, :], skips[0:m, 1, :]
                a, c = tmp[0:m, 0, :], tmp[0:m, 1, :]
                step(TT(a, wq, q[:, :, 0], ALU.add))
                step(TT(d[:, 0, :], a, k[:, :, 0], ALU.mult))
                step(TT(c, q[:, :, 1], k[:, :, 1], ALU.mult))
                step(TT(d[:, 0, :], d[:, 0, :], c, ALU.add))
                step(TT(c, wk, q[:, :, 0], ALU.mult))
                step(TT(d[:, 0, :], d[:, 0, :], c, ALU.add))
                step(TT(a, a, k[:, :, 1], ALU.mult))
                step(TT(c, wk, k[:, :, 0], ALU.add))
                step(TT(c, c, q[:, :, 1], ALU.mult))
                step(TT(d[:, 1, :], c, a, ALU.subtract))
                scale = 2.0 * unit if d is da else two[:, 0:1]
                step(dve.tensor_scalar(d[:, 0:2, :], d[:, 0:2, :], scale, None, ALU.mult))
                step(dve.tensor_scalar(d[:, 2, :], d[:, 1, :], -1.0, None, ALU.mult))
            step(TT(row[:, 0, :], skips[0:1, 0, :], skips[0:1, 1, :], ALU.mult))
            step(TT(row[:, 1, :], skips[0:1, 1, :], kb[0:1, :, 0], ALU.add))
            step(TT(row[:, 1, :], row[:, 1, :], skips[0:1, 4, :], ALU.mult))
            step(dve.tensor_scalar(row[:, :, :], row[:, :, :], unit, None, ALU.mult))
            dve.wait_ge(turned, 2)
            step(dve.tensor_copy(xa[:, :, :], ps_t[0:MA, 0:2 * BT].rearrange("p (a n) -> p a n", a=2)))
            step(dve.tensor_copy(xb[:, :, :], ps_t[0:MB, 2 * BT:4 * BT].rearrange("p (a n) -> p a n", a=2)))
            for b in range(B):
                step(dve.tensor_copy(xrow[:, b * T:(b + 1) * T, :],
                                     xb[0:1, 0, b * T:(b + 1) * T].unsqueeze(1).broadcast_to([1, T, T])))
            dve.sem_inc(d_ready, 1)
            for b in range(B):
                if b:
                    dve.wait_ge(scored, 2 * b)
                for x, p, m in ((xa, pa, MA), (xb, pb, MB)):
                    xt = [x[:, a, b * T:(b + 1) * T].unsqueeze(2).broadcast_to([m, T, T]) for a in range(2)]
                    xs = [x[:, a, b * T:(b + 1) * T].unsqueeze(1).broadcast_to([m, T, T]) for a in range(2)]
                    for j, (u, v) in enumerate(((0, 0), (1, 1), (1, 0), (0, 1))):
                        step.mark(TT(p[:, j, :, :], xt[u], xs[v], ALU.mult))
                step.join()
                dve.sem_inc(prods, 1)
            dve.wait_ge(sc_ready, 2 * B)
            step(dve.tensor_reduce(mx[:, :], sc[:, :, :], AX.X, ALU.max))
            step(TT(sc[:, :, :], sc[:, :, :], mx[:, :].unsqueeze(2).broadcast_to([NH, B * T, T]), ALU.subtract))
            dve.sem_inc(e_ready, 1)
            dve.wait_ge(e_ready, 2)
            step(dve.tensor_reduce(mx[:, :], sc[:, :, :], AX.X, ALU.add))
            step(dve.reciprocal(mx[:, :], mx[:, :]))
            step(TT(sc[:, :, :], sc[:, :, :], mx[:, :].unsqueeze(2).broadcast_to([NH, B * T, T]), ALU.mult))
            dve.sem_inc(p_ready, 1)
            step(TT(coef[:, :], skips[:, 2, :], skips[:, 3, :], ALU.mult))
            dve.wait_ge(pt_ready, 4)
            step(TT(mtt[:, :, :], pt[:, :, :], coef[:, :].unsqueeze(2).broadcast_to([P, NH, BT]), ALU.mult))
            step(dve.tensor_reduce(mt[:, :], mtt[:, :, :].rearrange("p h t -> p t h"), AX.X, ALU.add))


def attended_spectrum(nc, xh, pt, wts, wd, spec, const, tag="l1y"):
    K2 = 2 * NKX
    HF = LKY // 2
    with ExitStack() as ctx:
        s = Scope(nc, ctx, tag)
        ident = s.sb("ident", [P, P])
        sv = s.sb("sv", [NKY, NH, LKX, 2])
        rv = s.sb("rv", [NKY, NH, 2])
        pw = s.sb("pw", [NKY, NH, NKX, 2])
        sk = s.sb("sk", [P, 3, NH])
        pb0 = s.sb("pb0", [P, 1])
        p00 = s.sb("p00", [P, NH])
        a, c, d = (s.sb(n, [NKY, NH, NKX]) for n in ("a", "c", "d"))
        w = s.sb("w", [NKY, NH, 2, NKX])
        ccon = s.sb("ccon", [P, 2, NH])
        wh = [s.sb(f"wh{j}", [P, NKY, 2, NKX]) for j in range(2)]
        xw = [s.sb(f"xw{j}", [P, NKY, 2, NKX]) for j in range(2)]
        t1, t2 = (s.sb(n, [P, NKY, 2, NKX]) for n in ("t1", "t2"))
        yp = s.sb("yp", [P, NKY, 2, 32])
        ps = [s.ps(f"ps{j}") for j in range(3)]
        ps_t = [s.ps(f"ps_t{j}") for j in range(4)]
        (zeroed, loaded, w_ready, w_out, w_in, xw_ready, mixed, yp_ready, turned, copied, dch, pch, made) = (
            s.sem(n) for n in ("zeroed", "loaded", "w_ready", "w_out", "w_in", "xw_ready", "mixed",
                               "yp_ready", "turned", "copied", "dch", "pch", "made"))
        block = ctx.enter_context(nc.Block())
        NL = 1 + 2 + (1 + LKY) + 3 + 2

        @block.sync
        def _(sp):
            n = 0
            sp.wait_ge(zeroed, 1)
            src = wts["value_w"][0].rearrange("h y x a -> y h x a")
            vrow = lambda k: k % LKY
            sp.dma_start(pw[:, :, :, :], wts["proj_w"][:, 0].rearrange("h y x a -> y h x a")).then_inc(loaded, 16)
            sp.dma_start(sv[0:HF, :, :, :], src[0:HF]).then_inc(loaded, 16)
            sp.dma_start(sv[NKY - HF:NKY, :, :, :], src[HF:LKY]).then_inc(loaded, 16)
            n += 3
            for k in range(-HF + 1, HF + 1):
                at = k % NKY
                sp.dma_start(rv[at:at + 1, :, :], src[vrow(-k):vrow(-k) + 1, :, 0, :]).then_inc(loaded, 16)
                n += 1
            for j, name in enumerate(("value_skip_w", "proj_skip_w", "value_skip_b")):
                v = wts[name]
                flat = v.rearrange("a b -> (a b)") if len(v.shape) == 2 else v
                sp.dma_start(sk[:, j, :], flat.unsqueeze(0).broadcast_to([P, NH])).then_inc(loaded, 16)
                n += 1
            sp.dma_start(p00[:, :], wts["proj_w"][:, 0, 0, 0, 0].unsqueeze(0).broadcast_to([P, NH]),
                         allow_slow_non_contiguous=True).then_inc(loaded, 16)
            sp.dma_start(pb0[:, :], wts["proj_skip_b"].unsqueeze(0).broadcast_to([P, 1])).then_inc(loaded, 16)
            n += 2
            assert n == NL - 1, n
            sp.wait_ge(w_ready, 1)
            sp.dma_start(wd.rearrange("h y a x -> y h a x"), w[:, :, :, :]).then_inc(w_out, 16)
            sp.wait_ge(w_out, 16)
            for h in range(NH):
                if h >= 2:
                    sp.wait_ge(xw_ready, h - 1)
                sp.dma_start(wh[h % 2][:, :, :, :], wd[h].unsqueeze(0).broadcast_to([P, NKY, 2, NKX])).then_inc(w_in, 16)
                sp.wait_ge(w_in, 16 * h + 16)

        @block.gpsimd
        def _(pool):
            step = Chain(pool, pch)
            step(pool.memset(sv[:, :, :, :], 0.0))
            step(pool.memset(rv[:, :, :], 0.0))
            pool.sem_inc(zeroed, 1)
            fill_identity(pool, step, ident)
            step(pool.memset(yp[:, :, :, :], 0.0))
            pool.sem_inc(made, 1)

        @block.vector
        def _(dve):
            step = Chain(dve, dch)
            TT = dve.tensor_tensor
            dve.wait_ge(loaded, 16 * (NL - 1))
            dve.wait_ge(made, 1)
            step(TT(sv[:, :, 0, 0], sv[:, :, 0, 0], rv[:, :, 0], ALU.add))
            step(TT(sv[:, :, 0, 1], sv[:, :, 0, 1], rv[:, :, 1], ALU.subtract))
            step(dve.tensor_scalar(sv[:, :, 0, :], sv[:, :, 0, :], 0.5, None, ALU.mult))
            vs = sk[0:NKY, 0, :].unsqueeze(2)
            ps_ = sk[0:NKY, 1, :].unsqueeze(2)
            full, lowx = [NKY, NH, NKX], [NKY, NH, LKX]
            pr, pi = pw[:, :, :, 0], pw[:, :, :, 1]
            step(TT(w[:, :, 0, :], pr, vs.broadcast_to(full), ALU.mult))
            step(TT(w[:, :, 1, :], pi, vs.broadcast_to(full), ALU.mult))
            A_, C_, D_ = a[:, :, 0:LKX], c[:, :, 0:LKX], d[:, :, 0:LKX]
            vr, vi = sv[:, :, :, 0], sv[:, :, :, 1]
            prl, pil = pw[:, :, 0:LKX, 0], pw[:, :, 0:LKX, 1]
            step(TT(A_, prl, ps_.broadcast_to(lowx), ALU.add))
            for part, (u, v, op) in enumerate(((vr, vi, ALU.subtract), (vi, vr, ALU.add))):
                step(TT(C_, A_, u, ALU.mult))
                step(TT(D_, pil, v, ALU.mult))
                step(TT(C_, C_, D_, op))
                step(TT(w[:, :, part, 0:LKX], w[:, :, part, 0:LKX], C_, ALU.add))
            dve.sem_inc(w_ready, 1)
            step(TT(ccon[:, 0, :], p00[:, :], sk[:, 1, :], ALU.add))
            step(TT(ccon[:, 1, :], ccon[:, 0, :], sk[:, 2, :], ALU.mult))
            step(dve.tensor_reduce(const[:, 0:1], ccon[:, 1, :], AX.X, ALU.add))
            step(TT(const[:, 0:1], const[:, 0:1], pb0[:, :], ALU.add))
            for h in range(NH):
                W_ = wh[h % 2]
                dve.wait_ge(w_in, 16 * h + 16)
                if h >= 2:
                    dve.wait_ge(mixed, h - 1)
                both = [P, NKY, 2, NKX]
                step.mark(TT(t1[:, :, :, :], xh[:, :, :, :], W_[:, :, 0:1, :].broadcast_to(both), ALU.mult))
                step(TT(t2[:, :, :, :], xh[:, :, :, :], W_[:, :, 1:2, :].broadcast_to(both), ALU.mult))
                step.mark(TT(xw[h % 2][:, :, 0, :], t1[:, :, 0, :], t2[:, :, 1, :], ALU.subtract))
                step(TT(xw[h % 2][:, :, 1, :], t1[:, :, 1, :], t2[:, :, 0, :], ALU.add))
                dve.sem_inc(xw_ready, 1)
            dve.wait_ge(mixed, NH)
            n = 15
            for j in range(3):
                k0, k1 = n * j, min(n * j + n, NKY)
                step.mark(dve.tensor_copy(yp[:, k0:k1, :, 0:NKX],
                                          ps[j][:, 0:(k1 - k0) * K2].rearrange("p (k a x) -> p k a x", a=2, x=NKX)))
            step.join()
            dve.sem_inc(yp_ready, 1)
            for j in range(NKY // 4):
                dve.wait_ge(turned, j + 1)
                step(dve.tensor_copy(spec[:, :, 4 * j:4 * j + 4],
                                     ps_t[j % 4][0:2 * 32, :].rearrange("p (k t) -> p t k", k=4)))
                dve.sem_inc(copied, 1)

        @block.tensor
        def _(pe):
            pe.wait_ge(made, 1)
            n = 15
            for h in range(NH):
                pe.wait_ge(xw_ready, h + 1)
                for j in range(3):
                    k0, k1 = n * j, min(n * j + n, NKY)
                    last = pe.matmul(ps[j][:, 0:(k1 - k0) * K2], pt[:, h, :],
                                     xw[h % 2][:, k0:k1, :, :].rearrange("p k a x -> p (k a x)"),
                                     start=(h == 0), stop=(h == NH - 1))
                last.then_inc(mixed, 1)
            pe.wait_ge(yp_ready, 1)
            for j in range(NKY // 4):
                if j >= 4:
                    pe.wait_ge(copied, j - 3)
                for k in range(4):
                    last = pe.transpose(ps_t[j % 4][0:64, k * BT:(k + 1) * BT],
                                        yp[:, 4 * j + k, :, :].rearrange("p a x -> p (a x)"), ident[:, :])
                last.then_inc(turned, 1)


def mixed_images(nc, tnd, mt, u, tag="l1m"):
    N = 512
    CH = 4
    with ExitStack() as ctx:
        s = Scope(nc, ctx, tag)
        src = [s.sb(f"src{j}", [P, CH * N]) for j in range(2)]
        dst = [s.sb(f"dst{j}", [P, CH * N]) for j in range(2)]
        ps = [s.ps(f"ps{j}") for j in range(2 * CH)]
        mixed, stored, copied = (s.sem(n) for n in ("mixed", "stored", "copied"))
        loaded = [s.sem(f"loaded{j}") for j in range(2)]
        flat_in = tnd.rearrange("n r c -> n (r c)").rearrange("n (i j k) -> i j n k", j=2, k=CH * N)
        flat_out = u.rearrange("n r c -> n (r c)").rearrange("n (i j k) -> i j n k", j=2, k=CH * N)
        TURNS = IMG // (CH * N)
        block = ctx.enter_context(nc.Block())

        @block.sync
        def _(sp):
            with sp.Fori(0, TURNS // 2) as i:
                for j in range(2):
                    sp.wait_ge(mixed, 2 * i)
                    sp.dma_start(src[j][:, :], flat_in[i, j]).then_inc(loaded[j], 16)

        @block.tensor
        def _(pe):
            with pe.Fori(0, TURNS // 2) as i:
                for j in range(2):
                    pe.wait_ge(loaded[j], 16 * i + 16)
                    pe.wait_ge(copied, 2 * i)
                    for k in range(CH):
                        last = pe.matmul(ps[j * CH + k][:, :], mt[:, :], src[j][:, k * N:(k + 1) * N],
                                         start=True, stop=True)
                    last.then_inc(mixed, 1)

        @block.vector
        def _(dve):
            with dve.Fori(0, TURNS // 2) as i:
                for j in range(2):
                    dve.wait_ge(mixed, 2 * i + j + 1)
                    dve.wait_ge(stored, 32 * i)
                    for k in range(CH):
                        last = dve.tensor_copy(dst[j][:, k * N:(k + 1) * N], ps[j * CH + k][:, :])
                    last.then_inc(copied, 1)

        @block.scalar
        def _(act):
            with act.Fori(0, TURNS // 2) as i:
                for j in range(2):
                    act.wait_ge(copied, 2 * i + j + 1)
                    act.dma_start(flat_out[i, j], dst[j][:, :]).then_inc(stored, 16)
            act.wait_ge(stored, 16 * TURNS)


def token_mixer(nc, spec, const, u, tok, x1, wts, tabs, x2, tag="l1t", eps=1e-5):
    R = 4
    STREAMS = 2
    TURNS = BT // (R * STREAMS)
    NF = R * NKY
    with ExitStack() as ctx:
        s = Scope(nc, ctx, tag)
        rows_fwd = s.sb("rows_fwd", [P, 2 * NKY])
        cols_fwd = s.sb("cols_fwd", [P, 2, P])
        cols_inv = s.sb("cols_inv", [P, 2 * C])
        rows_inv = s.sb("rows_inv", [NKY, 2, P])
        names = ["attn_norm_g", "attn_norm_b", "norm2_g", "norm2_b", "mixer_norm_g1", "mixer_norm_b1",
                 "mixer_norm_g2", "mixer_norm_b2", "mixer_out_g", "mixer_out_b", "mixer_skip_w1",
                 "mixer_skip_b1", "mixer_skip_w2", "mixer_skip_b2"]
        par = s.sb("par", [P, len(names)])
        col = {n: par[:, j:j + 1] for j, n in enumerate(names)}
        wl = [s.sb(f"wl{j}", [P, NKY, 2]) for j in range(2)]
        mw = [s.sb(f"mw{j}", [P, NKY]) for j in range(2)]
        ones = s.sb("ones", [P, P])
        half = s.sb("half", [P, R])

        def per_stream(name, shape):
            return [s.sb(f"{name}{x}", shape) for x in range(STREAMS)]

        sg = per_stream("sg", [64, R, NKY])
        ut, tk, xx, a, xf, attn, m, m1, f, sq, out = (
            per_stream(n, [P, R, C]) for n in ("ut", "tk", "xx", "a", "xf", "attn", "m", "m1", "f", "sq", "out"))
        iv = per_stream("iv", [NKY, 2, R, C])
        o = per_stream("o", [P, 2, R, NKY])
        t = per_stream("t", [P, R, NKY])
        sums = per_stream("sums", [P, 2 * R])
        mean, var, rstd, scale, bias, v2 = (
            per_stream(n, [P, R]) for n in ("mean", "var", "rstd", "scale", "bias", "v2"))
        ps_i = [[s.ps(f"ps_i{x}{j}") for j in range(2)] for x in range(STREAMS)]
        ps_a = [s.ps(f"ps_a{x}") for x in range(STREAMS)]
        ps_m = [s.ps(f"ps_m{x}") for x in range(STREAMS)]
        F0, G0, S0 = 0, R * 64, R * 64 + NF

        def per_stream_sem(name):
            return [s.sem(f"{name}{x}") for x in range(STREAMS)]

        loaded, made, zeroed, prepared, stick, dtick, petick, dch = (s.sem(n) for n in (
            "loaded", "made", "zeroed", "prepared", "stick", "dtick", "petick", "dch"))
        INV, FWD, SUMS, NORMS = 3, 2, 4, 5
        (xin, staged, inv1, iv_ready, inv2, img_ready, fwd1, o_ready, fwd2, t_ready, have, squared, summed,
         totals, var_ready, rstd_ready, xf_ready, pre, stored, out_ready) = (
            per_stream_sem(n) for n in (
                "xin", "staged", "inv1_", "iv_ready", "inv2_", "img_ready", "fwd1_", "o_ready", "fwd2_",
                "t_ready", "have", "squared", "summed", "totals", "var_ready", "rstd_ready", "xf_ready",
                "pre", "stored", "out_ready"))
        block = ctx.enter_context(nc.Block())
        NL = 6 + len(names) + 4

        def view(v):
            return v.rearrange("(i x r) w c -> x i w r c", r=R, x=STREAMS)

        x1v = x1.rearrange("b t w c -> (b t) w c")
        x2v = x2.rearrange("b t w c -> (b t) w c")
        uv, tv, xv, ov = view(u), view(tok), view(x1v), view(x2v)

        @block.sync
        def _(sp):
            sp.wait_ge(zeroed, 1)
            sp.dma_start(rows_fwd[:, :], tabs["rows_fwd"]).then_inc(loaded, 16)
            sp.dma_start(rows_inv[:, :, :].rearrange("p a k -> p (a k)"), tabs["rows_inv"]).then_inc(loaded, 16)
            fwd = tabs["cols_fwd"].rearrange("c (a k) -> c a k", a=2)
            for q in range(2):
                sp.dma_start(cols_fwd[:, :, 64 * q:64 * q + 64], fwd).then_inc(loaded, 16)
                sp.dma_start(cols_inv[64 * q:64 * q + 64, :], tabs["cols_inv"][:, q * 2 * C:(q + 1) * 2 * C]
                             ).then_inc(loaded, 16)
            for n in names:
                v = wts[n]
                flat = v.rearrange("a b -> (a b)") if len(v.shape) == 2 else v
                sp.dma_start(col[n], flat.unsqueeze(0).broadcast_to([P, 1])).then_inc(loaded, 16)
            for j in range(2):
                src = wts[f"mixer_w{j + 1}"][0, 0].rearrange("y x a -> x y a")
                for q in range(2):
                    sp.dma_start(wl[j][32 * q:32 * q + NKX, :, :], src).then_inc(loaded, 16)
                    sp.dma_start(wl[j][64 + 32 * q:64 + 32 * q + NKX, :, :], src).then_inc(zeroed, 16)

            def load(i, x):
                sp.dma_start(ut[x][:, :, :], uv[x, i]).then_inc(xin[x], 16)
                sp.dma_start(tk[x][:, :, :], tv[x, i]).then_inc(xin[x], 16)
                sp.dma_start(xx[x][:, :, :], xv[x, i]).then_inc(xin[x], 16)

            for x in range(STREAMS):
                load(0, x)
            with sp.Fori(0, TURNS - 1) as i:
                for x in range(STREAMS):
                    sp.wait_ge(out_ready[x], i + 1)
                    sp.sem_inc(stick, 1)
                    sp.dma_start(ov[x, i], out[x][:, :, :]).then_inc(stored[x], 16)
                    load(i + 1, x)
            for x in range(STREAMS):
                sp.wait_ge(out_ready[x], TURNS)
                sp.dma_start(ov[x, TURNS - 1], out[x][:, :, :]).then_inc(stored[x], 16)
            for x in range(STREAMS):
                sp.wait_ge(stored[x], 16 * TURNS + 1)

        @block.gpsimd
        def _(pool):
            for j in range(2):
                pool.memset(wl[j][:, :, :], 0.0).then_inc(made, 1)
            pool.wait_ge(made, 2)
            pool.sem_inc(zeroed, 1)
            pool.memset(ones[:, :], 1.0 / IMG).then_inc(made, 1)
            pool.memset(half[:, :], -0.5).then_inc(made, 1)
            pool.wait_ge(made, 4)

            def stage(i, x):
                pool.tensor_copy(sg[x][:, :, :], spec[:, bass.ds((i * STREAMS + x) * R, R), :]).then_inc(staged[x], 1)

            def norms(i):
                for j in range(NORMS):
                    for x in range(STREAMS):
                        pool.wait_ge(var_ready[x], NORMS * i + j + 1)
                        pool.tensor_tensor(rstd[x][:, :], var[x][:, :], half[:, :], ALU.pow).then_inc(rstd_ready[x], 1)

            for x in range(STREAMS):
                stage(0, x)
            with pool.Fori(0, TURNS - 1) as i:
                norms(i)
                for x in range(STREAMS):
                    stage(i + 1, x)
            norms(TURNS - 1)

        @block.tensor
        def _(pe):
            pe.wait_ge(loaded, 16 * NL)
            pe.wait_ge(made, 4)
            pe.wait_ge(prepared, 1)

            def inverse_cols(i, x, src, K):
                for r in range(R):
                    dst = ps_i[x][r // 2][0:NKY, (r % 2) * 2 * C:(r % 2 + 1) * 2 * C]
                    last = pe.matmul(dst, src[:, r, :], cols_inv[0:K, :], start=True, stop=True)
                last.then_inc(inv1[x], 1)

            def inverse_rows(n, i, x):
                pe.wait_ge(iv_ready[x], INV * i + n + 1)
                for k in range(2):
                    last = pe.matmul(ps_a[x][:, :], rows_inv[:, k, :], iv[x][:, k, :, :].rearrange("p r c -> p (r c)"),
                                     start=(k == 0), stop=(k == 1))
                last.then_inc(inv2[x], 1)

            def forward_rows(n, i, x, src):
                pe.wait_ge(img_ready[x], FWD * i + n + 1)
                for r in range(R):
                    last = pe.matmul(ps_m[x][:, F0 + r * 64:F0 + (r + 1) * 64], src[:, r, :], rows_fwd[:, :],
                                     start=True, stop=True)
                last.then_inc(fwd1[x], 1)

            def forward_cols(n, i, x):
                pe.wait_ge(o_ready[x], FWD * i + n + 1)
                for k in range(2):
                    last = pe.matmul(ps_m[x][:, G0:G0 + NF], cols_fwd[:, k, :],
                                     o[x][:, k, :, :].rearrange("p r k -> p (r k)"), start=(k == 0), stop=(k == 1))
                last.then_inc(fwd2[x], 1)

            def total(n, i, x):
                pe.wait_ge(summed[x], SUMS * i + n + 1)
                pe.matmul(ps_m[x][:, S0:S0 + 2 * R], ones[:, :], sums[x][:, :], start=True, stop=True
                          ).then_inc(totals[x], 1)

            both = range(STREAMS)
            with pe.Fori(0, TURNS) as i:
                for x in both:
                    pe.wait_ge(staged[x], i + 1)
                    pe.sem_inc(petick, 1)
                    inverse_cols(i, x, sg[x], 64)
                for x in both:
                    inverse_rows(0, i, x)
                for x in both:
                    total(0, i, x)
                for n in range(2):
                    for x in both:
                        forward_rows(n, i, x, (m, m1)[n][x])
                    for x in both:
                        forward_cols(n, i, x)
                    for x in both:
                        pe.wait_ge(t_ready[x], FWD * i + n + 1)
                        inverse_cols(i, x, t[x], P)
                    for x in both:
                        inverse_rows(n + 1, i, x)
                    for x in both:
                        total(n + 1, i, x)
                for x in both:
                    total(3, i, x)

        @block.scalar
        def _(act):
            def copy_iv(n, i, x):
                act.wait_ge(inv1[x], INV * i + n + 1)
                for q in range(2):
                    last = act.copy(iv[x][:, :, 2 * q:2 * q + 2, :],
                                    ps_i[x][q][0:NKY, :].rearrange("p (r a c) -> p a r c", r=2, a=2))
                last.then_inc(iv_ready[x], 1)

            def square(n, i, x, src):
                act.wait_ge(have[x], 2 * i + n + 1)
                act.activation(sq[x][:, :, :], src[:, :, :], ACT.Square).then_inc(squared[x], 1)

            def copy_o(n, i, x):
                act.wait_ge(fwd1[x], FWD * i + n + 1)
                act.copy(o[x][:, :, :, :], ps_m[x][:, F0:F0 + R * 64].rearrange("p (r a k) -> p a r k", r=R, a=2)
                         ).then_inc(o_ready[x], 1)

            def image(n, i, x):
                act.wait_ge(inv2[x], INV * i + n + 1)
                pa = ps_a[x][:, :].rearrange("p (r c) -> p r c", r=R)
                act.copy(xf[x][:, :, :], pa).then_inc(xf_ready[x], 1)
                act.activation(sq[x][:, :, :], pa, ACT.Square).then_inc(squared[x], 1)

            both = range(STREAMS)
            act.wait_ge(loaded, 16 * NL)
            with act.Fori(0, TURNS) as i:
                for x in both:
                    copy_iv(0, i, x)
                for x in both:
                    square(0, i, x, a[x])
                for x in both:
                    copy_o(0, i, x)
                for x in both:
                    copy_iv(1, i, x)
                for x in both:
                    image(1, i, x)
                for x in both:
                    act.wait_ge(pre[x], i + 1)
                    act.activation(m1[x][:, :, :], f[x][:, :, :], ACT.Gelu, bias=col["mixer_skip_b1"]
                                   ).then_inc(img_ready[x], 1)
                for x in both:
                    copy_o(1, i, x)
                for x in both:
                    copy_iv(2, i, x)
                for x in both:
                    image(2, i, x)
                for x in both:
                    square(1, i, x, f[x])

        @block.vector
        def _(dve):
            step = Chain(dve, dch)
            TT, TS, STT = dve.tensor_tensor, dve.tensor_scalar, dve.scalar_tensor_tensor
            dve.wait_ge(loaded, 16 * NL)
            dve.wait_ge(zeroed, 1 + 16 * 4)
            for j in range(2):
                step(dve.tensor_copy(mw[j][0:64, :], wl[j][0:64, :, 0]))
                step(dve.tensor_copy(mw[j][64:P, :], wl[j][64:P, :, 1]))
            dve.sem_inc(prepared, 1)
            for x in range(STREAMS):
                dve.sem_inc(stored[x], 1)

            def affine(n, i, x, g, b, extra=None):
                dve.wait_ge(rstd_ready[x], NORMS * i + n + 1)
                step(TS(scale[x][:, :], rstd[x][:, :], col[g], None, ALU.mult))
                step(TT(bias[x][:, :], mean[x][:, :], scale[x][:, :], ALU.mult))
                step(TS(bias[x][:, :], bias[x][:, :], -1.0, col[b], ALU.mult, ALU.add))
                if extra:
                    step(TS(bias[x][:, :], bias[x][:, :], col[extra], None, ALU.add))

            def sum_up(n, i, x, src):
                step.mark(dve.tensor_reduce(sums[x][:, 0:R], src[:, :, :], AX.X, ALU.add))
                dve.wait_ge(squared[x], SUMS * i + n + 1)
                step(dve.tensor_reduce(sums[x][:, R:2 * R], sq[x][:, :, :], AX.X, ALU.add))
                dve.sem_inc(summed[x], 1)

            def moments(n, i, x):
                dve.wait_ge(totals[x], SUMS * i + n + 1)
                step(dve.tensor_copy(mean[x][:, :], ps_m[x][:, S0:S0 + R]))
                step(TT(var[x][:, :], mean[x][:, :], mean[x][:, :], ALU.mult))
                step(STT(out=var[x][:, :], in0=ps_m[x][:, S0 + R:S0 + 2 * R], scalar=eps, in1=var[x][:, :],
                         op0=ALU.add, op1=ALU.subtract))
                dve.sem_inc(var_ready[x], 1)

            SUMUP, MOMENTS, AFF = 2, 3, 3

            def apply(x, dst, src):
                for r in range(R):
                    step.mark(TS(dst[:, r, :], src[:, r, :], scale[x][:, r:r + 1], bias[x][:, r:r + 1], ALU.mult, ALU.add))
                step.join()

            def spectral(n, i, x):
                dve.wait_ge(fwd2[x], FWD * i + n + 1)
                step(TT(t[x][:, :, :], ps_m[x][:, G0:G0 + NF].rearrange("p (r k) -> p r k", r=R),
                        mw[n][:, :].unsqueeze(1).broadcast_to([P, R, NKY]), ALU.mult))
                dve.sem_inc(t_ready[x], 1)

            both = range(STREAMS)
            per = (2 + SUMUP + MOMENTS + AFF + R) + (4 + AFF + R) + 1 + (SUMUP + MOMENTS + AFF + R + 1) + 1 + (
                SUMUP + MOMENTS + AFF + 1 + R + 1) + (SUMUP + MOMENTS + AFF + R + 2)
            with step.loop(TURNS, STREAMS * per) as i:
                for x in both:
                    dve.wait_ge(xin[x], 48 * (i + 1))
                    dve.wait_ge(inv2[x], INV * i + 1)
                    pa = ps_a[x][:, :].rearrange("p (r c) -> p r c", r=R)
                    step(STT(out=a[x][:, :, :], in0=pa, scalar=const[:, 0:1], in1=ut[x][:, :, :], op0=ALU.add, op1=ALU.add))
                    step(TT(a[x][:, :, :], a[x][:, :, :], tk[x][:, :, :], ALU.add))
                    dve.sem_inc(have[x], 1)
                for x in both:
                    sum_up(0, i, x, a[x])
                for x in both:
                    moments(0, i, x)
                for x in both:
                    affine(0, i, x, "attn_norm_g", "attn_norm_b")
                    apply(x, attn[x], a[x])
                    step(STT(out=v2[x][:, :], in0=var[x][:, :], scalar=-eps, in1=scale[x][:, :], op0=ALU.add, op1=ALU.mult))
                    step(TT(v2[x][:, :], v2[x][:, :], scale[x][:, :], ALU.mult))
                    step(TS(var[x][:, :], v2[x][:, :], eps, None, ALU.add))
                    step(TS(mean[x][:, :], half[:, :], 0.0, col["attn_norm_b"], ALU.mult, ALU.add))
                    dve.sem_inc(var_ready[x], 1)
                for x in both:
                    affine(1, i, x, "norm2_g", "norm2_b")
                    apply(x, m[x], attn[x])
                    dve.sem_inc(img_ready[x], 1)
                for x in both:
                    spectral(0, i, x)
                for x in both:
                    dve.wait_ge(xf_ready[x], 2 * i + 1)
                    dve.sem_inc(dtick, 1)
                    sum_up(1, i, x, xf[x])
                for x in both:
                    moments(1, i, x)
                for x in both:
                    affine(2, i, x, "mixer_norm_g1", "mixer_norm_b1")
                    apply(x, f[x], xf[x])
                    step(STT(out=f[x][:, :, :], in0=m[x][:, :, :], scalar=col["mixer_skip_w1"], in1=f[x][:, :, :],
                             op0=ALU.mult, op1=ALU.add))
                    dve.sem_inc(pre[x], 1)
                for x in both:
                    spectral(1, i, x)
                for x in both:
                    dve.wait_ge(xf_ready[x], 2 * i + 2)
                    dve.sem_inc(dtick, 1)
                    sum_up(2, i, x, xf[x])
                for x in both:
                    moments(2, i, x)
                for x in both:
                    affine(3, i, x, "mixer_norm_g2", "mixer_norm_b2", "mixer_skip_b2")
                    apply(x, f[x], xf[x])
                    step(STT(out=f[x][:, :, :], in0=m1[x][:, :, :], scalar=col["mixer_skip_w2"], in1=f[x][:, :, :],
                             op0=ALU.mult, op1=ALU.add))
                    dve.sem_inc(have[x], 1)
                for x in both:
                    sum_up(3, i, x, f[x])
                for x in both:
                    moments(3, i, x)
                for x in both:
                    affine(4, i, x, "mixer_out_g", "mixer_out_b")
                    dve.wait_ge(stored[x], 16 * i + 1)
                    apply(x, out[x], f[x])
                    step(TT(out[x][:, :, :], out[x][:, :, :], attn[x][:, :, :], ALU.add))
                    step(TT(out[x][:, :, :], out[x][:, :, :], xx[x][:, :, :], ALU.add))
                    dve.sem_inc(out_ready[x], 1)


def batch_tokens(x, b):
    return x[b].rearrange("t w c -> w t c")


def linear_attention(nc, x2, Wq, bq, Wk, bk, Wv, bv, Wo, bo, x3, tag="lin", eps=1e-5):
    H = 8
    D = C // H
    R = 4
    KT = T // R
    with ExitStack() as ctx:
        s = Scope(nc, ctx, tag)
        wq, wk, wv, wo = (s.sb(n, [P, C]) for n in ("wq", "wk", "wv", "wo"))
        bqc = s.sb("bqc", [P, 1])
        bk_row, bo_row, ones1 = (s.sb(n, [1, C]) for n in ("bk_row", "bo_row", "ones1"))
        bv_b = s.sb("bv_b", [P, C])
        ident, ones = s.sb("ident", [P, P]), s.sb("ones", [P, P])
        heads = s.sb("heads", [P, H, D])
        xb = s.sb("xb", [P, T, C])
        u = s.sb("u", [P, T, C])
        uT = s.sb("uT", [P, T * W])
        us = s.sb("us", [P, R, C])
        uTs = s.sb("uTs", [P, R * W])
        st = s.sb("st", [P, T, 6])
        mv = s.sb("mv", [P, T, 2])
        ve, rstd, half = (s.sb(n, [P, T]) for n in ("ve", "rstd", "half"))
        mn, ex, phi = (s.sb(n, [P, R * C]) for n in ("mn", "ex", "phi"))
        acc = s.sb("acc", [P, 2, C])
        kv, kvt, g, kb = (s.sb(n, [P, C]) for n in ("kv", "kvt", "g", "kb"))
        rd = s.sb("rd", [P, R * W])
        phz = s.sb("phz", [P, R * W])
        out = s.sb("out", [P, R, C])
        ps_t, ps_k, ps_m, ps_n, ps_x, ps_q, ps_d, ps_o = (
            s.ps(n) for n in ("ps_t", "ps_k", "ps_m", "ps_n", "ps_x", "ps_q", "ps_d", "ps_o"))
        (loaded, made, xin, ve_ready, rstd_ready, u_ready, staged, turned, uT_ready, kept, k_done, mn_ready,
         ex_ready, phi_ready, acc_done, acc_read, kv_done, kv_ready, kvt_done, kvt_ready, g_done, g_ready,
         q_done, qmn, qex, qphi, den_done, phz_ready, o_done, out_ready, stored, dch, pch, tick) = (
            s.sem(n) for n in (
                "loaded", "made", "xin", "ve_ready", "rstd_ready", "u_ready", "staged", "turned", "uT_ready",
                "kept", "k_done", "mn_ready", "ex_ready", "phi_ready", "acc_done", "acc_read", "kv_done",
                "kv_ready", "kvt_done", "kvt_ready", "g_done", "g_ready", "q_done", "qmn", "qex", "qphi",
                "den_done", "phz_ready", "o_done", "out_ready", "stored", "dch", "pch", "tick"))
        block = ctx.enter_context(nc.Block())
        NL = 8

        @block.sync
        def _(sp):
            for dst, src in ((wq, Wq), (wk, Wk), (wv, Wv), (wo, Wo)):
                sp.dma_start(dst[:, :], src).then_inc(loaded, 16)
            sp.dma_start(bqc[:, :], bq.unsqueeze(1)).then_inc(loaded, 16)
            sp.dma_start(bk_row[:, :], bk.unsqueeze(0)).then_inc(loaded, 16)
            sp.dma_start(bo_row[:, :], bo.unsqueeze(0)).then_inc(loaded, 16)
            sp.dma_start(bv_b[:, :], bv.unsqueeze(0).broadcast_to([P, C])).then_inc(loaded, 16)
            rows = x3.rearrange("b (k r) w c -> b k w r c", r=R)
            with sp.Fori(0, B) as b:
                sp.wait_ge(out_ready, b * KT)
                for k in range(KT):
                    sp.dma_start(xb[:, k * R:(k + 1) * R, :], x2[b][k * R:(k + 1) * R].rearrange("t w c -> w t c")
                                 ).then_inc(xin, 16)
                with sp.Fori(0, KT) as k:
                    sp.wait_ge(out_ready, b * KT + k + 1)
                    sp.dma_start(rows[b, k], out[:, :, :]).then_inc(stored, 16)
            sp.wait_ge(stored, 16 * B * KT)

        @block.gpsimd
        def _(pool):
            step = Chain(pool, pch)
            fill_identity(pool, step, ident)
            step(pool.memset(ones[:, :], 1.0))
            step(pool.memset(ones1[:, :], 1.0))
            step(pool.memset(half[:, :], -0.5))
            step(pool.memset(heads[:, :, :], 1.0))
            step(pool.affine_select(out=heads[:, :, :], in_=heads[:, :, :], compare_op=ALU.is_ge, fill=0.0,
                                    base=0, pattern=[[-D, H], [0, D]], channel_multiplier=1))
            step(pool.affine_select(out=heads[:, :, :], in_=heads[:, :, :], compare_op=ALU.is_ge, fill=0.0,
                                    base=D - 1, pattern=[[D, H], [0, D]], channel_multiplier=-1))
            pool.sem_inc(made, 1)
            with pool.Fori(0, B) as b:
                pool.wait_ge(ve_ready, b + 1)
                pool.tensor_tensor(rstd[:, :], ve[:, :], half[:, :], ALU.pow).then_inc(rstd_ready, 1)
                pool.wait_ge(u_ready, b + 1)
                pool.sem_inc(tick, 1)
                with pool.Fori(0, KT) as k:
                    pool.wait_ge(acc_done, b * KT + k)
                    pool.tensor_copy(us[:, :, :], u[:, bass.ds(k * R, R), :]).then_inc(staged, 1)
                    pool.wait_ge(uT_ready, b * KT + k + 1)
                    pool.tensor_copy(uT[:, bass.ds(k * R * W, R * W)], uTs[:, :]).then_inc(kept, 1)

        @block.tensor
        def _(pe):
            pe.wait_ge(loaded, 16 * NL)
            pe.wait_ge(made, 1)
            with pe.Fori(0, B) as b:
                with pe.Fori(0, KT) as k:
                    n = b * KT + k
                    pe.wait_ge(staged, n + 1)
                    for r in range(R):
                        last = pe.transpose(ps_t[:, r * W:(r + 1) * W], us[:, r, :], ident[:, :])
                    last.then_inc(turned, 1)
                    pe.wait_ge(uT_ready, n + 1)
                    for r in range(R):
                        cols = slice(r * C, (r + 1) * C)
                        pe.matmul(ps_k[:, cols], uTs[:, r * W:(r + 1) * W], wk[:, :], start=True, stop=False)
                        last = pe.matmul(ps_k[:, cols], ones1[:, :], bk_row[:, :], start=False, stop=True)
                    last.then_inc(k_done, 1)
                    pe.wait_ge(phi_ready, n + 1)
                    pe.wait_ge(acc_read, n)
                    for r in range(R):
                        pe.matmul(ps_m[:, 0:C], us[:, r, :], phi[:, r * C:(r + 1) * C], start=(r == 0), stop=(r == R - 1))
                    for r in range(R):
                        last = pe.matmul(ps_n[:, 0:C], phi[:, r * C:(r + 1) * C], ones[:, :], start=(r == 0), stop=(r == R - 1))
                    last.then_inc(acc_done, 1)
                pe.wait_ge(acc_read, (b + 1) * KT)
                pe.matmul(ps_x[:, 0:C], acc[:, 0, :], wv[:, :], start=True, stop=True).then_inc(kv_done, 1)
                pe.wait_ge(kv_ready, b + 1)
                pe.transpose(ps_x[:, C:2 * C], kv[:, :], ident[:, :]).then_inc(kvt_done, 1)
                pe.wait_ge(kvt_ready, b + 1)
                pe.matmul(ps_x[:, 2 * C:3 * C], kvt[:, :], wo[:, :], start=True, stop=True).then_inc(g_done, 1)
                pe.wait_ge(g_ready, b + 1)
                pe.wait_ge(kept, (b + 1) * KT)
                pe.sem_inc(tick, 1)
                with pe.Fori(0, KT) as k:
                    n = b * KT + k
                    pe.matmul(ps_q[:, :], wq[:, :], uT[:, bass.ds(k * R * W, R * W)], start=True, stop=True).then_inc(q_done, 1)
                    pe.wait_ge(qphi, n + 1)
                    pe.matmul(ps_d[:, :], kb[:, :], phi[:, :], start=True, stop=True).then_inc(den_done, 1)
                    pe.wait_ge(phz_ready, n + 1)
                    for r in range(R):
                        cols = slice(r * C, (r + 1) * C)
                        pe.matmul(ps_o[:, cols], phz[:, r * W:(r + 1) * W], g[:, :], start=True, stop=False)
                        last = pe.matmul(ps_o[:, cols], ones1[:, :], bo_row[:, :], start=False, stop=True)
                    last.then_inc(o_done, 1)

        @block.scalar
        def _(act):
            with act.Fori(0, B) as b:
                with act.Fori(0, KT) as k:
                    n = b * KT + k
                    act.wait_ge(turned, n + 1)
                    act.wait_ge(kept, n)
                    act.copy(uTs[:, :], ps_t[:, :]).then_inc(uT_ready, 1)
                    act.wait_ge(mn_ready, n + 1)
                    act.activation(ex[:, :], mn[:, :], ACT.Exp).then_inc(ex_ready, 1)
                with act.Fori(0, KT) as k:
                    n = b * KT + k
                    act.wait_ge(qmn, n + 1)
                    act.activation(ex[:, :], mn[:, :], ACT.Exp).then_inc(qex, 1)

        @block.vector
        def _(dve):
            step = Chain(dve, dch)
            TT, TS, STT = dve.tensor_tensor, dve.tensor_scalar, dve.scalar_tensor_tensor
            dve.wait_ge(loaded, 16 * NL)
            dve.wait_ge(made, 1)
            hm = heads[:, :, :].rearrange("p h d -> p (h d)")
            BASE = 2 * T + 4
            P1, FIN, P2 = 3, 5, 6
            per = BASE + P1 * KT + FIN + P2 * KT
            with dve.Fori(0, B) as b:
                start = b * per
                step.base, step.k = start, 0
                dve.wait_ge(xin, 16 * KT * (b + 1))
                for t in range(T):
                    step.mark(dve.bn_stats(st[:, t, :], xb[:, t, :]))
                step.join()
                dve.sem_inc(tick, 1)
                for t in range(T):
                    step.mark(dve.bn_aggr(mv[:, t, :], st[:, t, :]))
                step.join()
                step(TS(ve[:, :], mv[:, :, 1], eps, None, ALU.add))
                dve.sem_inc(ve_ready, 1)
                dve.wait_ge(rstd_ready, b + 1)
                step(TT(u[:, :, :], xb[:, :, :], mv[:, :, 0:1].broadcast_to([P, T, C]), ALU.subtract))
                step(TT(u[:, :, :], u[:, :, :], rstd[:, :].unsqueeze(2).broadcast_to([P, T, C]), ALU.mult))
                dve.sem_inc(u_ready, 1)
                step(dve.memset(acc[:, :, :], 0.0))
                assert step.k == BASE
                dve.sem_inc(tick, 1)
                with dve.Fori(0, KT) as k:
                    n = b * KT + k
                    step.base, step.k = start + BASE + k * P1, 0
                    dve.wait_ge(k_done, n + 1)
                    dve.tensor_scalar(mn[:, :], ps_k[:, :], 0.0, None, ALU.min).then_inc(mn_ready, 1)
                    dve.wait_ge(ex_ready, n + 1)
                    step(STT(out=phi[:, :], in0=ps_k[:, :], scalar=0.0, in1=ex[:, :], op0=ALU.max, op1=ALU.add))
                    dve.sem_inc(phi_ready, 1)
                    dve.wait_ge(acc_done, n + 1)
                    step(TT(acc[:, 0, :], acc[:, 0, :], ps_m[:, 0:C], ALU.add))
                    step(TT(acc[:, 1, :], acc[:, 1, :], ps_n[:, 0:C], ALU.add))
                    dve.sem_inc(acc_read, 1)
                    assert step.k == P1
                step.base, step.k = start + BASE + P1 * KT, 0
                dve.wait_ge(kv_done, b + 1)
                step(TT(kv[:, :], acc[:, 1, :], bv_b[:, :], ALU.mult))
                step(TT(kv[:, :], kv[:, :], ps_x[:, 0:C], ALU.add))
                step(TT(kv[:, :], kv[:, :], hm, ALU.mult))
                dve.sem_inc(kv_ready, 1)
                step(TT(kb[:, :], acc[:, 1, :], hm, ALU.mult))
                dve.wait_ge(kvt_done, b + 1)
                dve.tensor_copy(kvt[:, :], ps_x[:, C:2 * C]).then_inc(kvt_ready, 1)
                dve.wait_ge(g_done, b + 1)
                step(dve.tensor_copy(g[:, :], ps_x[:, 2 * C:3 * C]))
                dve.sem_inc(g_ready, 1)
                assert step.k == FIN
                dve.sem_inc(tick, 1)
                with dve.Fori(0, KT) as k:
                    n = b * KT + k
                    step.base, step.k = start + BASE + P1 * KT + FIN + k * P2, 0
                    dve.wait_ge(q_done, n + 1)
                    dve.tensor_scalar(mn[:, :], ps_q[:, :], bqc[:, 0:1], 0.0, ALU.add, ALU.min).then_inc(qmn, 1)
                    step(TS(phi[:, :], ps_q[:, :], bqc[:, 0:1], 0.0, ALU.add, ALU.max))
                    dve.wait_ge(qex, n + 1)
                    step(TT(phi[:, :], phi[:, :], ex[:, :], ALU.add))
                    dve.sem_inc(qphi, 1)
                    dve.wait_ge(den_done, n + 1)
                    step(TS(rd[:, :], ps_d[:, :], eps, None, ALU.add))
                    step(dve.reciprocal(rd[:, :], rd[:, :]))
                    step(TT(phz[:, :], phi[:, :], rd[:, :], ALU.mult))
                    dve.sem_inc(phz_ready, 1)
                    dve.wait_ge(o_done, n + 1)
                    dve.wait_ge(stored, 16 * n)
                    step(TT(out[:, :, :], ps_o[:, :].rearrange("p (r c) -> p r c", r=R), xb[:, bass.ds(k * R, R), :], ALU.add))
                    dve.sem_inc(out_ready, 1)
                    assert step.k == P2


def routed_experts(nc, x3, gate_w, gate_b, w1, w2, x4, tag="moe", eps=1e-5):
    E = gate_w.shape[0]
    HID = w1.shape[2]
    HC = HID // P
    R = 4
    KT = T // R
    L = T * W
    NEG = -3.0e38
    with ExitStack() as ctx:
        s = Scope(nc, ctx, tag)
        ident = s.sb("ident", [P, P])
        gT = s.sb("gT", [P, E])
        wt = s.sb("wt", [P, 2, L])
        poolT = s.sb("poolT", [P, E, B])
        eo = s.sb("eo", [P, 2, C])
        u_d = nc.dram_tensor(f"{tag}_u", (BT, W, C), f32, kind="Internal").ap()
        with ExitStack() as c2:
            s2 = Scope(nc, c2, tag + "a")
            gw = s2.sb("gw", [E, C])
            gb = s2.sb("gb", [P, 1])
            xb = s2.sb("xb", [P, T, C])
            u = s2.sb("u", [P, T, C])
            us = s2.sb("us", [P, R, C])
            uTs = s2.sb("uTs", [P, R * W])
            st = s2.sb("st", [P, T, 6])
            mv = s2.sb("mv", [P, T, 2])
            ve, rstd, half = (s2.sb(n, [P, T]) for n in ("ve", "rstd", "half"))
            ps_t, ps_l, ps_g = s2.ps("ps_t"), s2.ps("ps_l"), s2.ps("ps_g")
            (loaded, made, g_done, g_ready, xin, ve_ready, rstd_ready, u_ready, staged, turned, uT_ready,
             l_done, l_ready, saved, dch, pch, tick) = (
                s2.sem(n) for n in ("loaded", "made", "g_done", "g_ready", "xin", "ve_ready", "rstd_ready",
                                    "u_ready", "staged", "turned", "uT_ready", "l_done", "l_ready", "saved",
                                    "dch", "pch", "tick"))
            block = c2.enter_context(nc.Block())

            @block.sync
            def _(sp):
                sp.dma_start(gw[:, :], gate_w).then_inc(loaded, 16)
                for j in range(2):
                    sp.dma_start(gb[j * E:(j + 1) * E, :], gate_b.unsqueeze(1)).then_inc(loaded, 16)
                for b in range(B):
                    if b:
                        sp.wait_ge(u_ready, b)
                    sp.dma_start(xb[:, :, :], batch_tokens(x3, b)).then_inc(xin, 16)
                    sp.wait_ge(u_ready, b + 1)
                    sp.dma_start(u_d[b * T:(b + 1) * T].rearrange("t w c -> w t c"), u[:, :, :]).then_inc(saved, 16)
                sp.wait_ge(saved, 16 * B)

            @block.gpsimd
            def _(pool):
                step = Chain(pool, pch)
                fill_identity(pool, step, ident)
                step(pool.memset(half[:, :], -0.5))
                pool.sem_inc(made, 1)
                for b in range(B):
                    pool.wait_ge(ve_ready, b + 1)
                    pool.tensor_tensor(rstd[:, :], ve[:, :], half[:, :], ALU.pow).then_inc(rstd_ready, 1)
                    pool.wait_ge(u_ready, b + 1)
                    with pool.Fori(0, KT) as k:
                        pool.wait_ge(turned, k + b * KT)
                        pool.tensor_copy(us[:, :, :], u[:, bass.ds(k * R, R), :]).then_inc(staged, 1)

            @block.tensor
            def _(pe):
                pe.wait_ge(loaded, 48)
                pe.wait_ge(made, 1)
                pe.transpose(ps_g[:, 0:E], gw[:, :], ident[0:E, 0:E]).then_inc(g_done, 1)
                pe.wait_ge(g_ready, 1)
                for b in range(B):
                    rows = slice((b % 2) * E, (b % 2 + 1) * E)
                    with pe.Fori(0, KT) as k:
                        n = k + b * KT
                        pe.wait_ge(staged, n + 1)
                        pe.wait_ge(uT_ready, n)
                        for r in range(R):
                            last = pe.transpose(ps_t[:, r * W:(r + 1) * W], us[:, r, :], ident[:, :])
                        last.then_inc(turned, 1)
                        pe.wait_ge(uT_ready, n + 1)
                        pe.wait_ge(l_ready, n)
                        pe.matmul(ps_l[rows, :], gT[:, :], uTs[:, :], start=True, stop=True,
                                  tile_position=(0, (b % 2) * E)).then_inc(l_done, 1)

            @block.scalar
            def _(act):
                act.wait_ge(g_done, 1)
                act.copy(gT[:, :], ps_g[:, 0:E]).then_inc(g_ready, 1)
                for b in range(B):
                    rows = slice((b % 2) * E, (b % 2 + 1) * E)
                    with act.Fori(0, KT) as k:
                        n = k + b * KT
                        act.wait_ge(turned, n + 1)
                        act.wait_ge(l_done, n)
                        act.copy(uTs[:, :], ps_t[:, :]).then_inc(uT_ready, 1)
                        act.wait_ge(l_done, n + 1)
                        act.activation(wt[rows, b // 2, bass.ds(k * R * W, R * W)], ps_l[rows, :], ACT.Identity,
                                       bias=gb[rows, 0:1]).then_inc(l_ready, 1)

            @block.vector
            def _(dve):
                step = Chain(dve, dch)
                TT = dve.tensor_tensor
                for b in range(B):
                    dve.wait_ge(xin, 16 * (b + 1))
                    for t in range(T):
                        step.mark(dve.bn_stats(st[:, t, :], xb[:, t, :]))
                    step.join()
                    for t in range(T):
                        step.mark(dve.bn_aggr(mv[:, t, :], st[:, t, :]))
                    step.join()
                    step(dve.tensor_scalar(ve[:, :], mv[:, :, 1], eps, None, ALU.add))
                    dve.sem_inc(ve_ready, 1)
                    dve.wait_ge(rstd_ready, b + 1)
                    if b:
                        dve.wait_ge(staged, b * KT)
                        dve.wait_ge(saved, 16 * b)
                    step(TT(u[:, :, :], xb[:, :, :], mv[:, :, 0:1].broadcast_to([P, T, C]), ALU.subtract))
                    step(TT(u[:, :, :], u[:, :, :], rstd[:, :].unsqueeze(2).broadcast_to([P, T, C]), ALU.mult))
                    dve.sem_inc(u_ready, 1)

        with ExitStack() as c2:
            s2 = Scope(nc, c2, tag + "b")
            top = s2.sb("top", [P, 2, 8])
            nmx = s2.sb("nmx", [P, 2])
            den = s2.sb("den", [P, 2])
            rest = s2.sb("rest", [P, 2, L])
            pr = s2.sb("pr", [P, 2, L])
            neg_ready, ex_ready, dch = s2.sem("neg_ready"), s2.sem("ex_ready"), s2.sem("dch")
            block = c2.enter_context(nc.Block())

            @block.scalar
            def _(act):
                for j in range(2):
                    act.wait_ge(neg_ready, j + 1)
                    act.activation(pr[:, j, :], wt[:, j, :], ACT.Exp, bias=nmx[:, j:j + 1],
                                   accum_out=den[:, j:j + 1]).then_inc(ex_ready, 1)

            @block.vector
            def _(dve):
                step = Chain(dve, dch)
                for j in range(2):
                    step(dve.max(top[:, j, :], wt[:, j, :]))
                    step(dve.tensor_scalar(nmx[:, j:j + 1], top[:, j, 0:1], -1.0, None, ALU.mult))
                    dve.sem_inc(neg_ready, 1)
                    step(dve.match_replace(rest[:, j, :], top[:, j, :], wt[:, j, :], NEG))
                for j in range(2):
                    dve.wait_ge(ex_ready, j + 1)
                    step(dve.tensor_tensor(rest[:, j, :], rest[:, j, :], wt[:, j, :], ALU.not_equal))
                    step(dve.reciprocal(den[:, j:j + 1], den[:, j:j + 1]))
                    step(dve.scalar_tensor_tensor(out=wt[:, j, :], in0=pr[:, j, :], scalar=den[:, j:j + 1],
                                                  in1=rest[:, j, :], op0=ALU.mult, op1=ALU.mult))

        with ExitStack() as c2:
            s2 = Scope(nc, c2, tag + "c")
            ur = [s2.sb(f"ur{j}", [P, R, C]) for j in range(2)]
            ws = s2.sb("ws", [P, R * W])
            wT = [s2.sb(f"wT{j}", [P, R, E]) for j in range(2)]
            acc = s2.sb("acc", [P, B, E])
            ps_w = s2.ps("ps_w")
            ps_p = [s2.ps(f"ps_p{j}") for j in range(2)]
            uin = [s2.sem(f"uin{j}") for j in range(2)]
            staged, turned, wT_ready, pooled, added, dch = (s2.sem(n) for n in (
                "staged", "turned", "wT_ready", "pooled", "added", "dch"))
            block = c2.enter_context(nc.Block())
            uv = u_d.rearrange("(b i j r) w c -> b i j w r c", b=B, j=2, r=R)

            @block.sync
            def _(sp):
                for b in range(B):
                    with sp.Fori(0, KT // 2) as i:
                        for j in range(2):
                            sp.wait_ge(pooled, i * 2 + b * KT + j - 1) if j else sp.wait_ge(pooled, i * 2 + b * KT)
                            sp.dma_start(ur[j][:, :, :], uv[b][i, j]).then_inc(uin[j], 16)

            @block.gpsimd
            def _(pool):
                for b in range(B):
                    rows = slice((b % 2) * E, (b % 2 + 1) * E)
                    with pool.Fori(0, KT) as k:
                        pool.wait_ge(turned, k + b * KT)
                        pool.tensor_copy(ws[:, :], wt[:, b // 2, bass.ds(k * R * W, R * W)]).then_inc(staged, 1)

            @block.tensor
            def _(pe):
                for b in range(B):
                    with pe.Fori(0, KT // 2) as i:
                        for j in range(2):
                            n = i * 2 + b * KT + j
                            pe.wait_ge(staged, n + 1)
                            pe.wait_ge(wT_ready, n)
                            for r in range(R):
                                last = pe.transpose(ps_w[:, r * P:(r + 1) * P], ws[:, r * W:(r + 1) * W], ident[:, :])
                            last.then_inc(turned, 1)
                            pe.wait_ge(wT_ready, n + 1)
                            pe.wait_ge(uin[j], i * 16 + b * 16 * (KT // 2) + 16)
                            pe.wait_ge(added, i * 2 + b * KT)
                            for r in range(R):
                                last = pe.matmul(ps_p[j][:, 0:E], ur[j][:, r, :], wT[j][:, r, :],
                                                 start=(r == 0), stop=(r == R - 1))
                            last.then_inc(pooled, 1)

            @block.scalar
            def _(act):
                for b in range(B):
                    cols = slice((b % 2) * E, (b % 2 + 1) * E)
                    with act.Fori(0, KT // 2) as i:
                        for j in range(2):
                            n = i * 2 + b * KT + j
                            act.wait_ge(turned, n + 1)
                            act.wait_ge(pooled, i * 2 + b * KT)
                            act.copy(wT[j][:, :, :], ps_w[:, :].rearrange("p (r e) -> p r e", r=R)[:, :, cols]
                                     ).then_inc(wT_ready, 1)

            @block.vector
            def _(dve):
                step = Chain(dve, dch)
                step(dve.memset(acc[:, :, :], 0.0))
                for b in range(B):
                    with step.loop(KT // 2, 2) as i:
                        for j in range(2):
                            dve.wait_ge(pooled, i * 2 + b * KT + j + 1)
                            step(dve.tensor_tensor(acc[:, b, :], acc[:, b, :], ps_p[j][:, 0:E], ALU.add))
                            dve.sem_inc(added, 1)
                step(dve.tensor_copy(poolT[:, :, :], acc[:, :, :].rearrange("p b e -> p e b")))

        with ExitStack() as c2:
            s2 = Scope(nc, c2, tag + "d")
            NB = 4
            wa = [s2.sb(f"wa{j}", [P, HID]) for j in range(NB)]
            ab = [s2.sb(f"ab{j}", [1, HID]) for j in range(NB)]
            wb = [s2.sb(f"wb{j}", [P, HC, C]) for j in range(NB)]
            bb = [s2.sb(f"bb{j}", [1, C]) for j in range(NB)]
            ones1 = s2.sb("ones1", [1, B])
            h = [s2.sb(f"h{j}", [P, HC * B]) for j in range(2)]
            eoT = s2.sb("eoT", [P, B, E])
            ps_h = [s2.ps(f"ps_h{j}") for j in range(2)]
            ps_e = s2.ps("ps_e")
            ps_f = s2.ps("ps_f")
            win = [s2.sem(f"win{j}") for j in range(NB)]
            made, hid, h_ready, outd, eo_t, flipped, eo_ready = (s2.sem(n) for n in (
                "made", "hid", "h_ready", "outd", "eo_t", "flipped", "eo_ready"))
            tick = s2.sem("tick")
            block = c2.enter_context(nc.Block())
            w1v = w1.rearrange("(i j) d h -> i j d h", j=NB)
            w2v = w2.rearrange("(i j) h o -> i j h o", j=NB)

            @block.sync
            def _(sp):
                with sp.Fori(0, E // NB) as i:
                    for j in range(NB):
                        sp.wait_ge(outd, i * NB)
                        sp.dma_start(wa[j][:, :], w1v[i, j][0:P]).then_inc(win[j], 16)
                        sp.dma_start(ab[j][:, :], w1v[i, j][P:P + 1]).then_inc(win[j], 16)
                        sp.dma_start(wb[j][:, :, :], w2v[i, j][0:HID].rearrange("(k p) o -> p k o", p=P)).then_inc(win[j], 16)
                        sp.dma_start(bb[j][:, :], w2v[i, j][HID:HID + 1]).then_inc(win[j], 16)

            @block.gpsimd
            def _(pool):
                pool.memset(ones1[:, :], 1.0).then_inc(made, 1)

            @block.tensor
            def _(pe):
                pe.wait_ge(made, 1)
                with pe.Fori(0, E // NB) as i:
                    for j in range(NB):
                        e = i * NB + j
                        pe.wait_ge(win[j], i * 64 + 64)
                        pe.wait_ge(h_ready, i * NB + j - 1) if j >= 2 else pe.wait_ge(h_ready, i * NB)
                        pe.sem_inc(tick, 1)
                        for k in range(HC):
                            cols = slice(k * P, (k + 1) * P)
                            dst = ps_h[j % 2][:, k * B:(k + 1) * B]
                            pe.matmul(dst, wa[j][:, cols], poolT[:, bass.ds(i * NB + j, 1), :].rearrange("p a b -> p (a b)"),
                                      start=True, stop=False)
                            last = pe.matmul(dst, ab[j][:, cols], ones1[:, :], start=False, stop=True)
                        last.then_inc(hid, 1)
                        pe.wait_ge(h_ready, i * NB + j + 1)
                        pe.sem_inc(tick, 1)
                        dst = ps_e[:, bass.ds((i * NB + j) * B, B)]
                        for k in range(HC):
                            pe.matmul(dst, wb[j][:, k, :], h[j % 2][:, k * B:(k + 1) * B], start=(k == 0), stop=False)
                        pe.matmul(dst, bb[j][:, :], ones1[:, :], start=False, stop=True).then_inc(outd, 1)
                pe.wait_ge(eo_t, 1)
                for j in range(2):
                    pe.transpose(ps_f[:, j * C:(j + 1) * C], eoT[:, 2 * j:2 * j + 2, :].rearrange("p b e -> p (b e)"),
                                 ident[:, :]).then_inc(flipped, 1)

            @block.scalar
            def _(act):
                with act.Fori(0, E // NB) as i:
                    for j in range(NB):
                        act.wait_ge(hid, i * NB + j + 1)
                        act.wait_ge(outd, i * NB + j - 1) if j >= 2 else act.wait_ge(outd, i * NB)
                        act.activation(h[j % 2][:, :], ps_h[j % 2][:, 0:HC * B], ACT.Gelu).then_inc(h_ready, 1)
                act.wait_ge(outd, E)
                act.copy(eoT[:, :, :], ps_e[:, 0:E * B].rearrange("p (e b) -> p b e", b=B)).then_inc(eo_t, 1)
                act.wait_ge(flipped, 2)
                act.copy(eo[:, :, :], ps_f[:, 0:2 * C].rearrange("p (j c) -> p j c", j=2)).then_inc(eo_ready, 1)

        with ExitStack() as c2:
            s2 = Scope(nc, c2, tag + "e")
            xr = [s2.sb(f"xr{j}", [P, R, C]) for j in range(2)]
            out = [s2.sb(f"out{j}", [P, R, C]) for j in range(2)]
            ws = [s2.sb(f"ws{j}", [P, R * W]) for j in range(2)]
            ps = [s2.ps(f"ps{j}") for j in range(2)]
            xin = [s2.sem(f"xin{j}") for j in range(2)]
            staged, given, added, stored = (s2.sem(n) for n in ("staged", "given", "added", "stored"))
            block = c2.enter_context(nc.Block())
            xv = x3.rearrange("b (i j r) w c -> b i j w r c", j=2, r=R)
            ov = x4.rearrange("b (i j r) w c -> b i j w r c", j=2, r=R)

            @block.sync
            def _(sp):
                for b in range(B):
                    with sp.Fori(0, KT // 2) as i:
                        for j in range(2):
                            sp.wait_ge(added, i * 2 + b * KT)
                            sp.dma_start(xr[j][:, :, :], xv[b][i, j]).then_inc(xin[j], 16)

            @block.gpsimd
            def _(pool):
                for b in range(B):
                    rows = slice((b % 2) * E, (b % 2 + 1) * E)
                    with pool.Fori(0, KT // 2) as i:
                        for j in range(2):
                            pool.wait_ge(given, i * 2 + b * KT)
                            pool.tensor_copy(ws[j][rows, :], wt[rows, b // 2, bass.ds(i * 2 * R * W + j * R * W, R * W)]
                                             ).then_inc(staged, 1)

            @block.tensor
            def _(pe):
                for b in range(B):
                    rows = slice((b % 2) * E, (b % 2 + 1) * E)
                    with pe.Fori(0, KT // 2) as i:
                        for j in range(2):
                            n = i * 2 + b * KT + j
                            pe.wait_ge(staged, n + 1)
                            pe.wait_ge(added, i * 2 + b * KT)
                            for r in range(R):
                                last = pe.matmul(ps[j][:, r * C:(r + 1) * C], ws[j][rows, r * W:(r + 1) * W],
                                                 eo[rows, b // 2, :], start=True, stop=True,
                                                 tile_position=((b % 2) * E, 0))
                            last.then_inc(given, 1)

            @block.vector
            def _(dve):
                for b in range(B):
                    with dve.Fori(0, KT // 2) as i:
                        for j in range(2):
                            n = i * 2 + b * KT + j
                            dve.wait_ge(given, n + 1)
                            dve.wait_ge(xin[j], i * 16 + b * 16 * (KT // 2) + 16)
                            dve.wait_ge(stored, (i * 2 + b * KT) * 16)
                            dve.tensor_tensor(out[j][:, :, :], xr[j][:, :, :],
                                              ps[j][:, :].rearrange("p (r c) -> p r c", r=R), ALU.add).then_inc(added, 1)

            @block.scalar
            def _(act):
                for b in range(B):
                    with act.Fori(0, KT // 2) as i:
                        for j in range(2):
                            act.wait_ge(added, i * 2 + b * KT + j + 1)
                            act.dma_start(ov[b][i, j], out[j][:, :, :]).then_inc(stored, 16)
                act.wait_ge(stored, 16 * B * KT)


def normalised_tokens(nc, x, u, tag, eps=1e-5):
    with ExitStack() as ctx:
        s = Scope(nc, ctx, tag)
        xb = [s.sb(f"xb{j}", [P, T // 2, C]) for j in range(2)]
        TH = T // 2
        st = s.sb("st", [P, TH, 6])
        mv = s.sb("mv", [P, TH, 2])
        ve, rstd, half = (s.sb(n, [P, TH]) for n in ("ve", "rstd", "half"))
        xin = [s.sem(f"xin{j}") for j in range(2)]
        made, ve_ready, rstd_ready, u_ready, dch = (s.sem(n) for n in ("made", "ve_ready", "rstd_ready", "u_ready", "dch"))
        block = ctx.enter_context(nc.Block())
        N = 2 * B
        xv = x.rearrange("b (j t) w c -> (b j) w t c", j=2)

        @block.sync
        def _(sp):
            for n in range(N):
                if n >= 2:
                    sp.wait_ge(u_ready, n - 1)
                sp.dma_start(xb[n % 2][:, :, :], xv[n]).then_inc(xin[n % 2], 16)

        @block.gpsimd
        def _(pool):
            pool.memset(half[:, :], -0.5).then_inc(made, 1)
            pool.wait_ge(made, 1)
            for n in range(N):
                pool.wait_ge(ve_ready, n + 1)
                pool.tensor_tensor(rstd[:, :], ve[:, :], half[:, :], ALU.pow).then_inc(rstd_ready, 1)

        @block.vector
        def _(dve):
            step = Chain(dve, dch)
            for n in range(N):
                dve.wait_ge(xin[n % 2], 16 * (n // 2 + 1))
                src = xb[n % 2]
                dst = u[:, n * TH:(n + 1) * TH, :]
                for t in range(TH):
                    step.mark(dve.bn_stats(st[:, t, :], src[:, t, :]))
                step.join()
                for t in range(TH):
                    step.mark(dve.bn_aggr(mv[:, t, :], st[:, t, :]))
                step.join()
                step(dve.tensor_scalar(ve[:, :], mv[:, :, 1], eps, None, ALU.add))
                dve.sem_inc(ve_ready, 1)
                step(dve.tensor_tensor(dst, src[:, :, :], mv[:, :, 0:1].broadcast_to([P, TH, C]), ALU.subtract))
                dve.wait_ge(rstd_ready, n + 1)
                step(dve.tensor_tensor(dst, dst, rstd[:, :].unsqueeze(2).broadcast_to([P, TH, C]), ALU.mult))
                dve.sem_inc(u_ready, 1)


def softmax_attention(nc, x4, w_in, w_out, b_out, ln_w, x5, tag="sma", eps=1e-5):
    H = 4
    D = C // H
    R = 4
    NT = BT // R
    TOK = BT * W
    with ExitStack() as ctx:
        s = Scope(nc, ctx, tag)
        u = s.sb("u", [P, BT, C])
        wT = s.sb("wT", [P, 4, C])
        ident, ones = s.sb("ident", [P, P]), s.sb("ones", [P, P])
        ones1 = s.sb("ones1", [1, P])
        negmax = s.sb("negmax", [1, C])
        heads = s.sb("heads", [P, H, D])
        g = s.sb("g", [P, C])
        normalised_tokens(nc, x4, u, tag + "n")
        with ExitStack() as c2:
            s2 = Scope(nc, c2, tag + "a")
            wl = s2.sb("wl", [P, 4, C])
            us = s2.sb("us", [P, R, C])
            uTs = [s2.sb(f"uTs{j}", [P, R * W]) for j in range(2)]
            mx = s2.sb("mx", [P, NT])
            m1 = s2.sb("m1", [P, 1])
            ps_w, ps_t, ps_m = s2.ps("ps_w"), s2.ps("ps_t"), s2.ps("ps_m")
            ps_k = [s2.ps(f"ps_k{j}") for j in range(2)]
            (loaded, made, w_done, w_ready, staged, turned, uT_ready, k_done, k_read, m_ready, m_done, dch, pch,
             tick) = (s2.sem(n) for n in ("loaded", "made", "w_done", "w_ready", "staged", "turned", "uT_ready",
                                          "k_done", "k_read", "m_ready", "m_done", "dch", "pch", "tick"))
            block = c2.enter_context(nc.Block())

            @block.sync
            def _(sp):
                sp.dma_start(wl[:, 0:3, :], w_in.rearrange("(j o) c -> o j c", j=3)).then_inc(loaded, 16)
                sp.dma_start(wl[:, 3, :], w_out).then_inc(loaded, 16)

            @block.gpsimd
            def _(pool):
                step = Chain(pool, pch)
                fill_identity(pool, step, ident)
                step(pool.memset(ones[:, :], 1.0))
                step(pool.memset(ones1[:, :], 1.0))
                step(pool.memset(heads[:, :, :], 1.0))
                step(pool.affine_select(out=heads[:, :, :], in_=heads[:, :, :], compare_op=ALU.is_ge, fill=0.0,
                                        base=0, pattern=[[-D, H], [0, D]], channel_multiplier=1))
                step(pool.affine_select(out=heads[:, :, :], in_=heads[:, :, :], compare_op=ALU.is_ge, fill=0.0,
                                        base=D - 1, pattern=[[D, H], [0, D]], channel_multiplier=-1))
                pool.sem_inc(made, 1)
                with pool.Fori(0, NT) as i:
                    pool.wait_ge(turned, i)
                    pool.tensor_copy(us[:, :, :], u[:, bass.ds(i * R, R), :]).then_inc(staged, 1)

            @block.tensor
            def _(pe):
                pe.wait_ge(loaded, 32)
                pe.wait_ge(made, 1)
                for j in range(4):
                    last = pe.transpose(ps_w[:, j * C:(j + 1) * C], wl[:, j, :], ident[:, :])
                last.then_inc(w_done, 1)
                pe.wait_ge(w_ready, 1)
                with pe.Fori(0, NT // 2) as i:
                    for j in range(2):
                        n = 2 * i + j
                        pe.wait_ge(staged, 2 * i + j + 1)
                        pe.wait_ge(uT_ready, 2 * i + j)
                        for r in range(R):
                            last = pe.transpose(ps_t[:, r * W:(r + 1) * W], us[:, r, :], ident[:, :])
                        last.then_inc(turned, 1)
                        pe.wait_ge(uT_ready, 2 * i + j + 1)
                        pe.wait_ge(k_read, 2 * i)
                        pe.matmul(ps_k[j][:, :], wT[:, 1, :], uTs[j][:, :], start=True, stop=True).then_inc(k_done, 1)
                pe.wait_ge(m_ready, 1)
                pe.transpose(ps_m[0:1, 0:P], m1[:, :], ident[:, :]).then_inc(m_done, 1)

            @block.scalar
            def _(act):
                act.wait_ge(w_done, 1)
                act.copy(wT[:, :, :], ps_w[:, :].rearrange("p (j c) -> p j c", j=4)).then_inc(w_ready, 1)
                with act.Fori(0, NT // 2) as i:
                    for j in range(2):
                        act.wait_ge(turned, 2 * i + j + 1)
                        act.wait_ge(k_done, 2 * i)
                        act.copy(uTs[j][:, :], ps_t[:, :]).then_inc(uT_ready, 1)
                act.wait_ge(m_done, 1)
                act.copy(negmax[:, :], ps_m[0:1, 0:P]).then_inc(tick, 1)

            @block.vector
            def _(dve):
                step = Chain(dve, dch)
                with dve.Fori(0, NT // 2) as i:
                    for j in range(2):
                        dve.wait_ge(k_done, 2 * i + j + 1)
                        dve.tensor_reduce(mx[:, bass.ds(i * 2 + j, 1)], ps_k[j][:, :], AX.X, ALU.max).then_inc(k_read, 1)
                dve.wait_ge(k_read, NT)
                step(dve.tensor_reduce(m1[:, :], mx[:, :], AX.X, ALU.max, negate=True))
                dve.sem_inc(m_ready, 1)

        with ExitStack() as c2:
            s2 = Scope(nc, c2, tag + "b")
            us = s2.sb("us", [P, R, C])
            uTs = s2.sb("uTs", [P, R * W])
            ek = s2.sb("ek", [P, R * C])
            acc = s2.sb("acc", [P, 2, C])
            ctxm, ctxt = s2.sb("ctxm", [P, C]), s2.sb("ctxt", [P, C])
            rsum = s2.sb("rsum", [P, 1])
            ps_t, ps_k, ps_m, ps_n, ps_x = (s2.ps(n) for n in ("ps_t", "ps_k", "ps_m", "ps_n", "ps_x"))
            (staged, turned, uT_ready, k_done, ek_ready, acc_done, acc_read, c_done, c_ready, ct_done, ct_ready,
             g_done, dch) = (s2.sem(n) for n in (
                 "staged", "turned", "uT_ready", "k_done", "ek_ready", "acc_done", "acc_read", "c_done",
                 "c_ready", "ct_done", "ct_ready", "g_done", "dch"))
            block = c2.enter_context(nc.Block())

            @block.gpsimd
            def _(pool):
                with pool.Fori(0, NT) as i:
                    pool.wait_ge(acc_done, i)
                    pool.tensor_copy(us[:, :, :], u[:, bass.ds(i * R, R), :]).then_inc(staged, 1)

            @block.tensor
            def _(pe):
                with pe.Fori(0, NT) as i:
                    pe.wait_ge(staged, i + 1)
                    for r in range(R):
                        last = pe.transpose(ps_t[:, r * W:(r + 1) * W], us[:, r, :], ident[:, :])
                    last.then_inc(turned, 1)
                    pe.wait_ge(uT_ready, i + 1)
                    for r in range(R):
                        cols = slice(r * C, (r + 1) * C)
                        pe.matmul(ps_k[:, cols], uTs[:, r * W:(r + 1) * W], wT[:, 1, :], start=True, stop=False)
                        last = pe.matmul(ps_k[:, cols], ones1[:, :], negmax[:, :], start=False, stop=True)
                    last.then_inc(k_done, 1)
                    pe.wait_ge(ek_ready, i + 1)
                    pe.wait_ge(acc_read, i)
                    for r in range(R):
                        pe.matmul(ps_m[:, 0:C], us[:, r, :], ek[:, r * C:(r + 1) * C], start=(r == 0), stop=(r == R - 1))
                    for r in range(R):
                        last = pe.matmul(ps_n[:, 0:C], ek[:, r * C:(r + 1) * C], ones[:, :], start=(r == 0), stop=(r == R - 1))
                    last.then_inc(acc_done, 1)
                pe.wait_ge(acc_read, NT)
                pe.matmul(ps_x[:, 0:C], acc[:, 0, :], wT[:, 2, :], start=True, stop=True).then_inc(c_done, 1)
                pe.wait_ge(c_ready, 1)
                pe.transpose(ps_x[:, C:2 * C], ctxm[:, :], ident[:, :]).then_inc(ct_done, 1)
                pe.wait_ge(ct_ready, 1)
                pe.matmul(ps_x[:, 2 * C:3 * C], ctxt[:, :], wT[:, 3, :], start=True, stop=True).then_inc(g_done, 1)

            @block.scalar
            def _(act):
                with act.Fori(0, NT) as i:
                    act.wait_ge(turned, i + 1)
                    act.wait_ge(k_done, i)
                    act.copy(uTs[:, :], ps_t[:, :]).then_inc(uT_ready, 1)
                    act.wait_ge(k_done, i + 1)
                    act.wait_ge(acc_done, i)
                    act.activation(ek[:, :], ps_k[:, :], ACT.Exp).then_inc(ek_ready, 1)

            @block.vector
            def _(dve):
                step = Chain(dve, dch)
                TT = dve.tensor_tensor
                step(dve.memset(acc[:, :, :], 0.0))
                with step.loop(NT, 2) as i:
                    dve.wait_ge(acc_done, i + 1)
                    step(TT(acc[:, 0, :], acc[:, 0, :], ps_m[:, 0:C], ALU.add))
                    step(TT(acc[:, 1, :], acc[:, 1, :], ps_n[:, 0:C], ALU.add))
                    dve.sem_inc(acc_read, 1)
                step(dve.tensor_scalar(rsum[:, :], acc[:, 1, 0:1], float(TOK) * math.sqrt(D), None, ALU.mult))
                step(dve.reciprocal(rsum[:, :], rsum[:, :]))
                dve.wait_ge(c_done, 1)
                step(dve.scalar_tensor_tensor(out=ctxm[:, :], in0=ps_x[:, 0:C], scalar=rsum[:, 0:1],
                                              in1=heads[:, :, :].rearrange("p h d -> p (h d)"), op0=ALU.mult, op1=ALU.mult))
                dve.sem_inc(c_ready, 1)
                dve.wait_ge(ct_done, 1)
                dve.tensor_copy(ctxt[:, :], ps_x[:, C:2 * C]).then_inc(ct_ready, 1)
                dve.wait_ge(g_done, 1)
                step(dve.tensor_copy(g[:, :], ps_x[:, 2 * C:3 * C]))

        with ExitStack() as c2:
            s2 = Scope(nc, c2, tag + "c")
            bo_row = s2.sb("bo_row", [1, C])
            lnw = s2.sb("lnw", [P, C])
            us = s2.sb("us", [P, R, C])
            uTs = s2.sb("uTs", [P, R * W])
            xr = s2.sb("xr", [P, R, C])
            q = s2.sb("q", [P, R * H, D])
            mx, den = s2.sb("mx", [P, R * H]), s2.sb("den", [P, R * H])
            qT = s2.sb("qT", [P, R * W])
            z = s2.sb("z", [P, R, C])
            out = s2.sb("out", [P, R, C])
            st, mv = s2.sb("st", [P, R, 6]), s2.sb("mv", [P, R, 2])
            ve, rstd, half = (s2.sb(n, [P, R]) for n in ("ve", "rstd", "half"))
            ps_t, ps_q, ps_y, ps_o = (s2.ps(n) for n in ("ps_t", "ps_q", "ps_y", "ps_o"))
            (loaded, made, xin, staged, turned, uT_ready, q_done, shifted, ex_ready, q_ready, flipped, qT_ready,
             o_done, ve_ready, rstd_ready, out_ready, stored, dch, tick) = (s2.sem(n) for n in (
                 "loaded", "made", "xin", "staged", "turned", "uT_ready", "q_done", "shifted", "ex_ready",
                 "q_ready", "flipped", "qT_ready", "o_done", "ve_ready", "rstd_ready", "out_ready", "stored",
                 "dch", "tick"))
            block = c2.enter_context(nc.Block())
            xv = x4.rearrange("b t w c -> (b t) w c").rearrange("(i r) w c -> i w r c", r=R)
            ov = x5.rearrange("b t w c -> (b t) w c").rearrange("(i r) w c -> i w r c", r=R)

            @block.sync
            def _(sp):
                sp.dma_start(bo_row[:, :], b_out.unsqueeze(0)).then_inc(loaded, 16)
                sp.dma_start(lnw[:, :], ln_w.unsqueeze(0).broadcast_to([P, C])).then_inc(loaded, 16)
                with sp.Fori(0, NT) as i:
                    sp.wait_ge(out_ready, i)
                    sp.dma_start(xr[:, :, :], xv[i]).then_inc(xin, 16)
                    sp.wait_ge(out_ready, i + 1)
                    sp.dma_start(ov[i], out[:, :, :]).then_inc(stored, 16)
                sp.wait_ge(stored, 16 * NT)

            @block.gpsimd
            def _(pool):
                pool.memset(half[:, :], -0.5).then_inc(made, 1)
                pool.wait_ge(made, 1)
                with pool.Fori(0, NT) as i:
                    pool.wait_ge(turned, i)
                    pool.tensor_copy(us[:, :, :], u[:, bass.ds(i * R, R), :]).then_inc(staged, 1)
                    pool.wait_ge(ve_ready, i + 1)
                    pool.tensor_tensor(rstd[:, :], ve[:, :], half[:, :], ALU.pow).then_inc(rstd_ready, 1)

            @block.tensor
            def _(pe):
                pe.wait_ge(loaded, 32)
                with pe.Fori(0, NT) as i:
                    pe.wait_ge(staged, i + 1)
                    for r in range(R):
                        last = pe.transpose(ps_t[:, r * W:(r + 1) * W], us[:, r, :], ident[:, :])
                    last.then_inc(turned, 1)
                    pe.wait_ge(uT_ready, i + 1)
                    pe.wait_ge(shifted, i)
                    for r in range(R):
                        last = pe.matmul(ps_q[:, r * C:(r + 1) * C], uTs[:, r * W:(r + 1) * W], wT[:, 0, :],
                                         start=True, stop=True)
                    last.then_inc(q_done, 1)
                    pe.wait_ge(q_ready, i + 1)
                    for r in range(R):
                        last = pe.transpose(ps_y[:, r * W:(r + 1) * W],
                                            q[:, r * H:(r + 1) * H, :].rearrange("p h d -> p (h d)"), ident[:, :])
                    last.then_inc(flipped, 1)
                    pe.wait_ge(qT_ready, i + 1)
                    for r in range(R):
                        cols = slice(r * C, (r + 1) * C)
                        pe.matmul(ps_o[:, cols], qT[:, r * W:(r + 1) * W], g[:, :], start=True, stop=False)
                        last = pe.matmul(ps_o[:, cols], ones1[:, :], bo_row[:, :], start=False, stop=True)
                    last.then_inc(o_done, 1)

            @block.scalar
            def _(act):
                with act.Fori(0, NT) as i:
                    act.wait_ge(turned, i + 1)
                    act.wait_ge(q_done, i)
                    act.copy(uTs[:, :], ps_t[:, :]).then_inc(uT_ready, 1)
                    act.wait_ge(shifted, i + 1)
                    act.activation(q[:, :, :], q[:, :, :], ACT.Exp).then_inc(ex_ready, 1)
                    act.wait_ge(flipped, i + 1)
                    act.copy(qT[:, :], ps_y[:, :]).then_inc(qT_ready, 1)

            @block.vector
            def _(dve):
                step = Chain(dve, dch)
                TT = dve.tensor_tensor
                dve.wait_ge(loaded, 32)
                with step.loop(NT, 2 + 3 + 1 + 2 * R + 1 + R + 2) as i:
                    dve.wait_ge(q_done, i + 1)
                    qv = ps_q[:, :].rearrange("p (h d) -> p h d", d=D)
                    step(dve.tensor_reduce(mx[:, :], qv, AX.X, ALU.max))
                    step(TT(q[:, :, :], qv, mx[:, :].unsqueeze(2).broadcast_to([P, R * H, D]), ALU.subtract))
                    dve.sem_inc(shifted, 1)
                    dve.wait_ge(ex_ready, i + 1)
                    step(dve.tensor_reduce(den[:, :], q[:, :, :], AX.X, ALU.add))
                    step(dve.reciprocal(den[:, :], den[:, :]))
                    step(TT(q[:, :, :], q[:, :, :], den[:, :].unsqueeze(2).broadcast_to([P, R * H, D]), ALU.mult))
                    dve.sem_inc(q_ready, 1)
                    dve.wait_ge(o_done, i + 1)
                    step(dve.tensor_copy(z[:, :, :], ps_o[:, :].rearrange("p (r c) -> p r c", r=R)))
                    for r in range(R):
                        step.mark(dve.bn_stats(st[:, r, :], z[:, r, :]))
                    step.join()
                    dve.sem_inc(tick, 1)
                    for r in range(R):
                        step.mark(dve.bn_aggr(mv[:, r, :], st[:, r, :]))
                    step.join()
                    step(dve.tensor_scalar(ve[:, :], mv[:, :, 1], eps, None, ALU.add))
                    dve.sem_inc(ve_ready, 1)
                    dve.wait_ge(rstd_ready, i + 1)
                    dve.wait_ge(stored, 16 * i)
                    for r in range(R):
                        step.mark(dve.tensor_scalar(out[:, r, :], z[:, r, :], mv[:, r, 0:1], rstd[:, r:r + 1],
                                                    ALU.subtract, ALU.mult))
                    step.join()
                    step(TT(out[:, :, :], out[:, :, :], lnw[:, :].unsqueeze(1).broadcast_to([P, R, C]), ALU.mult))
                    dve.wait_ge(xin, 16 * (i + 1))
                    step(TT(out[:, :, :], out[:, :, :], xr[:, :, :], ALU.add))
                    dve.sem_inc(out_ready, 1)


def recurrent_network(nc, x5, Wm, Vm, gamma, beta, y_out, tag="rnn", eps=1e-5):
    L = T * W
    S = 64
    CH = L // S
    N = B * CH
    G = 2
    NG = N // G
    WARM = 32
    TOL = 2.0 ** -19
    R = 4
    HALVES = W // S
    NT = BT // R
    with ExitStack() as ctx:
        s = Scope(nc, ctx, tag)
        uT = s.sb("uT", [P, S, N])
        ident = s.sb("ident", [P, P])
        wT = s.sb("wT", [P, C])
        wn = s.sb("wn", [P, C])
        wnT, vT = s.sb("wnT", [P, C]), s.sb("vT", [P, C])
        shift = s.sb("shift", [P, 1])
        with ExitStack() as cu:
            u = Scope(nc, cu, tag + "u").sb("u", [P, BT, C])
            normalised_tokens(nc, x5, u, tag + "n")
            s2 = Scope(nc, cu, tag + "a")
            wl = s2.sb("wl", [P, 2, C])
            gb = s2.sb("gb", [P, 2])
            us = [s2.sb(f"us{j}", [P, R, C]) for j in range(2)]
            uTs = [s2.sb(f"uTs{j}", [P, R * W]) for j in range(2)]
            st = s2.sb("st", [P, NT, 6])
            mv = s2.sb("mv", [P, 2])
            ve, rstd, half, a = (s2.sb(n, [P, 1]) for n in ("ve", "rstd", "half", "a"))
            ps_w = s2.ps("ps_w")
            ps_t = [s2.ps(f"ps_t{j}") for j in range(2)]
            ps_x = [s2.ps(f"ps_x{j}") for j in range(2)]
            (loaded, made, w_done, w_ready, staged, turned, uT_ready, placed, x_done, x_read, ve_ready,
             rstd_ready, wn_ready, wn_done, dch, pch, tick) = (s2.sem(n) for n in (
                 "loaded", "made", "w_done", "w_ready", "staged", "turned", "uT_ready", "placed", "x_done",
                 "x_read", "ve_ready", "rstd_ready", "wn_ready", "wn_done", "dch", "pch", "tick"))
            block = cu.enter_context(nc.Block())

            @block.sync
            def _(sp):
                sp.dma_start(wl[:, 0, :], Wm).then_inc(loaded, 16)
                sp.dma_start(wl[:, 1, :], Vm).then_inc(loaded, 16)
                sp.dma_start(gb[:, 0:1], gamma.unsqueeze(1)).then_inc(loaded, 16)
                sp.dma_start(gb[:, 1:2], beta.unsqueeze(1)).then_inc(loaded, 16)

            @block.gpsimd
            def _(pool):
                step = Chain(pool, pch)
                fill_identity(pool, step, ident)
                step(pool.memset(half[:, :], -0.5))
                pool.sem_inc(made, 1)
                with pool.Fori(0, NT // 2) as i:
                    for j in range(2):
                        pool.wait_ge(turned, 2 * i)
                        pool.tensor_copy(us[j][:, :, :], u[:, bass.ds(i * 2 * R + j * R, R), :]).then_inc(staged, 1)
                pool.wait_ge(ve_ready, 1)
                pool.tensor_tensor(rstd[:, :], ve[:, :], half[:, :], ALU.pow).then_inc(rstd_ready, 1)

            @block.tensor
            def _(pe):
                pe.wait_ge(loaded, 64)
                pe.wait_ge(made, 1)
                for j in range(2):
                    last = pe.transpose(ps_w[:, j * C:(j + 1) * C], wl[:, j, :], ident[:, :])
                last.then_inc(w_done, 1)
                pe.wait_ge(w_ready, 1)
                with pe.Fori(0, NT // 2) as i:
                    for j in range(2):
                        pe.wait_ge(staged, 2 * i + j + 1)
                        pe.wait_ge(placed, 2 * i)
                        for r in range(R):
                            last = pe.transpose(ps_t[j][:, r * W:(r + 1) * W], us[j][:, r, :], ident[:, :])
                        last.then_inc(turned, 1)
                        pe.wait_ge(uT_ready, 2 * i + j + 1)
                        pe.wait_ge(x_read, 2 * i)
                        pe.matmul(ps_x[j][:, :], wT[:, :], uTs[j][:, :], start=True, stop=True).then_inc(x_done, 1)
                pe.wait_ge(wn_ready, 1)
                pe.transpose(ps_w[:, 2 * C:3 * C], wn[:, :], ident[:, :]).then_inc(wn_done, 1)

            @block.scalar
            def _(act):
                act.wait_ge(w_done, 1)
                act.copy(wT[:, :], ps_w[:, 0:C]).then_inc(tick, 1)
                act.copy(vT[:, :], ps_w[:, C:2 * C]).then_inc(w_ready, 1)
                with act.Fori(0, NT // 2) as i:
                    for j in range(2):
                        act.wait_ge(turned, 2 * i + j + 1)
                        act.wait_ge(x_done, 2 * i)
                        act.copy(uTs[j][:, :], ps_t[j][:, :]).then_inc(uT_ready, 1)
                        col = bass.ds(i * 2 * R * HALVES + j * R * HALVES, R * HALVES)
                        act.copy(uT[:, :, col], ps_t[j][:, :].rearrange("p (q s) -> p s q", s=S)).then_inc(placed, 1)
                act.wait_ge(wn_done, 1)
                act.copy(wnT[:, :], ps_w[:, 2 * C:3 * C]).then_inc(tick, 1)

            @block.vector
            def _(dve):
                step = Chain(dve, dch)
                with dve.Fori(0, NT // 2) as i:
                    for j in range(2):
                        dve.wait_ge(x_done, 2 * i + j + 1)
                        dve.bn_stats(st[:, bass.ds(i * 2 + j, 1), :].rearrange("p a b -> p (a b)"), ps_x[j][:, :]).then_inc(x_read, 1)
                dve.wait_ge(x_read, NT)
                step(dve.bn_aggr(mv[:, :], st[:, :, :].rearrange("p n k -> p (n k)")))
                step(dve.tensor_scalar(ve[:, :], mv[:, 1:2], eps, None, ALU.add))
                dve.sem_inc(ve_ready, 1)
                dve.wait_ge(rstd_ready, 1)
                step(dve.tensor_tensor(a[:, :], rstd[:, :], gb[:, 0:1], ALU.mult))
                step(dve.tensor_scalar(wn[:, :], wl[:, 0, :], a[:, 0:1], None, ALU.mult))
                dve.sem_inc(wn_ready, 1)
                step(dve.tensor_tensor(shift[:, :], mv[:, 0:1], a[:, :], ALU.mult))
                step(dve.tensor_tensor(shift[:, :], gb[:, 1:2], shift[:, :], ALU.subtract))

        y = s.sb("y", [P, S + 1, N])
        ys = s.sb("ys", [P, 2, N])
        ends = s.sb("ends", [P, B, CH])
        diff = s.sb("diff", [P, N])
        worst = s.sb("worst", [P, 1])
        row = s.sb("row", [1, P])
        flag = s.sb("flag", [1, 1])
        flag_i = s.sb("flag_i", [1, 1], mybir.dt.int32)

        def pe_steps(pe, ps, states, first, steps, z_ready, y_ready):
            with pe.Fori(0, steps // 2) as i:
                for p in range(2):
                    for g in range(G):
                        cols = slice(g * NG, (g + 1) * NG)
                        inp = uT[:, bass.ds(i * 2 + (first + p), 1), cols].rearrange("p a n -> p (a n)")
                        prev = states(i, p)[0][:, :, cols].rearrange("p a n -> p (a n)")
                        dst = ps[p * G + g][:, 0:NG]
                        pe.matmul(dst, wnT[:, :], inp, start=True, stop=False)
                        pe.wait_ge(y_ready[g], i * 2 + p)
                        pe.matmul(dst, vT[:, :], prev, start=False, stop=True).then_inc(z_ready[g], 1)

        def act_steps(act, ps, states, steps, z_ready, y_ready):
            with act.Fori(0, steps // 2) as i:
                for p in range(2):
                    for g in range(G):
                        cols = slice(g * NG, (g + 1) * NG)
                        nxt = states(i, p)[1][:, :, cols].rearrange("p a n -> p (a n)")
                        act.wait_ge(z_ready[g], i * 2 + p + 1)
                        act.activation(nxt, ps[p * G + g][:, 0:NG], ACT.Sigmoid, bias=shift[:, 0:1]).then_inc(y_ready[g], 1)

        def in_y(i, p):
            return y[:, bass.ds(i * 2 + p, 1), :], y[:, bass.ds(i * 2 + p + 1, 1), :]

        def in_ys(i, p):
            return ys[:, p:p + 1, :], ys[:, 1 - p:2 - p, :]

        def block_of(name, states, first, steps, before, after):
            with ExitStack() as c2:
                s2 = Scope(nc, c2, f"{tag}{name}")
                ps = [s2.ps(f"ps{j}") for j in range(2 * G)]
                z_ready = [s2.sem(f"z_ready{g}") for g in range(G)]
                y_ready = [s2.sem(f"y_ready{g}") for g in range(G)]
                begun, dch = s2.sem("begun"), s2.sem("dch")
                block = c2.enter_context(nc.Block())

                @block.tensor
                def _(pe):
                    pe.wait_ge(begun, 1)
                    pe_steps(pe, ps, states, first, steps, z_ready, y_ready)

                @block.scalar
                def _(act):
                    act_steps(act, ps, states, steps, z_ready, y_ready)

                @block.vector
                def _(dve):
                    step = Chain(dve, dch)
                    before(dve, step)
                    dve.sem_inc(begun, 1)
                    for g in range(G):
                        dve.wait_ge(y_ready[g], steps)
                    after(dve, step)

        def starts_from(src):
            def do(dve, step):
                first = y[:, 0, :].rearrange("p (b k) -> p b k", b=B)
                step.mark(dve.memset(first[:, :, 0:1], 0.0))
                step.mark(dve.tensor_copy(first[:, :, 1:CH], src[:, :, 0:CH - 1]))
                step.join()
            return do

        def measure(dve, step):
            first = y[:, 0, :].rearrange("p (b k) -> p b k", b=B)
            d = diff[:, :].rearrange("p (b k) -> p b k", b=B)
            step(dve.tensor_copy(ends[:, :, :], y[:, S, :].rearrange("p (b k) -> p b k", b=B)))
            step(dve.memset(diff[:, :], 0.0))
            step(dve.tensor_tensor(d[:, :, 1:CH], ends[:, :, 0:CH - 1], first[:, :, 1:CH], ALU.subtract))
            step(dve.tensor_reduce(worst[:, :], diff[:, :], AX.X, ALU.max, apply_absolute_value=True))

        nothing = lambda dve, step: None
        block_of("w", in_ys, S - WARM, WARM, lambda dve, step: step(dve.memset(ys[:, 0, :], 0.0)), nothing)
        block_of("m", in_y, 0, S, starts_from(ys[:, 0, :].rearrange("p (b k) -> p b k", b=B)), measure)

        with ExitStack() as c2:
            s2 = Scope(nc, c2, tag + "f")
            ps = s2.ps("ps")
            turned, copied, dch = s2.sem("turned"), s2.sem("copied"), s2.sem("dch")
            block = c2.enter_context(nc.Block())

            @block.tensor
            def _(pe):
                pe.transpose(ps[0:1, 0:P], worst[:, :], ident[:, :]).then_inc(turned, 1)

            @block.vector
            def _(dve):
                step = Chain(dve, dch)
                dve.wait_ge(turned, 1)
                step(dve.tensor_reduce(flag[:, :], ps[0:1, 0:P], AX.X, ALU.max))
                step(dve.tensor_scalar(flag_i[:, :], flag[:, :], TOL, None, ALU.is_gt))

        again = nc.values_load(flag_i[0:1, 0:1], min_val=0, max_val=1)
        with nc.If(again > 0):
            with nc.Fori(0, CH - 1):
                block_of("r", in_y, 0, S, starts_from(ends), measure)

        with ExitStack() as c2:
            s2 = Scope(nc, c2, tag + "o")
            xr = [s2.sb(f"xr{j}", [P, R, C]) for j in range(2)]
            out = [s2.sb(f"out{j}", [P, R, C]) for j in range(2)]
            yst = [s2.sb(f"yst{j}", [P, R * W]) for j in range(2)]
            ps = [s2.ps(f"ps{j}") for j in range(2)]
            xin = [s2.sem(f"xin{j}") for j in range(2)]
            staged, turned, added, stored = (s2.sem(n) for n in ("staged", "turned", "added", "stored"))
            block = c2.enter_context(nc.Block())
            xv = x5.rearrange("b t w c -> (b t) w c").rearrange("(i j r) w c -> i j w r c", j=2, r=R)
            ov = y_out.rearrange("b t w c -> (b t) w c").rearrange("(i j r) w c -> i j w r c", j=2, r=R)

            @block.sync
            def _(sp):
                with sp.Fori(0, NT // 2) as i:
                    for j in range(2):
                        sp.wait_ge(added, 2 * i)
                        sp.dma_start(xr[j][:, :, :], xv[i, j]).then_inc(xin[j], 16)

            @block.gpsimd
            def _(pool):
                with pool.Fori(0, NT // 2) as i:
                    for j in range(2):
                        pool.wait_ge(turned, 2 * i)
                        col = bass.ds(i * 2 * R * HALVES + j * R * HALVES, R * HALVES)
                        pool.tensor_copy(yst[j][:, :].rearrange("p (q s) -> p s q", s=S), y[:, 1:S + 1, col]
                                         ).then_inc(staged, 1)

            @block.tensor
            def _(pe):
                with pe.Fori(0, NT // 2) as i:
                    for j in range(2):
                        pe.wait_ge(staged, 2 * i + j + 1)
                        pe.wait_ge(added, 2 * i)
                        for r in range(R):
                            last = pe.transpose(ps[j][:, r * C:(r + 1) * C], yst[j][:, r * W:(r + 1) * W], ident[:, :])
                        last.then_inc(turned, 1)

            @block.vector
            def _(dve):
                with dve.Fori(0, NT // 2) as i:
                    for j in range(2):
                        dve.wait_ge(turned, 2 * i + j + 1)
                        dve.wait_ge(xin[j], 16 * i + 16)
                        dve.wait_ge(stored, 32 * i)
                        dve.tensor_tensor(out[j][:, :, :], xr[j][:, :, :],
                                          ps[j][:, :].rearrange("p (r c) -> p r c", r=R), ALU.add).then_inc(added, 1)

            @block.scalar
            def _(act):
                with act.Fori(0, NT // 2) as i:
                    for j in range(2):
                        act.wait_ge(added, 2 * i + j + 1)
                        act.dma_start(ov[i, j], out[j][:, :, :]).then_inc(stored, 16)
                act.wait_ge(stored, 16 * NT)


def hybrid_stack(nc, d, out):
    shape = (B, T, W, C)

    def dram(name, shape):
        return nc.dram_tensor(name, shape, f32, kind="Internal").ap()

    def layer(prefix, *names):
        return [d[f"{prefix}_{n}"] for n in names]

    tabs = inline_tables(nc)
    x1, x2, x3, x4, x5 = (dram(f"x{n}", shape) for n in range(1, 6))

    h0 = dram("h0", (BT, W, C))
    with nc.sbuf_tensor("hg0", [P, BT, C], f32) as hg:
        group_norm(nc, d["x"], hg, "gn0")
        graph_attention(nc, hg, *layer("L0_conv", "adj", "Wq", "Wk", "Wv", "Wo", "bo", "ns_g", "ns_b"), h0)
    mamba(nc, h0, d["x"], *layer("L0_conv", "in_proj", "conv_w", "conv_b", "x_proj", "dt_w", "dt_b", "A_log", "Dp",
                                 "out_w", "out_b", "nt_g", "nt_b"), x1)

    wts = {n[len("L1_conv_"):]: v for n, v in d.items() if n.startswith("L1_conv_")}
    tok, tnd, mix = (dram(n, (BT, W, C)) for n in ("tokens", "tokens_normalised", "mix"))
    gram = dram("gram", (BT, BT))
    prob = dram("prob", (NH, B, T, T))
    wd = dram("mode_weights", (NH, NKY, 2, NKX))
    with ExitStack() as ctx:
        def sb(name, shape):
            return ctx.enter_context(nc.sbuf_tensor(name, shape, f32))

        spec = sb("spec", [2 * 32, BT, NKY])
        const = sb("const", [P, 1])
        xh = sb("xh", [P, NKY, 2, NKX])
        with nc.sbuf_tensor("hg1", [P, BT, C], f32) as hg:
            group_norm(nc, x1, hg, "gn1")
            token_images(nc, hg, wts["norm1_g"], wts["norm1_b"], tok, tnd)
            token_spectra(nc, hg, tabs, xh, gram)
        pt = sb("pt", [P, NH, BT])
        mt = sb("mt", [P, BT])
        token_attention(nc, xh, gram, tabs, wts, prob, pt, mt)
        attended_spectrum(nc, xh, pt, wts, wd, spec, const)
        mixed_images(nc, tnd, mt, mix)
        token_mixer(nc, spec, const, mix, tok, x1, wts, tabs, x2)

    linear_attention(nc, x2, *layer("L2_attn", "Wq", "bq", "Wk", "bk", "Wv", "bv", "Wo", "bo"), x3)
    routed_experts(nc, x3, *layer("L2_ffn", "gate_w", "gate_b", "weight1", "weight2"), x4)

    softmax_attention(nc, x4, *layer("L3_attn", "w_in", "w_out", "b_out", "ln_w"), x5)
    recurrent_network(nc, x5, *layer("L3_ffn", "W", "V", "gamma", "beta"), out)


def kernel(**inputs):
    import concourse.bacc as bacc
    from concourse.bass_utils import run_bass_kernel_spmd

    nc = bacc.Bacc("TRN2", target_bir_lowering=False, num_devices=1)
    arrays, d = {}, {}
    for name, a in inputs.items():
        a = np.ascontiguousarray(a)
        arrays[f"in_{name}"] = a
        d[name] = nc.dram_tensor(f"in_{name}", a.shape, mybir.dt.from_np(a.dtype), kind="ExternalInput").ap()
    out = nc.dram_tensor("out_0", (B, T, W, C), f32, kind="ExternalOutput").ap()
    hybrid_stack(nc, d, out)
    r = run_bass_kernel_spmd(nc, [arrays], core_ids=[0])
    return r.results[0]["out_0"]
```

```python
import math
from contextlib import ExitStack, contextmanager

import concourse.bass as bass
import numpy as np
from concourse import mybir

f32 = mybir.dt.float32
bf16 = mybir.dt.bfloat16
u8 = mybir.dt.uint8
ALU = mybir.AluOpType
ACT = mybir.ActivationFunctionType
AX = mybir.AxisListType

P = 128
B, T, W, C = 4, 32, 128, 128
BT = B * T


class Chain:

    def __init__(self, eng, sem):
        self.eng, self.sem, self.base, self.k = eng, sem, 0, 0

    def __call__(self, ins):
        ins.then_inc(self.sem, 1)
        self.k += 1
        self.eng.wait_ge(self.sem, self.base + self.k)

    def mark(self, ins):
        ins.then_inc(self.sem, 1)
        self.k += 1
        return self.k

    def wait(self, k):
        self.eng.wait_ge(self.sem, self.base + k)

    def join(self):
        self.eng.wait_ge(self.sem, self.base + self.k)

    @contextmanager
    def loop(self, turns, per):
        base, k = self.base, self.k
        with self.eng.Fori(0, turns) as i:
            self.base, self.k = base + k + i * per, 0
            yield i
            assert self.k == per, (self.k, per)
        self.base, self.k = base, k + turns * per


class Scope:

    def __init__(self, nc, ctx, tag):
        self.nc, self.ctx, self.tag, self.sems = nc, ctx, tag, []
        ctx.callback(self.clear)

    def sb(self, name, shape, dt=f32):
        return self.ctx.enter_context(self.nc.sbuf_tensor(f"{self.tag}_{name}", shape, dt))

    def ps(self, name, shape=(P, 512), dt=f32):
        return self.ctx.enter_context(self.nc.psum_tensor(f"{self.tag}_{name}", list(shape), dt))

    def sem(self, name):
        self.sems.append(self.nc.alloc_semaphore(f"{self.tag}_{name}"))
        return self.sems[-1]

    def clear(self):
        if self.sems:
            with self.nc.Block() as block:
                @block.sync
                def _(sp):
                    for q in self.sems:
                        sp.sem_clear(q)
            for q in self.sems:
                self.nc.release_semaphore(q)


def fill_identity(pool, chain, ident):
    chain(pool.memset(ident[:, :], 0.0))
    chain(pool.affine_select(out=ident[:, :], in_=ident[:, :], compare_op=ALU.not_equal, fill=1.0,
                             base=0, pattern=[[-1, ident.shape[1]]], channel_multiplier=1))


def group_norm(nc, src, hg, tag, G=32, eps=1e-5):
    J = C // G
    N = T * W * J
    with ExitStack() as ctx:
        s = Scope(nc, ctx, tag)
        xb = s.sb("xb", [P, 2, T * C])
        sq = s.sb("sq", [P, T * C])
        ones = s.sb("ones", [P, P])
        sums = s.sb("sums", [P, 2, G])
        var = s.sb("var", [P, G])
        rstd = s.sb("rstd", [P, G])
        half = s.sb("half", [P, G])
        ps = [s.ps(f"ps{j}") for j in range(2)]
        loaded, squared, summed, var_done, rstd_done, normed, ready = (
            s.sem(n) for n in ("loaded", "squared", "summed", "var_done", "rstd_done", "normed", "ready"))
        dch = s.sem("dch")
        block = ctx.enter_context(nc.Block())

        @block.sync
        def _(sp):
            for b in range(B):
                if b >= 2:
                    sp.wait_ge(normed, b - 1)
                sp.dma_start(xb[:, b % 2, :].rearrange("w (t c) -> w t c", t=T),
                             src[b].rearrange("t w c -> w t c")).then_inc(loaded, 16)
                sp.wait_ge(loaded, 16 * b + 16)

        @block.scalar
        def _(act):
            for b in range(B):
                act.wait_ge(loaded, 16 * b + 16)
                if b >= 1:
                    act.wait_ge(summed, b)
                act.activation(sq[:, :], xb[:, b % 2, :], ACT.Square).then_inc(squared, 1)

        @block.tensor
        def _(pe):
            pe.wait_ge(ready, 1)
            for b in range(B):
                pe.wait_ge(loaded, 16 * b + 16)
                if b >= 1:
                    pe.wait_ge(var_done, b)
                for j in range(8):
                    pe.matmul(ps[0][:, :], ones[:, :], xb[:, b % 2, 512 * j:512 * j + 512],
                              start=(j == 0), stop=(j == 7))
                pe.wait_ge(squared, b + 1)
                for j in range(8):
                    last = pe.matmul(ps[1][:, :], ones[:, :], sq[:, 512 * j:512 * j + 512],
                                     start=(j == 0), stop=(j == 7))
                last.then_inc(summed, 1)

        @block.gpsimd
        def _(pool):
            pool.memset(ones[:, :], 1.0 / N).then_inc(ready, 1)
            pool.memset(half[:, :], -0.5).then_inc(rstd_done, 1)
            pool.wait_ge(rstd_done, 1)
            for b in range(B):
                pool.wait_ge(var_done, b + 1)
                pool.tensor_tensor(rstd[:, :], var[:, :], half[:, :], ALU.pow).then_inc(rstd_done, 1)

        @block.vector
        def _(dve):
            step = Chain(dve, dch)
            for b in range(B):
                dve.wait_ge(summed, b + 1)
                for j in range(2):
                    step.mark(dve.tensor_reduce(
                        sums[:, j, :], ps[j][:, :].rearrange("p (q g j) -> p g q j", q=4, g=G), AX.XY, ALU.add))
                step.join()
                step(dve.tensor_tensor(var[:, :], sums[:, 0, :], sums[:, 0, :], ALU.mult))
                step(dve.scalar_tensor_tensor(out=var[:, :], in0=sums[:, 1, :], scalar=eps, in1=var[:, :],
                                              op0=ALU.add, op1=ALU.subtract))
                dve.sem_inc(var_done, 1)
                dve.wait_ge(rstd_done, b + 2)
                xv = xb[:, b % 2, :].rearrange("p (t g j) -> p t g j", t=T, g=G)
                hv = hg[:, b * T:(b + 1) * T, :].rearrange("p t (g j) -> p t g j", g=G)
                mean = sums[:, 0, :].unsqueeze(1).unsqueeze(3).broadcast_to([P, T, G, J])
                scale = rstd[:, :].unsqueeze(1).unsqueeze(3).broadcast_to([P, T, G, J])
                step(dve.tensor_tensor(hv, xv, mean, ALU.subtract))
                dve.tensor_tensor(hv, hv, scale, ALU.mult).then_inc(normed, 1)
                dve.wait_ge(normed, b + 1)


def graph_attention(nc, hg, adj, Wq, Wk, Wv, Wo, bo, gain, shift, h0, tag="gat", eps=1e-5):
    R, H = 4, 4
    D = C // H
    TURNS = BT // R
    BIG = 1e9 * math.sqrt(D)
    SCALE = 1.0 / math.sqrt(D)
    with ExitStack() as ctx:
        s = Scope(nc, ctx, tag)
        wq, wk, wv, wo = (s.sb(n, [P, C]) for n in ("wq", "wk", "wv", "wo"))
        ident = s.sb("ident", [P, P])
        ones1 = s.sb("ones1", [1, P])
        bo_row = s.sb("bo_row", [1, C])
        adj_sb = s.sb("adj", [P, P])
        drop = s.sb("drop", [P, P], u8)
        low = s.sb("low", [P, P])
        gain_b = s.sb("gain", [P, C])
        shift_b = s.sb("shift", [P, C])
        hl = [s.sb(f"hl{j}", [P, R, C]) for j in range(2)]
        hT = s.sb("hT", [P, R * W])
        qT = [s.sb(f"qT{j}", [P, R * W]) for j in range(2)]
        kT = [s.sb(f"kT{j}", [P, R * W]) for j in range(2)]
        vt = [s.sb(f"vt{j}", [P, R, C]) for j in range(2)]
        mx = s.sb("mx", [P, 2, R])
        neg = s.sb("neg", [P, 2, R])
        ex = s.sb("ex", [P, 2, R, W])
        den = [s.sb(f"den{j}", [P, R, H]) for j in range(2)]
        pT = s.sb("pT", [P, 2, R, W])
        on = s.sb("on", [P, R, C])
        oT = s.sb("oT", [P, R * W])
        z = s.sb("z", [P, R, C])
        out = s.sb("out", [P, R, C])
        st = s.sb("st", [P, R, 6])
        mv = s.sb("mv", [P, R, 2])
        ve = s.sb("ve", [P, R])
        rstd = s.sb("rstd", [P, R])
        half = s.sb("half", [P, R])
        ps_f = [s.ps(f"ps_f{j}") for j in range(2)]
        ps_s = [s.ps(f"ps_s{j}") for j in range(2)]
        ps_p = [s.ps(f"ps_p{j}") for j in range(2)]
        ps_o, ps_z = s.ps("ps_o"), s.ps("ps_z")

        (loaded, made, prepared, staged, turned, hT_ready, qk_done, qk_ready, v_done, v_ready, scored,
         peaked, exped, flipped, pT_ready, mixed, on_ready, on_turned, oT_ready, outed, z_ready, ve_ready,
         rstd_ready, scaled, out_ready, stored, dch, pch, tick) = (
            s.sem(n) for n in (
                "loaded", "made", "prepared", "staged", "turned", "hT_ready", "qk_done", "qk_ready", "v_done",
                "v_ready", "scored", "peaked", "exped", "flipped", "pT_ready", "mixed", "on_ready",
                "on_turned", "oT_ready", "outed", "z_ready", "ve_ready", "rstd_ready", "scaled", "out_ready",
                "stored", "dch", "pch", "tick"))
        LOADS = 8
        block = ctx.enter_context(nc.Block())
        HALF = TURNS // 2


        @block.sync
        def _(sp):
            for dst, src in ((wq, Wq), (wk, Wk), (wv, Wv), (wo, Wo), (adj_sb, adj)):
                sp.dma_start(dst[:, :], src).then_inc(loaded, 16)
            sp.dma_start(bo_row[:, :], bo.unsqueeze(0)).then_inc(loaded, 16)
            sp.dma_start(gain_b[:, :], gain.unsqueeze(0).broadcast_to([P, C])).then_inc(loaded, 16)
            sp.dma_start(shift_b[:, :], shift.unsqueeze(0).broadcast_to([P, C])).then_inc(loaded, 16)
            rows = h0.rearrange("(i r) w c -> i w r c", r=R)
            with sp.Fori(0, TURNS) as i:
                sp.wait_ge(out_ready, i + 1)
                sp.dma_start(rows[i], out[:, :, :]).then_inc(stored, 16)
            sp.wait_ge(stored, 16 * TURNS)

        @block.gpsimd
        def _(pool):
            step = Chain(pool, pch)
            fill_identity(pool, step, ident)
            step(pool.memset(half[:, :], -0.5))
            step(pool.memset(low[:, :], -BIG))
            step(pool.memset(ones1[:, :], 1.0))
            pool.sem_inc(made, 1)
            pool.wait_ge(loaded, 16 * LOADS)

            def stage(i, p):
                pool.tensor_copy(hl[p][:, :, :], hg[:, bass.ds(i * R, R), :]).then_inc(staged, 1)

            def finish(i):
                pool.wait_ge(ve_ready, i + 1)
                pool.tensor_tensor(rstd[:, :], ve[:, :], half[:, :], ALU.pow).then_inc(rstd_ready, 1)
                pool.wait_ge(scaled, i + 1)
                wide = [P, R, C]
                step(pool.tensor_tensor(out[:, :, :], out[:, :, :], gain_b[:, :].unsqueeze(1).broadcast_to(wide), ALU.mult))
                pool.tensor_tensor(out[:, :, :], out[:, :, :], shift_b[:, :].unsqueeze(1).broadcast_to(wide), ALU.add
                                   ).then_inc(out_ready, 1)

            stage(0, 0)
            stage(1, 1)
            with step.loop(HALF - 1, 2) as j:
                for p in range(2):
                    pool.wait_ge(turned, 2 * j + p + 1)
                    stage(2 * j + p + 2, p)
                    finish(2 * j + p)
            finish(TURNS - 2)
            finish(TURNS - 1)

        @block.tensor
        def _(pe):
            pe.wait_ge(loaded, 16 * LOADS)
            pe.wait_ge(made, 1)
            pe.wait_ge(prepared, 1)

            def turn_rows(i, p):
                pe.wait_ge(staged, i + 1)
                for r in range(R):
                    last = pe.transpose(ps_f[0][:, r * W:(r + 1) * W], hl[p][:, r, :], ident[:, :])
                last.then_inc(turned, 1)

            def project_qk(i):
                pe.wait_ge(hT_ready, i + 1)
                pe.matmul(ps_f[1][:, :], wq[:, :], hT[:, :], start=True, stop=True)
                pe.matmul(ps_f[0][:, :], wk[:, :], hT[:, :], start=True, stop=True).then_inc(qk_done, 1)

            def project_v(i):
                pe.wait_ge(qk_ready, i + 1)
                for r in range(R):
                    last = pe.matmul(ps_f[1][:, r * C:(r + 1) * C], hT[:, r * W:(r + 1) * W], wv[:, :],
                                     start=True, stop=True)
                last.then_inc(v_done, 1)

            def scores(h, p):
                d = slice(h * D, (h + 1) * D)
                for r in range(R):
                    last = pe.matmul(ps_s[h % 2][:, r * W:(r + 1) * W], qT[p][d, r * W:(r + 1) * W],
                                     kT[p][d, r * W:(r + 1) * W], start=True, stop=True,
                                     tile_position=(h * D, 0))
                last.then_inc(scored, 1)

            def mix(h, p):
                d = slice(h * D, (h + 1) * D)
                for r in range(R):
                    last = pe.matmul(ps_o[:, r * C + h * D:r * C + (h + 1) * D], pT[:, h % 2, r, :], vt[p][:, r, d],
                                     start=True, stop=True)
                if h == H - 1:
                    last.then_inc(mixed, 1)

            turn_rows(0, 0)
            project_qk(0)
            project_v(0)
            scores(0, 0)

            def turn(j, p, first=False, last=False):
                i, q = 2 * j + p, 1 - p
                for h in range(H):
                    if h + 1 < H:
                        if not (first and h == 0):
                            pe.wait_ge(exped, i * H + h)
                        scores(h + 1, p)
                    elif not last:
                        pe.wait_ge(qk_ready, i + 2)
                        pe.wait_ge(exped, i * H + h)
                        scores(0, q)
                    pe.wait_ge(exped, i * H + h + 1)
                    if not (first and h < 2):
                        pe.wait_ge(pT_ready, i * H + h - 1)
                    for r in range(R):
                        done = pe.transpose(ps_p[h % 2][:, r * W:(r + 1) * W], ex[:, h % 2, r, :], ident[:, :])
                    done.then_inc(flipped, 1)
                    if not (first and h == 0):
                        pe.wait_ge(pT_ready, i * H + h)
                        if h == 1:
                            if not first:
                                pe.wait_ge(on_ready, i)
                            pe.wait_ge(v_ready, i + 1)
                        mix((h - 1) % H, q if h == 0 else p)
                    if h == 1 and not first:
                        for r in range(R):
                            done = pe.transpose(ps_z[:, r * C:(r + 1) * C], on[:, r, :], ident[:, :])
                        done.then_inc(on_turned, 1)
                    if h == 2 and not first:
                        project_out(i - 1)
                    if not last:
                        if h == 0:
                            if not first:
                                pe.wait_ge(v_ready, i + 1)
                            turn_rows(i + 1, q)
                        elif h == 1:
                            project_qk(i + 1)
                        elif h == 2:
                            project_v(i + 1)

            def project_out(i):
                pe.wait_ge(oT_ready, i + 1)
                for r in range(R):
                    pe.matmul(ps_z[:, r * C:(r + 1) * C], oT[:, r * W:(r + 1) * W], wo[:, :],
                              start=True, stop=False)
                    done = pe.matmul(ps_z[:, r * C:(r + 1) * C], ones1[:, :], bo_row[:, :],
                                     start=False, stop=True)
                done.then_inc(outed, 1)

            turn(0, 0, first=True)
            turn(0, 1)
            with pe.Fori(0, HALF - 2) as j:
                turn(j + 1, 0)
                turn(j + 1, 1)
            turn(HALF - 1, 0)
            turn(HALF - 1, 1, last=True)
            pe.wait_ge(pT_ready, TURNS * H)
            mix(H - 1, 1)
            pe.wait_ge(on_ready, TURNS)
            for r in range(R):
                done = pe.transpose(ps_z[:, r * C:(r + 1) * C], on[:, r, :], ident[:, :])
            done.then_inc(on_turned, 1)
            project_out(TURNS - 1)

        @block.scalar
        def _(act):
            def rows_in(i):
                act.wait_ge(turned, i + 1)
                act.copy(hT[:, :], ps_f[0][:, :]).then_inc(hT_ready, 1)

            def qk_in(i, q):
                act.wait_ge(qk_done, i + 1)
                act.copy(qT[q][:, :], ps_f[1][:, :])
                act.copy(kT[q][:, :], ps_f[0][:, :]).then_inc(qk_ready, 1)

            def v_in(i, q):
                act.wait_ge(v_done, i + 1)
                act.copy(vt[q][:, :, :], ps_f[1][:, :].rearrange("p (r c) -> p r c", r=R)).then_inc(v_ready, 1)

            def probs_in(i, h):
                act.wait_ge(flipped, i * H + h + 1)
                act.copy(pT[:, h % 2, :, :], ps_p[h % 2][:, :].rearrange("p (r w) -> p r w", r=R)).then_inc(pT_ready, 1)

            def mixed_in(i):
                act.wait_ge(on_turned, i + 1)
                act.copy(oT[:, :], ps_z[:, :]).then_inc(oT_ready, 1)

            rows_in(0)
            qk_in(0, 0)
            v_in(0, 0)

            def turn(j, p, first=False, last=False):
                i, q = 2 * j + p, 1 - p
                for h in range(H):
                    act.wait_ge(peaked, i * H + h + 1)
                    if not (first and h < 2):
                        act.wait_ge(flipped, i * H + h - 1)
                    for r in range(R):
                        done = act.activation(ex[:, h % 2, r, :], ps_s[h % 2][:, r * W:(r + 1) * W], ACT.Exp,
                                              bias=neg[:, h % 2, r:r + 1], scale=SCALE, accum_out=den[p][:, r, h:h + 1])
                    done.then_inc(exped, 1)
                    if h:
                        probs_in(i, h - 1)
                    elif not first:
                        probs_in(i - 1, H - 1)
                    if not last:
                        if h == 1:
                            rows_in(i + 1)
                        elif h == 2:
                            qk_in(i + 1, q)
                        elif h == 3:
                            v_in(i + 1, q)
                    if h == 2 and not first:
                        mixed_in(i - 1)

            turn(0, 0, first=True)
            turn(0, 1)
            with act.Fori(0, HALF - 2) as j:
                turn(j + 1, 0)
                turn(j + 1, 1)
            turn(HALF - 1, 0)
            turn(HALF - 1, 1, last=True)
            probs_in(TURNS - 1, H - 1)
            mixed_in(TURNS - 1)

        @block.vector
        def _(dve):
            step = Chain(dve, dch)
            dve.wait_ge(loaded, 16 * LOADS)
            dve.wait_ge(made, 1)
            step(dve.tensor_scalar(drop[:, :], adj_sb[:, :], 0.0, None, ALU.is_equal))
            dve.sem_inc(prepared, 1)
            wide = [P, R, W]

            def mask(i, h):
                ps = ps_s[h % 2][:, :].rearrange("p (r w) -> p r w", r=R)
                dve.wait_ge(scored, i * H + h + 1)
                dve.sem_inc(tick, 1)
                step(dve.copy_predicated(ps, drop[:, :].unsqueeze(1).broadcast_to(wide),
                                         low[:, :].unsqueeze(1).broadcast_to(wide)))
                step(dve.tensor_reduce(mx[:, h % 2, :], ps, AX.X, ALU.max))
                step(dve.tensor_scalar(neg[:, h % 2, :], mx[:, h % 2, :], -SCALE, None, ALU.mult))
                dve.sem_inc(peaked, 1)

            def divide(i, q):
                dve.wait_ge(mixed, i + 1)
                step(dve.reciprocal(den[q][:, :, :], den[q][:, :, :]))
                step(dve.tensor_tensor(on[:, :, :].rearrange("p r (h d) -> p r h d", h=H),
                                       ps_o[:, :].rearrange("p (r h d) -> p r h d", r=R, h=H),
                                       den[q][:, :, :].unsqueeze(3).broadcast_to([P, R, H, D]), ALU.mult))
                dve.sem_inc(on_ready, 1)

            def sum_up(i):
                dve.wait_ge(outed, i + 1)
                step(dve.scalar_tensor_tensor(
                    out=z[:, :, :], in0=hg[:, bass.ds(i * R, R), :], scalar=2.0,
                    in1=ps_z[:, :].rearrange("p (r c) -> p r c", r=R), op0=ALU.mult, op1=ALU.add))
                for r in range(R):
                    step.mark(dve.bn_stats(st[:, r, :], z[:, r, :]))
                step.join()
                dve.sem_inc(tick, 1)
                for r in range(R):
                    step.mark(dve.bn_aggr(mv[:, r, :], st[:, r, :]))
                step.join()
                step(dve.tensor_scalar(ve[:, :], mv[:, :, 1], eps, None, ALU.add))
                dve.sem_inc(ve_ready, 1)

            def scale(i, fresh=False):
                dve.wait_ge(rstd_ready, i + 1)
                if not fresh:
                    dve.wait_ge(stored, i * 16)
                for r in range(R):
                    step.mark(dve.tensor_scalar(out[:, r, :], z[:, r, :], mv[:, r, 0:1], rstd[:, r:r + 1],
                                                ALU.subtract, ALU.mult))
                step.join()
                dve.sem_inc(scaled, 1)

            mask(0, 0)

            def turn(j, p, first=False, last=False):
                i, q = 2 * j + p, 1 - p
                for h in range(H):
                    if h == 3 and not first:
                        sum_up(i - 1)
                    if h + 1 < H:
                        mask(i, h + 1)
                    elif not last:
                        mask(i + 1, 0)
                    if h == 0 and not first:
                        divide(i - 1, q)
                    if h == 3 and not first:
                        scale(i - 1, fresh=isinstance(i, int) and i == 1)

            turn(0, 0, first=True)
            turn(0, 1)
            with step.loop(HALF - 2, 2 * (3 * H + 2 + 1 + 2 * R + 1 + R)) as j:
                turn(j + 1, 0)
                turn(j + 1, 1)
            turn(HALF - 1, 0)
            turn(HALF - 1, 1, last=True)
            divide(TURNS - 1, 1)
            sum_up(TURNS - 1)
            scale(TURNS - 1)


def mamba(nc, h0, x, in_proj, conv_w, conv_b, x_proj, dt_w, dt_b, A_log, Dp, out_w, out_b, gain, shift,
          x1, tag="mam", eps=1e-5):
    Q = 16
    G, J = 4, 4
    NQ = W // Q
    N = Q * T
    K = conv_w.shape[1]
    S = A_log.shape[1]
    DI = A_log.shape[0]
    HV = DI // P
    RK = dt_w.shape[0]
    PADT = T + K - 1
    TURNS = B * NQ
    with ExitStack() as ctx:
        s = Scope(nc, ctx, tag)
        w_in = s.sb("w_in", [P, 2 * DI])
        w_conv = s.sb("w_conv", [P, K, DI])
        cw_b = s.sb("cw_b", [P, DI, K])
        cb = s.sb("cb", [P, HV])
        xp = s.sb("xp", [P, HV, RK + 2 * S])
        xp3 = s.sb("xp3", [P, HV, 3, 2 * S])
        dtw = s.sb("dtw", [RK, DI])
        dtb = s.sb("dtb", [P, HV])
        A = s.sb("A", [P, HV, S])
        dp = s.sb("dp", [P, HV])
        ow = s.sb("ow", [P, HV, C])
        ob = s.sb("ob", [1, C])
        gain_b = s.sb("gain", [P, C])
        shift_b = s.sb("shift", [P, C])
        ident = s.sb("ident", [P, P])
        ones1 = s.sb("ones1", [1, P])
        half_c = s.sb("half", [P, G])
        sel = s.sb("sel", [96, 2 * S, P], bf16)

        ht = [s.sb(f"ht{j}", [P, G, C]) for j in range(2)]
        hr = [s.sb(f"hr{j}", [P, G, C]) for j in range(2)]
        xt = [s.sb(f"xt{j}", [P, G, C]) for j in range(2)]
        hT = s.sb("hT", [P, Q, PADT])
        xs = [s.sb(f"xs{j}", [P, HV, N]) for j in range(2)]
        sz = [s.sb(f"sz{j}", [P, HV, N]) for j in range(2)]
        dt = [s.sb(f"dt{j}", [P, HV, N]) for j in range(2)]
        dtx = [s.sb(f"dtx{j}", [P, HV, N]) for j in range(2)]
        bc3 = [s.sb(f"bc3_{j}", [96, N], bf16) for j in range(2)]
        dtr = s.sb("dtr", [RK, N])
        bcf = s.sb("bcf", [96, N])
        mid = s.sb("mid", [96, N], bf16)
        e = s.sb("e", [P, HV, N])
        ln = s.sb("ln", [P, HV, N])
        po, lin, e2 = (s.sb(n, [P, HV, N]) for n in ("po", "lin", "e2"))
        small = s.sb("small", [P, HV, N], u8)
        third = s.sb("third", [P, 1])
        dA = [s.sb(f"dA{j}", [P, HV, Q, T]) for j in range(4)]
        dBx = [s.sb(f"dBx{j}", [P, HV, N]) for j in range(2)]
        hs = [s.sb(f"hs{j}", [P, HV, N]) for j in range(2)]
        hc = [s.sb(f"hc{j}", [P, HV, N]) for j in range(4)]
        y = s.sb("y", [P, HV, N])
        z = s.sb("z", [P, G, C])
        out = s.sb("out", [P, G, C])
        st = s.sb("st", [P, G, 6])
        mv = s.sb("mv", [P, G, 2])
        ve = s.sb("ve", [P, G])
        rstd = s.sb("rstd", [P, G])
        ps_b = [s.ps(f"ps_b{j}") for j in range(2)]
        ps_c = [s.ps(f"ps_c{j}") for j in range(2)]
        ps_y = [s.ps(f"ps_y{j}") for j in range(2)]
        ps_0, ps_1 = s.ps("ps_0"), s.ps("ps_1")

        (loaded, made, prepared, turned, hT_ready, conv_done, gate_done, xs_ready, sz_ready, bc_made,
         bc_copied, bc_ready, dt_made, soft_step, e_ready, po_ready, dt_ready, spread, dA_ready, hc_ready,
         y_done, y_taken, y_ready, outed, z_ready, ve_ready, rstd_ready, scaled, out_ready, stored, dch, pch,
         ach, dtick, ptick, ln_ready, stick, ln_chosen, dtx_ready) = (
            s.sem(n) for n in (
                "loaded", "made", "prepared", "turned", "hT_ready", "conv_done", "gate_done", "xs_ready",
                "sz_ready", "bc_made", "bc_copied", "bc_ready", "dt_made", "soft_step", "e_ready", "po_ready",
                "dt_ready", "spread", "dA_ready", "hc_ready", "y_done", "y_taken", "y_ready", "outed",
                "z_ready", "ve_ready", "rstd_ready", "scaled", "out_ready", "stored", "dch", "pch", "ach",
                "dtick", "ptick", "ln_ready", "stick", "ln_chosen", "dtx_ready"))
        hin = [s.sem(f"hin{j}") for j in range(2)]
        rin = [s.sem(f"rin{j}") for j in range(2)]
        block = ctx.enter_context(nc.Block())
        LOADS = 13
        LOAD = 16 * J

        def tokens(v, b, k, j):
            return v[b].rearrange("t (k g j) c -> k j t g c", k=NQ, g=G)[k, j]

        h0v = h0.rearrange("(b t) w c -> b t w c", b=B)


        @block.sync
        def _(sp):
            sp.dma_start(w_in[:, :], in_proj).then_inc(loaded, 16)
            sp.dma_start(cw_b[:, :, :], conv_w.rearrange("d k -> (d k)").unsqueeze(0)
                         .broadcast_to([P, DI * K]).rearrange("p (d k) -> p d k", k=K)).then_inc(loaded, 16)
            sp.dma_start(xp[:, :, :], x_proj.rearrange("(h d) r -> d h r", h=HV)).then_inc(loaded, 16)
            sp.dma_start(dtw[:, :], dt_w).then_inc(loaded, 16)
            sp.dma_start(A[:, :, :], A_log.rearrange("(h d) s -> d h s", h=HV)).then_inc(loaded, 16)
            sp.dma_start(ow[:, :, :], out_w.rearrange("(h d) c -> d h c", h=HV)).then_inc(loaded, 16)
            for dst, src in ((cb, conv_b), (dtb, dt_b), (dp, Dp)):
                for h in range(HV):
                    sp.dma_start(dst[:, h:h + 1], src[h * P:(h + 1) * P].unsqueeze(1)).then_inc(loaded, 16)
            sp.dma_start(ob[:, :], out_b.unsqueeze(0)).then_inc(loaded, 16)
            for dst, src in ((gain_b, gain), (shift_b, shift)):
                sp.dma_start(dst[:, :], src.unsqueeze(0).broadcast_to([P, C])).then_inc(made, 16)
            for b in range(2):
                for j in range(J):
                    sp.dma_start(ht[b][j * T:(j + 1) * T, :, :], tokens(h0v, b, 0, j)).then_inc(hin[b], 16)

            def turn(k, b, first=False, last=False):
                i, p = k * B + b, b % 2
                k2, b2 = (k, b + 2) if b + 2 < B else (k + 1, b + 2 - B)
                k1, b1 = (k, b - 1) if b else (k - 1, B - 1)
                if not (last and b + 2 >= B):
                    sp.wait_ge(turned, i + 1)
                    sp.sem_inc(stick, 1)
                    for j in range(J):
                        sp.dma_start(ht[p][j * T:(j + 1) * T, :, :], tokens(h0v, b2, k2, j)).then_inc(hin[p], 16)
                if not (first and b < 2):
                    sp.wait_ge(out_ready, i - 1)
                    sp.sem_inc(stick, 1)
                for j in range(J):
                    sp.dma_start(hr[p][j * T:(j + 1) * T, :, :], tokens(h0v, b, k, j)).then_inc(rin[p], 16)
                    sp.dma_start(xt[p][j * T:(j + 1) * T, :, :], tokens(x, b, k, j)).then_inc(rin[p], 16)
                if not (first and b == 0):
                    sp.wait_ge(out_ready, i)
                    sp.sem_inc(stick, 1)
                    for j in range(J):
                        sp.dma_start(tokens(x1, b1, k1, j), out[j * T:(j + 1) * T, :, :]).then_inc(stored, 16)

            for b in range(B):
                turn(0, b, first=True)
            with sp.Fori(0, NQ - 2) as k:
                for b in range(B):
                    turn(k + 1, b)
            for b in range(B):
                turn(NQ - 1, b, last=True)
            sp.wait_ge(out_ready, TURNS)
            for j in range(J):
                sp.dma_start(tokens(x1, B - 1, NQ - 1, j), out[j * T:(j + 1) * T, :, :]).then_inc(stored, 16)
            sp.wait_ge(stored, LOAD * TURNS)

        @block.gpsimd
        def _(pool):
            step = Chain(pool, pch)
            fill_identity(pool, step, ident)
            step(pool.memset(half_c[:, :], -0.5))
            step(pool.memset(third[:, :], 1.0 / 3))
            step(pool.memset(ones1[:, :], 1.0))
            step(pool.memset(hT[:, :, :], 0.0))
            for a in dA:
                step(pool.memset(a[:, :, :, :], 0.0))
            step(pool.memset(sel[:, :, :], 0.0))
            for j in range(3):
                step(pool.affine_select(out=sel[:, :, :], in_=sel[:, :, :], compare_op=ALU.not_equal, fill=1.0,
                                        base=-32 * j, pattern=[[-1, 2 * S], [0, P]], channel_multiplier=1))
            pool.wait_ge(loaded, 16 * LOADS)
            for k in range(K):
                step(pool.tensor_tensor(w_conv[:, k, :], w_in[:, 0:DI], cw_b[:, :, k], ALU.mult))
            for j in range(3):
                step(pool.tensor_copy(xp3[:, :, j, :], xp[:, :, RK:RK + 2 * S]))
            pool.sem_inc(prepared, 1)
            pool.wait_ge(made, 32)
            pool.sem_inc(ptick, 1)

            def finish(i, p):
                pool.wait_ge(y_taken, i + 1)
                pool.tensor_tensor(y[:, :, :], y[:, :, :], sz[p][:, :, :], ALU.mult).then_inc(y_ready, 1)
                pool.wait_ge(ve_ready, i + 1)
                pool.tensor_tensor(rstd[:, :], ve[:, :], half_c[:, :], ALU.pow).then_inc(rstd_ready, 1)
                pool.wait_ge(scaled, i + 1)
                wide = [P, G, C]
                step(pool.tensor_tensor(out[:, :, :], out[:, :, :], gain_b[:, :].unsqueeze(1).broadcast_to(wide), ALU.mult))
                step(pool.tensor_tensor(out[:, :, :], out[:, :, :], shift_b[:, :].unsqueeze(1).broadcast_to(wide), ALU.add))
                pool.tensor_tensor(out[:, :, :], out[:, :, :], xt[p][:, :, :], ALU.add).then_inc(out_ready, 1)

            def prepare(i, q):
                pool.wait_ge(e_ready, i + 1)
                step(pool.tensor_tensor(po[:, :, :], po[:, :, :], e2[:, :, :], ALU.mult))
                step(pool.tensor_tensor(po[:, :, :], po[:, :, :], lin[:, :, :], ALU.add))
                pool.tensor_tensor(po[:, :, :], po[:, :, :], e[:, :, :], ALU.mult).then_inc(po_ready, 1)
                pool.wait_ge(ln_chosen, i + 1)
                step(pool.tensor_tensor(dt[q][:, :, :], dt[q][:, :, :], ln[:, :, :], ALU.add))
                pool.sem_inc(dt_ready, 1)
                pool.tensor_tensor(dtx[q][:, :, :], dt[q][:, :, :], xs[q][:, :, :], ALU.mult).then_inc(dtx_ready, 1)

            prepare(0, 0)
            prepare(1, 1)
            with step.loop(TURNS // 2 - 1, 2 * 5) as j:
                for p in range(2):
                    finish(2 * j + p, p)
                    prepare(2 * j + p + 2, p)
            finish(TURNS - 2, 0)
            finish(TURNS - 1, 1)

        @block.tensor
        def _(pe):
            pe.wait_ge(loaded, 16 * LOADS)
            pe.wait_ge(prepared, 1)

            def nodes(ps):
                return ps[:, :].rearrange("p (q t) -> p q t", q=Q)

            def turn_tokens(i, j, p):
                pe.wait_ge(hin[p], LOAD * (j + 1))
                for g in range(G):
                    last = pe.transpose(ps_0[:, g * P:(g + 1) * P], ht[p][:, g, :], ident[:, :])
                last.then_inc(turned, 1)

            def convolve(h, taps, ps):
                for k in taps:
                    last = pe.matmul(nodes(ps), w_conv[:, k, h * P:(h + 1) * P], hT[:, :, k:k + T],
                                     start=(k == 0), stop=(k == K - 1))
                if K - 1 in taps:
                    last.then_inc(conv_done, 1)

            def gate(h):
                pe.matmul(nodes(ps_0), w_in[:, DI + h * P:DI + (h + 1) * P], hT[:, :, K - 1:K - 1 + T],
                          start=True, stop=True).then_inc(gate_done, 1)

            def project():
                for h in range(HV):
                    pe.matmul(ps_1[0:RK, :], xp[:, h, 0:RK], xs_now[:, h, :], start=(h == 0), stop=(h == HV - 1))
                for h in range(HV):
                    last = pe.matmul(ps_0[0:96, :], xp3[:, h, :, :].rearrange("p a s -> p (a s)"), xs_now[:, h, :],
                                     start=(h == 0), stop=(h == HV - 1))
                last.then_inc(bc_made, 1)

            def time_steps():
                pe.matmul(ps_1[:, :], dtw[:, 0:P], dtr[:, :], start=True, stop=True)
                pe.matmul(ps_0[:, :], dtw[:, P:2 * P], dtr[:, :], start=True, stop=True).then_inc(dt_made, 1)

            def spread_state(n, p):
                pe.matmul(ps_b[n % 2][:, :], sel[:, n, :], bc3[p][:, :], start=True, stop=True)
                pe.matmul(ps_c[n % 2][:, :], sel[:, S + n, :], bc3[p][:, :], start=True, stop=True
                          ).then_inc(spread, 1)

            def project_out():
                for g in range(G):
                    cols = slice(g * P, (g + 1) * P)
                    for h in range(HV):
                        pe.matmul(ps_1[:, cols], y[:, h, cols], ow[:, h, :], start=(h == 0), stop=False)
                    last = pe.matmul(ps_1[:, cols], ones1[:, :], ob[:, :], start=False, stop=True)
                last.then_inc(outed, 1)

            xs_now = xs[0]
            turn_tokens(0, 0, 0)
            pe.wait_ge(hT_ready, 1)
            for h, ps in ((0, ps_0), (1, ps_1)):
                convolve(h, range(K), ps)
                pe.wait_ge(xs_ready, h + 1)
                gate(h)
            pe.wait_ge(sz_ready, 2)
            project()
            pe.wait_ge(bc_copied, 1)
            time_steps()
            pe.wait_ge(bc_ready, 1)
            spread_state(0, 0)
            spread_state(1, 0)

            def turn(j, p, first=False, last=False):
                nonlocal xs_now
                i = 2 * j + p
                jn, q = (j, 1) if p == 0 else (j + 1, 0)
                xs_now = xs[q]
                for n in range(S):
                    pe.wait_ge(hc_ready, i * S + n + 1)
                    if n + 2 < S:
                        spread_state(n + 2, p)
                    elif not last:
                        if n + 2 == S:
                            pe.wait_ge(bc_ready, i + 2)
                        spread_state(n + 2 - S, q)
                    if n == 0 and not first:
                        pe.wait_ge(y_taken, i)
                    for h in range(HV):
                        done = pe.matmul(ps_y[h][:, :], ident[:, :], hc[n % 4][:, h, :],
                                         start=(n == 0), stop=(n == S - 1))
                    done.then_inc(y_done, 1)
                    if n == 2 and not first:
                        pe.wait_ge(y_ready, i)
                        project_out()
                    if last:
                        continue
                    if n == 0:
                        pe.wait_ge(e_ready, i + 1)
                        turn_tokens(i + 1, jn, q)
                    elif n == 1:
                        pe.wait_ge(hT_ready, i + 2)
                        convolve(0, (0, 1), ps_0)
                    elif n == 3:
                        convolve(0, (2, 3), ps_0)
                    elif n == 4:
                        pe.wait_ge(xs_ready, 2 * i + 3)
                        gate(0)
                    elif n == 5:
                        if not first:
                            pe.wait_ge(z_ready, i)
                        convolve(1, (0, 1), ps_1)
                    elif n == 6:
                        convolve(1, (2, 3), ps_1)
                        pe.wait_ge(sz_ready, 2 * i + 3)
                        gate(1)
                    elif n == 7:
                        pe.wait_ge(xs_ready, 2 * i + 4)
                        pe.wait_ge(sz_ready, 2 * i + 4)
                        project()
                    elif n == 8:
                        pe.wait_ge(bc_copied, i + 2)
                        time_steps()

            turn(0, 0, first=True)
            turn(0, 1)
            with pe.Fori(0, TURNS // 2 - 2) as j:
                turn(j + 1, 0)
                turn(j + 1, 1)
            turn(TURNS // 2 - 1, 0)
            turn(TURNS // 2 - 1, 1, last=True)
            pe.wait_ge(y_ready, TURNS)
            project_out()

        @block.scalar
        def _(act):
            step = Chain(act, ach)
            act.wait_ge(loaded, 16 * LOADS)
            step(act.activation(A[:, :, :], A[:, :, :], ACT.Exp))
            step(act.mul(A[:, :, :], A[:, :, :], -1.0))
            act.wait_ge(prepared, 1)

            def tokens_in(i):
                act.wait_ge(turned, i + 1)
                act.copy(hT[:, :, K - 1:], ps_0[:, :].rearrange("p (q t) -> p q t", q=Q)).then_inc(hT_ready, 1)

            def silu_x(i, h, q, ps):
                act.wait_ge(conv_done, 2 * i + h + 1)
                act.activation(xs[q][:, h, :], ps[:, :], ACT.Silu, bias=cb[:, h:h + 1]).then_inc(xs_ready, 1)

            def silu_z(i, h, q):
                act.wait_ge(gate_done, 2 * i + h + 1)
                act.activation(sz[q][:, h, :], ps_0[:, :], ACT.Silu).then_inc(sz_ready, 1)

            def projections_in(i, q):
                act.wait_ge(bc_made, i + 1)
                act.copy(bcf[:, :], ps_0[0:96, :])
                act.copy(bc3[q][:, :], ps_0[0:96, :])
                act.copy(dtr[:, :], ps_1[0:RK, :]).then_inc(bc_copied, 1)

            def softplus(i, q):
                act.wait_ge(dt_made, i + 1)
                for h, ps in ((0, ps_1), (1, ps_0)):
                    act.activation(e[:, h, :], ps[:, :], ACT.Abs, bias=dtb[:, h:h + 1])
                    last = act.activation(dt[q][:, h, :], ps[:, :], ACT.Relu, bias=dtb[:, h:h + 1])
                last.then_inc(soft_step, 1)
                act.wait_ge(soft_step, 2 * i + 1)
                act.activation(e[:, :, :], e[:, :, :], ACT.Exp, scale=-1.0).then_inc(soft_step, 1)
                act.wait_ge(soft_step, 2 * i + 2)
                act.activation(e2[:, :, :], e[:, :, :], ACT.Square)
                act.activation(lin[:, :, :], e[:, :, :], ACT.Identity, bias=1.0, scale=-0.5)
                act.activation(po[:, :, :], e[:, :, :], ACT.Identity, bias=third[:, :], scale=-0.25
                               ).then_inc(e_ready, 1)

            def logarithm():
                act.activation(ln[:, :, :], e[:, :, :], ACT.Ln, bias=1.0).then_inc(ln_ready, 1)

            tokens_in(0)
            silu_x(0, 0, 0, ps_0)
            silu_z(0, 0, 0)
            silu_x(0, 1, 0, ps_1)
            silu_z(0, 1, 0)
            projections_in(0, 0)
            softplus(0, 0)
            logarithm()

            def turn(j, p, first=False, last=False):
                i = 2 * j + p
                q = 1 - p
                act.wait_ge(dt_ready, i + 1)
                for n in range(S):
                    if not (first and n < 4):
                        act.wait_ge(hc_ready, i * S + n - 3)
                    for h in range(HV):
                        done = act.activation(dA[n % 4][:, h, :, 1:],
                                              dt[p][:, h, :].rearrange("p (q t) -> p q t", q=Q)[:, :, 1:],
                                              ACT.Exp, scale=A[:, h, n:n + 1])
                    done.then_inc(dA_ready, 1)
                    if last:
                        continue
                    if n == 3:
                        tokens_in(i + 1)
                    elif n == 5:
                        if not first:
                            act.wait_ge(y_ready, i)
                        silu_x(i + 1, 0, q, ps_0)
                    elif n == 7:
                        silu_z(i + 1, 0, q)
                    elif n == 8:
                        silu_x(i + 1, 1, q, ps_1)
                        silu_z(i + 1, 1, q)
                    elif n == 10:
                        projections_in(i + 1, q)
                    elif n == 11:
                        softplus(i + 1, q)
                    elif n == 12:
                        logarithm()

            turn(0, 0, first=True)
            turn(0, 1)
            with act.Fori(0, TURNS // 2 - 2) as j:
                turn(j + 1, 0)
                turn(j + 1, 1)
            turn(TURNS // 2 - 1, 0)
            turn(TURNS // 2 - 1, 1, last=True)

        @block.vector
        def _(dve):
            step = Chain(dve, dch)
            both = [P, HV, N]
            dve.wait_ge(loaded, 16 * LOADS)
            dve.wait_ge(prepared, 1)

            def parts(i, q):
                dve.wait_ge(bc_copied, i + 1)
                step(dve.tensor_tensor(bcf[:, :], bcf[:, :], bc3[q][:, :], ALU.subtract))
                step(dve.tensor_copy(mid[:, :], bcf[:, :]))
                step.mark(dve.tensor_copy(bc3[q][32:64, :], mid[32:64, :]))
                step(dve.tensor_tensor(bc3[q][64:96, :], bcf[64:96, :], mid[64:96, :], ALU.subtract))
                dve.sem_inc(bc_ready, 1)

            def time_step(i, part):
                if part == 0:
                    dve.wait_ge(e_ready, i + 1)
                    step.mark(dve.tensor_scalar(small[:, :, :], e[:, :, :], 0.06, None, ALU.is_lt))
                else:
                    dve.wait_ge(po_ready, i + 1)
                    dve.wait_ge(ln_ready, i + 1)
                    dve.sem_inc(dtick, 1)
                    step(dve.copy_predicated(ln[:, :, :], small[:, :, :], po[:, :, :]))
                    dve.sem_inc(ln_chosen, 1)

            parts(0, 0)
            for part in range(2):
                time_step(0, part)
                step.join()

            def take_y(i, q):
                dve.wait_ge(y_done, (i + 1) * S)
                for h in range(HV):
                    step.mark(dve.scalar_tensor_tensor(out=y[:, h, :], in0=xs[q][:, h, :], scalar=dp[:, h:h + 1],
                                                       in1=ps_y[h][:, :], op0=ALU.mult, op1=ALU.add))
                step.join()
                dve.sem_inc(y_taken, 1)

            def residual(i, j, q):
                dve.wait_ge(outed, i + 1)
                dve.wait_ge(rin[q], 2 * LOAD * (j + 1))
                step(dve.tensor_tensor(z[:, :, :], hr[q][:, :, :], ps_1[:, :].rearrange("p (g c) -> p g c", g=G), ALU.add))
                dve.sem_inc(z_ready, 1)

            def statistics():
                for g in range(G):
                    step.mark(dve.bn_stats(st[:, g, :], z[:, g, :]))

            def moments():
                dve.sem_inc(dtick, 1)
                for g in range(G):
                    step.mark(dve.bn_aggr(mv[:, g, :], st[:, g, :]))
                step.join()
                step(dve.tensor_scalar(ve[:, :], mv[:, :, 1], eps, None, ALU.add))
                dve.sem_inc(ve_ready, 1)

            def scale(i, fresh=False):
                dve.wait_ge(rstd_ready, i + 1)
                if not fresh:
                    dve.wait_ge(stored, i * LOAD)
                for g in range(G):
                    step.mark(dve.tensor_scalar(out[:, g, :], z[:, g, :], mv[:, g, 0:1], rstd[:, g:g + 1],
                                                ALU.subtract, ALU.mult))
                step.join()
                dve.sem_inc(scaled, 1)

            PREPARE, FINISH = 4 + 2, 2 + 1 + G + G + 1 + G

            def turn(j, p, first=False, last=False):
                i, q = 2 * j + p, 1 - p
                jq = j if p else j - 1
                dve.wait_ge(spread, i * S + 1)
                dve.wait_ge(dtx_ready, i + 1)
                ready = step.mark(dve.tensor_tensor(
                    dBx[0][:, :, :], dtx[p][:, :, :], ps_b[0][:, :].unsqueeze(1).broadcast_to(both), ALU.mult))
                for n in range(S):
                    dve.wait_ge(dA_ready, i * S + n + 1)
                    step.wait(ready)
                    scanned = step.mark(dve.tensor_tensor_scan(
                        hs[n % 2][:, :, :].rearrange("p h n -> p (h n)"),
                        dA[n % 4][:, :, :, :].rearrange("p h q t -> p (h q t)"),
                        dBx[n % 2][:, :, :].rearrange("p h n -> p (h n)"), 0.0, ALU.mult, ALU.add))
                    if n + 1 < S:
                        dve.wait_ge(spread, i * S + n + 2)
                        ready = step.mark(dve.tensor_tensor(
                            dBx[(n + 1) % 2][:, :, :], dtx[p][:, :, :],
                            ps_b[(n + 1) % 2][:, :].unsqueeze(1).broadcast_to(both), ALU.mult))
                    if not last:
                        if n == 10:
                            parts(i + 1, q)
                        elif n == 11:
                            time_step(i + 1, 0)
                        elif n == 13:
                            step.join()
                            time_step(i + 1, 1)
                    if not first:
                        if n == 0:
                            take_y(i - 1, q)
                        elif n == 4:
                            residual(i - 1, jq, q)
                        elif n == 5:
                            statistics()
                        elif n == 6:
                            step.join()
                            moments()
                        elif n == 8:
                            scale(i - 1, fresh=isinstance(i, int) and i == 1)
                    step.wait(scanned)
                    if not (first and n < 4):
                        dve.wait_ge(y_done, i * S + n - 3)
                    dve.tensor_tensor(hc[n % 4][:, :, :], hs[n % 2][:, :, :],
                                      ps_c[n % 2][:, :].unsqueeze(1).broadcast_to(both), ALU.mult
                                      ).then_inc(hc_ready, 1)
                step.join()

            turn(0, 0, first=True)
            turn(0, 1)
            with step.loop(TURNS // 2 - 2, 2 * (2 * S + PREPARE + FINISH)) as j:
                turn(j + 1, 0)
                turn(j + 1, 1)
            turn(TURNS // 2 - 1, 0)
            turn(TURNS // 2 - 1, 1, last=True)
            take_y(TURNS - 1, 1)
            residual(TURNS - 1, TURNS // 2 - 1, 1)
            statistics()
            step.join()
            moments()
            scale(TURNS - 1)


NKY, NKX = 32, 17
LKY, LKX = 16, 9
SR = 64
ROWS = [k if k < NKY // 2 else k - NKY for k in range(NKY)]
IMG = W * C


def fourier_tables():
    n = np.arange(W, dtype=np.float64)
    al = 2 * np.pi / W
    r2 = SR // 2
    k = np.arange(r2 + 1)
    cos, sin = np.cos(al * np.outer(n, k)), np.sin(al * np.outer(n, k))
    scale = np.where((k == 0) | (k == r2), 1.0, np.sqrt(2.0))
    t = {}
    t["rows_all"] = np.concatenate([cos, sin[:, 1:]], 1) / W
    t["gram_cols"] = np.concatenate([cos * scale, sin * scale], 1) / W
    cx, sx = cos[:, :NKX], sin[:, :NKX]
    t["tok_cols"] = np.concatenate([cx, -sx, -sx, -cx, sx, cx], 1) / W
    kr = np.array(ROWS)
    cr, sr = np.cos(al * np.outer(n, kr)), np.sin(al * np.outer(n, kr))
    t["rows_fwd"] = np.concatenate([cr, -sr], 1) / W
    z = np.zeros((W, 32 - NKX))
    t["cols_fwd"] = np.concatenate([cx, z, -sx, z, sx, z, cx, z], 1) / W
    m = np.where(np.arange(NKX) == 0, 1.0, 2.0)[:, None]
    mc, ms, zz = m * cx.T, m * sx.T, np.zeros((32 - NKX, W))
    g1 = np.concatenate([np.concatenate([mc, zz, -ms, zz]), np.concatenate([ms, zz, mc, zz])], 1)
    g2 = np.concatenate([np.concatenate([-ms, zz, -mc, zz]), np.concatenate([mc, zz, -ms, zz])], 1)
    t["cols_inv"] = np.concatenate([g1, g2], 1)
    t["rows_inv"] = np.concatenate([cr.T, -sr.T], 1)
    return {a: np.ascontiguousarray(b.astype(np.float32)) for a, b in t.items()}


def inline_tables(nc):
    return {a: nc.inline_tensor(b, name=f"table_{a}").ap()
            for a, b in fourier_tables().items()}


def token_images(nc, hg, g1, b1, tok, tnd, tag="l1n", eps=1e-5):
    with ExitStack() as ctx:
        s = Scope(nc, ctx, tag)
        sq = s.sb("sq", [P, 8, C])
        sums = s.sb("sums", [P, 2, BT])
        ones = s.sb("ones", [P, P])
        gb = s.sb("gb", [P, 2])
        var, rstd, half, scale, bias = (s.sb(n, [P, BT]) for n in ("var", "rstd", "half", "scale", "bias"))
        ps = s.ps("ps")
        loaded, made, saved, squared, reduced, summed, var_ready, rstd_ready, ready, dch = (
            s.sem(n) for n in ("loaded", "made", "saved", "squared", "reduced", "summed", "var_ready",
                               "rstd_ready", "ready", "dch"))
        block = ctx.enter_context(nc.Block())

        @block.sync
        def _(sp):
            for j, src in enumerate((g1, b1)):
                sp.dma_start(gb[:, j:j + 1], src.unsqueeze(0).broadcast_to([P, 1])).then_inc(loaded, 16)
            sp.dma_start(tok.rearrange("n r c -> r n c"), hg[:, :, :]).then_inc(saved, 16)
            sp.wait_ge(ready, BT // 8)
            sp.dma_start(tnd.rearrange("n r c -> r n c"), hg[:, :, :]).then_inc(saved, 16)
            sp.wait_ge(saved, 32)

        @block.gpsimd
        def _(pool):
            pool.memset(ones[:, :], 1.0 / IMG).then_inc(made, 1)
            pool.memset(half[:, :], -0.5).then_inc(made, 1)
            pool.wait_ge(made, 2)
            pool.wait_ge(var_ready, 1)
            pool.tensor_tensor(rstd[:, :], var[:, :], half[:, :], ALU.pow).then_inc(rstd_ready, 1)

        @block.scalar
        def _(act):
            with act.Fori(0, BT // 8) as i:
                act.wait_ge(reduced, i)
                act.activation(sq[:, :, :], hg[:, bass.ds(i * 8, 8), :], ACT.Square).then_inc(squared, 1)

        @block.tensor
        def _(pe):
            pe.wait_ge(made, 2)
            pe.wait_ge(reduced, BT // 8)
            pe.matmul(ps[:, 0:2 * BT], ones[:, :], sums[:, :, :].rearrange("p a n -> p (a n)"),
                      start=True, stop=True).then_inc(summed, 1)

        @block.vector
        def _(dve):
            step = Chain(dve, dch)
            with step.loop(BT // 8, 2) as i:
                step.mark(dve.tensor_reduce(sums[:, 0, bass.ds(i * 8, 8)], hg[:, bass.ds(i * 8, 8), :], AX.X, ALU.add))
                dve.wait_ge(squared, i + 1)
                step(dve.tensor_reduce(sums[:, 1, bass.ds(i * 8, 8)], sq[:, :, :], AX.X, ALU.add))
                dve.sem_inc(reduced, 1)
            dve.wait_ge(summed, 1)
            dve.wait_ge(loaded, 32)
            step(dve.tensor_copy(sums[:, :, :], ps[:, 0:2 * BT].rearrange("p (a n) -> p a n", a=2)))
            step(dve.tensor_tensor(var[:, :], sums[:, 0, :], sums[:, 0, :], ALU.mult))
            step(dve.scalar_tensor_tensor(out=var[:, :], in0=sums[:, 1, :], scalar=eps, in1=var[:, :],
                                          op0=ALU.add, op1=ALU.subtract))
            dve.sem_inc(var_ready, 1)
            dve.wait_ge(rstd_ready, 1)
            step(dve.tensor_scalar(scale[:, :], rstd[:, :], gb[:, 0:1], None, ALU.mult))
            step(dve.tensor_tensor(bias[:, :], sums[:, 0, :], scale[:, :], ALU.mult))
            step(dve.tensor_scalar(bias[:, :], bias[:, :], -1.0, gb[:, 1:2], ALU.mult, ALU.add))
            dve.wait_ge(saved, 16)
            with step.loop(BT // 8, 2) as i:
                v = hg[:, bass.ds(i * 8, 8), :]
                step(dve.tensor_tensor(v, v, scale[:, bass.ds(i * 8, 8)].unsqueeze(2).broadcast_to([P, 8, C]), ALU.mult))
                step(dve.tensor_tensor(v, v, bias[:, bass.ds(i * 8, 8)].unsqueeze(2).broadcast_to([P, 8, C]), ALU.add))
                dve.sem_inc(ready, 1)


def token_spectra(nc, tn, tabs, xh, gram_d, tag="l1f"):
    R = 4
    KA = SR + 1
    h = SR // 2
    with ExitStack() as ctx:
        s = Scope(nc, ctx, tag)
        rows = s.sb("rows", [P, KA])
        cols = s.sb("cols", [P, 2 * (h + 1)])
        tcols = s.sb("tcols", [P, 3, 2 * NKX])
        o1 = s.sb("o1", [P, KA, BT])
        img = [s.sb(f"img{j}", [P, R, C]) for j in range(2)]
        loaded, staged, done, copied = (s.sem(n) for n in ("loaded", "staged", "done", "copied"))
        with ExitStack() as c2:
            s2 = Scope(nc, c2, tag + "a")
            ps = [s2.ps(f"ps{j}") for j in range(2)]
            block = c2.enter_context(nc.Block())

            @block.sync
            def _(sp):
                for dst, src in ((rows[:, :], tabs["rows_all"]), (cols[:, :], tabs["gram_cols"]),
                                 (tcols[:, :, :].rearrange("p a k -> p (a k)"), tabs["tok_cols"])):
                    sp.dma_start(dst, src).then_inc(loaded, 16)

            @block.gpsimd
            def _(pool):
                with pool.Fori(0, BT // R // 2) as i:
                    for j in range(2):
                        pool.wait_ge(done, 2 * i + j - 1) if j else pool.wait_ge(done, 2 * i)
                        pool.tensor_copy(img[j][:, :, :], tn[:, bass.ds(i * 2 * R + j * R, R), :]).then_inc(staged, 1)

            @block.tensor
            def _(pe):
                pe.wait_ge(loaded, 48)
                with pe.Fori(0, BT // R // 2) as i:
                    for j in range(2):
                        pe.wait_ge(staged, 2 * i + j + 1)
                        pe.wait_ge(copied, 2 * i)
                        for r in range(R):
                            last = pe.matmul(ps[j][:, r * KA:(r + 1) * KA], img[j][:, r, :], rows[:, :],
                                             start=True, stop=True)
                        last.then_inc(done, 1)

            @block.scalar
            def _(act):
                with act.Fori(0, BT // R // 2) as i:
                    for j in range(2):
                        act.wait_ge(done, 2 * i + j + 1)
                        act.copy(o1[:, :, bass.ds(i * 2 * R + j * R, R)],
                                 ps[j][:, 0:R * KA].rearrange("p (r k) -> p k r", r=R)).then_inc(copied, 1)

        with ExitStack() as c2:
            s2 = Scope(nc, c2, tag + "b")
            NB = 4
            ps = [s2.ps(f"ps{j}") for j in range(NB)]
            made, read = s2.sem("made"), s2.sem("read")
            PER = 8
            block = c2.enter_context(nc.Block())

            @block.tensor
            def _(pe):
                for n, ky in enumerate(ROWS):
                    at = (n % PER) * 2 * NKX
                    dst = ps[n // PER][:, at:at + 2 * NKX]
                    last = pe.matmul(dst, o1[:, abs(ky), :], tcols[:, 0, :], start=True, stop=(ky == 0))
                    if ky:
                        last = pe.matmul(dst, o1[:, h + abs(ky), :], tcols[:, 1 if ky > 0 else 2, :],
                                         start=False, stop=True)
                    if n % PER == PER - 1:
                        last.then_inc(made, 1)

            @block.scalar
            def _(act):
                for n in range(NB):
                    act.wait_ge(made, n + 1)
                    act.copy(xh[:, n * PER:(n + 1) * PER, :, :],
                             ps[n][:, 0:PER * 2 * NKX].rearrange("p (k a x) -> p k a x", k=PER, a=2)).then_inc(read, 1)

        with ExitStack() as c2:
            s2 = Scope(nc, c2, tag + "c")
            H1 = h + 1
            z = [s2.sb(f"z{j}", [H1, KA, BT]) for j in range(2)]
            p12 = s2.sb("p12", [H1, 2, BT])
            inner = s2.sb("inner", [H1, 1])
            gs = s2.sb("gs", [P, BT])
            ps = [s2.ps(f"ps{j}") for j in range(4)]
            ps_g = s2.ps("ps_g")
            made, read, zready, gdone, gcopied, stored, dch, pch = (
                s2.sem(n) for n in ("made", "read", "zready", "gdone", "gcopied", "stored", "dch", "pch"))
            block = c2.enter_context(nc.Block())
            PER = 4
            parts = [(k, min(PER, KA - k)) for k in range(0, KA, PER)]
            units = [(k, n, a) for k, n in parts for a in range(2)]

            @block.tensor
            def _(pe):
                for u, (k, n, a) in enumerate(units):
                    if u >= 4:
                        pe.wait_ge(read, u - 3)
                    pe.matmul(ps[u % 4][0:H1, 0:n * BT], cols[:, a * H1:(a + 1) * H1],
                              o1[:, k:k + n, :].rearrange("p k n -> p (k n)"),
                              start=True, stop=True).then_inc(made, 1)
                pe.wait_ge(zready, 1)
                first = True
                for k in range(KA):
                    if k == h or k == 2 * h:
                        continue
                    pe.matmul(ps_g[:, 0:BT], z[0][:, k, :], z[0][:, k, :], start=first, stop=False)
                    pe.matmul(ps_g[:, 0:BT], z[1][0:h, k, :], z[1][0:h, k, :], start=False, stop=False)
                    first = False
                pe.matmul(ps_g[:, 0:BT], p12[:, 0, :], p12[:, 0, :], start=False, stop=False)
                pe.matmul(ps_g[:, 0:BT], p12[0:h, 1, :], p12[0:h, 1, :], start=False, stop=True).then_inc(gdone, 1)

            @block.gpsimd
            def _(pool):
                step = Chain(pool, pch)
                step(pool.memset(inner[:, :], 1.0))
                step(pool.affine_select(out=inner[:, :], in_=inner[:, :], compare_op=ALU.not_equal, fill=0.0,
                                        base=0, pattern=[[0, 1]], channel_multiplier=1))

            @block.scalar
            def _(act):
                for u, (k, n, a) in enumerate(units):
                    act.wait_ge(made, u + 1)
                    act.mul(z[a][:, k:k + n, :], ps[u % 4][0:H1, 0:n * BT].rearrange("p (k n) -> p k n", k=n),
                            math.sqrt(2.0)).then_inc(read, 1)
                act.wait_ge(gdone, 1)
                act.copy(gs[:, :], ps_g[:, 0:BT]).then_inc(gcopied, 1)

            @block.vector
            def _(dve):
                step = Chain(dve, dch)
                dve.wait_ge(read, len(units))
                for a in range(2):
                    for k in (0, h, 2 * h):
                        step(dve.tensor_scalar(z[a][:, k, :], z[a][:, k, :], math.sqrt(0.5), None, ALU.mult))
                step(dve.tensor_tensor(p12[:, 0, :], z[0][:, h, :], z[1][:, 2 * h, :], ALU.add))
                step(dve.tensor_tensor(p12[:, 1, :], z[0][:, 2 * h, :], z[1][:, h, :], ALU.subtract))
                dve.wait_ge(pch, 2)
                step(dve.tensor_scalar(p12[:, 1, :], p12[:, 1, :], inner[:, 0:1], None, ALU.mult))
                dve.sem_inc(zready, 1)

            @block.sync
            def _(sp):
                sp.wait_ge(gcopied, 1)
                sp.dma_start(gram_d, gs[:, :]).then_inc(stored, 16)
                sp.wait_ge(stored, 16)


NH = 16


def token_attention(nc, xh, gram_d, tabs, wts, prob_d, pt, mt, tag="l1s"):
    L = LKX - 1
    MA = LKY * L
    MB = LKY // 2 + 1
    low = [n for n in range(NKY) if -LKY // 2 <= ROWS[n] < LKY // 2]
    unit = float(SR * SR) / math.sqrt(SR * SR)
    with ExitStack() as ctx:
        s = Scope(nc, ctx, tag)
        ident = s.sb("ident", [P, P])
        skips = s.sb("skips", [P, 6, NH])
        qa, ka = (s.sb(n, [MA, NH, 2]) for n in ("qa", "ka"))
        qb, kb, qr, kr = (s.sb(n, [MB, NH, 2]) for n in ("qb", "kb", "qr", "kr"))
        da = s.sb("da", [MA, 3, NH])
        db = s.sb("db", [MB, 3, NH])
        two = s.sb("two", [MB, 1])
        sgn = s.sb("sgn", [MB, 1])
        tmp = s.sb("tmp", [P, 4, NH])
        row = s.sb("row", [1, 2, NH])
        xlow = s.sb("xlow", [P, 2, LKY, L])
        xlob = s.sb("xlob", [P, 2, MB])
        xa = s.sb("xa", [MA, 2, BT])
        xb = s.sb("xb", [MB, 2, BT])
        grow = s.sb("grow", [1, B, T, T])
        xrow = s.sb("xrow", [1, BT, T])
        pa = s.sb("pa", [MA, 4, T, T])
        pb = s.sb("pb", [MB, 4, T, T])
        sc = s.sb("sc", [NH, B * T, T])
        mx = s.sb("mx", [NH, B * T])
        pl = s.sb("pl", [P, NH, BT])
        coef = s.sb("coef", [P, NH])
        mtt = s.sb("mtt", [P, NH, BT])
        ps_t = s.ps("ps_t")
        ps = [s.ps(f"ps{j}") for j in range(2)]
        ps_p = [s.ps(f"ps_p{j}") for j in range(4)]
        (loaded, zeroed, made, turned, x_ready, d_ready, prods, scored, sc_ready, e_ready, p_ready, p_out,
         p_in, flipped, pt_ready, dch, pch, low_ready) = (
            s.sem(n) for n in ("loaded", "zeroed", "made", "turned", "x_ready", "d_ready", "prods", "scored",
                               "sc_ready", "e_ready", "p_ready", "p_out", "p_in", "flipped", "pt_ready", "dch",
                               "pch", "low_ready"))
        LOADS = 6 + 2 * (LKY + 2) + 2 * (LKY // 2) + 1
        block = ctx.enter_context(nc.Block())

        @block.sync
        def _(sp):
            n = 0
            names = ("query_skip_w", "key_skip_w", "value_skip_w", "proj_skip_w", "query_skip_b", "key_skip_b")
            for j, name in enumerate(names):
                src = wts[name]
                flat = src.rearrange("a b -> (a b)") if len(src.shape) == 2 else src
                sp.dma_start(skips[:, j, :], flat.unsqueeze(0).broadcast_to([P, NH])).then_inc(loaded, 16)
                n += 1
            sp.wait_ge(zeroed, 1)
            for w, ta, tb, tr in (("query_w", qa, qb, qr), ("key_w", ka, kb, kr)):
                src = wts[w][0].rearrange("h y x a -> y x h a")
                for y in range(LKY):
                    sp.dma_start(ta[y * L:(y + 1) * L, :, :], src[y, 1:LKX]).then_inc(loaded, 16)
                    n += 1
                sp.dma_start(tb[0:LKY // 2, :, :], src[0:LKY // 2, 0]).then_inc(loaded, 16)
                sp.dma_start(tr[0:1, :, :], src[0:1, 0]).then_inc(loaded, 16)
                n += 2
                for y in range(1, MB):
                    sp.dma_start(tr[y:y + 1, :, :], src[LKY - y:LKY - y + 1, 0]).then_inc(loaded, 16)
                    n += 1
            for b in range(B):
                sp.dma_start(grow[:, b, :, :], gram_d[b * T:(b + 1) * T, b * T:(b + 1) * T].unsqueeze(0)
                             ).then_inc(made, 16)
            assert n == LOADS - 1, n
            sp.wait_ge(p_ready, 1)
            sp.dma_start(prob_d.rearrange("h b t s -> h (b t) s"), sc[:, :, :]).then_inc(p_out, 16)
            sp.wait_ge(p_out, 16)
            for b in range(B):
                sp.dma_start(pl[b * T:(b + 1) * T, :, b * T:(b + 1) * T],
                             prob_d[:, b].rearrange("h t s -> t h s")).then_inc(p_in, 16)
            sp.wait_ge(p_in, 16 * B)

        @block.gpsimd
        def _(pool):
            step = Chain(pool, pch)
            for t in (qb, kb, qr, kr):
                step(pool.memset(t[:, :, :], 0.0))
            pool.sem_inc(zeroed, 1)
            fill_identity(pool, step, ident)
            step(pool.memset(pl[:, :, :], 0.0))
            step(pool.memset(two[:, :], 2.0 * unit))
            step(pool.affine_select(out=two[:, :], in_=two[:, :], compare_op=ALU.not_equal, fill=unit,
                                    base=0, pattern=[[0, 1]], channel_multiplier=1))

        @block.tensor
        def _(pe):
            pe.wait_ge(pch, 6)
            pe.wait_ge(low_ready, 1)
            for a in range(2):
                pe.transpose(ps_t[0:MA, a * BT:(a + 1) * BT], xlow[:, a, :, :].rearrange("p y x -> p (y x)"), ident[:, :])
                pe.transpose(ps_t[0:MB, (2 + a) * BT:(3 + a) * BT], xlob[:, a, :], ident[:, :]).then_inc(turned, 1)
            pe.wait_ge(d_ready, 1)
            pe.wait_ge(made, 16 * B)
            NS = T // 2
            for b in range(B):
                pe.wait_ge(prods, b + 1)
                if b:
                    pe.wait_ge(sc_ready, 2 * b)
                for g in range(2):
                    rows = slice(g * NS, (g + 1) * NS)
                    dst = ps[g][0:NH, :]
                    for n, (d, j) in enumerate(((0, 0), (0, 1), (2, 2), (1, 3))):
                        pe.matmul(dst, da[:, d, :], pa[:, j, rows, :].rearrange("p t s -> p (t s)"),
                                  start=(n == 0), stop=False)
                        pe.matmul(dst, db[:, d, :], pb[:, j, rows, :].rearrange("p t s -> p (t s)"),
                                  start=False, stop=False)
                    pe.matmul(dst, row[:, 0, :], grow[:, b, rows, :].rearrange("p t s -> p (t s)"),
                              start=False, stop=False)
                    pe.matmul(dst, row[:, 1, :], xrow[:, b * T + g * NS:b * T + (g + 1) * NS, :].rearrange("p t s -> p (t s)"),
                              start=False, stop=True).then_inc(scored, 1)
            pe.wait_ge(p_in, 16 * B)
            for h in range(NH):
                last = pe.transpose(ps_p[h // 4][:, (h % 4) * BT:(h % 4 + 1) * BT], pl[:, h, :], ident[:, :])
            last.then_inc(flipped, 1)

        @block.scalar
        def _(act):
            for k in range(2 * B):
                b, g = divmod(k, 2)
                act.wait_ge(scored, k + 1)
                act.copy(sc[:, b * T + g * (T // 2):b * T + (g + 1) * (T // 2), :],
                         ps[g][0:NH, :].rearrange("p (t s) -> p t s", s=T)).then_inc(sc_ready, 1)
            act.wait_ge(e_ready, 1)
            act.activation(sc[:, :, :], sc[:, :, :], ACT.Exp).then_inc(e_ready, 1)
            act.wait_ge(flipped, 1)
            for j in range(4):
                act.copy(pt[:, 4 * j:4 * j + 4, :], ps_p[j][:, :].rearrange("p (h t) -> p h t", h=4)).then_inc(pt_ready, 1)

        @block.vector
        def _(dve):
            step = Chain(dve, dch)
            n0 = LKY // 2
            for a in range(2):
                for j, n in ((0, 0), (1, NKY - n0)):
                    step.mark(dve.tensor_copy(xlow[:, a, j * n0:(j + 1) * n0, :], xh[:, n:n + n0, a, 1:LKX]))
                step.mark(dve.tensor_copy(xlob[:, a, :], xh[:, 0:MB, a, 0]))
            step.join()
            dve.sem_inc(low_ready, 1)
            dve.wait_ge(loaded, 16 * (LOADS - 1))
            dve.wait_ge(pch, 9)
            TT, STT = dve.tensor_tensor, dve.scalar_tensor_tensor
            for t, r in ((qb, qr), (kb, kr)):
                step(TT(t[:, :, 0], t[:, :, 0], r[:, :, 0], ALU.add))
                step(TT(t[:, :, 1], t[:, :, 1], r[:, :, 1], ALU.subtract))
                step(dve.tensor_scalar(t[:, :, :], t[:, :, :], 0.5, None, ALU.mult))
            for q, k, d, m in ((qa, ka, da, MA), (qb, kb, db, MB)):
                wq, wk = skips[0:m, 0, :], skips[0:m, 1, :]
                a, c = tmp[0:m, 0, :], tmp[0:m, 1, :]
                step(TT(a, wq, q[:, :, 0], ALU.add))
                step(TT(d[:, 0, :], a, k[:, :, 0], ALU.mult))
                step(TT(c, q[:, :, 1], k[:, :, 1], ALU.mult))
                step(TT(d[:, 0, :], d[:, 0, :], c, ALU.add))
                step(TT(c, wk, q[:, :, 0], ALU.mult))
                step(TT(d[:, 0, :], d[:, 0, :], c, ALU.add))
                step(TT(a, a, k[:, :, 1], ALU.mult))
                step(TT(c, wk, k[:, :, 0], ALU.add))
                step(TT(c, c, q[:, :, 1], ALU.mult))
                step(TT(d[:, 1, :], c, a, ALU.subtract))
                scale = 2.0 * unit if d is da else two[:, 0:1]
                step(dve.tensor_scalar(d[:, 0:2, :], d[:, 0:2, :], scale, None, ALU.mult))
                step(dve.tensor_scalar(d[:, 2, :], d[:, 1, :], -1.0, None, ALU.mult))
            step(TT(row[:, 0, :], skips[0:1, 0, :], skips[0:1, 1, :], ALU.mult))
            step(TT(row[:, 1, :], skips[0:1, 1, :], kb[0:1, :, 0], ALU.add))
            step(TT(row[:, 1, :], row[:, 1, :], skips[0:1, 4, :], ALU.mult))
            step(dve.tensor_scalar(row[:, :, :], row[:, :, :], unit, None, ALU.mult))
            dve.wait_ge(turned, 2)
            step(dve.tensor_copy(xa[:, :, :], ps_t[0:MA, 0:2 * BT].rearrange("p (a n) -> p a n", a=2)))
            step(dve.tensor_copy(xb[:, :, :], ps_t[0:MB, 2 * BT:4 * BT].rearrange("p (a n) -> p a n", a=2)))
            for b in range(B):
                step(dve.tensor_copy(xrow[:, b * T:(b + 1) * T, :],
                                     xb[0:1, 0, b * T:(b + 1) * T].unsqueeze(1).broadcast_to([1, T, T])))
            dve.sem_inc(d_ready, 1)
            for b in range(B):
                if b:
                    dve.wait_ge(scored, 2 * b)
                for x, p, m in ((xa, pa, MA), (xb, pb, MB)):
                    xt = [x[:, a, b * T:(b + 1) * T].unsqueeze(2).broadcast_to([m, T, T]) for a in range(2)]
                    xs = [x[:, a, b * T:(b + 1) * T].unsqueeze(1).broadcast_to([m, T, T]) for a in range(2)]
                    for j, (u, v) in enumerate(((0, 0), (1, 1), (1, 0), (0, 1))):
                        step.mark(TT(p[:, j, :, :], xt[u], xs[v], ALU.mult))
                step.join()
                dve.sem_inc(prods, 1)
            dve.wait_ge(sc_ready, 2 * B)
            step(dve.tensor_reduce(mx[:, :], sc[:, :, :], AX.X, ALU.max))
            step(TT(sc[:, :, :], sc[:, :, :], mx[:, :].unsqueeze(2).broadcast_to([NH, B * T, T]), ALU.subtract))
            dve.sem_inc(e_ready, 1)
            dve.wait_ge(e_ready, 2)
            step(dve.tensor_reduce(mx[:, :], sc[:, :, :], AX.X, ALU.add))
            step(dve.reciprocal(mx[:, :], mx[:, :]))
            step(TT(sc[:, :, :], sc[:, :, :], mx[:, :].unsqueeze(2).broadcast_to([NH, B * T, T]), ALU.mult))
            dve.sem_inc(p_ready, 1)
            step(TT(coef[:, :], skips[:, 2, :], skips[:, 3, :], ALU.mult))
            dve.wait_ge(pt_ready, 4)
            step(TT(mtt[:, :, :], pt[:, :, :], coef[:, :].unsqueeze(2).broadcast_to([P, NH, BT]), ALU.mult))
            step(dve.tensor_reduce(mt[:, :], mtt[:, :, :].rearrange("p h t -> p t h"), AX.X, ALU.add))


def attended_spectrum(nc, xh, pt, wts, wd, spec, const, tag="l1y"):
    K2 = 2 * NKX
    HF = LKY // 2
    with ExitStack() as ctx:
        s = Scope(nc, ctx, tag)
        ident = s.sb("ident", [P, P])
        sv = s.sb("sv", [NKY, NH, LKX, 2])
        rv = s.sb("rv", [NKY, NH, 2])
        pw = s.sb("pw", [NKY, NH, NKX, 2])
        sk = s.sb("sk", [P, 3, NH])
        pb0 = s.sb("pb0", [P, 1])
        p00 = s.sb("p00", [P, NH])
        a, c, d = (s.sb(n, [NKY, NH, NKX]) for n in ("a", "c", "d"))
        w = s.sb("w", [NKY, NH, 2, NKX])
        ccon = s.sb("ccon", [P, 2, NH])
        wh = [s.sb(f"wh{j}", [P, NKY, 2, NKX]) for j in range(2)]
        xw = [s.sb(f"xw{j}", [P, NKY, 2, NKX]) for j in range(2)]
        t1, t2 = (s.sb(n, [P, NKY, 2, NKX]) for n in ("t1", "t2"))
        yp = s.sb("yp", [P, NKY, 2, 32])
        ps = [s.ps(f"ps{j}") for j in range(3)]
        ps_t = [s.ps(f"ps_t{j}") for j in range(4)]
        (zeroed, loaded, w_ready, w_out, w_in, xw_ready, mixed, yp_ready, turned, copied, dch, pch, made) = (
            s.sem(n) for n in ("zeroed", "loaded", "w_ready", "w_out", "w_in", "xw_ready", "mixed",
                               "yp_ready", "turned", "copied", "dch", "pch", "made"))
        block = ctx.enter_context(nc.Block())
        NL = 1 + 2 + (1 + LKY) + 3 + 2

        @block.sync
        def _(sp):
            n = 0
            sp.wait_ge(zeroed, 1)
            src = wts["value_w"][0].rearrange("h y x a -> y h x a")
            vrow = lambda k: k % LKY
            sp.dma_start(pw[:, :, :, :], wts["proj_w"][:, 0].rearrange("h y x a -> y h x a")).then_inc(loaded, 16)
            sp.dma_start(sv[0:HF, :, :, :], src[0:HF]).then_inc(loaded, 16)
            sp.dma_start(sv[NKY - HF:NKY, :, :, :], src[HF:LKY]).then_inc(loaded, 16)
            n += 3
            for k in range(-HF + 1, HF + 1):
                at = k % NKY
                sp.dma_start(rv[at:at + 1, :, :], src[vrow(-k):vrow(-k) + 1, :, 0, :]).then_inc(loaded, 16)
                n += 1
            for j, name in enumerate(("value_skip_w", "proj_skip_w", "value_skip_b")):
                v = wts[name]
                flat = v.rearrange("a b -> (a b)") if len(v.shape) == 2 else v
                sp.dma_start(sk[:, j, :], flat.unsqueeze(0).broadcast_to([P, NH])).then_inc(loaded, 16)
                n += 1
            sp.dma_start(p00[:, :], wts["proj_w"][:, 0, 0, 0, 0].unsqueeze(0).broadcast_to([P, NH]),
                         allow_slow_non_contiguous=True).then_inc(loaded, 16)
            sp.dma_start(pb0[:, :], wts["proj_skip_b"].unsqueeze(0).broadcast_to([P, 1])).then_inc(loaded, 16)
            n += 2
            assert n == NL - 1, n
            sp.wait_ge(w_ready, 1)
            sp.dma_start(wd.rearrange("h y a x -> y h a x"), w[:, :, :, :]).then_inc(w_out, 16)
            sp.wait_ge(w_out, 16)
            for h in range(NH):
                if h >= 2:
                    sp.wait_ge(xw_ready, h - 1)
                sp.dma_start(wh[h % 2][:, :, :, :], wd[h].unsqueeze(0).broadcast_to([P, NKY, 2, NKX])).then_inc(w_in, 16)
                sp.wait_ge(w_in, 16 * h + 16)

        @block.gpsimd
        def _(pool):
            step = Chain(pool, pch)
            step(pool.memset(sv[:, :, :, :], 0.0))
            step(pool.memset(rv[:, :, :], 0.0))
            pool.sem_inc(zeroed, 1)
            fill_identity(pool, step, ident)
            step(pool.memset(yp[:, :, :, :], 0.0))
            pool.sem_inc(made, 1)

        @block.vector
        def _(dve):
            step = Chain(dve, dch)
            TT = dve.tensor_tensor
            dve.wait_ge(loaded, 16 * (NL - 1))
            dve.wait_ge(made, 1)
            step(TT(sv[:, :, 0, 0], sv[:, :, 0, 0], rv[:, :, 0], ALU.add))
            step(TT(sv[:, :, 0, 1], sv[:, :, 0, 1], rv[:, :, 1], ALU.subtract))
            step(dve.tensor_scalar(sv[:, :, 0, :], sv[:, :, 0, :], 0.5, None, ALU.mult))
            vs = sk[0:NKY, 0, :].unsqueeze(2)
            ps_ = sk[0:NKY, 1, :].unsqueeze(2)
            full, lowx = [NKY, NH, NKX], [NKY, NH, LKX]
            pr, pi = pw[:, :, :, 0], pw[:, :, :, 1]
            step(TT(w[:, :, 0, :], pr, vs.broadcast_to(full), ALU.mult))
            step(TT(w[:, :, 1, :], pi, vs.broadcast_to(full), ALU.mult))
            A_, C_, D_ = a[:, :, 0:LKX], c[:, :, 0:LKX], d[:, :, 0:LKX]
            vr, vi = sv[:, :, :, 0], sv[:, :, :, 1]
            prl, pil = pw[:, :, 0:LKX, 0], pw[:, :, 0:LKX, 1]
            step(TT(A_, prl, ps_.broadcast_to(lowx), ALU.add))
            for part, (u, v, op) in enumerate(((vr, vi, ALU.subtract), (vi, vr, ALU.add))):
                step(TT(C_, A_, u, ALU.mult))
                step(TT(D_, pil, v, ALU.mult))
                step(TT(C_, C_, D_, op))
                step(TT(w[:, :, part, 0:LKX], w[:, :, part, 0:LKX], C_, ALU.add))
            dve.sem_inc(w_ready, 1)
            step(TT(ccon[:, 0, :], p00[:, :], sk[:, 1, :], ALU.add))
            step(TT(ccon[:, 1, :], ccon[:, 0, :], sk[:, 2, :], ALU.mult))
            step(dve.tensor_reduce(const[:, 0:1], ccon[:, 1, :], AX.X, ALU.add))
            step(TT(const[:, 0:1], const[:, 0:1], pb0[:, :], ALU.add))
            for h in range(NH):
                W_ = wh[h % 2]
                dve.wait_ge(w_in, 16 * h + 16)
                if h >= 2:
                    dve.wait_ge(mixed, h - 1)
                both = [P, NKY, 2, NKX]
                step.mark(TT(t1[:, :, :, :], xh[:, :, :, :], W_[:, :, 0:1, :].broadcast_to(both), ALU.mult))
                step(TT(t2[:, :, :, :], xh[:, :, :, :], W_[:, :, 1:2, :].broadcast_to(both), ALU.mult))
                step.mark(TT(xw[h % 2][:, :, 0, :], t1[:, :, 0, :], t2[:, :, 1, :], ALU.subtract))
                step(TT(xw[h % 2][:, :, 1, :], t1[:, :, 1, :], t2[:, :, 0, :], ALU.add))
                dve.sem_inc(xw_ready, 1)
            dve.wait_ge(mixed, NH)
            n = 15
            for j in range(3):
                k0, k1 = n * j, min(n * j + n, NKY)
                step.mark(dve.tensor_copy(yp[:, k0:k1, :, 0:NKX],
                                          ps[j][:, 0:(k1 - k0) * K2].rearrange("p (k a x) -> p k a x", a=2, x=NKX)))
            step.join()
            dve.sem_inc(yp_ready, 1)
            for j in range(NKY // 4):
                dve.wait_ge(turned, j + 1)
                step(dve.tensor_copy(spec[:, :, 4 * j:4 * j + 4],
                                     ps_t[j % 4][0:2 * 32, :].rearrange("p (k t) -> p t k", k=4)))
                dve.sem_inc(copied, 1)

        @block.tensor
        def _(pe):
            pe.wait_ge(made, 1)
            n = 15
            for h in range(NH):
                pe.wait_ge(xw_ready, h + 1)
                for j in range(3):
                    k0, k1 = n * j, min(n * j + n, NKY)
                    last = pe.matmul(ps[j][:, 0:(k1 - k0) * K2], pt[:, h, :],
                                     xw[h % 2][:, k0:k1, :, :].rearrange("p k a x -> p (k a x)"),
                                     start=(h == 0), stop=(h == NH - 1))
                last.then_inc(mixed, 1)
            pe.wait_ge(yp_ready, 1)
            for j in range(NKY // 4):
                if j >= 4:
                    pe.wait_ge(copied, j - 3)
                for k in range(4):
                    last = pe.transpose(ps_t[j % 4][0:64, k * BT:(k + 1) * BT],
                                        yp[:, 4 * j + k, :, :].rearrange("p a x -> p (a x)"), ident[:, :])
                last.then_inc(turned, 1)


def mixed_images(nc, tnd, mt, u, tag="l1m"):
    N = 512
    CH = 4
    with ExitStack() as ctx:
        s = Scope(nc, ctx, tag)
        src = [s.sb(f"src{j}", [P, CH * N]) for j in range(2)]
        dst = [s.sb(f"dst{j}", [P, CH * N]) for j in range(2)]
        ps = [s.ps(f"ps{j}") for j in range(2 * CH)]
        mixed, stored, copied = (s.sem(n) for n in ("mixed", "stored", "copied"))
        loaded = [s.sem(f"loaded{j}") for j in range(2)]
        flat_in = tnd.rearrange("n r c -> n (r c)").rearrange("n (i j k) -> i j n k", j=2, k=CH * N)
        flat_out = u.rearrange("n r c -> n (r c)").rearrange("n (i j k) -> i j n k", j=2, k=CH * N)
        TURNS = IMG // (CH * N)
        block = ctx.enter_context(nc.Block())

        @block.sync
        def _(sp):
            with sp.Fori(0, TURNS // 2) as i:
                for j in range(2):
                    sp.wait_ge(mixed, 2 * i)
                    sp.dma_start(src[j][:, :], flat_in[i, j]).then_inc(loaded[j], 16)

        @block.tensor
        def _(pe):
            with pe.Fori(0, TURNS // 2) as i:
                for j in range(2):
                    pe.wait_ge(loaded[j], 16 * i + 16)
                    pe.wait_ge(copied, 2 * i)
                    for k in range(CH):
                        last = pe.matmul(ps[j * CH + k][:, :], mt[:, :], src[j][:, k * N:(k + 1) * N],
                                         start=True, stop=True)
                    last.then_inc(mixed, 1)

        @block.vector
        def _(dve):
            with dve.Fori(0, TURNS // 2) as i:
                for j in range(2):
                    dve.wait_ge(mixed, 2 * i + j + 1)
                    dve.wait_ge(stored, 32 * i)
                    for k in range(CH):
                        last = dve.tensor_copy(dst[j][:, k * N:(k + 1) * N], ps[j * CH + k][:, :])
                    last.then_inc(copied, 1)

        @block.scalar
        def _(act):
            with act.Fori(0, TURNS // 2) as i:
                for j in range(2):
                    act.wait_ge(copied, 2 * i + j + 1)
                    act.dma_start(flat_out[i, j], dst[j][:, :]).then_inc(stored, 16)
            act.wait_ge(stored, 16 * TURNS)


def token_mixer(nc, spec, const, u, tok, x1, wts, tabs, x2, tag="l1t", eps=1e-5):
    R = 4
    STREAMS = 2
    TURNS = BT // (R * STREAMS)
    NF = R * NKY
    with ExitStack() as ctx:
        s = Scope(nc, ctx, tag)
        rows_fwd = s.sb("rows_fwd", [P, 2 * NKY])
        cols_fwd = s.sb("cols_fwd", [P, 2, P])
        cols_inv = s.sb("cols_inv", [P, 2 * C])
        rows_inv = s.sb("rows_inv", [NKY, 2, P])
        names = ["attn_norm_g", "attn_norm_b", "norm2_g", "norm2_b", "mixer_norm_g1", "mixer_norm_b1",
                 "mixer_norm_g2", "mixer_norm_b2", "mixer_out_g", "mixer_out_b", "mixer_skip_w1",
                 "mixer_skip_b1", "mixer_skip_w2", "mixer_skip_b2"]
        par = s.sb("par", [P, len(names)])
        col = {n: par[:, j:j + 1] for j, n in enumerate(names)}
        wl = [s.sb(f"wl{j}", [P, NKY, 2]) for j in range(2)]
        mw = [s.sb(f"mw{j}", [P, NKY]) for j in range(2)]
        ones = s.sb("ones", [P, P])
        half = s.sb("half", [P, R])

        def per_stream(name, shape):
            return [s.sb(f"{name}{x}", shape) for x in range(STREAMS)]

        sg = per_stream("sg", [64, R, NKY])
        ut, tk, xx, a, xf, attn, m, m1, f, sq, out = (
            per_stream(n, [P, R, C]) for n in ("ut", "tk", "xx", "a", "xf", "attn", "m", "m1", "f", "sq", "out"))
        iv = per_stream("iv", [NKY, 2, R, C])
        o = per_stream("o", [P, 2, R, NKY])
        t = per_stream("t", [P, R, NKY])
        sums = per_stream("sums", [P, 2 * R])
        mean, var, rstd, scale, bias, v2 = (
            per_stream(n, [P, R]) for n in ("mean", "var", "rstd", "scale", "bias", "v2"))
        ps_i = [[s.ps(f"ps_i{x}{j}") for j in range(2)] for x in range(STREAMS)]
        ps_a = [s.ps(f"ps_a{x}") for x in range(STREAMS)]
        ps_m = [s.ps(f"ps_m{x}") for x in range(STREAMS)]
        F0, G0, S0 = 0, R * 64, R * 64 + NF

        def per_stream_sem(name):
            return [s.sem(f"{name}{x}") for x in range(STREAMS)]

        loaded, made, zeroed, prepared, stick, dtick, petick, dch = (s.sem(n) for n in (
            "loaded", "made", "zeroed", "prepared", "stick", "dtick", "petick", "dch"))
        INV, FWD, SUMS, NORMS = 3, 2, 4, 5
        (xin, staged, inv1, iv_ready, inv2, img_ready, fwd1, o_ready, fwd2, t_ready, have, squared, summed,
         totals, var_ready, rstd_ready, xf_ready, pre, stored, out_ready) = (
            per_stream_sem(n) for n in (
                "xin", "staged", "inv1_", "iv_ready", "inv2_", "img_ready", "fwd1_", "o_ready", "fwd2_",
                "t_ready", "have", "squared", "summed", "totals", "var_ready", "rstd_ready", "xf_ready",
                "pre", "stored", "out_ready"))
        block = ctx.enter_context(nc.Block())
        NL = 6 + len(names) + 4

        def view(v):
            return v.rearrange("(i x r) w c -> x i w r c", r=R, x=STREAMS)

        x1v = x1.rearrange("b t w c -> (b t) w c")
        x2v = x2.rearrange("b t w c -> (b t) w c")
        uv, tv, xv, ov = view(u), view(tok), view(x1v), view(x2v)

        @block.sync
        def _(sp):
            sp.wait_ge(zeroed, 1)
            sp.dma_start(rows_fwd[:, :], tabs["rows_fwd"]).then_inc(loaded, 16)
            sp.dma_start(rows_inv[:, :, :].rearrange("p a k -> p (a k)"), tabs["rows_inv"]).then_inc(loaded, 16)
            fwd = tabs["cols_fwd"].rearrange("c (a k) -> c a k", a=2)
            for q in range(2):
                sp.dma_start(cols_fwd[:, :, 64 * q:64 * q + 64], fwd).then_inc(loaded, 16)
                sp.dma_start(cols_inv[64 * q:64 * q + 64, :], tabs["cols_inv"][:, q * 2 * C:(q + 1) * 2 * C]
                             ).then_inc(loaded, 16)
            for n in names:
                v = wts[n]
                flat = v.rearrange("a b -> (a b)") if len(v.shape) == 2 else v
                sp.dma_start(col[n], flat.unsqueeze(0).broadcast_to([P, 1])).then_inc(loaded, 16)
            for j in range(2):
                src = wts[f"mixer_w{j + 1}"][0, 0].rearrange("y x a -> x y a")
                for q in range(2):
                    sp.dma_start(wl[j][32 * q:32 * q + NKX, :, :], src).then_inc(loaded, 16)
                    sp.dma_start(wl[j][64 + 32 * q:64 + 32 * q + NKX, :, :], src).then_inc(zeroed, 16)

            def load(i, x):
                sp.dma_start(ut[x][:, :, :], uv[x, i]).then_inc(xin[x], 16)
                sp.dma_start(tk[x][:, :, :], tv[x, i]).then_inc(xin[x], 16)
                sp.dma_start(xx[x][:, :, :], xv[x, i]).then_inc(xin[x], 16)

            for x in range(STREAMS):
                load(0, x)
            with sp.Fori(0, TURNS - 1) as i:
                for x in range(STREAMS):
                    sp.wait_ge(out_ready[x], i + 1)
                    sp.sem_inc(stick, 1)
                    sp.dma_start(ov[x, i], out[x][:, :, :]).then_inc(stored[x], 16)
                    load(i + 1, x)
            for x in range(STREAMS):
                sp.wait_ge(out_ready[x], TURNS)
                sp.dma_start(ov[x, TURNS - 1], out[x][:, :, :]).then_inc(stored[x], 16)
            for x in range(STREAMS):
                sp.wait_ge(stored[x], 16 * TURNS + 1)

        @block.gpsimd
        def _(pool):
            for j in range(2):
                pool.memset(wl[j][:, :, :], 0.0).then_inc(made, 1)
            pool.wait_ge(made, 2)
            pool.sem_inc(zeroed, 1)
            pool.memset(ones[:, :], 1.0 / IMG).then_inc(made, 1)
            pool.memset(half[:, :], -0.5).then_inc(made, 1)
            pool.wait_ge(made, 4)

            def stage(i, x):
                pool.tensor_copy(sg[x][:, :, :], spec[:, bass.ds((i * STREAMS + x) * R, R), :]).then_inc(staged[x], 1)

            def norms(i):
                for j in range(NORMS):
                    for x in range(STREAMS):
                        pool.wait_ge(var_ready[x], NORMS * i + j + 1)
                        pool.tensor_tensor(rstd[x][:, :], var[x][:, :], half[:, :], ALU.pow).then_inc(rstd_ready[x], 1)

            for x in range(STREAMS):
                stage(0, x)
            with pool.Fori(0, TURNS - 1) as i:
                norms(i)
                for x in range(STREAMS):
                    stage(i + 1, x)
            norms(TURNS - 1)

        @block.tensor
        def _(pe):
            pe.wait_ge(loaded, 16 * NL)
            pe.wait_ge(made, 4)
            pe.wait_ge(prepared, 1)

            def inverse_cols(i, x, src, K):
                for r in range(R):
                    dst = ps_i[x][r // 2][0:NKY, (r % 2) * 2 * C:(r % 2 + 1) * 2 * C]
                    last = pe.matmul(dst, src[:, r, :], cols_inv[0:K, :], start=True, stop=True)
                last.then_inc(inv1[x], 1)

            def inverse_rows(n, i, x):
                pe.wait_ge(iv_ready[x], INV * i + n + 1)
                for k in range(2):
                    last = pe.matmul(ps_a[x][:, :], rows_inv[:, k, :], iv[x][:, k, :, :].rearrange("p r c -> p (r c)"),
                                     start=(k == 0), stop=(k == 1))
                last.then_inc(inv2[x], 1)

            def forward_rows(n, i, x, src):
                pe.wait_ge(img_ready[x], FWD * i + n + 1)
                for r in range(R):
                    last = pe.matmul(ps_m[x][:, F0 + r * 64:F0 + (r + 1) * 64], src[:, r, :], rows_fwd[:, :],
                                     start=True, stop=True)
                last.then_inc(fwd1[x], 1)

            def forward_cols(n, i, x):
                pe.wait_ge(o_ready[x], FWD * i + n + 1)
                for k in range(2):
                    last = pe.matmul(ps_m[x][:, G0:G0 + NF], cols_fwd[:, k, :],
                                     o[x][:, k, :, :].rearrange("p r k -> p (r k)"), start=(k == 0), stop=(k == 1))
                last.then_inc(fwd2[x], 1)

            def total(n, i, x):
                pe.wait_ge(summed[x], SUMS * i + n + 1)
                pe.matmul(ps_m[x][:, S0:S0 + 2 * R], ones[:, :], sums[x][:, :], start=True, stop=True
                          ).then_inc(totals[x], 1)

            both = range(STREAMS)
            with pe.Fori(0, TURNS) as i:
                for x in both:
                    pe.wait_ge(staged[x], i + 1)
                    pe.sem_inc(petick, 1)
                    inverse_cols(i, x, sg[x], 64)
                for x in both:
                    inverse_rows(0, i, x)
                for x in both:
                    total(0, i, x)
                for n in range(2):
                    for x in both:
                        forward_rows(n, i, x, (m, m1)[n][x])
                    for x in both:
                        forward_cols(n, i, x)
                    for x in both:
                        pe.wait_ge(t_ready[x], FWD * i + n + 1)
                        inverse_cols(i, x, t[x], P)
                    for x in both:
                        inverse_rows(n + 1, i, x)
                    for x in both:
                        total(n + 1, i, x)
                for x in both:
                    total(3, i, x)

        @block.scalar
        def _(act):
            def copy_iv(n, i, x):
                act.wait_ge(inv1[x], INV * i + n + 1)
                for q in range(2):
                    last = act.copy(iv[x][:, :, 2 * q:2 * q + 2, :],
                                    ps_i[x][q][0:NKY, :].rearrange("p (r a c) -> p a r c", r=2, a=2))
                last.then_inc(iv_ready[x], 1)

            def square(n, i, x, src):
                act.wait_ge(have[x], 2 * i + n + 1)
                act.activation(sq[x][:, :, :], src[:, :, :], ACT.Square).then_inc(squared[x], 1)

            def copy_o(n, i, x):
                act.wait_ge(fwd1[x], FWD * i + n + 1)
                act.copy(o[x][:, :, :, :], ps_m[x][:, F0:F0 + R * 64].rearrange("p (r a k) -> p a r k", r=R, a=2)
                         ).then_inc(o_ready[x], 1)

            def image(n, i, x):
                act.wait_ge(inv2[x], INV * i + n + 1)
                pa = ps_a[x][:, :].rearrange("p (r c) -> p r c", r=R)
                act.copy(xf[x][:, :, :], pa).then_inc(xf_ready[x], 1)
                act.activation(sq[x][:, :, :], pa, ACT.Square).then_inc(squared[x], 1)

            both = range(STREAMS)
            act.wait_ge(loaded, 16 * NL)
            with act.Fori(0, TURNS) as i:
                for x in both:
                    copy_iv(0, i, x)
                for x in both:
                    square(0, i, x, a[x])
                for x in both:
                    copy_o(0, i, x)
                for x in both:
                    copy_iv(1, i, x)
                for x in both:
                    image(1, i, x)
                for x in both:
                    act.wait_ge(pre[x], i + 1)
                    act.activation(m1[x][:, :, :], f[x][:, :, :], ACT.Gelu, bias=col["mixer_skip_b1"]
                                   ).then_inc(img_ready[x], 1)
                for x in both:
                    copy_o(1, i, x)
                for x in both:
                    copy_iv(2, i, x)
                for x in both:
                    image(2, i, x)
                for x in both:
                    square(1, i, x, f[x])

        @block.vector
        def _(dve):
            step = Chain(dve, dch)
            TT, TS, STT = dve.tensor_tensor, dve.tensor_scalar, dve.scalar_tensor_tensor
            dve.wait_ge(loaded, 16 * NL)
            dve.wait_ge(zeroed, 1 + 16 * 4)
            for j in range(2):
                step(dve.tensor_copy(mw[j][0:64, :], wl[j][0:64, :, 0]))
                step(dve.tensor_copy(mw[j][64:P, :], wl[j][64:P, :, 1]))
            dve.sem_inc(prepared, 1)
            for x in range(STREAMS):
                dve.sem_inc(stored[x], 1)

            def affine(n, i, x, g, b, extra=None):
                dve.wait_ge(rstd_ready[x], NORMS * i + n + 1)
                step(TS(scale[x][:, :], rstd[x][:, :], col[g], None, ALU.mult))
                step(TT(bias[x][:, :], mean[x][:, :], scale[x][:, :], ALU.mult))
                step(TS(bias[x][:, :], bias[x][:, :], -1.0, col[b], ALU.mult, ALU.add))
                if extra:
                    step(TS(bias[x][:, :], bias[x][:, :], col[extra], None, ALU.add))

            def sum_up(n, i, x, src):
                step.mark(dve.tensor_reduce(sums[x][:, 0:R], src[:, :, :], AX.X, ALU.add))
                dve.wait_ge(squared[x], SUMS * i + n + 1)
                step(dve.tensor_reduce(sums[x][:, R:2 * R], sq[x][:, :, :], AX.X, ALU.add))
                dve.sem_inc(summed[x], 1)

            def moments(n, i, x):
                dve.wait_ge(totals[x], SUMS * i + n + 1)
                step(dve.tensor_copy(mean[x][:, :], ps_m[x][:, S0:S0 + R]))
                step(TT(var[x][:, :], mean[x][:, :], mean[x][:, :], ALU.mult))
                step(STT(out=var[x][:, :], in0=ps_m[x][:, S0 + R:S0 + 2 * R], scalar=eps, in1=var[x][:, :],
                         op0=ALU.add, op1=ALU.subtract))
                dve.sem_inc(var_ready[x], 1)

            SUMUP, MOMENTS, AFF = 2, 3, 3

            def apply(x, dst, src):
                for r in range(R):
                    step.mark(TS(dst[:, r, :], src[:, r, :], scale[x][:, r:r + 1], bias[x][:, r:r + 1], ALU.mult, ALU.add))
                step.join()

            def spectral(n, i, x):
                dve.wait_ge(fwd2[x], FWD * i + n + 1)
                step(TT(t[x][:, :, :], ps_m[x][:, G0:G0 + NF].rearrange("p (r k) -> p r k", r=R),
                        mw[n][:, :].unsqueeze(1).broadcast_to([P, R, NKY]), ALU.mult))
                dve.sem_inc(t_ready[x], 1)

            both = range(STREAMS)
            per = (2 + SUMUP + MOMENTS + AFF + R) + (4 + AFF + R) + 1 + (SUMUP + MOMENTS + AFF + R + 1) + 1 + (
                SUMUP + MOMENTS + AFF + 1 + R + 1) + (SUMUP + MOMENTS + AFF + R + 2)
            with step.loop(TURNS, STREAMS * per) as i:
                for x in both:
                    dve.wait_ge(xin[x], 48 * (i + 1))
                    dve.wait_ge(inv2[x], INV * i + 1)
                    pa = ps_a[x][:, :].rearrange("p (r c) -> p r c", r=R)
                    step(STT(out=a[x][:, :, :], in0=pa, scalar=const[:, 0:1], in1=ut[x][:, :, :], op0=ALU.add, op1=ALU.add))
                    step(TT(a[x][:, :, :], a[x][:, :, :], tk[x][:, :, :], ALU.add))
                    dve.sem_inc(have[x], 1)
                for x in both:
                    sum_up(0, i, x, a[x])
                for x in both:
                    moments(0, i, x)
                for x in both:
                    affine(0, i, x, "attn_norm_g", "attn_norm_b")
                    apply(x, attn[x], a[x])
                    step(STT(out=v2[x][:, :], in0=var[x][:, :], scalar=-eps, in1=scale[x][:, :], op0=ALU.add, op1=ALU.mult))
                    step(TT(v2[x][:, :], v2[x][:, :], scale[x][:, :], ALU.mult))
                    step(TS(var[x][:, :], v2[x][:, :], eps, None, ALU.add))
                    step(TS(mean[x][:, :], half[:, :], 0.0, col["attn_norm_b"], ALU.mult, ALU.add))
                    dve.sem_inc(var_ready[x], 1)
                for x in both:
                    affine(1, i, x, "norm2_g", "norm2_b")
                    apply(x, m[x], attn[x])
                    dve.sem_inc(img_ready[x], 1)
                for x in both:
                    spectral(0, i, x)
                for x in both:
                    dve.wait_ge(xf_ready[x], 2 * i + 1)
                    dve.sem_inc(dtick, 1)
                    sum_up(1, i, x, xf[x])
                for x in both:
                    moments(1, i, x)
                for x in both:
                    affine(2, i, x, "mixer_norm_g1", "mixer_norm_b1")
                    apply(x, f[x], xf[x])
                    step(STT(out=f[x][:, :, :], in0=m[x][:, :, :], scalar=col["mixer_skip_w1"], in1=f[x][:, :, :],
                             op0=ALU.mult, op1=ALU.add))
                    dve.sem_inc(pre[x], 1)
                for x in both:
                    spectral(1, i, x)
                for x in both:
                    dve.wait_ge(xf_ready[x], 2 * i + 2)
                    dve.sem_inc(dtick, 1)
                    sum_up(2, i, x, xf[x])
                for x in both:
                    moments(2, i, x)
                for x in both:
                    affine(3, i, x, "mixer_norm_g2", "mixer_norm_b2", "mixer_skip_b2")
                    apply(x, f[x], xf[x])
                    step(STT(out=f[x][:, :, :], in0=m1[x][:, :, :], scalar=col["mixer_skip_w2"], in1=f[x][:, :, :],
                             op0=ALU.mult, op1=ALU.add))
                    dve.sem_inc(have[x], 1)
                for x in both:
                    sum_up(3, i, x, f[x])
                for x in both:
                    moments(3, i, x)
                for x in both:
                    affine(4, i, x, "mixer_out_g", "mixer_out_b")
                    dve.wait_ge(stored[x], 16 * i + 1)
                    apply(x, out[x], f[x])
                    step(TT(out[x][:, :, :], out[x][:, :, :], attn[x][:, :, :], ALU.add))
                    step(TT(out[x][:, :, :], out[x][:, :, :], xx[x][:, :, :], ALU.add))
                    dve.sem_inc(out_ready[x], 1)


def batch_tokens(x, b):
    return x[b].rearrange("t w c -> w t c")


def linear_attention(nc, x2, Wq, bq, Wk, bk, Wv, bv, Wo, bo, x3, tag="lin", eps=1e-5):
    H = 8
    D = C // H
    R = 4
    KT = T // R
    RH = R * H
    with ExitStack() as ctx:
        s = Scope(nc, ctx, tag)
        wq, wk, wv, wo = (s.sb(n, [P, C]) for n in ("wq", "wk", "wv", "wo"))
        bqc = s.sb("bqc", [P, 1])
        bk_row, bo_row, ones1 = (s.sb(n, [1, C]) for n in ("bk_row", "bo_row", "ones1"))
        bv_b = s.sb("bv_b", [P, C])
        ident, ones = s.sb("ident", [P, P]), s.sb("ones", [P, 1])
        heads = s.sb("heads", [P, H, D])
        pick = s.sb("pick", [RH, R, H, D])
        xb = s.sb("xb", [P, T, C])
        u = s.sb("u", [P, T, C])
        uT = s.sb("uT", [P, T * W])
        st = s.sb("st", [P, R, 6])
        mv = [s.sb(f"mv{j}", [P, R, 2]) for j in range(2)]
        ve, rstd, half = (s.sb(n, [P, R]) for n in ("ve", "rstd", "half"))
        rl, ex = ([s.sb(f"{n}{j}", [P, R * C]) for j in range(2)] for n in ("rl", "ex"))
        phi = [s.sb(f"phi{j}", [P, R * C]) for j in range(4)]
        ksum = s.sb("ksum", [P, 1])
        kbh = s.sb("kbh", [P, H])
        uk, kv, kvt, g = (s.sb(n, [P, C]) for n in ("uk", "kv", "kvt", "g"))
        rd = [s.sb(f"rd{j}", [P, RH]) for j in range(2)]
        rT = [s.sb(f"rT{j}", [RH, W]) for j in range(2)]
        phz, out = ([s.sb(f"{n}{j}", [P, R * C]) for j in range(2)] for n in ("phz", "out"))
        ps_t, ps_k, ps_m, ps_x = ([s.ps(f"{n}{j}") for j in range(2)] for n in ("ps_t", "ps_k", "ps_m", "ps_x"))
        ps_q, ps_d, ps_o = ps_t, ps_k, ps_m
        (loaded, made, ve_ready, rstd_ready, u_ready, turned, uT_ready, k_done, k_in, phi_ready, acc_done,
         uk_ready, kv_done, kv_ready, kvt_done, kvt_ready, g_done, g_ready, q_done, q_in, qphi, den_done,
         rd_ready, rd_turned, rT_ready, rd_wide, phz_ready, o_done, out_ready, dch, pch, tick) = (
            s.sem(n) for n in (
                "loaded", "made", "ve_ready", "rstd_ready", "u_ready", "turned", "uT_ready", "k_done", "k_in",
                "phi_ready", "acc_done", "uk_ready", "kv_done", "kv_ready", "kvt_done", "kvt_ready", "g_done",
                "g_ready", "q_done", "q_in", "qphi", "den_done", "rd_ready", "rd_turned", "rT_ready",
                "rd_wide", "phz_ready", "o_done", "out_ready", "dch", "pch", "tick"))
        petick, stick = s.sem("petick"), s.sem("stick")
        xin = [s.sem(f"xin{k}") for k in range(KT)]
        stored = [s.sem(f"stored{j}") for j in range(2)]
        block = ctx.enter_context(nc.Block())
        NL = 8

        def rows(k):
            return slice(k * R, (k + 1) * R)

        @block.sync
        def _(sp):
            for dst, src in ((wq, Wq), (wk, Wk), (wv, Wv), (wo, Wo)):
                sp.dma_start(dst[:, :], src).then_inc(loaded, 16)
            sp.dma_start(bqc[:, :], bq.unsqueeze(1)).then_inc(loaded, 16)
            sp.dma_start(bk_row[:, :], bk.unsqueeze(0)).then_inc(loaded, 16)
            sp.dma_start(bo_row[:, :], bo.unsqueeze(0)).then_inc(loaded, 16)
            sp.dma_start(bv_b[:, :], bv.unsqueeze(0).broadcast_to([P, C])).then_inc(loaded, 16)

            def load(b, k):
                sp.dma_start(xb[:, rows(k), :], x2[b][rows(k)].rearrange("t w c -> w t c")).then_inc(xin[k], 16)

            def batch(b, more):
                for k in range(KT):
                    sp.wait_ge(out_ready, b * KT + k + 1)
                    sp.sem_inc(stick, 1)
                    sp.dma_start(x3[b][rows(k)].rearrange("t w c -> w t c"),
                                 out[k % 2][:, :].rearrange("p (r c) -> p r c", r=R)).then_inc(stored[k % 2], 16)
                    if more:
                        load(b + 1, k)

            for k in range(KT):
                load(0, k)
            with sp.Fori(0, B - 1) as b:
                batch(b, True)
            batch(B - 1, False)
            for j in range(2):
                sp.wait_ge(stored[j], 16 * B * KT // 2 + 1)

        @block.gpsimd
        def _(pool):
            step = Chain(pool, pch)
            fill_identity(pool, step, ident)
            step(pool.memset(ones[:, :], 1.0))
            step(pool.memset(ones1[:, :], 1.0))
            step(pool.memset(half[:, :], -0.5))
            step(pool.memset(heads[:, :, :], 1.0))
            step(pool.affine_select(out=heads[:, :, :], in_=heads[:, :, :], compare_op=ALU.is_ge, fill=0.0,
                                    base=0, pattern=[[-D, H], [0, D]], channel_multiplier=1))
            step(pool.affine_select(out=heads[:, :, :], in_=heads[:, :, :], compare_op=ALU.is_ge, fill=0.0,
                                    base=D - 1, pattern=[[D, H], [0, D]], channel_multiplier=-1))
            step(pool.memset(pick[:, :, :, :], 0.0))
            step(pool.affine_select(out=pick[:, :, :, :], in_=pick[:, :, :, :], compare_op=ALU.not_equal, fill=1.0,
                                    base=0, pattern=[[-H, R], [-1, H], [0, D]], channel_multiplier=1))
            pool.sem_inc(made, 1)
            with pool.Fori(0, B * KT) as n:
                pool.wait_ge(ve_ready, n + 1)
                pool.tensor_tensor(rstd[:, :], ve[:, :], half[:, :], ALU.pow).then_inc(rstd_ready, 1)

        @block.tensor
        def _(pe):
            pe.wait_ge(loaded, 16 * NL)
            pe.wait_ge(made, 1)

            def turn_rows(b, k):
                pe.wait_ge(u_ready, b * KT + k + 1)
                for r in range(R):
                    last = pe.transpose(ps_t[k % 2][:, r * W:(r + 1) * W], u[:, k * R + r, :], ident[:, :])
                last.then_inc(turned, 1)

            def keys(b, k):
                pe.wait_ge(uT_ready, b * KT + k + 1)
                for r in range(R):
                    cols = slice(r * C, (r + 1) * C)
                    pe.matmul(ps_k[k % 2][:, cols], uT[:, (k * R + r) * W:(k * R + r + 1) * W], wk[:, :],
                              start=True, stop=False)
                    last = pe.matmul(ps_k[k % 2][:, cols], ones1[:, :], bk_row[:, :], start=False, stop=True)
                last.then_inc(k_done, 1)

            def accumulate(b, k):
                pe.wait_ge(phi_ready, b * KT + k + 1)
                for r in range(R):
                    first, end = k == 0 and r == 0, k == KT - 1 and r == R - 1
                    ph = phi[k % 4][:, r * C:(r + 1) * C]
                    pe.matmul(ps_m[0][:, 0:C], u[:, k * R + r, :], ph, start=first, stop=end)
                    last = pe.matmul(ps_m[1][:, 0:1], ph, ones[:, :], start=first, stop=end)
                last.then_inc(acc_done, 1)

            def queries(b, k):
                pe.matmul(ps_q[k % 2][:, :], wq[:, :], uT[:, k * R * W:(k + 1) * R * W], start=True, stop=True
                          ).then_inc(q_done, 1)

            def denominators(b, k):
                pe.wait_ge(qphi, b * KT + k + 1)
                for r in range(R):
                    last = pe.matmul(ps_x[k % 2][:, r * H:(r + 1) * H], phi[k % 4][:, r * W:(r + 1) * W], kbh[:, :],
                                     start=True, stop=True)
                last.then_inc(den_done, 1)

            def turn_denominators(b, k):
                pe.wait_ge(rd_ready, b * KT + k + 1)
                pe.transpose(ps_x[k % 2][0:RH, P:2 * P], rd[k % 2][:, :], ident[:, :]).then_inc(rd_turned, 1)

            def widen(b, k):
                pe.wait_ge(rT_ready, b * KT + k + 1)
                pe.sem_inc(petick, 1)
                for r in range(R):
                    last = pe.matmul(ps_d[k % 2][:, r * W:(r + 1) * W], pick[:, r, :, :].rearrange("p h d -> p (h d)"),
                                     rT[k % 2][:, :], start=True, stop=True)
                last.then_inc(rd_wide, 1)

            def project(b, k):
                pe.wait_ge(phz_ready, b * KT + k + 1)
                if k >= 2:
                    pe.wait_ge(out_ready, b * KT + k - 1)
                for r in range(R):
                    cols = slice(r * C, (r + 1) * C)
                    pe.matmul(ps_o[k % 2][:, cols], phz[k % 2][:, r * W:(r + 1) * W], g[:, :], start=True, stop=False)
                    last = pe.matmul(ps_o[k % 2][:, cols], ones1[:, :], bo_row[:, :], start=False, stop=True)
                last.then_inc(o_done, 1)

            def batch(b, again):
                if again:
                    pe.wait_ge(out_ready, b * KT)
                for n in range(KT + 2):
                    if n < KT:
                        turn_rows(b, n)
                    if 0 <= n - 1 < KT:
                        keys(b, n - 1)
                    if 0 <= n - 2:
                        accumulate(b, n - 2)
                pe.wait_ge(uk_ready, b + 1)
                pe.matmul(ps_x[0][:, 0:C], uk[:, :], wv[:, :], start=True, stop=True).then_inc(kv_done, 1)
                pe.wait_ge(kv_ready, b + 1)
                pe.transpose(ps_x[0][:, C:2 * C], kv[:, :], ident[:, :]).then_inc(kvt_done, 1)
                pe.wait_ge(kvt_ready, b + 1)
                pe.matmul(ps_x[0][:, 2 * C:3 * C], kvt[:, :], wo[:, :], start=True, stop=True).then_inc(g_done, 1)
                pe.wait_ge(g_ready, b + 1)
                for n in range(KT + 4):
                    if 0 <= n - 4:
                        project(b, n - 4)
                    if 0 <= n - 3 < KT:
                        widen(b, n - 3)
                    if 0 <= n - 2 < KT:
                        turn_denominators(b, n - 2)
                    if 0 <= n - 1 < KT:
                        denominators(b, n - 1)
                    if n < KT:
                        queries(b, n)

            batch(0, False)
            with pe.Fori(0, B - 1) as b:
                batch(b + 1, True)

        @block.scalar
        def _(act):
            act.wait_ge(loaded, 16 * NL)

            def rows_in(b, k):
                act.wait_ge(turned, b * KT + k + 1)
                act.copy(uT[:, k * R * W:(k + 1) * R * W], ps_t[k % 2][:, :]).then_inc(uT_ready, 1)

            def keys_in(b, k):
                act.wait_ge(k_done, b * KT + k + 1)
                if k >= 2:
                    act.wait_ge(phi_ready, b * KT + k - 1)
                act.activation(rl[k % 2][:, :], ps_k[k % 2][:, :], ACT.Relu)
                act.activation(ex[k % 2][:, :], ps_k[k % 2][:, :], ACT.Exp).then_inc(k_in, 1)

            def queries_in(b, k):
                act.wait_ge(q_done, b * KT + k + 1)
                if k >= 2:
                    act.wait_ge(qphi, b * KT + k - 1)
                act.activation(rl[k % 2][:, :], ps_q[k % 2][:, :], ACT.Relu, bias=bqc[:, 0:1])
                act.activation(ex[k % 2][:, :], ps_q[k % 2][:, :], ACT.Exp, bias=bqc[:, 0:1]).then_inc(q_in, 1)

            def denominators_in(b, k):
                act.wait_ge(rd_turned, b * KT + k + 1)
                act.copy(rT[k % 2][:, :], ps_x[k % 2][0:RH, P:2 * P]).then_inc(rT_ready, 1)

            with act.Fori(0, B) as b:
                for n in range(KT + 1):
                    if n < KT:
                        rows_in(b, n)
                    if 0 <= n - 1:
                        keys_in(b, n - 1)
                for n in range(KT + 2):
                    if n < KT:
                        queries_in(b, n)
                    if 0 <= n - 2:
                        denominators_in(b, n - 2)

        @block.vector
        def _(dve):
            step = Chain(dve, dch)
            TT, TS, STT = dve.tensor_tensor, dve.tensor_scalar, dve.scalar_tensor_tensor
            dve.wait_ge(loaded, 16 * NL)
            dve.wait_ge(made, 1)
            for j in range(2):
                dve.sem_inc(stored[j], 1)
            hm = heads[:, :, :].rearrange("p h d -> p (h d)")

            def moments(b, k):
                dve.wait_ge(xin[k], 16 * b + 16)
                dve.sem_inc(tick, 1)
                for r in range(R):
                    step.mark(dve.bn_stats(st[:, r, :], xb[:, k * R + r, :]))
                step.join()
                dve.sem_inc(tick, 1)
                for r in range(R):
                    step.mark(dve.bn_aggr(mv[k % 2][:, r, :], st[:, r, :]))
                step.join()
                step(TS(ve[:, :], mv[k % 2][:, :, 1], eps, None, ALU.add))
                dve.sem_inc(ve_ready, 1)

            def normalise(b, k):
                dve.wait_ge(rstd_ready, b * KT + k + 1)
                for r in range(R):
                    last = step.mark(TS(u[:, k * R + r, :], xb[:, k * R + r, :], mv[k % 2][:, r, 0:1], rstd[:, r:r + 1],
                                        ALU.subtract, ALU.mult))
                step.join()
                dve.sem_inc(u_ready, 1)

            def key_features(b, k):
                dve.wait_ge(k_in, b * KT + k + 1)
                if k >= 4:
                    dve.wait_ge(acc_done, b * KT + k - 3)
                STT(out=phi[k % 4][:, :], in0=ex[k % 2][:, :], scalar=1.0, in1=rl[k % 2][:, :],
                    op0=ALU.min, op1=ALU.add).then_inc(phi_ready, 1)

            def query_features(b, k):
                dve.wait_ge(q_in, b * KT + k + 1)
                step(STT(out=phi[k % 4][:, :], in0=ex[k % 2][:, :], scalar=1.0, in1=rl[k % 2][:, :],
                         op0=ALU.min, op1=ALU.add))
                dve.sem_inc(qphi, 1)

            def invert(b, k):
                dve.wait_ge(den_done, b * KT + k + 1)
                step(TS(rd[k % 2][:, :], ps_x[k % 2][:, 0:RH], eps, None, ALU.add))
                step(dve.reciprocal(rd[k % 2][:, :], rd[k % 2][:, :]))
                dve.sem_inc(rd_ready, 1)

            def divide(b, k):
                dve.wait_ge(rd_wide, b * KT + k + 1)
                if k >= 2:
                    dve.wait_ge(o_done, b * KT + k - 1)
                TT(phz[k % 2][:, :], phi[k % 4][:, :], ps_d[k % 2][:, :], ALU.mult).then_inc(phz_ready, 1)

            def add(b, k):
                dve.wait_ge(o_done, b * KT + k + 1)
                dve.wait_ge(stored[k % 2], 16 * (b * (KT // 2) + k // 2) + 1)
                TT(out[k % 2][:, :].rearrange("p (r c) -> p r c", r=R),
                   ps_o[k % 2][:, :].rearrange("p (r c) -> p r c", r=R), xb[:, rows(k), :], ALU.add).then_inc(out_ready, 1)

            def batch(b, more):
                for k in range(KT):
                    key_features(b, k)
                dve.wait_ge(acc_done, (b + 1) * KT)
                step(dve.tensor_copy(uk[:, :], ps_m[0][:, 0:C]))
                dve.sem_inc(uk_ready, 1)
                step(dve.tensor_copy(ksum[:, :], ps_m[1][:, 0:1]))
                step(TS(kbh[:, :], heads[:, :, 0], ksum[:, 0:1], None, ALU.mult))
                dve.wait_ge(kv_done, b + 1)
                step(STT(out=kv[:, :], in0=bv_b[:, :], scalar=ksum[:, 0:1], in1=ps_x[0][:, 0:C], op0=ALU.mult, op1=ALU.add))
                step(TT(kv[:, :], kv[:, :], hm, ALU.mult))
                dve.sem_inc(kv_ready, 1)
                dve.wait_ge(kvt_done, b + 1)
                dve.tensor_copy(kvt[:, :], ps_x[0][:, C:2 * C]).then_inc(kvt_ready, 1)
                dve.wait_ge(g_done, b + 1)
                step(dve.tensor_copy(g[:, :], ps_x[0][:, 2 * C:3 * C]))
                dve.sem_inc(g_ready, 1)
                for n in range(KT + 8):
                    if n < KT:
                        query_features(b, n)
                    if 0 <= n - 1 < KT:
                        invert(b, n - 1)
                    if 0 <= n - 3 < KT:
                        divide(b, n - 3)
                    if 0 <= n - 4 < KT:
                        add(b, n - 4)
                    if more and 0 <= n - 7 < KT:
                        normalise(b + 1, n - 7)
                    if more and 0 <= n - 6 < KT:
                        moments(b + 1, n - 6)

            for k in range(KT):
                moments(0, k)
                normalise(0, k)
            with step.loop(B - 1, 6 + 3 * KT + (3 * R + 1) * KT) as b:
                batch(b, True)
            batch(B - 1, False)


def routed_experts(nc, x3, gate_w, gate_b, w1, w2, x4, tag="moe", eps=1e-5):
    E = gate_w.shape[0]
    HID = w1.shape[2]
    HC = HID // P
    R = 4
    KT = T // R
    L = T * W
    NEG = -3.0e38
    with ExitStack() as ctx:
        s = Scope(nc, ctx, tag)
        ident = s.sb("ident", [P, P])
        gT = s.sb("gT", [P, E])
        wt = s.sb("wt", [P, 2, L])
        poolT = s.sb("poolT", [P, E, B])
        eo = s.sb("eo", [P, 2, C])
        u_d = nc.dram_tensor(f"{tag}_u", (BT, W, C), f32, kind="Internal").ap()
        NP = 2 * KT
        with ExitStack() as c2:
            s2 = Scope(nc, c2, tag + "a")
            gw = s2.sb("gw", [E, C])
            gb = s2.sb("gb", [P, 1])
            xb, u = ([s2.sb(f"{n}{j}", [P, R, C]) for j in range(4)] for n in ("xb", "u"))
            uTs = [s2.sb(f"uTs{j}", [P, R * W]) for j in range(2)]
            st = s2.sb("st", [P, R, 6])
            mv = [s2.sb(f"mv{j}", [P, R, 2]) for j in range(2)]
            ve, rstd, half = (s2.sb(n, [P, R]) for n in ("ve", "rstd", "half"))
            ps_t, ps_l = ([s2.ps(f"{n}{j}") for j in range(2)] for n in ("ps_t", "ps_l"))
            ps_g = s2.ps("ps_g")
            (loaded, made, g_done, g_ready, ve_ready, rstd_ready, u_ready, turned, uT_ready,
             l_done, l_ready, dch, pch, group_done, dtick) = (
                s2.sem(n) for n in ("loaded", "made", "g_done", "g_ready", "ve_ready", "rstd_ready",
                                    "u_ready", "turned", "uT_ready", "l_done", "l_ready", "dch", "pch", "group_done",
                                    "dtick"))
            xin, saved = ([s2.sem(f"{n}{j}") for j in range(4)] for n in ("xin", "saved"))
            block = c2.enter_context(nc.Block())
            xv = x3.rearrange("b t w c -> (b t) w c").rearrange("(g n r) w c -> g n w r c", g=2, r=R)
            uv = u_d.rearrange("(g n r) w c -> g n w r c", g=2, r=R)

            @block.sync
            def _(sp):
                sp.dma_start(gw[:, :], gate_w).then_inc(loaded, 16)
                for j in range(2):
                    sp.dma_start(gb[j * E:(j + 1) * E, :], gate_b.unsqueeze(1)).then_inc(loaded, 16)
                for g in range(2):
                    for n in range(4):
                        sp.dma_start(xb[n][:, :, :], xv[g, n]).then_inc(xin[n], 16)
                    for n in range(NP):
                        sp.wait_ge(u_ready, g * NP + n + 1)
                        sp.dma_start(uv[g, n], u[n % 4][:, :, :]).then_inc(saved[n % 4], 16)
                        if n + 4 < NP:
                            sp.dma_start(xb[n % 4][:, :, :], xv[g, n + 4]).then_inc(xin[n % 4], 16)
                for j in range(4):
                    sp.wait_ge(saved[j], 16 * 2 * NP // 4 + 1)

            @block.gpsimd
            def _(pool):
                step = Chain(pool, pch)
                fill_identity(pool, step, ident)
                step(pool.memset(half[:, :], -0.5))
                pool.sem_inc(made, 1)
                with pool.Fori(0, 2 * NP) as n:
                    pool.wait_ge(ve_ready, n + 1)
                    pool.tensor_tensor(rstd[:, :], ve[:, :], half[:, :], ALU.pow).then_inc(rstd_ready, 1)

            @block.tensor
            def _(pe):
                pe.wait_ge(loaded, 48)
                pe.wait_ge(made, 1)
                pe.transpose(ps_g[:, 0:E], gw[:, :], ident[0:E, 0:E]).then_inc(g_done, 1)
                pe.wait_ge(g_ready, 1)

                def turn_rows(g, n):
                    pe.wait_ge(u_ready, g * NP + n + 1)
                    for r in range(R):
                        last = pe.transpose(ps_t[n % 2][:, r * W:(r + 1) * W], u[n % 4][:, r, :], ident[:, :])
                    last.then_inc(turned, 1)

                def logits(g, n):
                    q = n // KT
                    pe.wait_ge(uT_ready, g * NP + n + 1)
                    if n >= 2:
                        pe.wait_ge(l_ready, g * NP + n - 1)
                    pe.matmul(ps_l[n % 2][q * E:(q + 1) * E, :], gT[:, :], uTs[n % 2][:, :], start=True, stop=True,
                              tile_position=(0, q * E)).then_inc(l_done, 1)

                with pe.Fori(0, 2) as g:
                    for n in range(NP + 1):
                        if n < NP:
                            turn_rows(g, n)
                        if n >= 1:
                            logits(g, n - 1)
                    pe.wait_ge(l_ready, (g + 1) * NP)
                    pe.sem_inc(group_done, 1)

            @block.scalar
            def _(act):
                act.wait_ge(g_done, 1)
                act.copy(gT[:, :], ps_g[:, 0:E]).then_inc(g_ready, 1)
                act.wait_ge(loaded, 48)
                with act.Fori(0, 2) as g:
                    for n in range(NP + 1):
                        if n < NP:
                            act.wait_ge(turned, g * NP + n + 1)
                            if n >= 2:
                                act.wait_ge(l_done, g * NP + n - 1)
                            act.copy(uTs[n % 2][:, :], ps_t[n % 2][:, :]).then_inc(uT_ready, 1)
                        if n >= 1:
                            q, k = divmod(n - 1, KT)
                            rows = slice(q * E, (q + 1) * E)
                            act.wait_ge(l_done, g * NP + n)
                            act.activation(wt[rows, bass.ds(g, 1), k * R * W:(k + 1) * R * W].rearrange("p a n -> p (a n)"),
                                           ps_l[(n - 1) % 2][rows, :], ACT.Identity, bias=gb[rows, 0:1]).then_inc(l_ready, 1)

            @block.vector
            def _(dve):
                step = Chain(dve, dch)
                dve.sem_inc(group_done, 1)
                for j in range(4):
                    dve.sem_inc(saved[j], 1)

                def moments(g, n):
                    dve.wait_ge(xin[n % 4], 16 * (g * (NP // 4) + n // 4) + 16)
                    dve.sem_inc(dtick, 1)
                    for r in range(R):
                        step.mark(dve.bn_stats(st[:, r, :], xb[n % 4][:, r, :]))
                    step.join()
                    dve.sem_inc(dtick, 1)
                    for r in range(R):
                        step.mark(dve.bn_aggr(mv[n % 2][:, r, :], st[:, r, :]))
                    step.join()
                    step(dve.tensor_scalar(ve[:, :], mv[n % 2][:, :, 1], eps, None, ALU.add))
                    dve.sem_inc(ve_ready, 1)

                def normalise(g, n):
                    dve.wait_ge(rstd_ready, g * NP + n + 1)
                    if n >= 4:
                        dve.wait_ge(turned, g * NP + n - 3)
                        dve.wait_ge(saved[n % 4], 16 * (g * (NP // 4) + n // 4) + 1)
                    for r in range(R):
                        step.mark(dve.tensor_scalar(u[n % 4][:, r, :], xb[n % 4][:, r, :], mv[n % 2][:, r, 0:1],
                                                    rstd[:, r:r + 1], ALU.subtract, ALU.mult))
                    step.join()
                    dve.sem_inc(u_ready, 1)

                with step.loop(2, (3 * R + 1) * NP) as g:
                    dve.wait_ge(group_done, g + 1)
                    for j in range(4):
                        dve.wait_ge(saved[j], 16 * g * (NP // 4) + 1)
                    for n in range(NP):
                        moments(g, n)
                        normalise(g, n)

        with ExitStack() as c2:
            s2 = Scope(nc, c2, tag + "b")
            top = s2.sb("top", [P, 2, 8])
            nmx = s2.sb("nmx", [P, 2])
            den = s2.sb("den", [P, 2])
            rest = s2.sb("rest", [P, 2, L])
            pr = s2.sb("pr", [P, 2, L])
            neg_ready, ex_ready, dch = s2.sem("neg_ready"), s2.sem("ex_ready"), s2.sem("dch")
            block = c2.enter_context(nc.Block())

            @block.scalar
            def _(act):
                for j in range(2):
                    act.wait_ge(neg_ready, j + 1)
                    act.activation(pr[:, j, :], wt[:, j, :], ACT.Exp, bias=nmx[:, j:j + 1],
                                   accum_out=den[:, j:j + 1]).then_inc(ex_ready, 1)

            @block.vector
            def _(dve):
                step = Chain(dve, dch)
                for j in range(2):
                    step(dve.max(top[:, j, :], wt[:, j, :]))
                    step(dve.tensor_scalar(nmx[:, j:j + 1], top[:, j, 0:1], -1.0, None, ALU.mult))
                    dve.sem_inc(neg_ready, 1)
                    step(dve.match_replace(rest[:, j, :], top[:, j, :], wt[:, j, :], NEG))
                for j in range(2):
                    dve.wait_ge(ex_ready, j + 1)
                    step(dve.tensor_tensor(rest[:, j, :], rest[:, j, :], wt[:, j, :], ALU.not_equal))
                    step(dve.reciprocal(den[:, j:j + 1], den[:, j:j + 1]))
                    step(dve.scalar_tensor_tensor(out=wt[:, j, :], in0=pr[:, j, :], scalar=den[:, j:j + 1],
                                                  in1=rest[:, j, :], op0=ALU.mult, op1=ALU.mult))

        with ExitStack() as c2:
            s2 = Scope(nc, c2, tag + "c")
            ur = [[s2.sb(f"ur{j}{q}", [P, R, C]) for q in range(2)] for j in range(2)]
            ws = [s2.sb(f"ws{j}", [P, R * W]) for j in range(2)]
            wT = [s2.sb(f"wT{j}", [P, R, 2 * E]) for j in range(2)]
            acc = s2.sb("acc", [P, 2, 2, E])
            ps_w, ps_p = ([s2.ps(f"{n}{j}") for j in range(2)] for n in ("ps_w", "ps_p"))
            uin = [[s2.sem(f"uin{j}{q}") for q in range(2)] for j in range(2)]
            staged, turned, wT_ready, pooled, added = ([s2.sem(f"{n}{j}") for j in range(2)] for n in (
                "staged", "turned", "wT_ready", "pooled", "added"))
            dch, stick = s2.sem("dch"), s2.sem("stick")
            block = c2.enter_context(nc.Block())
            uv = u_d.rearrange("(g q i j r) w c -> g q i j w r c", g=2, q=2, j=2, r=R)
            HK = KT // 2

            @block.sync
            def _(sp):
                for j in range(2):
                    sp.sem_inc(pooled[j], 1)
                for g in range(2):
                    with sp.Fori(0, HK) as i:
                        for j in range(2):
                            sp.wait_ge(pooled[j], i + g * HK + 1)
                            sp.sem_inc(stick, 1)
                            for q in range(2):
                                sp.dma_start(ur[j][q][:, :, :], uv[g, q][i, j]).then_inc(uin[j][q], 16)

            @block.tensor
            def _(pe):
                with pe.Fori(0, 2 * HK) as i:
                    for j in range(2):
                        pe.wait_ge(staged[j], i + 1)
                        for r in range(R):
                            last = pe.transpose(ps_w[j][:, r * P:(r + 1) * P], ws[j][:, r * W:(r + 1) * W], ident[:, :])
                        last.then_inc(turned[j], 1)
                    for j in range(2):
                        pe.wait_ge(wT_ready[j], i + 1)
                        pe.wait_ge(added[j], i + 1)
                        for q in range(2):
                            pe.wait_ge(uin[j][q], i * 16 + 16)
                            for r in range(R):
                                last = pe.matmul(ps_p[j][:, q * E:(q + 1) * E], ur[j][q][:, r, :],
                                                 wT[j][:, r, q * E:(q + 1) * E], start=(r == 0), stop=(r == R - 1))
                        last.then_inc(pooled[j], 1)

            @block.scalar
            def _(act):
                for g in range(2):
                    with act.Fori(0, HK) as i:
                        for j in range(2):
                            n = i + g * HK
                            act.copy(ws[j][:, :], wt[:, g, bass.ds(i * 2 * R * W + j * R * W, R * W)]).then_inc(staged[j], 1)
                        for j in range(2):
                            act.wait_ge(turned[j], n + 1)
                            act.wait_ge(pooled[j], n + 1)
                            act.copy(wT[j][:, :, :], ps_w[j][:, :].rearrange("p (r e) -> p r e", r=R)).then_inc(wT_ready[j], 1)

            @block.vector
            def _(dve):
                step = Chain(dve, dch)
                step(dve.memset(acc[:, :, :, :], 0.0))
                for j in range(2):
                    dve.sem_inc(added[j], 1)
                for g in range(2):
                    with step.loop(HK, 2) as i:
                        for j in range(2):
                            dve.wait_ge(pooled[j], i + g * HK + 2)
                            step(dve.tensor_tensor(acc[:, g, :, :], acc[:, g, :, :],
                                                   ps_p[j][:, 0:2 * E].rearrange("p (q e) -> p q e", q=2), ALU.add))
                            dve.sem_inc(added[j], 1)
                step(dve.tensor_copy(poolT[:, :, :], acc[:, :, :, :].rearrange("p g q e -> p e (g q)")))

        with ExitStack() as c2:
            s2 = Scope(nc, c2, tag + "d")
            NE, SLOTS = 2, 4
            NT = E // (NE * SLOTS)
            wa = [s2.sb(f"wa{j}", [P, NE, P, HC]) for j in range(SLOTS)]
            ab = [s2.sb(f"ab{j}", [1, NE, P, HC]) for j in range(SLOTS)]
            wb = [s2.sb(f"wb{j}", [P, NE, HC, C]) for j in range(SLOTS)]
            bb = [s2.sb(f"bb{j}", [1, NE, C]) for j in range(SLOTS)]
            ones1 = s2.sb("ones1", [1, B])
            h = [s2.sb(f"h{j}", [P, HC * B]) for j in range(2)]
            eoT = s2.sb("eoT", [P, B, E])
            ps_h = [s2.ps(f"ps_h{j}") for j in range(2)]
            ps_e = s2.ps("ps_e")
            ps_f = s2.ps("ps_f")
            win = [s2.sem(f"win{j}") for j in range(SLOTS)]
            used = [s2.sem(f"used{j}") for j in range(SLOTS)]
            made, hid, h_ready, outd, eo_t, flipped, eo_ready, tick, stick = (s2.sem(n) for n in (
                "made", "hid", "h_ready", "outd", "eo_t", "flipped", "eo_ready", "tick", "stick"))
            block = c2.enter_context(nc.Block())
            w1v = w1.rearrange("(i j e) d h -> i j d e h", j=SLOTS, e=NE)
            w2v = w2.rearrange("(i j e) h o -> i j h e o", j=SLOTS, e=NE)

            @block.sync
            def _(sp):
                for j in range(SLOTS):
                    sp.sem_inc(used[j], 1)
                with sp.Fori(0, NT) as i:
                    for j in range(SLOTS):
                        sp.wait_ge(used[j], i + 1)
                        sp.sem_inc(stick, 1)
                        sp.dma_start(wa[j][:, :, :, :].rearrange("p e a k -> p e (a k)"), w1v[i, j][0:P]).then_inc(win[j], 16)
                        sp.dma_start(ab[j][:, :, :, :].rearrange("p e a k -> p e (a k)"), w1v[i, j][P:P + 1]).then_inc(win[j], 16)
                        for e in range(NE):
                            sp.dma_start(wb[j][:, e, :, :].rearrange("p k o -> p (k o)"),
                                         w2v[i, j][0:HID, e].rearrange("(p k) o -> p (k o)", k=HC)).then_inc(win[j], 16)
                        sp.dma_start(bb[j][:, :, :], w2v[i, j][HID:HID + 1]).then_inc(win[j], 16)

            @block.gpsimd
            def _(pool):
                pool.memset(ones1[:, :], 1.0).then_inc(made, 1)

            @block.tensor
            def _(pe):
                pe.wait_ge(made, 1)
                NX = NE * SLOTS

                def hidden(i, n):
                    j, e = divmod(n, NE)
                    if e == 0:
                        pe.wait_ge(win[j], 16 * (3 + NE) * (i + 1))
                        pe.sem_inc(tick, 1)
                    for k in range(HC):
                        dst = ps_h[n % 2][:, k * B:(k + 1) * B]
                        pe.matmul(dst, wa[j][:, e, :, k], poolT[:, bass.ds(i * NX + n, 1), :].rearrange("p a b -> p (a b)"),
                                  start=True, stop=False)
                        last = pe.matmul(dst, ab[j][:, e, :, k], ones1[:, :], start=False, stop=True)
                    last.then_inc(hid, 1)

                def output(i, n):
                    j, e = divmod(n, NE)
                    pe.wait_ge(h_ready, i * NX + n + 1)
                    pe.sem_inc(tick, 1)
                    dst = ps_e[:, bass.ds((i * NX + n) * B, B)]
                    for k in range(HC):
                        pe.matmul(dst, wb[j][:, e, k, :], h[n % 2][:, k * B:(k + 1) * B], start=(k == 0), stop=False)
                    pe.matmul(dst, bb[j][:, e, :], ones1[:, :], start=False, stop=True).then_inc(
                        used[j] if e == NE - 1 else outd, 1)

                with pe.Fori(0, NT) as i:
                    hidden(i, 0)
                    for n in range(NX):
                        if n + 1 < NX:
                            hidden(i, n + 1)
                        output(i, n)
                pe.wait_ge(eo_t, 1)
                for j in range(2):
                    pe.transpose(ps_f[:, j * C:(j + 1) * C], eoT[:, 2 * j:2 * j + 2, :].rearrange("p b e -> p (b e)"),
                                 ident[:, :]).then_inc(flipped, 1)

            @block.scalar
            def _(act):
                with act.Fori(0, E // 2) as i:
                    for j in range(2):
                        act.wait_ge(hid, i * 2 + j + 1)
                        act.activation(h[j][:, :], ps_h[j][:, 0:HC * B], ACT.Gelu).then_inc(h_ready, 1)
                for j in range(SLOTS):
                    act.wait_ge(used[j], NT + 1)
                act.copy(eoT[:, :, :], ps_e[:, 0:E * B].rearrange("p (e b) -> p b e", b=B)).then_inc(eo_t, 1)
                act.wait_ge(flipped, 2)
                act.copy(eo[:, :, :], ps_f[:, 0:2 * C].rearrange("p (j c) -> p j c", j=2)).then_inc(eo_ready, 1)

        with ExitStack() as c2:
            s2 = Scope(nc, c2, tag + "e")
            xr = [s2.sb(f"xr{j}", [P, R, C]) for j in range(2)]
            out = [s2.sb(f"out{j}", [P, R, C]) for j in range(2)]
            ws = [s2.sb(f"ws{j}", [P, R * W]) for j in range(2)]
            ps = [s2.ps(f"ps{j}") for j in range(2)]
            xin = [s2.sem(f"xin{j}") for j in range(2)]
            staged, given, added, stored = (s2.sem(n) for n in ("staged", "given", "added", "stored"))
            block = c2.enter_context(nc.Block())
            xv = x3.rearrange("b (i j r) w c -> b i j w r c", j=2, r=R)
            ov = x4.rearrange("b (i j r) w c -> b i j w r c", j=2, r=R)

            @block.sync
            def _(sp):
                for b in range(B):
                    with sp.Fori(0, KT // 2) as i:
                        for j in range(2):
                            sp.wait_ge(added, i * 2 + b * KT)
                            sp.dma_start(xr[j][:, :, :], xv[b][i, j]).then_inc(xin[j], 16)

            @block.gpsimd
            def _(pool):
                for b in range(B):
                    rows = slice((b % 2) * E, (b % 2 + 1) * E)
                    with pool.Fori(0, KT // 2) as i:
                        for j in range(2):
                            pool.wait_ge(given, i * 2 + b * KT)
                            pool.tensor_copy(ws[j][rows, :], wt[rows, b // 2, bass.ds(i * 2 * R * W + j * R * W, R * W)]
                                             ).then_inc(staged, 1)

            @block.tensor
            def _(pe):
                for b in range(B):
                    rows = slice((b % 2) * E, (b % 2 + 1) * E)
                    with pe.Fori(0, KT // 2) as i:
                        for j in range(2):
                            n = i * 2 + b * KT + j
                            pe.wait_ge(staged, n + 1)
                            pe.wait_ge(added, i * 2 + b * KT)
                            for r in range(R):
                                last = pe.matmul(ps[j][:, r * C:(r + 1) * C], ws[j][rows, r * W:(r + 1) * W],
                                                 eo[rows, b // 2, :], start=True, stop=True,
                                                 tile_position=((b % 2) * E, 0))
                            last.then_inc(given, 1)

            @block.vector
            def _(dve):
                for b in range(B):
                    with dve.Fori(0, KT // 2) as i:
                        for j in range(2):
                            n = i * 2 + b * KT + j
                            dve.wait_ge(given, n + 1)
                            dve.wait_ge(xin[j], i * 16 + b * 16 * (KT // 2) + 16)
                            dve.wait_ge(stored, (i * 2 + b * KT) * 16)
                            dve.tensor_tensor(out[j][:, :, :], xr[j][:, :, :],
                                              ps[j][:, :].rearrange("p (r c) -> p r c", r=R), ALU.add).then_inc(added, 1)

            @block.scalar
            def _(act):
                for b in range(B):
                    with act.Fori(0, KT // 2) as i:
                        for j in range(2):
                            act.wait_ge(added, i * 2 + b * KT + j + 1)
                            act.dma_start(ov[b][i, j], out[j][:, :, :]).then_inc(stored, 16)
                act.wait_ge(stored, 16 * B * KT)


def normalised_tokens(nc, x, u, tag, eps=1e-5):
    with ExitStack() as ctx:
        s = Scope(nc, ctx, tag)
        xb = [s.sb(f"xb{j}", [P, T // 2, C]) for j in range(2)]
        TH = T // 2
        st = s.sb("st", [P, TH, 6])
        mv = s.sb("mv", [P, TH, 2])
        ve, rstd, half = (s.sb(n, [P, TH]) for n in ("ve", "rstd", "half"))
        xin = [s.sem(f"xin{j}") for j in range(2)]
        made, ve_ready, rstd_ready, u_ready, dch = (s.sem(n) for n in ("made", "ve_ready", "rstd_ready", "u_ready", "dch"))
        block = ctx.enter_context(nc.Block())
        N = 2 * B
        xv = x.rearrange("b (j t) w c -> (b j) w t c", j=2)

        @block.sync
        def _(sp):
            for n in range(N):
                if n >= 2:
                    sp.wait_ge(u_ready, n - 1)
                sp.dma_start(xb[n % 2][:, :, :], xv[n]).then_inc(xin[n % 2], 16)

        @block.gpsimd
        def _(pool):
            pool.memset(half[:, :], -0.5).then_inc(made, 1)
            pool.wait_ge(made, 1)
            for n in range(N):
                pool.wait_ge(ve_ready, n + 1)
                pool.tensor_tensor(rstd[:, :], ve[:, :], half[:, :], ALU.pow).then_inc(rstd_ready, 1)

        @block.vector
        def _(dve):
            step = Chain(dve, dch)
            for n in range(N):
                dve.wait_ge(xin[n % 2], 16 * (n // 2 + 1))
                src = xb[n % 2]
                dst = u[:, n * TH:(n + 1) * TH, :]
                for t in range(TH):
                    step.mark(dve.bn_stats(st[:, t, :], src[:, t, :]))
                step.join()
                for t in range(TH):
                    step.mark(dve.bn_aggr(mv[:, t, :], st[:, t, :]))
                step.join()
                step(dve.tensor_scalar(ve[:, :], mv[:, :, 1], eps, None, ALU.add))
                dve.sem_inc(ve_ready, 1)
                step(dve.tensor_tensor(dst, src[:, :, :], mv[:, :, 0:1].broadcast_to([P, TH, C]), ALU.subtract))
                dve.wait_ge(rstd_ready, n + 1)
                step(dve.tensor_tensor(dst, dst, rstd[:, :].unsqueeze(2).broadcast_to([P, TH, C]), ALU.mult))
                dve.sem_inc(u_ready, 1)


def softmax_attention(nc, x4, w_in, w_out, b_out, ln_w, x5, tag="sma", eps=1e-5):
    H = 4
    D = C // H
    R = 4
    NT = BT // R
    TOK = BT * W
    with ExitStack() as ctx:
        s = Scope(nc, ctx, tag)
        u = s.sb("u", [P, BT, C])
        wT = s.sb("wT", [P, 4, C])
        ident, ones = s.sb("ident", [P, P]), s.sb("ones", [P, P])
        ones1 = s.sb("ones1", [1, P])
        negmax = s.sb("negmax", [1, C])
        heads = s.sb("heads", [P, H, D])
        g = s.sb("g", [P, C])
        normalised_tokens(nc, x4, u, tag + "n")
        with ExitStack() as c2:
            s2 = Scope(nc, c2, tag + "a")
            wl = s2.sb("wl", [P, 4, C])
            us = s2.sb("us", [P, R, C])
            uTs = [s2.sb(f"uTs{j}", [P, R * W]) for j in range(2)]
            mx = s2.sb("mx", [P, NT])
            m1 = s2.sb("m1", [P, 1])
            ps_w, ps_t, ps_m = s2.ps("ps_w"), s2.ps("ps_t"), s2.ps("ps_m")
            ps_k = [s2.ps(f"ps_k{j}") for j in range(2)]
            (loaded, made, w_done, w_ready, staged, turned, uT_ready, k_done, k_read, m_ready, m_done, dch, pch,
             tick) = (s2.sem(n) for n in ("loaded", "made", "w_done", "w_ready", "staged", "turned", "uT_ready",
                                          "k_done", "k_read", "m_ready", "m_done", "dch", "pch", "tick"))
            block = c2.enter_context(nc.Block())

            @block.sync
            def _(sp):
                sp.dma_start(wl[:, 0:3, :], w_in.rearrange("(j o) c -> o j c", j=3)).then_inc(loaded, 16)
                sp.dma_start(wl[:, 3, :], w_out).then_inc(loaded, 16)

            @block.gpsimd
            def _(pool):
                step = Chain(pool, pch)
                fill_identity(pool, step, ident)
                step(pool.memset(ones[:, :], 1.0))
                step(pool.memset(ones1[:, :], 1.0))
                step(pool.memset(heads[:, :, :], 1.0))
                step(pool.affine_select(out=heads[:, :, :], in_=heads[:, :, :], compare_op=ALU.is_ge, fill=0.0,
                                        base=0, pattern=[[-D, H], [0, D]], channel_multiplier=1))
                step(pool.affine_select(out=heads[:, :, :], in_=heads[:, :, :], compare_op=ALU.is_ge, fill=0.0,
                                        base=D - 1, pattern=[[D, H], [0, D]], channel_multiplier=-1))
                pool.sem_inc(made, 1)
                with pool.Fori(0, NT) as i:
                    pool.wait_ge(turned, i)
                    pool.tensor_copy(us[:, :, :], u[:, bass.ds(i * R, R), :]).then_inc(staged, 1)

            @block.tensor
            def _(pe):
                pe.wait_ge(loaded, 32)
                pe.wait_ge(made, 1)
                for j in range(4):
                    last = pe.transpose(ps_w[:, j * C:(j + 1) * C], wl[:, j, :], ident[:, :])
                last.then_inc(w_done, 1)
                pe.wait_ge(w_ready, 1)
                with pe.Fori(0, NT // 2) as i:
                    for j in range(2):
                        n = 2 * i + j
                        pe.wait_ge(staged, 2 * i + j + 1)
                        pe.wait_ge(uT_ready, 2 * i + j)
                        for r in range(R):
                            last = pe.transpose(ps_t[:, r * W:(r + 1) * W], us[:, r, :], ident[:, :])
                        last.then_inc(turned, 1)
                        pe.wait_ge(uT_ready, 2 * i + j + 1)
                        pe.wait_ge(k_read, 2 * i)
                        pe.matmul(ps_k[j][:, :], wT[:, 1, :], uTs[j][:, :], start=True, stop=True).then_inc(k_done, 1)
                pe.wait_ge(m_ready, 1)
                pe.transpose(ps_m[0:1, 0:P], m1[:, :], ident[:, :]).then_inc(m_done, 1)

            @block.scalar
            def _(act):
                act.wait_ge(w_done, 1)
                act.copy(wT[:, :, :], ps_w[:, :].rearrange("p (j c) -> p j c", j=4)).then_inc(w_ready, 1)
                with act.Fori(0, NT // 2) as i:
                    for j in range(2):
                        act.wait_ge(turned, 2 * i + j + 1)
                        act.wait_ge(k_done, 2 * i)
                        act.copy(uTs[j][:, :], ps_t[:, :]).then_inc(uT_ready, 1)
                act.wait_ge(m_done, 1)
                act.copy(negmax[:, :], ps_m[0:1, 0:P]).then_inc(tick, 1)

            @block.vector
            def _(dve):
                step = Chain(dve, dch)
                with dve.Fori(0, NT // 2) as i:
                    for j in range(2):
                        dve.wait_ge(k_done, 2 * i + j + 1)
                        dve.tensor_reduce(mx[:, bass.ds(i * 2 + j, 1)], ps_k[j][:, :], AX.X, ALU.max).then_inc(k_read, 1)
                dve.wait_ge(k_read, NT)
                step(dve.tensor_reduce(m1[:, :], mx[:, :], AX.X, ALU.max, negate=True))
                dve.sem_inc(m_ready, 1)

        with ExitStack() as c2:
            s2 = Scope(nc, c2, tag + "b")
            us = [s2.sb(f"us{x}", [P, R, C]) for x in range(2)]
            uTs = [s2.sb(f"uTs{x}", [P, R * W]) for x in range(2)]
            ek = [s2.sb(f"ek{x}", [P, R * C]) for x in range(2)]
            acc = s2.sb("acc", [P, 2, C])
            ctxm, ctxt = s2.sb("ctxm", [P, C]), s2.sb("ctxt", [P, C])
            rsum = s2.sb("rsum", [P, 1])
            ps_t, ps_k, ps_m = ([s2.ps(f"{n}{x}") for x in range(2)] for n in ("ps_t", "ps_k", "ps_m"))
            ps_x = s2.ps("ps_x")
            staged, turned, uT_ready, k_done, ek_ready, acc_done, acc_read = (
                [s2.sem(f"{n}{x}") for x in range(2)]
                for n in ("staged", "turned", "uT_ready", "k_done", "ek_ready", "acc_done", "acc_read"))
            c_done, c_ready, ct_done, ct_ready, g_done, dch = (
                s2.sem(n) for n in ("c_done", "c_ready", "ct_done", "ct_ready", "g_done", "dch"))
            block = c2.enter_context(nc.Block())

            @block.gpsimd
            def _(pool):
                for x in range(2):
                    pool.sem_inc(acc_done[x], 1)
                with pool.Fori(0, NT // 2) as i:
                    for x in range(2):
                        pool.wait_ge(acc_done[x], i + 1)
                        pool.tensor_copy(us[x][:, :, :], u[:, bass.ds(i * 2 * R + x * R, R), :]).then_inc(staged[x], 1)

            @block.tensor
            def _(pe):
                with pe.Fori(0, NT // 2) as i:
                    for x in range(2):
                        pe.wait_ge(staged[x], i + 1)
                        for r in range(R):
                            last = pe.transpose(ps_t[x][:, r * W:(r + 1) * W], us[x][:, r, :], ident[:, :])
                        last.then_inc(turned[x], 1)
                    for x in range(2):
                        pe.wait_ge(uT_ready[x], i + 1)
                        for r in range(R):
                            cols = slice(r * C, (r + 1) * C)
                            pe.matmul(ps_k[x][:, cols], uTs[x][:, r * W:(r + 1) * W], wT[:, 1, :], start=True, stop=False)
                            last = pe.matmul(ps_k[x][:, cols], ones1[:, :], negmax[:, :], start=False, stop=True)
                        last.then_inc(k_done[x], 1)
                    for x in range(2):
                        pe.wait_ge(ek_ready[x], i + 1)
                        pe.wait_ge(acc_read[x], i + 1)
                        for r in range(R):
                            pe.matmul(ps_m[x][:, 0:C], us[x][:, r, :], ek[x][:, r * C:(r + 1) * C],
                                      start=(r == 0), stop=(r == R - 1))
                        for r in range(R):
                            last = pe.matmul(ps_m[x][:, C:2 * C], ek[x][:, r * C:(r + 1) * C], ones[:, :],
                                             start=(r == 0), stop=(r == R - 1))
                        last.then_inc(acc_done[x], 1)
                for x in range(2):
                    pe.wait_ge(acc_read[x], NT // 2 + 1)
                pe.matmul(ps_x[:, 0:C], acc[:, 0, :], wT[:, 2, :], start=True, stop=True).then_inc(c_done, 1)
                pe.wait_ge(c_ready, 1)
                pe.transpose(ps_x[:, C:2 * C], ctxm[:, :], ident[:, :]).then_inc(ct_done, 1)
                pe.wait_ge(ct_ready, 1)
                pe.matmul(ps_x[:, 2 * C:3 * C], ctxt[:, :], wT[:, 3, :], start=True, stop=True).then_inc(g_done, 1)

            @block.scalar
            def _(act):
                with act.Fori(0, NT // 2) as i:
                    for x in range(2):
                        act.wait_ge(turned[x], i + 1)
                        act.copy(uTs[x][:, :], ps_t[x][:, :]).then_inc(uT_ready[x], 1)
                    for x in range(2):
                        act.wait_ge(k_done[x], i + 1)
                        act.wait_ge(acc_done[x], i + 1)
                        act.activation(ek[x][:, :], ps_k[x][:, :], ACT.Exp).then_inc(ek_ready[x], 1)

            @block.vector
            def _(dve):
                step = Chain(dve, dch)
                TT = dve.tensor_tensor
                step(dve.memset(acc[:, :, :], 0.0))
                for x in range(2):
                    dve.sem_inc(acc_read[x], 1)
                with step.loop(NT // 2, 2) as i:
                    for x in range(2):
                        dve.wait_ge(acc_done[x], i + 2)
                        step(TT(acc[:, :, :], acc[:, :, :], ps_m[x][:, 0:2 * C].rearrange("p (a c) -> p a c", a=2), ALU.add))
                        dve.sem_inc(acc_read[x], 1)
                step(dve.tensor_scalar(rsum[:, :], acc[:, 1, 0:1], float(TOK) * math.sqrt(D), None, ALU.mult))
                step(dve.reciprocal(rsum[:, :], rsum[:, :]))
                dve.wait_ge(c_done, 1)
                step(dve.scalar_tensor_tensor(out=ctxm[:, :], in0=ps_x[:, 0:C], scalar=rsum[:, 0:1],
                                              in1=heads[:, :, :].rearrange("p h d -> p (h d)"), op0=ALU.mult, op1=ALU.mult))
                dve.sem_inc(c_ready, 1)
                dve.wait_ge(ct_done, 1)
                dve.tensor_copy(ctxt[:, :], ps_x[:, C:2 * C]).then_inc(ct_ready, 1)
                dve.wait_ge(g_done, 1)
                step(dve.tensor_copy(g[:, :], ps_x[:, 2 * C:3 * C]))

        with ExitStack() as c2:
            s2 = Scope(nc, c2, tag + "c")
            bo_row = s2.sb("bo_row", [1, C])
            lnw = s2.sb("lnw", [P, C])

            def pair(name, shape):
                return [s2.sb(f"{name}{x}", shape) for x in range(2)]

            us, xr, z, out = (pair(n, [P, R, C]) for n in ("us", "xr", "z", "out"))
            uTs, qT = pair("uTs", [P, R * W]), pair("qT", [P, R * W])
            q = pair("q", [P, R * H, D])
            mx, den = pair("mx", [P, R * H]), pair("den", [P, R * H])
            st, mv = pair("st", [P, R, 6]), pair("mv", [P, R, 2])
            ve, rstd = pair("ve", [P, R]), pair("rstd", [P, R])
            half = s2.sb("half", [P, R])
            ps_t, ps_q, ps_y, ps_o = ([s2.ps(f"{n}{x}") for x in range(2)] for n in ("ps_t", "ps_q", "ps_y", "ps_o"))
            (xin, staged, turned, uT_ready, q_done, shifted, ex_ready, q_ready, flipped, qT_ready, o_done, z_ready,
             ve_ready, rstd_ready, scaled, out_ready, stored) = ([s2.sem(f"{n}{x}") for x in range(2)] for n in (
                 "xin", "staged", "turned", "uT_ready", "q_done", "shifted", "ex_ready", "q_ready", "flipped",
                 "qT_ready", "o_done", "z_ready", "ve_ready", "rstd_ready", "scaled", "out_ready", "stored"))
            loaded, made, dch, pch, tick, stick = (s2.sem(n) for n in ("loaded", "made", "dch", "pch", "tick", "stick"))
            block = c2.enter_context(nc.Block())
            xv = x4.rearrange("b t w c -> (b t) w c").rearrange("(i x r) w c -> x i w r c", r=R, x=2)
            ov = x5.rearrange("b t w c -> (b t) w c").rearrange("(i x r) w c -> x i w r c", r=R, x=2)
            TURNS = NT // 2

            @block.sync
            def _(sp):
                sp.dma_start(bo_row[:, :], b_out.unsqueeze(0)).then_inc(loaded, 16)
                sp.dma_start(lnw[:, :], ln_w.unsqueeze(0).broadcast_to([P, C])).then_inc(loaded, 16)
                for x in range(2):
                    sp.dma_start(xr[x][:, :, :], xv[x, 0]).then_inc(xin[x], 16)
                with sp.Fori(0, TURNS - 1) as i:
                    for x in range(2):
                        sp.wait_ge(out_ready[x], i + 1)
                        sp.sem_inc(stick, 1)
                        sp.dma_start(ov[x, i], out[x][:, :, :]).then_inc(stored[x], 16)
                        sp.dma_start(xr[x][:, :, :], xv[x, i + 1]).then_inc(xin[x], 16)
                for x in range(2):
                    sp.wait_ge(out_ready[x], TURNS)
                    sp.dma_start(ov[x, TURNS - 1], out[x][:, :, :]).then_inc(stored[x], 16)
                for x in range(2):
                    sp.wait_ge(stored[x], 16 * TURNS + 1)


            @block.gpsimd
            def _(pool):
                step = Chain(pool, pch)
                pool.memset(half[:, :], -0.5).then_inc(made, 1)
                pool.wait_ge(made, 1)
                pool.wait_ge(loaded, 32)
                with step.loop(TURNS, 2) as i:
                    for x in range(2):
                        pool.wait_ge(ve_ready[x], i + 1)
                        pool.tensor_tensor(rstd[x][:, :], ve[x][:, :], half[:, :], ALU.pow).then_inc(rstd_ready[x], 1)
                    for x in range(2):
                        pool.wait_ge(scaled[x], i + 2)
                        step(pool.tensor_tensor(out[x][:, :, :], out[x][:, :, :],
                                                lnw[:, :].unsqueeze(1).broadcast_to([P, R, C]), ALU.mult))
                        pool.wait_ge(xin[x], 16 * (i + 1))
                        pool.tensor_tensor(out[x][:, :, :], out[x][:, :, :], xr[x][:, :, :], ALU.add
                                           ).then_inc(out_ready[x], 1)

            @block.tensor
            def _(pe):
                pe.wait_ge(loaded, 32)

                def turn_rows(i, x):
                    pe.wait_ge(staged[x], i + 1)
                    for r in range(R):
                        last = pe.transpose(ps_t[x][:, r * W:(r + 1) * W], us[x][:, r, :], ident[:, :])
                    last.then_inc(turned[x], 1)

                def queries(i, x):
                    pe.wait_ge(uT_ready[x], i + 1)
                    for r in range(R):
                        last = pe.matmul(ps_q[x][:, r * C:(r + 1) * C], uTs[x][:, r * W:(r + 1) * W], wT[:, 0, :],
                                         start=True, stop=True)
                    last.then_inc(q_done[x], 1)

                def turn_queries(i, x):
                    pe.wait_ge(q_ready[x], i + 1)
                    for r in range(R):
                        last = pe.transpose(ps_y[x][:, r * W:(r + 1) * W],
                                            q[x][:, r * H:(r + 1) * H, :].rearrange("p h d -> p (h d)"), ident[:, :])
                    last.then_inc(flipped[x], 1)

                def project(i, x):
                    pe.wait_ge(qT_ready[x], i + 1)
                    for r in range(R):
                        cols = slice(r * C, (r + 1) * C)
                        pe.matmul(ps_o[x][:, cols], qT[x][:, r * W:(r + 1) * W], g[:, :], start=True, stop=False)
                        last = pe.matmul(ps_o[x][:, cols], ones1[:, :], bo_row[:, :], start=False, stop=True)
                    last.then_inc(o_done[x], 1)

                for part in (turn_rows, queries, turn_queries):
                    for x in range(2):
                        part(0, x)
                with pe.Fori(0, TURNS - 1) as i:
                    for x in range(2):
                        turn_rows(i + 1, x)
                    for x in range(2):
                        project(i, x)
                    for x in range(2):
                        queries(i + 1, x)
                    for x in range(2):
                        turn_queries(i + 1, x)
                for x in range(2):
                    project(TURNS - 1, x)

            @block.scalar
            def _(act):
                def stage(i, x):
                    act.copy(us[x][:, :, :], u[:, bass.ds(i * 2 * R + x * R, R), :]).then_inc(staged[x], 1)

                def rows_in(i, x):
                    act.wait_ge(turned[x], i + 1)
                    act.copy(uTs[x][:, :], ps_t[x][:, :]).then_inc(uT_ready[x], 1)

                def exponentials(i, x):
                    act.wait_ge(shifted[x], i + 1)
                    act.activation(q[x][:, :, :], q[x][:, :, :], ACT.Exp).then_inc(ex_ready[x], 1)

                def queries_in(i, x):
                    act.wait_ge(flipped[x], i + 1)
                    act.copy(qT[x][:, :], ps_y[x][:, :]).then_inc(qT_ready[x], 1)

                def sums_in(i, x):
                    act.wait_ge(o_done[x], i + 1)
                    act.wait_ge(scaled[x], i + 1)
                    act.copy(z[x][:, :, :], ps_o[x][:, :].rearrange("p (r c) -> p r c", r=R)).then_inc(z_ready[x], 1)

                def turn(i, first=False, last=False):
                    for x in range(2):
                        rows_in(i, x)
                    if not last:
                        for x in range(2):
                            stage(i + 1, x)
                    if not first:
                        for x in range(2):
                            sums_in(i - 1, x)
                    for x in range(2):
                        exponentials(i, x)
                    for x in range(2):
                        queries_in(i, x)

                for x in range(2):
                    stage(0, x)
                turn(0, first=True)
                with act.Fori(0, TURNS - 2) as i:
                    turn(i + 1)
                turn(TURNS - 1, last=True)
                for x in range(2):
                    sums_in(TURNS - 1, x)

            @block.vector
            def _(dve):
                step = Chain(dve, dch)
                TT = dve.tensor_tensor

                def shift(i, x):
                    dve.wait_ge(q_done[x], i + 1)
                    qv = ps_q[x][:, :].rearrange("p (h d) -> p h d", d=D)
                    step(dve.tensor_reduce(mx[x][:, :], qv, AX.X, ALU.max))
                    step(TT(q[x][:, :, :], qv, mx[x][:, :].unsqueeze(2).broadcast_to([P, R * H, D]), ALU.subtract))
                    dve.sem_inc(shifted[x], 1)

                def divide(i, x):
                    dve.wait_ge(ex_ready[x], i + 1)
                    step(dve.tensor_reduce(den[x][:, :], q[x][:, :, :], AX.X, ALU.add))
                    step(dve.reciprocal(den[x][:, :], den[x][:, :]))
                    step(TT(q[x][:, :, :], q[x][:, :, :], den[x][:, :].unsqueeze(2).broadcast_to([P, R * H, D]), ALU.mult))
                    dve.sem_inc(q_ready[x], 1)

                def moments(i, x):
                    dve.wait_ge(z_ready[x], i + 1)
                    dve.sem_inc(tick, 1)
                    for r in range(R):
                        step.mark(dve.bn_stats(st[x][:, r, :], z[x][:, r, :]))
                    step.join()
                    dve.sem_inc(tick, 1)
                    for r in range(R):
                        step.mark(dve.bn_aggr(mv[x][:, r, :], st[x][:, r, :]))
                    step.join()
                    step(dve.tensor_scalar(ve[x][:, :], mv[x][:, :, 1], eps, None, ALU.add))
                    dve.sem_inc(ve_ready[x], 1)

                def scale(i, x):
                    dve.wait_ge(rstd_ready[x], i + 1)
                    dve.wait_ge(stored[x], 16 * i + 1)
                    for r in range(R):
                        step.mark(dve.tensor_scalar(out[x][:, r, :], z[x][:, r, :], mv[x][:, r, 0:1],
                                                    rstd[x][:, r:r + 1], ALU.subtract, ALU.mult))
                    step.join()
                    dve.sem_inc(scaled[x], 1)

                for x in range(2):
                    dve.sem_inc(stored[x], 1)
                    dve.sem_inc(scaled[x], 1)
                for x in range(2):
                    shift(0, x)
                for x in range(2):
                    divide(0, x)
                with step.loop(TURNS - 1, 2 * (2 + 3 + 2 * R + 1 + R)) as i:
                    for x in range(2):
                        shift(i + 1, x)
                        moments(i, x)
                    for x in range(2):
                        divide(i + 1, x)
                        scale(i, x)
                for part in (moments, scale):
                    for x in range(2):
                        part(TURNS - 1, x)


def recurrent_network(nc, x5, Wm, Vm, gamma, beta, y_out, tag="rnn", eps=1e-5):
    L = T * W
    S = 64
    CH = L // S
    N = B * CH
    G = 2
    NG = N // G
    WARM = 32
    TOL = 2.0 ** -19
    R = 4
    HALVES = W // S
    NT = BT // R
    with ExitStack() as ctx:
        s = Scope(nc, ctx, tag)
        uT = s.sb("uT", [P, S, N])
        ident = s.sb("ident", [P, P])
        wT = s.sb("wT", [P, C])
        wn = s.sb("wn", [P, C])
        wnT, vT = s.sb("wnT", [P, C]), s.sb("vT", [P, C])
        shift = s.sb("shift", [P, 1])
        with ExitStack() as cu:
            u = Scope(nc, cu, tag + "u").sb("u", [P, BT, C])
            normalised_tokens(nc, x5, u, tag + "n")
            s2 = Scope(nc, cu, tag + "a")
            wl = s2.sb("wl", [P, 2, C])
            gb = s2.sb("gb", [P, 2])
            us = [s2.sb(f"us{j}", [P, R, C]) for j in range(2)]
            uTs = [s2.sb(f"uTs{j}", [P, R * W]) for j in range(2)]
            st = s2.sb("st", [P, NT, 6])
            mv = s2.sb("mv", [P, 2])
            ve, rstd, half, a = (s2.sb(n, [P, 1]) for n in ("ve", "rstd", "half", "a"))
            ps_w = s2.ps("ps_w")
            ps_t = [s2.ps(f"ps_t{j}") for j in range(2)]
            ps_x = [s2.ps(f"ps_x{j}") for j in range(2)]
            (loaded, made, w_done, w_ready, staged, turned, uT_ready, placed, x_done, x_read, ve_ready,
             rstd_ready, wn_ready, wn_done, dch, pch, tick) = (s2.sem(n) for n in (
                 "loaded", "made", "w_done", "w_ready", "staged", "turned", "uT_ready", "placed", "x_done",
                 "x_read", "ve_ready", "rstd_ready", "wn_ready", "wn_done", "dch", "pch", "tick"))
            block = cu.enter_context(nc.Block())

            @block.sync
            def _(sp):
                sp.dma_start(wl[:, 0, :], Wm).then_inc(loaded, 16)
                sp.dma_start(wl[:, 1, :], Vm).then_inc(loaded, 16)
                sp.dma_start(gb[:, 0:1], gamma.unsqueeze(1)).then_inc(loaded, 16)
                sp.dma_start(gb[:, 1:2], beta.unsqueeze(1)).then_inc(loaded, 16)

            @block.gpsimd
            def _(pool):
                step = Chain(pool, pch)
                fill_identity(pool, step, ident)
                step(pool.memset(half[:, :], -0.5))
                pool.sem_inc(made, 1)
                with pool.Fori(0, NT // 2) as i:
                    for j in range(2):
                        pool.wait_ge(turned, 2 * i)
                        pool.tensor_copy(us[j][:, :, :], u[:, bass.ds(i * 2 * R + j * R, R), :]).then_inc(staged, 1)
                pool.wait_ge(ve_ready, 1)
                pool.tensor_tensor(rstd[:, :], ve[:, :], half[:, :], ALU.pow).then_inc(rstd_ready, 1)

            @block.tensor
            def _(pe):
                pe.wait_ge(loaded, 64)
                pe.wait_ge(made, 1)
                for j in range(2):
                    last = pe.transpose(ps_w[:, j * C:(j + 1) * C], wl[:, j, :], ident[:, :])
                last.then_inc(w_done, 1)
                pe.wait_ge(w_ready, 1)
                with pe.Fori(0, NT // 2) as i:
                    for j in range(2):
                        pe.wait_ge(staged, 2 * i + j + 1)
                        pe.wait_ge(placed, 2 * i)
                        for r in range(R):
                            last = pe.transpose(ps_t[j][:, r * W:(r + 1) * W], us[j][:, r, :], ident[:, :])
                        last.then_inc(turned, 1)
                        pe.wait_ge(uT_ready, 2 * i + j + 1)
                        pe.wait_ge(x_read, 2 * i)
                        pe.matmul(ps_x[j][:, :], wT[:, :], uTs[j][:, :], start=True, stop=True).then_inc(x_done, 1)
                pe.wait_ge(wn_ready, 1)
                pe.transpose(ps_w[:, 2 * C:3 * C], wn[:, :], ident[:, :]).then_inc(wn_done, 1)

            @block.scalar
            def _(act):
                act.wait_ge(w_done, 1)
                act.copy(wT[:, :], ps_w[:, 0:C]).then_inc(tick, 1)
                act.copy(vT[:, :], ps_w[:, C:2 * C]).then_inc(w_ready, 1)
                with act.Fori(0, NT // 2) as i:
                    for j in range(2):
                        act.wait_ge(turned, 2 * i + j + 1)
                        act.wait_ge(x_done, 2 * i)
                        act.copy(uTs[j][:, :], ps_t[j][:, :]).then_inc(uT_ready, 1)
                        col = bass.ds(i * 2 * R * HALVES + j * R * HALVES, R * HALVES)
                        act.copy(uT[:, :, col], ps_t[j][:, :].rearrange("p (q s) -> p s q", s=S)).then_inc(placed, 1)
                act.wait_ge(wn_done, 1)
                act.copy(wnT[:, :], ps_w[:, 2 * C:3 * C]).then_inc(tick, 1)

            @block.vector
            def _(dve):
                step = Chain(dve, dch)
                with dve.Fori(0, NT // 2) as i:
                    for j in range(2):
                        dve.wait_ge(x_done, 2 * i + j + 1)
                        dve.bn_stats(st[:, bass.ds(i * 2 + j, 1), :].rearrange("p a b -> p (a b)"), ps_x[j][:, :]).then_inc(x_read, 1)
                dve.wait_ge(x_read, NT)
                step(dve.bn_aggr(mv[:, :], st[:, :, :].rearrange("p n k -> p (n k)")))
                step(dve.tensor_scalar(ve[:, :], mv[:, 1:2], eps, None, ALU.add))
                dve.sem_inc(ve_ready, 1)
                dve.wait_ge(rstd_ready, 1)
                step(dve.tensor_tensor(a[:, :], rstd[:, :], gb[:, 0:1], ALU.mult))
                step(dve.tensor_scalar(wn[:, :], wl[:, 0, :], a[:, 0:1], None, ALU.mult))
                dve.sem_inc(wn_ready, 1)
                step(dve.tensor_tensor(shift[:, :], mv[:, 0:1], a[:, :], ALU.mult))
                step(dve.tensor_tensor(shift[:, :], gb[:, 1:2], shift[:, :], ALU.subtract))

        y = s.sb("y", [P, S + 1, N])
        ys = s.sb("ys", [P, 2, N])
        ends = s.sb("ends", [P, B, CH])
        diff = s.sb("diff", [P, N])
        worst = s.sb("worst", [P, 1])
        row = s.sb("row", [1, P])
        flag = s.sb("flag", [1, 1])
        flag_i = s.sb("flag_i", [1, 1], mybir.dt.int32)

        def pe_steps(pe, ps, states, first, steps, z_ready, y_ready):
            with pe.Fori(0, steps // 2) as i:
                for p in range(2):
                    for g in range(G):
                        cols = slice(g * NG, (g + 1) * NG)
                        inp = uT[:, bass.ds(i * 2 + (first + p), 1), cols].rearrange("p a n -> p (a n)")
                        prev = states(i, p)[0][:, :, cols].rearrange("p a n -> p (a n)")
                        dst = ps[p * G + g][:, 0:NG]
                        pe.matmul(dst, wnT[:, :], inp, start=True, stop=False)
                        pe.wait_ge(y_ready[g], i * 2 + p)
                        pe.matmul(dst, vT[:, :], prev, start=False, stop=True).then_inc(z_ready[g], 1)

        def act_steps(act, ps, states, steps, z_ready, y_ready):
            with act.Fori(0, steps // 2) as i:
                for p in range(2):
                    for g in range(G):
                        cols = slice(g * NG, (g + 1) * NG)
                        nxt = states(i, p)[1][:, :, cols].rearrange("p a n -> p (a n)")
                        act.wait_ge(z_ready[g], i * 2 + p + 1)
                        act.activation(nxt, ps[p * G + g][:, 0:NG], ACT.Sigmoid, bias=shift[:, 0:1]).then_inc(y_ready[g], 1)

        def in_y(i, p):
            return y[:, bass.ds(i * 2 + p, 1), :], y[:, bass.ds(i * 2 + p + 1, 1), :]

        def in_ys(i, p):
            return ys[:, p:p + 1, :], ys[:, 1 - p:2 - p, :]

        def block_of(name, states, first, steps, before, after):
            with ExitStack() as c2:
                s2 = Scope(nc, c2, f"{tag}{name}")
                ps = [s2.ps(f"ps{j}") for j in range(2 * G)]
                z_ready = [s2.sem(f"z_ready{g}") for g in range(G)]
                y_ready = [s2.sem(f"y_ready{g}") for g in range(G)]
                begun, dch = s2.sem("begun"), s2.sem("dch")
                block = c2.enter_context(nc.Block())

                @block.tensor
                def _(pe):
                    pe.wait_ge(begun, 1)
                    pe_steps(pe, ps, states, first, steps, z_ready, y_ready)

                @block.scalar
                def _(act):
                    act_steps(act, ps, states, steps, z_ready, y_ready)

                @block.vector
                def _(dve):
                    step = Chain(dve, dch)
                    before(dve, step)
                    dve.sem_inc(begun, 1)
                    for g in range(G):
                        dve.wait_ge(y_ready[g], steps)
                    after(dve, step)

        def starts_from(src):
            def do(dve, step):
                first = y[:, 0, :].rearrange("p (b k) -> p b k", b=B)
                step.mark(dve.memset(first[:, :, 0:1], 0.0))
                step.mark(dve.tensor_copy(first[:, :, 1:CH], src[:, :, 0:CH - 1]))
                step.join()
            return do

        def measure(dve, step):
            first = y[:, 0, :].rearrange("p (b k) -> p b k", b=B)
            d = diff[:, :].rearrange("p (b k) -> p b k", b=B)
            step(dve.tensor_copy(ends[:, :, :], y[:, S, :].rearrange("p (b k) -> p b k", b=B)))
            step(dve.memset(diff[:, :], 0.0))
            step(dve.tensor_tensor(d[:, :, 1:CH], ends[:, :, 0:CH - 1], first[:, :, 1:CH], ALU.subtract))
            step(dve.tensor_reduce(worst[:, :], diff[:, :], AX.X, ALU.max, apply_absolute_value=True))

        nothing = lambda dve, step: None
        block_of("w", in_ys, S - WARM, WARM, lambda dve, step: step(dve.memset(ys[:, 0, :], 0.0)), nothing)
        block_of("m", in_y, 0, S, starts_from(ys[:, 0, :].rearrange("p (b k) -> p b k", b=B)), measure)

        with ExitStack() as c2:
            s2 = Scope(nc, c2, tag + "f")
            ps = s2.ps("ps")
            turned, copied, dch = s2.sem("turned"), s2.sem("copied"), s2.sem("dch")
            block = c2.enter_context(nc.Block())

            @block.tensor
            def _(pe):
                pe.transpose(ps[0:1, 0:P], worst[:, :], ident[:, :]).then_inc(turned, 1)

            @block.vector
            def _(dve):
                step = Chain(dve, dch)
                dve.wait_ge(turned, 1)
                step(dve.tensor_reduce(flag[:, :], ps[0:1, 0:P], AX.X, ALU.max))
                step(dve.tensor_scalar(flag_i[:, :], flag[:, :], TOL, None, ALU.is_gt))

        again = nc.values_load(flag_i[0:1, 0:1], min_val=0, max_val=1)
        with nc.If(again > 0):
            with nc.Fori(0, CH - 1):
                block_of("r", in_y, 0, S, starts_from(ends), measure)

        with ExitStack() as c2:
            s2 = Scope(nc, c2, tag + "o")
            xr = [s2.sb(f"xr{j}", [P, R, C]) for j in range(2)]
            out = [s2.sb(f"out{j}", [P, R, C]) for j in range(2)]
            yst = [s2.sb(f"yst{j}", [P, R * W]) for j in range(2)]
            ps = [s2.ps(f"ps{j}") for j in range(2)]
            xin = [s2.sem(f"xin{j}") for j in range(2)]
            staged, turned, added, stored = (s2.sem(n) for n in ("staged", "turned", "added", "stored"))
            block = c2.enter_context(nc.Block())
            xv = x5.rearrange("b t w c -> (b t) w c").rearrange("(i j r) w c -> i j w r c", j=2, r=R)
            ov = y_out.rearrange("b t w c -> (b t) w c").rearrange("(i j r) w c -> i j w r c", j=2, r=R)

            @block.sync
            def _(sp):
                with sp.Fori(0, NT // 2) as i:
                    for j in range(2):
                        sp.wait_ge(added, 2 * i)
                        sp.dma_start(xr[j][:, :, :], xv[i, j]).then_inc(xin[j], 16)

            @block.gpsimd
            def _(pool):
                with pool.Fori(0, NT // 2) as i:
                    for j in range(2):
                        pool.wait_ge(turned, 2 * i)
                        col = bass.ds(i * 2 * R * HALVES + j * R * HALVES, R * HALVES)
                        pool.tensor_copy(yst[j][:, :].rearrange("p (q s) -> p s q", s=S), y[:, 1:S + 1, col]
                                         ).then_inc(staged, 1)

            @block.tensor
            def _(pe):
                with pe.Fori(0, NT // 2) as i:
                    for j in range(2):
                        pe.wait_ge(staged, 2 * i + j + 1)
                        pe.wait_ge(added, 2 * i)
                        for r in range(R):
                            last = pe.transpose(ps[j][:, r * C:(r + 1) * C], yst[j][:, r * W:(r + 1) * W], ident[:, :])
                        last.then_inc(turned, 1)

            @block.vector
            def _(dve):
                with dve.Fori(0, NT // 2) as i:
                    for j in range(2):
                        dve.wait_ge(turned, 2 * i + j + 1)
                        dve.wait_ge(xin[j], 16 * i + 16)
                        dve.wait_ge(stored, 32 * i)
                        dve.tensor_tensor(out[j][:, :, :], xr[j][:, :, :],
                                          ps[j][:, :].rearrange("p (r c) -> p r c", r=R), ALU.add).then_inc(added, 1)

            @block.scalar
            def _(act):
                with act.Fori(0, NT // 2) as i:
                    for j in range(2):
                        act.wait_ge(added, 2 * i + j + 1)
                        act.dma_start(ov[i, j], out[j][:, :, :]).then_inc(stored, 16)
                act.wait_ge(stored, 16 * NT)


def hybrid_stack(nc, d, out):
    shape = (B, T, W, C)

    def dram(name, shape):
        return nc.dram_tensor(name, shape, f32, kind="Internal").ap()

    def layer(prefix, *names):
        return [d[f"{prefix}_{n}"] for n in names]

    tabs = inline_tables(nc)
    x1, x2, x3, x4, x5 = (dram(f"x{n}", shape) for n in range(1, 6))

    h0 = dram("h0", (BT, W, C))
    with nc.sbuf_tensor("hg0", [P, BT, C], f32) as hg:
        group_norm(nc, d["x"], hg, "gn0")
        graph_attention(nc, hg, *layer("L0_conv", "adj", "Wq", "Wk", "Wv", "Wo", "bo", "ns_g", "ns_b"), h0)
    mamba(nc, h0, d["x"], *layer("L0_conv", "in_proj", "conv_w", "conv_b", "x_proj", "dt_w", "dt_b", "A_log", "Dp",
                                 "out_w", "out_b", "nt_g", "nt_b"), x1)

    wts = {n[len("L1_conv_"):]: v for n, v in d.items() if n.startswith("L1_conv_")}
    tok, tnd, mix = (dram(n, (BT, W, C)) for n in ("tokens", "tokens_normalised", "mix"))
    gram = dram("gram", (BT, BT))
    prob = dram("prob", (NH, B, T, T))
    wd = dram("mode_weights", (NH, NKY, 2, NKX))
    with ExitStack() as ctx:
        def sb(name, shape):
            return ctx.enter_context(nc.sbuf_tensor(name, shape, f32))

        spec = sb("spec", [2 * 32, BT, NKY])
        const = sb("const", [P, 1])
        xh = sb("xh", [P, NKY, 2, NKX])
        with nc.sbuf_tensor("hg1", [P, BT, C], f32) as hg:
            group_norm(nc, x1, hg, "gn1")
            token_images(nc, hg, wts["norm1_g"], wts["norm1_b"], tok, tnd)
            token_spectra(nc, hg, tabs, xh, gram)
        pt = sb("pt", [P, NH, BT])
        mt = sb("mt", [P, BT])
        token_attention(nc, xh, gram, tabs, wts, prob, pt, mt)
        attended_spectrum(nc, xh, pt, wts, wd, spec, const)
        mixed_images(nc, tnd, mt, mix)
        token_mixer(nc, spec, const, mix, tok, x1, wts, tabs, x2)

    linear_attention(nc, x2, *layer("L2_attn", "Wq", "bq", "Wk", "bk", "Wv", "bv", "Wo", "bo"), x3)
    routed_experts(nc, x3, *layer("L2_ffn", "gate_w", "gate_b", "weight1", "weight2"), x4)

    softmax_attention(nc, x4, *layer("L3_attn", "w_in", "w_out", "b_out", "ln_w"), x5)
    recurrent_network(nc, x5, *layer("L3_ffn", "W", "V", "gamma", "beta"), out)


def kernel(**inputs):
    import concourse.bacc as bacc
    from concourse.bass_utils import run_bass_kernel_spmd

    nc = bacc.Bacc("TRN2", target_bir_lowering=False, num_devices=1)
    arrays, d = {}, {}
    for name, a in inputs.items():
        a = np.ascontiguousarray(a)
        arrays[f"in_{name}"] = a
        d[name] = nc.dram_tensor(f"in_{name}", a.shape, mybir.dt.from_np(a.dtype), kind="ExternalInput").ap()
    out = nc.dram_tensor("out_0", (B, T, W, C), f32, kind="ExternalOutput").ap()
    hybrid_stack(nc, d, out)
    r = run_bass_kernel_spmd(nc, [arrays], core_ids=[0])
    return r.results[0]["out_0"]
```
